# Optimizing a Trainium2 kernel written in Bass

```python
import numpy as np
import jax
import jax.numpy as jnp

def _softmax(x, axis=-1):
    return jax.nn.softmax(x, axis=axis)

def _gelu(x):
    return jax.nn.gelu(x, approximate=True)

def _silu(x):
    return jax.nn.silu(x)

def _sigmoid(x):
    return jax.nn.sigmoid(x)

def _layernorm(x, axis=-1, eps=1e-05):
    m = jnp.mean(x, axis=axis, keepdims=True)
    v = jnp.var(x, axis=axis, keepdims=True)
    return (x - m) / jnp.sqrt(v + eps)

def _scatter_add(tgt, idx, src, axis=0):
    return tgt.at[idx].add(src)

def _segment_sum(src, seg, n):
    return jax.ops.segment_sum(src, seg, n)
kernel_name = 'mk_seq_preln_d4_jaxref_r8_dcc6ca'

def setup_inputs(seed: int=0):
    np.random.seed(seed)
    _w = jnp.asarray

    def _L0_attn_setup():
        import jax, jax.numpy as jnp
        import numpy as np
        B, T, D = (4, 512, 256)
        LAYER_ID, N_LAYERS = (0, 12)
        LN_EPS = 1e-05

        def _wkv(w, u, k, v):
            Bb, Tt, Dd = k.shape
            neg_ew = -jnp.exp(w)

            def step(carry, kv):
                aa, bb, pp = carry
                kt, vt = kv
                qt = jnp.maximum(pp, kt + u)
                e1 = jnp.exp(pp - qt)
                e2 = jnp.exp(kt + u - qt)
                out = (e1 * aa + e2 * vt) / (e1 * bb + e2)
                pp_new = jnp.maximum(pp + neg_ew, kt)
                f1 = jnp.exp(pp - pp_new)
                f2 = jnp.exp(kt - pp_new)
                return ((f1 * aa + f2 * vt, f1 * bb + f2, pp_new), out)
            init = (jnp.zeros((Bb, Dd), k.dtype), jnp.zeros((Bb, Dd), k.dtype), jnp.full((Bb, Dd), -1e+38, k.dtype))
            kT = jnp.swapaxes(k, 0, 1)
            vT = jnp.swapaxes(v, 0, 1)
            _, outT = jax.lax.scan(step, init, (kT, vT))
            return jnp.swapaxes(outT, 0, 1)
        key = jax.random.key(seed)
        ks = jax.random.split(key, 9)
        s = 0.02
        x = jax.random.normal(ks[0], (B, T, D), jnp.float32)
        Wk = jax.random.normal(ks[1], (D, D), jnp.float32) * s
        Wv = jax.random.normal(ks[2], (D, D), jnp.float32) * s
        Wr = jax.random.normal(ks[3], (D, D), jnp.float32) * s
        Wo = jax.random.normal(ks[4], (D, D), jnp.float32) * s
        tm_k = jax.random.uniform(ks[5], (1, 1, D), jnp.float32)
        tm_v = jax.random.uniform(ks[6], (1, 1, D), jnp.float32)
        tm_r = jax.random.uniform(ks[7], (1, 1, D), jnp.float32)
        ratio_0_to_1 = LAYER_ID / max(N_LAYERS - 1, 1)
        ratio_1_to_almost_0 = 1.0 - LAYER_ID / N_LAYERS
        i = jnp.arange(D, dtype=jnp.float32)
        time_decay = -5.0 + 8.0 * (i / (D - 1)) ** (0.7 + 1.3 * ratio_0_to_1)
        zigzag = (jnp.arange(D) % 3 - 1).astype(jnp.float32) * ratio_1_to_almost_0
        time_first = jnp.full((D,), jnp.log(jnp.float32(0.3))) + zigzag
        ln_g = jnp.ones((D,), jnp.float32)
        ln_b = jnp.zeros((D,), jnp.float32)
        return {'x': x, 'Wk': Wk, 'Wv': Wv, 'Wr': Wr, 'Wo': Wo, 'tm_k': tm_k, 'tm_v': tm_v, 'tm_r': tm_r, 'time_decay': time_decay, 'time_first': time_first, 'ln_g': ln_g, 'ln_b': ln_b}
    _L0_attn_in = _L0_attn_setup()

    def _L0_ffn_setup():
        import jax, jax.numpy as jnp
        import numpy as np
        B, S, D_IN, D_OUT = (4, 256, 256, 256)
        EPS = 1e-10
        key = jax.random.key(seed)
        kx, kw, kb = jax.random.split(key, 3)
        x = jax.random.normal(kx, (B, S, D_IN), dtype=jnp.float32)
        weight = jax.random.normal(kw, (D_OUT, D_IN), dtype=jnp.float32) * 0.02
        bias = jax.random.normal(kb, (D_OUT,), dtype=jnp.float32) * 0.02
        return {'x': x, 'weight': weight, 'bias': bias}
    _L0_ffn_in = _L0_ffn_setup()

    def _L1_attn_setup():
        import jax, jax.numpy as jnp
        import numpy as np
        D_MODEL = 256
        NHEADS = 16
        NOPE = 128
        ROPE = 64
        VDIM = 128
        QLORA = 192
        KVLORA = 64
        QHD = NOPE + ROPE
        B, T = (1, 512)

        def rms_norm(x, w):
            eps = jnp.finfo(x.dtype).eps
            var = jnp.mean(x * x, axis=-1, keepdims=True)
            return x * jax.lax.rsqrt(var + eps) * w

        def rope_cos_sin(T, dim):
            freqs = 1.0 / 10000.0 ** (jnp.arange(0, dim, 2, dtype=jnp.float32) / dim)
            ang = jnp.arange(T, dtype=jnp.float32)[:, None] * freqs[None, :]
            return (jnp.cos(ang), jnp.sin(ang))

        def apply_rope(x, cos, sin):
            xe = x[..., 0::2]
            xo = x[..., 1::2]
            re = xe * cos - xo * sin
            ro = xo * cos + xe * sin
            return jnp.stack([re, ro], axis=-1).reshape(x.shape)
        key = jax.random.key(seed)
        ks = jax.random.split(key, 6)
        s = 0.02
        return {'x': jax.random.normal(ks[0], (B, T, D_MODEL), jnp.float32), 'Wqa': jax.random.normal(ks[1], (D_MODEL, QLORA), jnp.float32) * s, 'q_ln_w': jnp.ones((QLORA,), jnp.float32), 'Wqb': jax.random.normal(ks[2], (QLORA, NHEADS * QHD), jnp.float32) * s, 'Wkva': jax.random.normal(ks[3], (D_MODEL, KVLORA + ROPE), jnp.float32) * s, 'kv_ln_w': jnp.ones((KVLORA,), jnp.float32), 'Wkvb': jax.random.normal(ks[4], (KVLORA, NHEADS * (NOPE + VDIM)), jnp.float32) * s, 'Wo': jax.random.normal(ks[5], (NHEADS * VDIM, D_MODEL), jnp.float32) * s}
    _L1_attn_in = _L1_attn_setup()

    def _L1_ffn_setup():
        import jax, jax.numpy as jnp
        import numpy as np
        DIM = 256
        HID = 704
        ZERO_POINT = 128.0

        def _qlinear(x, wq, scale):
            W = (wq.astype(jnp.float32) - ZERO_POINT) * scale[:, None]
            return jnp.einsum('bsd,hd->bsh', x, W)
        key = jax.random.key(seed)
        ks = jax.random.split(key, 7)
        B, S = (4, 256)
        sg = jax.random.uniform(ks[1], (HID,)) * (0.02 / np.sqrt(DIM)) + 0.0001
        su = jax.random.uniform(ks[3], (HID,)) * (0.02 / np.sqrt(DIM)) + 0.0001
        sd = jax.random.uniform(ks[5], (DIM,)) * (0.02 / np.sqrt(HID)) + 0.0001
        return {'x': jax.random.normal(ks[0], (B, S, DIM), dtype=jnp.float32), 'wq_gate': jax.random.randint(ks[2], (HID, DIM), 0, 32, dtype=jnp.int32), 's_gate': sg, 'wq_up': jax.random.randint(ks[4], (HID, DIM), 0, 32, dtype=jnp.int32), 's_up': su, 'wq_down': jax.random.randint(ks[6], (DIM, HID), 0, 32, dtype=jnp.int32), 's_down': sd}
    _L1_ffn_in = _L1_ffn_setup()

    def _L2_attn_setup():
        import jax, jax.numpy as jnp
        import numpy as np
        B, T, FEATS, HEAD = (2, 256, 256, 16)
        DIM_HEAD = FEATS // HEAD
        EPS = float(jnp.finfo(jnp.float32).eps)

        def _rms_norm(u, g):
            return u * jax.lax.rsqrt(jnp.mean(u * u, axis=-1, keepdims=True) + EPS) * g
        key = jax.random.key(seed)
        kx, kw = jax.random.split(key)
        x = jax.random.normal(kx, (B, T, FEATS), dtype=jnp.float32)
        W = jax.random.normal(kw, (FEATS, FEATS), dtype=jnp.float32) / np.sqrt(FEATS)
        g1 = jnp.ones((DIM_HEAD,), dtype=jnp.float32)
        g2 = jnp.ones((DIM_HEAD,), dtype=jnp.float32)
        g3 = jnp.ones((DIM_HEAD,), dtype=jnp.float32)
        return {'x': x, 'W': W, 'g1': g1, 'g2': g2, 'g3': g3}
    _L2_attn_in = _L2_attn_setup()

    def _L2_ffn_setup():
        import jax, jax.numpy as jnp
        import numpy as np
        B, S, D_IN, D_OUT, E = (4, 128, 256, 256, 32)
        MASK_DENSITY = 0.3
        THRESH = 0.5
        key = jax.random.key(seed)
        k_x, k_w, k_m, k_r = jax.random.split(key, 4)
        x = jax.random.normal(k_x, (B, S, D_IN), dtype=jnp.float32)
        bound = np.sqrt(1.0 / D_IN) * np.sqrt(3.0)
        weight = jax.random.uniform(k_w, (D_OUT, D_IN), minval=-bound, maxval=bound, dtype=jnp.float32)
        scale = jnp.ones((D_OUT,), dtype=jnp.float32)
        expert_masks = (jax.random.uniform(k_m, (E, D_OUT, D_IN)) < MASK_DENSITY).astype(jnp.float32)
        router_w = 0.01 * jax.random.normal(k_r, (E, D_IN), dtype=jnp.float32)
        return {'x': x, 'weight': weight, 'scale': scale, 'expert_masks': expert_masks, 'router_w': router_w}
    _L2_ffn_in = _L2_ffn_setup()

    def _L3_attn_setup():
        import jax, jax.numpy as jnp
        import numpy as np
        SEQ, BATCH, HIDDEN = (256, 2, 256)
        NUM_HEADS = 16
        HEAD_DIM = HIDDEN // NUM_HEADS
        key = jax.random.key(seed)
        k1, k2, k3, k4, k5 = jax.random.split(key, 5)
        scale = 1.0 / np.sqrt(HIDDEN)
        return {'hidden_states': jax.random.normal(k1, (SEQ, BATCH, HIDDEN), dtype=jnp.float32), 'w_qkv': jax.random.normal(k2, (3 * HIDDEN, HIDDEN), dtype=jnp.float32) * scale, 'b_qkv': jax.random.normal(k3, (3 * HIDDEN,), dtype=jnp.float32) * 0.01, 'w_dense': jax.random.normal(k4, (HIDDEN, HIDDEN), dtype=jnp.float32) * scale, 'b_dense': jax.random.normal(k5, (HIDDEN,), dtype=jnp.float32) * 0.01}
    _L3_attn_in = _L3_attn_setup()

    def _L3_ffn_setup():
        import jax, jax.numpy as jnp
        import numpy as np
        B, S, H = (1, 256, 256)
        E, K, I = (16, 4, 176)
        IS = 352
        CAP = 128
        key = jax.random.key(seed)
        ks = jax.random.split(key, 8)
        sc = 0.02
        return {'hidden_states': jax.random.normal(ks[0], (B, S, H), jnp.float32), 'gate_w': jax.random.normal(ks[1], (E, H), jnp.float32) * sc, 'w_gate': jax.random.normal(ks[2], (E, H, I), jnp.float32) * sc, 'w_up': jax.random.normal(ks[3], (E, H, I), jnp.float32) * sc, 'w_down': jax.random.normal(ks[4], (E, I, H), jnp.float32) * sc, 'sw_gate': jax.random.normal(ks[5], (H, IS), jnp.float32) * sc, 'sw_up': jax.random.normal(ks[6], (H, IS), jnp.float32) * sc, 'sw_down': jax.random.normal(ks[7], (IS, H), jnp.float32) * sc}
    _L3_ffn_in = _L3_ffn_setup()
    _d = {'L0_attn_x': _L0_attn_in['x'], 'L0_attn_Wk': _L0_attn_in['Wk'], 'L0_attn_Wv': _L0_attn_in['Wv'], 'L0_attn_Wr': _L0_attn_in['Wr'], 'L0_attn_Wo': _L0_attn_in['Wo'], 'L0_attn_tm_k': _L0_attn_in['tm_k'], 'L0_attn_tm_v': _L0_attn_in['tm_v'], 'L0_attn_tm_r': _L0_attn_in['tm_r'], 'L0_attn_time_decay': _L0_attn_in['time_decay'], 'L0_attn_time_first': _L0_attn_in['time_first'], 'L0_attn_ln_g': _L0_attn_in['ln_g'], 'L0_attn_ln_b': _L0_attn_in['ln_b'], 'L0_ffn_weight': _L0_ffn_in['weight'], 'L0_ffn_bias': _L0_ffn_in['bias'], 'L1_attn_Wqa': _L1_attn_in['Wqa'], 'L1_attn_q_ln_w': _L1_attn_in['q_ln_w'], 'L1_attn_Wqb': _L1_attn_in['Wqb'], 'L1_attn_Wkva': _L1_attn_in['Wkva'], 'L1_attn_kv_ln_w': _L1_attn_in['kv_ln_w'], 'L1_attn_Wkvb': _L1_attn_in['Wkvb'], 'L1_attn_Wo': _L1_attn_in['Wo'], 'L1_ffn_wq_gate': _L1_ffn_in['wq_gate'], 'L1_ffn_s_gate': _L1_ffn_in['s_gate'], 'L1_ffn_wq_up': _L1_ffn_in['wq_up'], 'L1_ffn_s_up': _L1_ffn_in['s_up'], 'L1_ffn_wq_down': _L1_ffn_in['wq_down'], 'L1_ffn_s_down': _L1_ffn_in['s_down'], 'L2_attn_W': _L2_attn_in['W'], 'L2_attn_g1': _L2_attn_in['g1'], 'L2_attn_g2': _L2_attn_in['g2'], 'L2_attn_g3': _L2_attn_in['g3'], 'L2_ffn_weight': _L2_ffn_in['weight'], 'L2_ffn_scale': _L2_ffn_in['scale'], 'L2_ffn_expert_masks': _L2_ffn_in['expert_masks'], 'L2_ffn_router_w': _L2_ffn_in['router_w'], 'L3_attn_w_qkv': _L3_attn_in['w_qkv'], 'L3_attn_b_qkv': _L3_attn_in['b_qkv'], 'L3_attn_w_dense': _L3_attn_in['w_dense'], 'L3_attn_b_dense': _L3_attn_in['b_dense'], 'L3_ffn_gate_w': _L3_ffn_in['gate_w'], 'L3_ffn_w_gate': _L3_ffn_in['w_gate'], 'L3_ffn_w_up': _L3_ffn_in['w_up'], 'L3_ffn_w_down': _L3_ffn_in['w_down'], 'L3_ffn_sw_gate': _L3_ffn_in['sw_gate'], 'L3_ffn_sw_up': _L3_ffn_in['sw_up'], 'L3_ffn_sw_down': _L3_ffn_in['sw_down']}
    _x0 = _d['L0_attn_x']
    _d['L0_attn_x'] = jax.random.normal(jax.random.fold_in(jax.random.key(seed), 1), (16, 256, 256), dtype=_x0.dtype)
    del _x0
    return _d

def reference(L0_attn_x, L0_attn_Wk, L0_attn_Wv, L0_attn_Wr, L0_attn_Wo, L0_attn_tm_k, L0_attn_tm_v, L0_attn_tm_r, L0_attn_time_decay, L0_attn_time_first, L0_attn_ln_g, L0_attn_ln_b, L0_ffn_weight, L0_ffn_bias, L1_attn_Wqa, L1_attn_q_ln_w, L1_attn_Wqb, L1_attn_Wkva, L1_attn_kv_ln_w, L1_attn_Wkvb, L1_attn_Wo, L1_ffn_wq_gate, L1_ffn_s_gate, L1_ffn_wq_up, L1_ffn_s_up, L1_ffn_wq_down, L1_ffn_s_down, L2_attn_W, L2_attn_g1, L2_attn_g2, L2_attn_g3, L2_ffn_weight, L2_ffn_scale, L2_ffn_expert_masks, L2_ffn_router_w, L3_attn_w_qkv, L3_attn_b_qkv, L3_attn_w_dense, L3_attn_b_dense, L3_ffn_gate_w, L3_ffn_w_gate, L3_ffn_w_up, L3_ffn_w_down, L3_ffn_sw_gate, L3_ffn_sw_up, L3_ffn_sw_down):

    def _L0_attn_ref(x, Wk, Wv, Wr, Wo, tm_k, tm_v, tm_r, time_decay, time_first, ln_g, ln_b):
        import jax, jax.numpy as jnp
        import numpy as np
        B, T, D = (4, 512, 256)
        LAYER_ID, N_LAYERS = (0, 12)
        LN_EPS = 1e-05

        def _wkv(w, u, k, v):
            Bb, Tt, Dd = k.shape
            neg_ew = -jnp.exp(w)

            def step(carry, kv):
                aa, bb, pp = carry
                kt, vt = kv
                qt = jnp.maximum(pp, kt + u)
                e1 = jnp.exp(pp - qt)
                e2 = jnp.exp(kt + u - qt)
                out = (e1 * aa + e2 * vt) / (e1 * bb + e2)
                pp_new = jnp.maximum(pp + neg_ew, kt)
                f1 = jnp.exp(pp - pp_new)
                f2 = jnp.exp(kt - pp_new)
                return ((f1 * aa + f2 * vt, f1 * bb + f2, pp_new), out)
            init = (jnp.zeros((Bb, Dd), k.dtype), jnp.zeros((Bb, Dd), k.dtype), jnp.full((Bb, Dd), -1e+38, k.dtype))
            kT = jnp.swapaxes(k, 0, 1)
            vT = jnp.swapaxes(v, 0, 1)
            _, outT = jax.lax.scan(step, init, (kT, vT))
            return jnp.swapaxes(outT, 0, 1)
        xs = jnp.pad(x, ((0, 0), (1, 0), (0, 0)))[:, :-1, :]
        xk = x * tm_k + xs * (1.0 - tm_k)
        xv = x * tm_v + xs * (1.0 - tm_v)
        xr = x * tm_r + xs * (1.0 - tm_r)
        k = jnp.einsum('btd,ed->bte', xk, Wk)
        v = jnp.einsum('btd,ed->bte', xv, Wv)
        r = jax.nn.sigmoid(jnp.einsum('btd,ed->bte', xr, Wr))
        wkv = _wkv(time_decay, time_first, k, v)
        mu = jnp.mean(wkv, axis=-1, keepdims=True)
        var = jnp.mean(jnp.square(wkv - mu), axis=-1, keepdims=True)
        ln = (wkv - mu) * jax.lax.rsqrt(var + LN_EPS) * ln_g + ln_b
        rwkv = r * ln
        return jnp.einsum('btd,ed->bte', rwkv, Wo)

    def _L0_ffn_ref(x, weight, bias):
        import jax, jax.numpy as jnp
        import numpy as np
        B, S, D_IN, D_OUT = (4, 256, 256, 256)
        EPS = 1e-10
        scale = jnp.mean(jnp.abs(weight))
        w_t = jnp.clip(jnp.round(weight / (scale + EPS)), -1.0, 1.0)
        w_ste = weight + jax.lax.stop_gradient(w_t * scale - weight)
        return jnp.einsum('bsi,oi->bso', x, w_ste) + bias

    def _L1_attn_ref(x, Wqa, q_ln_w, Wqb, Wkva, kv_ln_w, Wkvb, Wo):
        import jax, jax.numpy as jnp
        import numpy as np
        D_MODEL = 256
        NHEADS = 16
        NOPE = 128
        ROPE = 64
        VDIM = 128
        QLORA = 192
        KVLORA = 64
        QHD = NOPE + ROPE
        B, T = (1, 512)

        def rms_norm(x, w):
            eps = jnp.finfo(x.dtype).eps
            var = jnp.mean(x * x, axis=-1, keepdims=True)
            return x * jax.lax.rsqrt(var + eps) * w

        def rope_cos_sin(T, dim):
            freqs = 1.0 / 10000.0 ** (jnp.arange(0, dim, 2, dtype=jnp.float32) / dim)
            ang = jnp.arange(T, dtype=jnp.float32)[:, None] * freqs[None, :]
            return (jnp.cos(ang), jnp.sin(ang))

        def apply_rope(x, cos, sin):
            xe = x[..., 0::2]
            xo = x[..., 1::2]
            re = xe * cos - xo * sin
            ro = xo * cos + xe * sin
            return jnp.stack([re, ro], axis=-1).reshape(x.shape)
        Bx, Tx, _ = x.shape
        cos, sin = rope_cos_sin(Tx, ROPE)
        q = rms_norm(x @ Wqa, q_ln_w) @ Wqb
        q = q.reshape(Bx, Tx, NHEADS, QHD).transpose(0, 2, 1, 3)
        q_nope = q[..., :NOPE]
        q_rope = apply_rope(q[..., NOPE:], cos, sin)
        kv = x @ Wkva
        kv_c = kv[..., :KVLORA]
        k_rope = apply_rope(kv[..., KVLORA:], cos, sin)
        kvb = (rms_norm(kv_c, kv_ln_w) @ Wkvb).reshape(Bx, Tx, NHEADS, NOPE + VDIM)
        k_nope = kvb[..., :NOPE].transpose(0, 2, 1, 3)
        v = kvb[..., NOPE:].transpose(0, 2, 1, 3)
        scale = 1.0 / jnp.sqrt(jnp.float32(QHD))
        s = jnp.einsum('bhqd,bhkd->bhqk', q_nope, k_nope)
        s = s + jnp.einsum('bhqd,bkd->bhqk', q_rope, k_rope)
        s = s * scale
        mask = jnp.tril(jnp.ones((Tx, Tx), dtype=bool))
        s = jnp.where(mask, s, -jnp.inf)
        a = jax.nn.softmax(s, axis=-1)
        o = jnp.einsum('bhqk,bhkd->bhqd', a, v)
        o = o.transpose(0, 2, 1, 3).reshape(Bx, Tx, NHEADS * VDIM)
        return o @ Wo

    def _L1_ffn_ref(x, wq_gate, s_gate, wq_up, s_up, wq_down, s_down):
        import jax, jax.numpy as jnp
        import numpy as np
        DIM = 256
        HID = 704
        ZERO_POINT = 128.0

        def _qlinear(x, wq, scale):
            W = (wq.astype(jnp.float32) - ZERO_POINT) * scale[:, None]
            return jnp.einsum('bsd,hd->bsh', x, W)
        gate = _qlinear(x, wq_gate, s_gate)
        gate = jax.nn.silu(gate)
        up = _qlinear(x, wq_up, s_up)
        return _qlinear(gate * up, wq_down, s_down)

    def _L2_attn_ref(x, W, g1, g2, g3):
        import jax, jax.numpy as jnp
        import numpy as np
        B, T, FEATS, HEAD = (2, 256, 256, 16)
        DIM_HEAD = FEATS // HEAD
        EPS = float(jnp.finfo(jnp.float32).eps)

        def _rms_norm(u, g):
            return u * jax.lax.rsqrt(jnp.mean(u * u, axis=-1, keepdims=True) + EPS) * g
        Bb, Tt, C = x.shape
        sqrt_d = jnp.asarray(DIM_HEAD ** 0.5, dtype=x.dtype)
        w = (x @ W.T).reshape(Bb, Tt, HEAD, DIM_HEAD).transpose(0, 2, 1, 3)
        q = _rms_norm(w, g1)
        k = _rms_norm(w, g2)
        v = _rms_norm(w, g3)
        att = jnp.einsum('bhid,bhjd->bhij', q, k) / sqrt_d
        score = jax.nn.softmax(att, axis=-1) + jax.nn.softmax(att, axis=-2)
        y = jnp.einsum('bhij,bhjd->bihd', score, v).reshape(Bb, Tt, C)
        return y @ W

    def _L2_ffn_ref(x, weight, scale, expert_masks, router_w):
        import jax, jax.numpy as jnp
        import numpy as np
        B, S, D_IN, D_OUT, E = (4, 128, 256, 256, 32)
        MASK_DENSITY = 0.3
        THRESH = 0.5
        logits = jnp.einsum('bsd,ed->bse', x, router_w)
        probs = jax.nn.softmax(logits, axis=-1)
        top1_w = jnp.max(probs, axis=-1)
        top1_idx = jnp.argmax(probs, axis=-1)
        w_q = jnp.clip(jnp.round(weight / THRESH), -1.0, 1.0)
        w_scaled = w_q * scale[:, None]
        out0 = jnp.zeros((x.shape[0], x.shape[1], weight.shape[0]), dtype=x.dtype)

        def body(out, inputs):
            e_idx, mask_e = inputs
            y = jnp.einsum('bsi,oi->bso', x, w_scaled * mask_e)
            sel = (top1_idx == e_idx)[..., None]
            out = jnp.where(sel, y * top1_w[..., None], out)
            return (out, None)
        out, _ = jax.lax.scan(body, out0, (jnp.arange(E), expert_masks))
        return out

    def _L3_attn_ref(hidden_states, w_qkv, b_qkv, w_dense, b_dense):
        import jax, jax.numpy as jnp
        import numpy as np
        SEQ, BATCH, HIDDEN = (256, 2, 256)
        NUM_HEADS = 16
        HEAD_DIM = HIDDEN // NUM_HEADS
        s, b, H = hidden_states.shape
        nh, d = (NUM_HEADS, HEAD_DIM)
        norm_factor = jnp.asarray(np.sqrt(d), dtype=hidden_states.dtype)
        mixed = hidden_states @ w_qkv.T + b_qkv
        mixed = mixed.reshape(s, b, nh, 3 * d)
        q, k, v = jnp.split(mixed, 3, axis=-1)
        scores = jnp.einsum('sbhd,tbhd->bhst', q, k) / norm_factor
        causal = jnp.tril(jnp.ones((s, s), dtype=bool))
        scores = jnp.where(causal[None, None, :, :], scores, jnp.asarray(-10000.0, scores.dtype))
        probs = jax.nn.softmax(scores, axis=-1)
        ctx = jnp.einsum('bhst,tbhd->sbhd', probs, v).reshape(s, b, H)
        return ctx @ w_dense.T + b_dense

    def _L3_ffn_ref(hidden_states, gate_w, w_gate, w_up, w_down, sw_gate, sw_up, sw_down):
        import jax, jax.numpy as jnp
        import numpy as np
        B, S, H = (1, 256, 256)
        E, K, I = (16, 4, 176)
        IS = 352
        CAP = 128
        b, s, h = hidden_states.shape
        x = hidden_states.reshape(-1, h)
        T = x.shape[0]
        scores = jax.nn.softmax(x @ gate_w.T, axis=-1)
        topk_w, topk_i = jax.lax.top_k(scores, K)
        topk_w = topk_w / (topk_w.sum(-1, keepdims=True) + 1e-20)
        flat_i = topk_i.reshape(-1)
        flat_w = topk_w.reshape(-1)
        order = jnp.argsort(flat_i)
        se = flat_i[order]
        counts = jax.ops.segment_sum(jnp.ones_like(flat_i), flat_i, num_segments=E)
        starts = jnp.cumsum(counts) - counts
        rank = jnp.arange(T * K) - starts[se]
        tok = order // K
        slot = jnp.where(rank < CAP, rank, CAP)
        buf = jnp.full((E, CAP + 1), T, dtype=jnp.int32).at[se, slot].set(tok)[:, :CAP]
        wbuf = jnp.zeros((E, CAP + 1), x.dtype).at[se, slot].set(flat_w[order])[:, :CAP]
        xpad = jnp.concatenate([x, jnp.zeros((1, h), x.dtype)], axis=0)
        xg = xpad[buf]
        gact = jax.nn.silu(jnp.einsum('ech,ehi->eci', xg, w_gate))
        mid = gact * jnp.einsum('ech,ehi->eci', xg, w_up)
        eout = jnp.einsum('eci,eih->ech', mid, w_down) * wbuf[..., None]
        y = jnp.zeros((T + 1, h), x.dtype).at[buf.reshape(-1)].add(eout.reshape(-1, h))[:T]
        shared = jax.nn.silu(x @ sw_gate) * (x @ sw_up) @ sw_down
        return (y + shared).reshape(b, s, h)
    x = L0_attn_x
    x = x + _L0_attn_ref(_layernorm(x, axis=-1), L0_attn_Wk, L0_attn_Wv, L0_attn_Wr, L0_attn_Wo, L0_attn_tm_k, L0_attn_tm_v, L0_attn_tm_r, L0_attn_time_decay, L0_attn_time_first, L0_attn_ln_g, L0_attn_ln_b)
    x = x + _L0_ffn_ref(_layernorm(x, axis=-1), L0_ffn_weight, L0_ffn_bias)
    x = x + _L1_attn_ref(_layernorm(x, axis=-1), L1_attn_Wqa, L1_attn_q_ln_w, L1_attn_Wqb, L1_attn_Wkva, L1_attn_kv_ln_w, L1_attn_Wkvb, L1_attn_Wo)
    x = x + _L1_ffn_ref(_layernorm(x, axis=-1), L1_ffn_wq_gate, L1_ffn_s_gate, L1_ffn_wq_up, L1_ffn_s_up, L1_ffn_wq_down, L1_ffn_s_down)
    x = x + _L2_attn_ref(_layernorm(x, axis=-1), L2_attn_W, L2_attn_g1, L2_attn_g2, L2_attn_g3)
    x = x + _L2_ffn_ref(_layernorm(x, axis=-1), L2_ffn_weight, L2_ffn_scale, L2_ffn_expert_masks, L2_ffn_router_w)
    x = x + _L3_attn_ref(_layernorm(x, axis=-1), L3_attn_w_qkv, L3_attn_b_qkv, L3_attn_w_dense, L3_attn_b_dense)
    x = x + _L3_ffn_ref(_layernorm(x, axis=-1), L3_ffn_gate_w, L3_ffn_w_gate, L3_ffn_w_up, L3_ffn_w_down, L3_ffn_sw_gate, L3_ffn_sw_up, L3_ffn_sw_down)
    return x

_drawn_inputs = setup_inputs


def setup_inputs(seed=0):
    import zlib

    import numpy as np

    out = dict(_drawn_inputs(seed))
    spreads = {'L0_attn_ln_g': (1.0, 0.2),
     'L0_attn_ln_b': (0.0, 0.1),
     'L1_attn_q_ln_w': (1.0, 0.6),
     'L1_attn_kv_ln_w': (1.0, 0.6),
     'L2_attn_g1': (1.0, 0.536),
     'L2_attn_g2': (1.0, 0.2),
     'L2_attn_g3': (1.0, 0.2),
     'L2_ffn_scale': (1.0, 0.2)}
    factors = {'L0_attn_tm_r': 5.035,
     'L0_attn_time_decay': 200.0,
     'L0_attn_time_first': 180.712,
     'L1_attn_Wqa': 8.0,
     'L1_attn_Wqb': 8.0,
     'L1_ffn_s_gate': 8.0,
     'L1_ffn_s_up': 8.0,
     'L1_ffn_s_down': 8.0,
     'L3_attn_b_qkv': 8.0,
     'L3_attn_b_dense': 8.0,
     'L3_ffn_gate_w': 8.0,
     'L3_ffn_w_gate': 8.0,
     'L3_ffn_w_up': 8.0,
     'L3_ffn_w_down': 8.0,
     'L3_ffn_sw_gate': 6.181,
     'L3_ffn_sw_up': 6.162,
     'L3_ffn_sw_down': 6.137}
    for name, (base, spread) in spreads.items():
        noise = np.random.default_rng([zlib.crc32(name.encode()), seed]).standard_normal(out[name].shape)
        drawn = base * np.exp(spread * noise) if base else spread * noise
        out[name] = jnp.asarray(drawn.astype(out[name].dtype))
    for name, factor in factors.items():
        out[name] = (out[name] * factor).astype(out[name].dtype)
    return out
```

```python
import numpy as np
import concourse.bass as bass
from concourse import mybir
from contextlib import ExitStack, contextmanager

F32 = mybir.dt.float32
BF16 = mybir.dt.bfloat16
I32 = mybir.dt.int32
U32 = mybir.dt.uint32
ALU = mybir.AluOpType
ACT = mybir.ActivationFunctionType
AX = mybir.AxisListType

P = 128
D = 256
DH = D // P
B, T = 16, 256
N = B * T
NT = N // P
TPB = T // P
LN_EPS = 1e-5


class Chain:

    def __init__(self, eng, sem, per):
        self.eng, self.sem, self.per, self.base, self.n = eng, sem, per, 0, 0

    def start(self, t, at=0):
        self.base, self.n = t * self.per + at, 0

    def __call__(self, instruction):
        self.n += 1
        instruction.then_inc(self.sem, 1)
        self.eng.wait_ge(self.sem, self.base + self.n)


def in_pairs(eng, n, step):
    with eng.Fori(0, n // 2) as i:
        step(2 * i, 0)
        step(2 * i + 1, 1)


def skewed(eng, n, front, back):
    front(0, 0)
    with eng.Fori(0, n // 2 - 1) as i:
        front(2 * i + 1, 1)
        back(2 * i, 0)
        front(2 * i + 2, 0)
        back(2 * i + 1, 1)
    front(n - 1, 1)
    back(n - 2, 0)
    back(n - 1, 1)


class Core:

    def __init__(self, nc, dram, stack):
        self.nc, self.dram = nc, dram
        self.X = stack.enter_context(nc.sbuf_tensor("X", [P, NT, D], F32))
        self.ident = stack.enter_context(nc.sbuf_tensor("ident", [P, P], F32))
        self.identb = stack.enter_context(nc.sbuf_tensor("identb", [P, P], BF16))
        self.half = stack.enter_context(nc.sbuf_tensor("minus_half", [P, 64], F32))
        self.stats = stack.enter_context(nc.sbuf_tensor("bn_stats", [P, NT, 6], F32))
        self.mean = stack.enter_context(nc.sbuf_tensor("mean", [P, NT], F32))
        self.rstd = stack.enter_context(nc.sbuf_tensor("rstd", [P, NT], F32))
        self.tmp = stack.enter_context(nc.sbuf_tensor("stat_tmp", [P, 3, NT], F32))
        self.slots_x = nc.dram_tensor("slots_x", (SLOTS * P, D), F32, kind="Internal").ap()
        self.slots_y = nc.dram_tensor("slots_y", (SLOTS * P, D), F32, kind="Internal").ap()
        self.scratch_x = nc.dram_tensor("scratch_x", (N, D), F32, kind="Internal").ap()
        self.scratch_t = nc.dram_tensor("scratch_t", (N, 2), F32, kind="Internal").ap()
        self.rows_x = nc.dram_tensor("rows_x", (N + P, D), F32, kind="Internal").ap()
        self.rows_y = nc.dram_tensor("rows_y", (N + P, D), F32, kind="Internal").ap()
        self.PS = stack.enter_context(nc.psum_tensor("banks", [P, 8, 512], F32))

    @contextmanager
    def stage(self, name):
        nc, sems = self.nc, []
        with ExitStack() as stack:
            def sb(tag, shape, dt=F32):
                return stack.enter_context(nc.sbuf_tensor(f"{name}_{tag}", shape, dt))

            def sem(tag):
                sems.append(stack.enter_context(nc.semaphore(f"{name}_{tag}")))
                return sems[-1]

            yield sb, sem
            with nc.Block() as block:
                @block.gpsimd
                def _(pool):
                    for s in sems:
                        pool.sem_clear(s)


def constants(core):
    nc = core.nc
    with core.stage("const") as (sb, sem):
        zeroed = sem("zeroed")
        with nc.Block() as block:
            @block.gpsimd
            def _(pool):
                pool.memset(core.ident[:, :], 0.0).then_inc(zeroed, 1)
                pool.memset(core.identb[:, :], 0.0).then_inc(zeroed, 1)
                pool.memset(core.half[:, :], -0.5)
                pool.wait_ge(zeroed, 2)
                for m in (core.ident, core.identb):
                    pool.affine_select(out=m[:, :], in_=m[:, :], compare_op=ALU.not_equal, fill=1.0, base=0,
                                       pattern=[[-1, P]], channel_multiplier=1)


def statistics(core, tag, source, eps):
    nc = core.nc
    m, t0, t1, t2 = core.mean, core.tmp[:, 0, :], core.tmp[:, 1, :], core.tmp[:, 2, :]
    with core.stage("st" + tag) as (sb, sem):
        stats_done, own, var_ready, rstd_done = sem("stats"), sem("own"), sem("var"), sem("rstd")
        with nc.Block() as block:
            @block.vector
            def _(dve):
                link = Chain(dve, own, 8)
                with dve.Fori(0, NT // 4) as i:
                    for k in range(4):
                        dve.bn_stats(out=core.stats[:, bass.ds(4 * i + k, 1), :],
                                     in_=source[:, bass.ds(4 * i + k, 1), :]).then_inc(stats_done, 1)
                dve.wait_ge(stats_done, NT)
                me, ve, mo, vo = (core.stats[:, :, k] for k in (1, 2, 4, 5))
                link(dve.tensor_tensor(out=t0, in0=me, in1=mo, op=ALU.add))
                link(dve.tensor_scalar(out=m[:, :], in0=t0, scalar1=0.5, scalar2=None, op0=ALU.mult))
                link(dve.tensor_tensor(out=t0, in0=me, in1=mo, op=ALU.subtract))
                link(dve.tensor_tensor(out=t1, in0=t0, in1=t0, op=ALU.mult))
                link(dve.tensor_tensor(out=t2, in0=ve, in1=vo, op=ALU.add))
                link(dve.scalar_tensor_tensor(out=t1, in0=t1, scalar=D / 4.0, in1=t2, op0=ALU.mult, op1=ALU.add))
                dve.tensor_scalar(out=t0, in0=t1, scalar1=1.0 / D, scalar2=eps,
                                  op0=ALU.mult, op1=ALU.add).then_inc(var_ready, 1)

            @block.gpsimd
            def _(pool):
                pool.wait_ge(var_ready, 1)
                pool.tensor_tensor(out=core.rstd[:, :], in0=t0, in1=core.half[:, 0:NT],
                                   op=ALU.pow).then_inc(rstd_done, 1)


def rwkv(core):
    nc, X, PS = core.nc, core.X, core.PS
    with ExitStack() as keep:
        gate = keep.enter_context(nc.sbuf_tensor("rw_gate", [P, NT, D], F32))
        wkv = keep.enter_context(nc.sbuf_tensor("rw_wkv", [P, NT, D], F32))
        statistics(core, "0a", X, LN_EPS)
        rwkv_recurrence(core, gate, wkv)
        statistics(core, "0b", wkv, LN_EPS)
        rwkv_output(core, gate, wkv)


def rwkv_recurrence(core, gate, wkv):
    nc, X, PS = core.nc, core.X, core.PS
    START = -1e38
    with core.stage("rw") as (sb, sem):
        W = sb("W", [P, 3, DH, D])
        WA = sb("WA", [P, 3, DH, D])
        WB = sb("WB", [P, 3, DH, D])
        tm = sb("tm", [P, 3, DH])
        decay = sb("decay", [P, DH])
        first = sb("first", [P, DH])
        negdecay = sb("negdecay", [P, DH, T])
        xn = sb("xn", [P, 2, TPB, D])
        xnT = sb("xnT", [P, 2, DH, T + 1])
        pp = sb("pp", [P, 2, DH, T + 1])
        q = sb("q", [P, 2, DH, T])
        ex = sb("ex", [P, 2, 4, DH, T])
        f2v = sb("f2v", [P, DH, T])
        e2v = sb("e2v", [P, 2, DH, T])
        ab = sb("ab", [P, 2, 2, DH, T + 1])
        nd = sb("nd", [P, 2, 2, DH, T])
        rec = sb("rec", [P, DH, T])
        out = sb("out", [P, 2, DH, T])

        loaded, zeroed, edges, clamped = sem("loaded"), sem("zeroed"), sem("edges"), sem("clamped")
        exp_ready, weights_ready, xn_ready, xn_free = sem("expd"), sem("weights"), sem("xn_ready"), sem("xn_free")
        xt_ps, xt_ready, kvr_ready, r_free, kv_free = sem("xt_ps"), sem("xt_ready"), sem("kvr"), sem("r_free"), sem("kv_free")
        pp_ready, q_ready, args_dve, args_pool = sem("pp_ready"), sem("q_ready"), sem("args_d"), sem("args_p")
        exps_ready, scans_ready, e2v_ready, nd_ready = sem("exps"), sem("scans"), sem("e2v_ready"), sem("nd_ready")
        out_ready, out_free, w_ps, w_free = sem("out_ready"), sem("out_free"), sem("w_ps"), sem("w_free")
        own_prep, own_front, own_scans, own_finish, own_pool = (sem(f"own{k}") for k in range(5))

        with nc.Block() as block:
            @block.sync
            def _(sp):
                for n, name in enumerate(("WkT", "WvT", "WrT")):
                    sp.dma_start(W[:, n, :, :], core.dram[name].rearrange("(h p) e -> p h e", p=P)).then_inc(loaded, 16)
                sp.dma_start(tm[:, :, :], core.dram["tm"]).then_inc(loaded, 16)
                sp.dma_start(decay[:, :], core.dram["time_decay"]).then_inc(loaded, 16)
                sp.dma_start(first[:, :], core.dram["time_first"]).then_inc(loaded, 16)

            @block.tensor
            def _(pe):
                def front(b, u):
                    pe.wait_ge(xn_ready, b + 1)
                    for h in range(DH):
                        for k in range(TPB):
                            last = pe.transpose(PS[:, 0, h * T + k * P:h * T + k * P + P],
                                                xn[:, u, k, h * P:h * P + P], core.ident[:, :])
                    last.then_inc(xt_ps, 1)
                    pe.wait_ge(xt_ready, b + 1)
                    pe.wait_ge(kv_free, b + 1)
                    pe.wait_ge(r_free, b + 1)
                    for n in range(2):
                        for e in range(DH):
                            for j in range(4):
                                w, h = (WA, WB)[j % 2], j // 2
                                pe.matmul(PS[:, 2 + 2 * n + u, e * T:e * T + T], w[:, n, h, e * P:e * P + P],
                                          xnT[:, u, h, 1 - j % 2:1 - j % 2 + T], start=(j == 0), stop=(j == 3))
                    for k in range(TPB):
                        for j in range(4):
                            w, h = (WA, WB)[j % 2], j // 2
                            at = 1 - j % 2 + k * P
                            last = pe.matmul(PS[:, 6 + u, k * D:k * D + D], xnT[:, u, h, at:at + P], w[:, 2, h, :],
                                             start=(j == 0), stop=(j == 3))
                    last.then_inc(kvr_ready, 1)

                def back(b, u):
                    pe.wait_ge(out_ready, b + 1)
                    pe.wait_ge(w_free, b + 1)
                    for k in range(TPB):
                        for h in range(DH):
                            last = pe.transpose(PS[:, 1, k * D + h * P:k * D + h * P + P],
                                                out[:, u, h, k * P:k * P + P], core.ident[:, :])
                    last.then_inc(w_ps, 1)

                pe.wait_ge(weights_ready, 1)
                skewed(pe, B, front, back)

            @block.scalar
            def _(act):
                act.wait_ge(zeroed, 1)
                act.wait_ge(clamped, 1)
                act.activation(decay[:, :], decay[:, :], ACT.Exp).then_inc(exp_ready, 1)
                act.sem_inc(r_free, 2)
                act.sem_inc(w_free, 1)

                def front(b, u):
                    act.wait_ge(xt_ps, b + 1)
                    act.sem_inc(xn_free, 1)
                    act.activation(xnT[:, u, :, 1:T + 1], PS[:, 0, :].rearrange("p (h t) -> p h t", h=DH),
                                   ACT.Copy).then_inc(xt_ready, 1)
                    act.wait_ge(kvr_ready, b + 1)
                    act.activation(gate[:, bass.ds(TPB * b, TPB), :], PS[:, 6 + u, :].rearrange("p (k d) -> p k d", k=TPB),
                                   ACT.Tanh, scale=0.5).then_inc(r_free, 1)
                    act.wait_ge(args_dve, b + 1)
                    act.wait_ge(args_pool, b + 1)
                    act.activation(ex[:, u, :, :, :], ex[:, u, :, :, :], ACT.Exp).then_inc(exps_ready, 1)

                def back(b, u):
                    act.wait_ge(w_ps, b + 1)
                    act.sem_inc(out_free, 1)
                    act.activation(wkv[:, bass.ds(TPB * b, TPB), :], PS[:, 1, :].rearrange("p (k d) -> p k d", k=TPB),
                                   ACT.Copy).then_inc(w_free, 1)

                skewed(act, B, front, back)

            @block.gpsimd
            def _(pool):
                pool.memset(xnT[:, :, :, 0:1], 0.0).then_inc(zeroed, 1)
                pool.memset(pp[:, :, :, 0:1], START).then_inc(edges, 1)
                pool.memset(ab[:, :, :, :, 0:1], 0.0).then_inc(edges, 1)
                pool.wait_ge(edges, 2)
                link = Chain(pool, own_pool, 4)

                def step(b, u):
                    pool.wait_ge(pp_ready, b + 1)
                    pool.tensor_tensor(out=ex[:, u, 0, :, :], in0=pp[:, u, :, 0:T], in1=pp[:, u, :, 1:T + 1],
                                       op=ALU.subtract)
                    pool.wait_ge(q_ready, b + 1)
                    pool.tensor_tensor(out=ex[:, u, 2, :, :], in0=pp[:, u, :, 0:T], in1=q[:, u, :, :],
                                       op=ALU.subtract).then_inc(args_pool, 1)
                    pool.wait_ge(scans_ready, b + 1)
                    link.start(b)
                    for k in range(2):
                        link(pool.tensor_tensor(out=nd[:, u, k, :, :], in0=ab[:, u, k, :, 0:T], in1=ex[:, u, 2, :, :],
                                                op=ALU.mult))
                    pool.wait_ge(e2v_ready, b + 1)
                    link(pool.tensor_tensor(out=nd[:, u, 0, :, :], in0=nd[:, u, 0, :, :], in1=e2v[:, u, :, :],
                                            op=ALU.add))
                    link(pool.tensor_tensor(out=nd[:, u, 1, :, :], in0=nd[:, u, 1, :, :], in1=ex[:, u, 3, :, :],
                                            op=ALU.add))
                    pool.sem_inc(nd_ready, 1)

                in_pairs(pool, B, step)

            @block.vector
            def _(dve):
                dve.sem_inc(kv_free, 2)
                dve.sem_inc(xn_free, 2)
                dve.sem_inc(out_free, 2)
                dve.wait_ge(loaded, 6 * 16)
                link = Chain(dve, own_prep, 9)
                dve.tensor_scalar(out=decay[:, :], in0=decay[:, :], scalar1=87.0, scalar2=None,
                                  op0=ALU.min).then_inc(clamped, 1)
                link(dve.memset(negdecay[:, :, :], 0.0))
                for n in range(3):
                    for h in range(DH):
                        link(dve.tensor_scalar(out=WA[:, n, h, :], in0=W[:, n, h, :], scalar1=tm[:, n, h:h + 1],
                                               scalar2=None, op0=ALU.mult))
                dve.tensor_tensor(out=WB[:, :, :, :], in0=W[:, :, :, :], in1=WA[:, :, :, :],
                                  op=ALU.subtract).then_inc(weights_ready, 1)
                dve.wait_ge(exp_ready, 1)
                for h in range(DH):
                    link(dve.tensor_scalar(out=negdecay[:, h, :], in0=negdecay[:, h, :], scalar1=decay[:, h:h + 1],
                                           scalar2=None, op0=ALU.subtract))
                dve.wait_ge(edges, 2)
                link_front, link_scans, link_finish = (Chain(dve, own_front, 4), Chain(dve, own_scans, 2),
                                                       Chain(dve, own_finish, 2))

                def normalise(b, u):
                    dve.wait_ge(xn_free, b + 1)
                    for k in range(TPB):
                        t = TPB * b + k
                        last = dve.tensor_scalar(out=xn[:, u, k, :], in0=X[:, bass.ds(t, 1), :],
                                                 scalar1=core.mean[:, bass.ds(t, 1)], scalar2=core.rstd[:, bass.ds(t, 1)],
                                                 op0=ALU.subtract, op1=ALU.mult)
                    last.then_inc(xn_ready, 1)

                def front(b, u):
                    kp = PS[:, 2 + u, :].rearrange("p (h t) -> p h t", h=DH)
                    link = link_front
                    link.start(b)
                    dve.wait_ge(kvr_ready, b + 1)
                    for h in range(DH):
                        link(dve.tensor_tensor_scan(out=pp[:, u, h, 1:T + 1], data0=negdecay[:, h, :],
                                                    data1=kp[:, h, :], initial=START, op0=ALU.add, op1=ALU.max))
                    dve.sem_inc(pp_ready, 1)
                    dve.tensor_tensor(out=ex[:, u, 1, :, :], in0=kp, in1=pp[:, u, :, 1:T + 1], op=ALU.subtract)
                    for h in range(DH):
                        link(dve.scalar_tensor_tensor(out=q[:, u, h, :], in0=kp[:, h, :], scalar=first[:, h:h + 1],
                                                      in1=pp[:, u, h, 0:T], op0=ALU.add, op1=ALU.max))
                    dve.sem_inc(q_ready, 1)
                    for h in range(DH):
                        last = dve.scalar_tensor_tensor(out=ex[:, u, 3, h, :], in0=kp[:, h, :],
                                                        scalar=first[:, h:h + 1], in1=q[:, u, h, :],
                                                        op0=ALU.add, op1=ALU.subtract)
                    last.then_inc(args_dve, 1)

                def scans(b, u):
                    vp = PS[:, 4 + u, :].rearrange("p (h t) -> p h t", h=DH)
                    link = link_scans
                    link.start(b)
                    dve.wait_ge(exps_ready, b + 1)
                    link(dve.tensor_tensor(out=f2v[:, :, :], in0=ex[:, u, 1, :, :], in1=vp, op=ALU.mult))
                    for h in range(DH):
                        dve.tensor_tensor_scan(out=ab[:, u, 0, h, 1:T + 1], data0=ex[:, u, 0, h, :],
                                               data1=f2v[:, h, :], initial=0.0, op0=ALU.mult, op1=ALU.add)
                        last = dve.tensor_tensor_scan(out=ab[:, u, 1, h, 1:T + 1], data0=ex[:, u, 0, h, :],
                                                      data1=ex[:, u, 1, h, :], initial=0.0, op0=ALU.mult, op1=ALU.add)
                    last.then_inc(scans_ready, 1)
                    link(dve.tensor_tensor(out=e2v[:, u, :, :], in0=ex[:, u, 3, :, :], in1=vp, op=ALU.mult))
                    dve.sem_inc(kv_free, 1)
                    dve.sem_inc(e2v_ready, 1)

                def finish(b, u):
                    link = link_finish
                    link.start(b)
                    dve.wait_ge(nd_ready, b + 1)
                    link(dve.reciprocal(out=rec[:, :, :], in_=nd[:, u, 1, :, :]))
                    dve.wait_ge(out_free, b + 1)
                    link(dve.tensor_tensor(out=out[:, u, :, :], in0=nd[:, u, 0, :, :], in1=rec[:, :, :], op=ALU.mult))
                    dve.sem_inc(out_ready, 1)

                normalise(0, 0)
                normalise(1, 1)
                front(0, 0)
                scans(0, 0)
                with dve.Fori(0, B // 2 - 1) as i:
                    for k in (1, 2):
                        b, u = 2 * i + k, k % 2
                        normalise(b + 1, 1 - u)
                        front(b, u)
                        finish(b - 1, 1 - u)
                        scans(b, u)
                front(B - 1, 1)
                finish(B - 2, 0)
                scans(B - 1, 1)
                finish(B - 1, 1)


def rwkv_output(core, gate, wkv):
    nc, X, PS = core.nc, core.X, core.PS
    with core.stage("ro") as (sb, sem):
        WoT = sb("WoT", [P, DH, D])
        g = sb("g", [P, D])
        c = sb("c", [P, D])
        n = sb("n", [P, 2, D])
        ng = sb("ng", [P, 2, D])
        rn = sb("rn", [P, 2, D])
        rT = sb("rT", [P, 2, DH, P])
        loaded, w_ready, n_ready, ng_ready, rn_ready = (sem(x) for x in ("loaded", "w_ready", "n_ready", "ng_ready", "rn_ready"))
        rt_ps, rt_ready, y_ps, added, own = (sem(x) for x in ("rt_ps", "rt_ready", "y_ps", "added", "own"))
        with nc.Block() as block:
            @block.sync
            def _(sp):
                sp.dma_start(WoT[:, :, :], core.dram["WoT"].rearrange("(h p) e -> p h e", p=P)).then_inc(loaded, 16)
                sp.dma_start(g[:, :], core.dram["ln_g"]).then_inc(loaded, 16)
                sp.dma_start(c[:, :], core.dram["ln_b"]).then_inc(loaded, 16)

            @block.vector
            def _(dve):
                dve.sem_inc(added, 2)
                dve.wait_ge(loaded, 3 * 16)
                dve.tensor_scalar(out=WoT[:, :, :], in0=WoT[:, :, :], scalar1=0.5, scalar2=None,
                                  op0=ALU.mult).then_inc(w_ready, 1)

                def normalise(t, u):
                    dve.tensor_scalar(out=n[:, u, :], in0=wkv[:, bass.ds(t, 1), :], scalar1=core.mean[:, bass.ds(t, 1)],
                                      scalar2=core.rstd[:, bass.ds(t, 1)], op0=ALU.subtract,
                                      op1=ALU.mult).then_inc(n_ready, 1)

                def gated(t, u):
                    dve.wait_ge(ng_ready, t + 1)
                    dve.scalar_tensor_tensor(out=rn[:, u, :], in0=gate[:, bass.ds(t, 1), :], scalar=1.0, in1=ng[:, u, :],
                                             op0=ALU.add, op1=ALU.mult).then_inc(rn_ready, 1)

                def add(t, u):
                    dve.wait_ge(y_ps, t + 1)
                    dve.tensor_tensor(out=X[:, bass.ds(t, 1), :], in0=X[:, bass.ds(t, 1), :], in1=PS[:, 2 + u, 0:D],
                                      op=ALU.add).then_inc(added, 1)

                normalise(0, 0)
                normalise(1, 1)
                gated(0, 0)
                gated(1, 1)
                with dve.Fori(0, NT // 2 - 1) as i:
                    for k in range(2):
                        t = 2 * i + k
                        normalise(t + 2, k)
                        add(t, k)
                        gated(t + 2, k)
                add(NT - 2, 0)
                add(NT - 1, 1)

            @block.gpsimd
            def _(pool):
                pool.wait_ge(loaded, 3 * 16)
                link = Chain(pool, own, 1)

                def step(t, u):
                    pool.wait_ge(n_ready, t + 1)
                    link.start(t)
                    link(pool.tensor_tensor(out=ng[:, u, :], in0=n[:, u, :], in1=g[:, :], op=ALU.mult))
                    pool.tensor_tensor(out=ng[:, u, :], in0=ng[:, u, :], in1=c[:, :], op=ALU.add).then_inc(ng_ready, 1)

                in_pairs(pool, NT, step)

            @block.scalar
            def _(act):
                def step(t, u):
                    act.wait_ge(rt_ps, t + 1)
                    act.activation(rT[:, u, :, :], PS[:, u, 0:D].rearrange("p (h t) -> p h t", h=DH),
                                   ACT.Copy).then_inc(rt_ready, 1)

                in_pairs(act, NT, step)

            @block.tensor
            def _(pe):
                pe.wait_ge(w_ready, 1)

                def front(t, u):
                    pe.wait_ge(rn_ready, t + 1)
                    for h in range(DH):
                        last = pe.transpose(PS[:, u, h * P:h * P + P], rn[:, u, h * P:h * P + P], core.ident[:, :])
                    last.then_inc(rt_ps, 1)

                def back(t, u):
                    pe.wait_ge(rt_ready, t + 1)
                    pe.wait_ge(added, t + 1)
                    for h in range(DH):
                        last = pe.matmul(PS[:, 2 + u, 0:D], rT[:, u, h, :], WoT[:, h, :], start=(h == 0), stop=(h == DH - 1))
                    last.then_inc(y_ps, 1)

                skewed(pe, NT, front, back)


def ahead(eng, n, first, body):
    first(0, 0)
    with eng.Fori(0, n // 2 - 1) as i:
        body(2 * i, 0, True)
        body(2 * i + 1, 1, True)
    body(n - 2, 0, True)
    body(n - 1, 1, False)


def ternary(core):
    nc, X, PS = core.nc, core.X, core.PS
    ROUND = 1.5 * 2.0 ** 23
    statistics(core, "1", X, LN_EPS)
    with core.stage("te") as (sb, sem):
        W = sb("W", [P, DH, D])
        Wq = sb("Wq", [P, DH, D])
        ones = sb("ones", [P, P])
        part = sb("part", [P, 3])
        bias = sb("bias", [P, D])
        xn = sb("xn", [P, 2, D])
        xT = sb("xT", [P, 2, DH, P])
        loaded, ones_ready, part_ready, total_ps, w_ready = (sem(x) for x in ("loaded", "ones", "part", "total", "w_ready"))
        own, xn_ready, biased, xt_ps, xt_ready, y_ps, added = (
            sem(x) for x in ("own", "xn_ready", "biased", "xt_ps", "xt_ready", "y_ps", "added"))
        with nc.Block() as block:
            @block.sync
            def _(sp):
                sp.dma_start(W[:, :, :], core.dram["WtT"].rearrange("(h p) e -> p h e", p=P)).then_inc(loaded, 16)
                sp.dma_start(bias[:, :], core.dram["t_bias"]).then_inc(loaded, 16)

            @block.gpsimd
            def _(pool):
                pool.memset(ones[:, :], 1.0).then_inc(ones_ready, 1)
                pool.wait_ge(loaded, 2 * 16)

                def step(t, u):
                    pool.wait_ge(xn_ready, t + 1)
                    pool.tensor_tensor(out=X[:, bass.ds(t, 1), :], in0=X[:, bass.ds(t, 1), :], in1=bias[:, :],
                                       op=ALU.add).then_inc(biased, 1)

                in_pairs(pool, NT, step)

            @block.vector
            def _(dve):
                link = Chain(dve, own, 8)
                dve.sem_inc(added, 2)
                dve.wait_ge(loaded, 2 * 16)
                dve.tensor_reduce(out=part[:, 0:1], in_=W[:, :, :], axis=AX.XY, op=ALU.add,
                                  apply_absolute_value=True).then_inc(part_ready, 1)
                dve.wait_ge(total_ps, 1)
                link(dve.tensor_scalar(out=part[:, 1:2], in0=PS[:, 7, 0:1], scalar1=1.0 / (D * D), scalar2=None, op0=ALU.mult))
                link(dve.tensor_scalar(out=part[:, 0:1], in0=part[:, 1:2], scalar1=1e-10, scalar2=None, op0=ALU.add))
                link(dve.reciprocal(out=part[:, 2:3], in_=part[:, 0:1]))
                link(dve.tensor_scalar(out=Wq[:, :, :], in0=W[:, :, :], scalar1=part[:, 2:3], scalar2=ROUND,
                                       op0=ALU.mult, op1=ALU.add))
                link(dve.tensor_scalar(out=Wq[:, :, :], in0=Wq[:, :, :], scalar1=ROUND, scalar2=1.0,
                                       op0=ALU.subtract, op1=ALU.min))
                link(dve.tensor_scalar(out=Wq[:, :, :], in0=Wq[:, :, :], scalar1=-1.0, scalar2=part[:, 1:2],
                                       op0=ALU.max, op1=ALU.mult))
                link(dve.tensor_tensor(out=Wq[:, :, :], in0=Wq[:, :, :], in1=W[:, :, :], op=ALU.subtract))
                link(dve.tensor_tensor(out=Wq[:, :, :], in0=Wq[:, :, :], in1=W[:, :, :], op=ALU.add))
                dve.sem_inc(w_ready, 1)

                def normalise(t, u):
                    dve.tensor_scalar(out=xn[:, u, :], in0=X[:, bass.ds(t, 1), :], scalar1=core.mean[:, bass.ds(t, 1)],
                                      scalar2=core.rstd[:, bass.ds(t, 1)], op0=ALU.subtract,
                                      op1=ALU.mult).then_inc(xn_ready, 1)

                def add(t, u):
                    dve.wait_ge(y_ps, t + 1)
                    dve.wait_ge(biased, t + 1)
                    dve.tensor_tensor(out=X[:, bass.ds(t, 1), :], in0=X[:, bass.ds(t, 1), :], in1=PS[:, 2 + u, 0:D],
                                      op=ALU.add).then_inc(added, 1)

                normalise(0, 0)
                normalise(1, 1)
                with dve.Fori(0, NT // 2 - 1) as i:
                    for k in range(2):
                        add(2 * i + k, k)
                        normalise(2 * i + k + 2, k)
                add(NT - 2, 0)
                add(NT - 1, 1)

            @block.scalar
            def _(act):
                def step(t, u):
                    act.wait_ge(xt_ps, t + 1)
                    act.activation(xT[:, u, :, :], PS[:, u, 0:D].rearrange("p (h t) -> p h t", h=DH),
                                   ACT.Copy).then_inc(xt_ready, 1)

                in_pairs(act, NT, step)

            @block.tensor
            def _(pe):
                pe.wait_ge(ones_ready, 1)
                pe.wait_ge(part_ready, 1)
                pe.matmul(PS[:, 7, 0:1], ones[:, :], part[:, 0:1], start=True, stop=True).then_inc(total_ps, 1)
                pe.wait_ge(w_ready, 1)

                def front(t, u):
                    pe.wait_ge(xn_ready, t + 1)
                    for h in range(DH):
                        last = pe.transpose(PS[:, u, h * P:h * P + P], xn[:, u, h * P:h * P + P], core.ident[:, :])
                    last.then_inc(xt_ps, 1)

                def back(t, u):
                    pe.wait_ge(xt_ready, t + 1)
                    pe.wait_ge(added, t + 1)
                    for h in range(DH):
                        last = pe.matmul(PS[:, 2 + u, 0:D], xT[:, u, h, :], Wq[:, h, :], start=(h == 0), stop=(h == DH - 1))
                    last.then_inc(y_ps, 1)

                skewed(pe, NT, front, back)


HID = 704
ZERO_POINT = 128.0
GT = 4


def blocks(hid):
    return [min(P, hid - at) for at in range(0, hid, P)]


def gated_ffn(core, tag, hid, prepare, router=None):
    nc, X, PS = core.nc, core.X, core.PS
    NG = NT // GT
    size = blocks(hid)
    M = len(size)
    with core.stage(tag) as (sb, sem):
        Wg = sb("Wg", [P, DH, hid])
        Wu = sb("Wu", [P, DH, hid])
        Wd = sb("Wd", [P, M, D])
        xn = sb("xn", [P, 2, GT, D])
        xT = sb("xT", [P, 2, DH, GT * P])
        sg = sb("sg", [P, 2, GT * P])
        hT = sb("hT", [P, M, GT * P])
        w_ready = sem("w_ready")
        load, make = prepare(sb, sem, Wg, Wu, Wd, w_ready)
        xn_ready, xt_ps, xt_ready, gu_ps, silu_ready, h_ready, y_ps, added, lg_ps, lg_ready, n_stored, n_free = (
            sem(x) for x in ("xn_ready", "xt_ps", "xt_ready", "gu_ps", "silu", "h_ready", "y_ps", "added", "lg_ps",
                             "lg_ready", "n_stored", "n_free"))
        with nc.Block() as block:
            @block.sync
            def _(sp):
                load(sp)
                if router:
                    rows_of = router["rows"].rearrange("(n p) d -> p n d", p=P)

                    def store(g, u):
                        sp.wait_ge(xn_ready, g + 1)
                        sp.dma_start(rows_of[:, bass.ds(GT * g, GT), :], xn[:, u, :, :]).then_inc(n_stored, 16)
                        sp.wait_ge(n_stored, 16 * g + 16)
                        sp.sem_inc(n_free, 1)

                    in_pairs(sp, NG, store)

            @block.vector
            def _(dve):
                make(dve)
                dve.sem_inc(h_ready, 2)
                dve.sem_inc(added, 2)
                dve.sem_inc(n_free, 2)

                def normalise(g, u):
                    if router:
                        dve.wait_ge(n_free, g + 1)
                    for k in range(GT):
                        t = GT * g + k
                        last = dve.tensor_scalar(out=xn[:, u, k, :], in0=X[:, bass.ds(t, 1), :],
                                                 scalar1=core.mean[:, bass.ds(t, 1)], scalar2=core.rstd[:, bass.ds(t, 1)],
                                                 op0=ALU.subtract, op1=ALU.mult)
                    last.then_inc(xn_ready, 1)

                def body(g, u, more):
                    if more:
                        normalise(g + 1, 1 - u)
                    for m in range(M):
                        dve.wait_ge(silu_ready, M * g + m + 1)
                        r = slice(0, size[m])
                        dve.tensor_tensor(out=hT[r, m, :], in0=sg[r, (M * u + m) % 2, :],
                                          in1=PS[r, 4 + (M * u + m) % 2, :], op=ALU.mult).then_inc(h_ready, 1)
                    for k in range(2):
                        dve.wait_ge(y_ps, 2 * g + k + 1)
                        t = GT * g + 2 * k
                        dve.tensor_tensor(out=X[:, bass.ds(t, 2), :], in0=X[:, bass.ds(t, 2), :],
                                          in1=PS[:, 6 + k, :].rearrange("p (k d) -> p k d", k=2),
                                          op=ALU.add).then_inc(added, 1)

                ahead(dve, NG, normalise, body)

            @block.scalar
            def _(act):
                def copy(g, u):
                    for h in range(DH):
                        act.wait_ge(xt_ps, DH * g + h + 1)
                        act.activation(xT[:, u, h, :], PS[:, h, :], ACT.Copy).then_inc(xt_ready, 1)

                def body(g, u, more):
                    if router:
                        act.wait_ge(lg_ps, g + 1)
                        act.activation(router["logits"][:, bass.ds(GT * g, GT), :],
                                       PS[:, 0, 0:GT * router["E"]].rearrange("p (k e) -> p k e", k=GT),
                                       ACT.Copy).then_inc(lg_ready, 1)
                    for m in range(M):
                        act.wait_ge(gu_ps, M * g + m + 1)
                        r = slice(0, size[m])
                        act.activation(sg[r, (M * u + m) % 2, :], PS[r, 2 + (M * u + m) % 2, :],
                                       ACT.Silu).then_inc(silu_ready, 1)
                    if more:
                        copy(g + 1, 1 - u)

                ahead(act, NG, copy, body)

            @block.tensor
            def _(pe):
                def transposes(g, u):
                    pe.wait_ge(xn_ready, g + 1)
                    for h in range(DH):
                        for k in range(GT):
                            last = pe.transpose(PS[:, h, k * P:k * P + P], xn[:, u, k, h * P:h * P + P], core.ident[:, :])
                        last.then_inc(xt_ps, 1)

                def body(g, u, more):
                    pe.wait_ge(xt_ready, DH * g + DH)
                    if router:
                        E = router["E"]
                        for k in range(GT):
                            for h in range(DH):
                                last = pe.matmul(PS[:, 0, k * E:k * E + E], xT[:, u, h, k * P:k * P + P],
                                                 router["W"][:, h, :], start=(h == 0), stop=(h == DH - 1))
                        last.then_inc(lg_ps, 1)
                    for m in range(M):
                        pe.wait_ge(h_ready, M * g + m + 1)
                        for w, bank in ((Wg, 2), (Wu, 4)):
                            for h in range(DH):
                                last = pe.matmul(PS[0:size[m], bank + (M * u + m) % 2, :], w[:, h, m * P:m * P + size[m]],
                                                 xT[:, u, h, :], start=(h == 0), stop=(h == DH - 1))
                        last.then_inc(gu_ps, 1)
                    if more:
                        if router:
                            pe.wait_ge(lg_ready, g + 1)
                        transposes(g + 1, 1 - u)
                    pe.wait_ge(h_ready, M * g + M + 2)
                    for k in range(GT):
                        if k % 2 == 0:
                            pe.wait_ge(added, 2 * g + k // 2 + 1)
                        for m in range(M):
                            last = pe.matmul(PS[:, 6 + k // 2, k % 2 * D:k % 2 * D + D],
                                             hT[0:size[m], m, k * P:k * P + P], Wd[0:size[m], m, :],
                                             start=(m == 0), stop=(m == M - 1))
                        if k % 2:
                            last.then_inc(y_ps, 1)

                pe.wait_ge(w_ready, 1)
                ahead(pe, NG, transposes, body)


def quantised_ffn(core):
    statistics(core, "3", core.X, LN_EPS)
    size = blocks(HID)
    M = len(size)

    def prepare(sb, sem, Wg, Wu, Wd, w_ready):
        raw = sb("raw", [P, DH, HID], I32)
        raw_d = sb("raw_d", [P, M, D], I32)
        s_row = sb("s_row", [P, HID])
        s_down = sb("s_down", [P, D])
        load_g, load_u, load_d, own, gate_made = (sem(x) for x in ("load_g", "load_u", "load_d", "own", "gate_made"))

        def load(sp):
            full = (M - 1) * P
            sp.dma_start(raw[:, :, :], core.dram["wq_gateT"].rearrange("(h p) e -> p h e", p=P)).then_inc(load_g, 16)
            sp.dma_start(s_row[:, :], core.dram["s_gate"]).then_inc(load_g, 16)
            sp.dma_start(raw_d[:, 0:M - 1, :], core.dram["wq_downT"][0:full, :].rearrange("(m p) e -> p m e", p=P)).then_inc(load_d, 16)
            sp.dma_start(raw_d[0:size[-1], M - 1, :], core.dram["wq_downT"][full:HID, :]).then_inc(load_d, 16)
            sp.dma_start(s_down[:, :], core.dram["s_down"]).then_inc(load_d, 16)
            sp.wait_ge(gate_made, 1)
            sp.dma_start(raw[:, :, :], core.dram["wq_upT"].rearrange("(h p) e -> p h e", p=P)).then_inc(load_u, 16)
            sp.dma_start(s_row[:, :], core.dram["s_up"]).then_inc(load_u, 16)

        def make(dve):
            link = Chain(dve, own, 2)

            def dequantise(w, r, s):
                return dve.scalar_tensor_tensor(out=w, in0=r, scalar=ZERO_POINT, in1=s, op0=ALU.subtract, op1=ALU.mult)

            dve.wait_ge(load_g, 2 * 16)
            for h in range(DH):
                link(dequantise(Wg[:, h, :], raw[:, h, :], s_row[:, :]))
            dve.sem_inc(gate_made, 1)
            dve.wait_ge(load_d, 3 * 16)
            for m in range(M):
                dequantise(Wd[0:size[m], m, :], raw_d[0:size[m], m, :], s_down[0:size[m], :])
            dve.wait_ge(load_u, 2 * 16)
            for h in range(DH):
                last = dequantise(Wu[:, h, :], raw[:, h, :], s_row[:, :])
            last.then_inc(w_ready, 1)

        return load, make

    gated_ffn(core, "qf", HID, prepare)


HEADS = 16
NOPE, ROPE, VDIM = 128, 64, 128
QL, KL = 192, 64
QK = KL + ROPE
LOW = QL + KL + ROPE
RMS_EPS = float(np.finfo(np.float32).eps)


def latent_attention(core):
    with ExitStack() as keep:
        def sb(tag, shape, dt=F32):
            return keep.enter_context(core.nc.sbuf_tensor("la_" + tag, shape, dt))

        q1 = sb("q1", [P, HEADS, QK])
        q2 = sb("q2", [QL - P, HEADS, QK])
        out = sb("out", [P, HEADS // 2, D])
        latent_weights(core, q1, q2, out)
        statistics(core, "2", core.X, LN_EPS)
        latent_heads(core, q1, q2, out)


def latent_weights(core, q1, q2, out):
    nc, PS = core.nc, core.PS
    SCALE = 1.0 / float(np.sqrt(np.float32(NOPE + ROPE)))
    R2 = QL - P
    with core.stage("lw") as (sb, sem):
        wq = sb("wq", [P, HEADS, QL])
        wk = sb("wk", [P, HEADS, KL])
        wv = sb("wv", [P, HEADS, KL])
        wo = sb("wo", [P, HEADS, D])
        g1 = sb("g1", [P, 1])
        g2 = sb("g2", [R2, 1])
        loaded, loaded_o, own, prod_ps, prod_free, prod2_ps, rope_done = (
            sem(x) for x in ("loaded", "loaded_o", "own", "prod_ps", "prod_free", "prod2", "rope"))
        with nc.Block() as block:
            @block.sync
            def _(sp):
                for a, name in ((wq, "Wqb_nopeT"), (wk, "Wkvb_kT")):
                    sp.dma_start(a[:, :, :], core.dram[name]).then_inc(loaded, 16)
                sp.dma_start(q1[:, :, KL:QK], core.dram["Wqb_rope"][0:P, :, :]).then_inc(loaded, 16)
                sp.dma_start(q2[:, :, KL:QK], core.dram["Wqb_rope"][P:QL, :, :]).then_inc(loaded, 16)
                sp.dma_start(g1[:, :], core.dram["q_ln_w"][0:P, :]).then_inc(loaded, 16)
                sp.dma_start(g2[:, :], core.dram["q_ln_w"][P:QL, :]).then_inc(loaded, 16)
                for a, name in ((wv, "Wkvb_vT"), (wo, "Wo_heads")):
                    sp.dma_start(a[:, :, :], core.dram[name]).then_inc(loaded_o, 16)

            @block.tensor
            def _(pe):
                pe.wait_ge(loaded, 6 * 16)
                for h in range(HEADS):
                    at = h % 8 * KL
                    pe.matmul(PS[:, h // 8, at:at + KL], wq[:, h, 0:P], wk[:, h, :], start=True, stop=True)
                    last = pe.matmul(PS[0:R2, 2 + h // 8, at:at + KL], wq[:, h, P:QL], wk[:, h, :], start=True, stop=True)
                last.then_inc(prod_ps, 1)
                pe.wait_ge(loaded_o, 2 * 16)
                for j in range(HEADS // 2):
                    if j == 4:
                        pe.wait_ge(prod_free, 1)
                    for k in range(2):
                        last = pe.matmul(PS[k * KL:k * KL + KL, (4 + j) % 8, 0:D], wv[:, 2 * j + k, :],
                                         wo[:, 2 * j + k, :], start=True, stop=True)
                    last.then_inc(prod2_ps, 1)

            @block.vector
            def _(dve):
                link = Chain(dve, own, 4)
                dve.wait_ge(loaded, 6 * 16)
                link(dve.tensor_scalar(out=g1[:, :], in0=g1[:, :], scalar1=SCALE, scalar2=None, op0=ALU.mult))
                link(dve.tensor_scalar(out=g2[:, :], in0=g2[:, :], scalar1=SCALE, scalar2=None, op0=ALU.mult))
                for w, g in ((q1, g1), (q2, g2)):
                    dve.tensor_scalar(out=w[:, :, KL:QK], in0=w[:, :, KL:QK], scalar1=g[:, 0:1], scalar2=None, op0=ALU.mult)
                dve.wait_ge(prod_ps, 1)
                for k in range(2):
                    dve.tensor_scalar(out=q1[:, 8 * k:8 * k + 8, 0:KL], in0=PS[:, k, :].rearrange("p (h c) -> p h c", h=8),
                                      scalar1=g1[:, 0:1], scalar2=None, op0=ALU.mult)
                    link(dve.tensor_scalar(out=q2[:, 8 * k:8 * k + 8, 0:KL],
                                           in0=PS[0:R2, 2 + k, :].rearrange("p (h c) -> p h c", h=8),
                                           scalar1=g2[:, 0:1], scalar2=None, op0=ALU.mult))
                dve.sem_inc(prod_free, 1)

            @block.scalar
            def _(act):
                for j in range(HEADS // 2):
                    act.wait_ge(prod2_ps, j + 1)
                    act.activation(out[:, j, :], PS[:, (4 + j) % 8, 0:D], ACT.Copy)


def latent_heads(core, q1, q2, out):
    nc, X, PS = core.nc, core.X, core.PS
    R2 = QL - P
    PAIRS = HEADS // 2
    H2 = ROPE // 2
    with core.stage("lh") as (sb, sem):
        Wa = sb("Wa", [P, DH, LOW])
        kvw = sb("kvw", [P, KL])
        cos = sb("cos", [P, TPB, ROPE])
        sin = sb("sin", [P, TPB, ROPE])
        mask = sb("mask", [P, P], BF16)
        xn = sb("xn", [P, TPB, D])
        xT = sb("xT", [P, DH, T])
        low = sb("low", [P, TPB, LOW])
        junk = sb("junk", [P, TPB, QL + KL])
        eps = sb("eps", [P, TPB, 2])
        ms = sb("ms", [P, TPB, 2])
        rs = sb("rs", [P, TPB, 2])
        qn = sb("qn", [P, TPB, QL])
        ktok = sb("ktok", [P, TPB, QK])
        c1 = sb("c1", [P, TPB, KL + 1])
        qc1 = sb("qc1", [P, T])
        qc2 = sb("qc2", [R2, T])
        KT = sb("KT", [P, T])
        qtok = sb("qtok", [P, TPB, HEADS, QK])
        ra = sb("ra", [P, HEADS, ROPE])
        rb = sb("rb", [P, HEADS, ROPE])
        QT = sb("QT", [P, HEADS, T])
        negm = sb("negm", [P, 2, 4])
        p0 = sb("p0", [P, 2, 2, P])
        p1 = sb("p1", [P, 2, 2, T])
        t0 = sb("t0", [P, 2, 2, T])
        t1 = sb("t1", [P, 2, 2, P])
        rz = sb("rz", [P, 2, 4])
        oc = sb("oc", [P, TPB, HEADS * KL])
        oT = sb("oT", [P, PAIRS, T])
        names = ("loaded consts mask_made xn_ready xt_ps xt_ready low_ps low_ready ms_ready rs_ready qn_ready c_ready kr_ready "
                 "qct_ps qct_ready kt_ps kt_ready q_ps q_ready roped qt_ps qt_a qt_d s_ps negm_ready exp_done pt_ps pt_a "
                 "pt_d o_ps o_done oct_ps oct_ready y_ps added own own2 own3 pown").split()
        S = {n: sem(n) for n in names}

        with nc.Block() as block:
            @block.sync
            def _(sp):
                sp.dma_start(Wa[:, :, :], core.dram["Wa"].rearrange("(h p) e -> p h e", p=P)).then_inc(S["loaded"], 16)
                sp.dma_start(kvw[:, :], core.dram["kv_ln_w"]).then_inc(S["loaded"], 16)
                sp.dma_start(cos[:, :, :], core.dram["cos"].rearrange("(k p) e -> p k e", p=P)).then_inc(S["loaded"], 16)
                sp.dma_start(sin[:, :, :], core.dram["sin"].rearrange("(k p) e -> p k e", p=P)).then_inc(S["loaded"], 16)

            @block.tensor
            def _(pe):
                pe.wait_ge(S["loaded"], 4 * 16)
                pe.wait_ge(S["mask_made"], 1)
                with pe.Fori(0, B) as b:
                    pe.wait_ge(S["xn_ready"], b + 1)
                    for h in range(DH):
                        for k in range(TPB):
                            last = pe.transpose(PS[:, 0, h * T + k * P:h * T + k * P + P], xn[:, k, h * P:h * P + P],
                                                core.ident[:, :])
                    last.then_inc(S["xt_ps"], 1)
                    pe.wait_ge(S["xt_ready"], b + 1)
                    for k in range(TPB):
                        for h in range(DH):
                            last = pe.matmul(PS[:, 1 + k, 0:LOW], xT[:, h, k * P:k * P + P], Wa[:, h, :],
                                             start=(h == 0), stop=(h == DH - 1))
                        last.then_inc(S["low_ps"], 1)
                    pe.wait_ge(S["qn_ready"], TPB * b + TPB)
                    for k in range(TPB):
                        pe.transpose(PS[:, 3, k * P:k * P + P], qn[:, k, 0:P], core.ident[:, :])
                        last = pe.transpose(PS[0:R2, 3, T + k * P:T + k * P + P], qn[:, k, P:QL], core.ident[:, :])
                    last.then_inc(S["qct_ps"], 1)
                    pe.wait_ge(S["c_ready"], b + 1)
                    pe.wait_ge(S["kr_ready"], b + 1)
                    pe.wait_ge(S["added"], TPB * b + TPB)
                    for k in range(TPB):
                        last = pe.transpose(PS[:, 4, k * P:k * P + P], ktok[:, k, :], core.ident[:, :])
                    last.then_inc(S["kt_ps"], 1)
                    pe.wait_ge(S["qct_ready"], b + 1)
                    pe.wait_ge(S["kt_ready"], b + 1)
                    for k in range(TPB):
                        for j in range(4):
                            pe.matmul(PS[:, 4 * k + j, :], qc1[:, k * P:k * P + P], q1[:, 4 * j:4 * j + 4, :],
                                      start=True, stop=False)
                            pe.matmul(PS[:, 4 * k + j, :], qc2[:, k * P:k * P + P], q2[:, 4 * j:4 * j + 4, :],
                                      start=False, stop=True).then_inc(S["q_ps"], 1)
                    pe.wait_ge(S["roped"], TPB * b + TPB)
                    for j in range(PAIRS):
                        for i in range(2):
                            for k in range(TPB):
                                last = pe.transpose(PS[:, j, i * T + k * P:i * T + k * P + P], qtok[:, k, 2 * j + i, :],
                                                    core.ident[:, :])
                        last.then_inc(S["qt_ps"], 1)
                    pe.wait_ge(S["qt_a"], PAIRS // 2 * b + PAIRS // 2)
                    pe.wait_ge(S["qt_d"], PAIRS // 2 * b + PAIRS // 2)

                    def scores(g):
                        u = g % 2
                        if g >= 2:
                            pe.wait_ge(S["exp_done"], PAIRS * b + g - 1)
                        for i in range(2):
                            h = 2 * g + i
                            pe.matmul(PS[:, 2 * u, i * T:i * T + T], QT[:, h, P:T], KT[:, :], start=True, stop=False)
                            pe.matmul(PS[:, 2 * u, i * T + P:i * T + T], core.identb[:, :], mask[:, :],
                                      start=False, stop=True)
                        for i in range(2):
                            h = 2 * g + i
                            pe.matmul(PS[:, 2 * u + 1, i * P:i * P + P], QT[:, h, 0:P], KT[:, 0:P], start=True, stop=False)
                            last = pe.matmul(PS[:, 2 * u + 1, i * P:i * P + P], core.identb[:, :], mask[:, :],
                                             start=False, stop=True)
                        last.then_inc(S["s_ps"], 1)

                    scores(0)
                    scores(1)
                    for g in range(PAIRS):
                        u = g % 2
                        pe.wait_ge(S["exp_done"], PAIRS * b + g + 1)
                        for i in range(2):
                            pe.transpose(PS[:, 4, i * T:i * T + P], p0[:, u, i, :], core.ident[:, :])
                            pe.transpose(PS[:, 4, i * T + P:i * T + T], p1[:, u, i, 0:P], core.ident[:, :])
                            last = pe.transpose(PS[:, 5, i * P:i * P + P], p1[:, u, i, P:T], core.ident[:, :])
                        last.then_inc(S["pt_ps"], 1)
                        if g + 2 < PAIRS:
                            scores(g + 2)
                        pe.wait_ge(S["pt_a"], PAIRS * b + g + 1)
                        pe.wait_ge(S["pt_d"], PAIRS * b + g + 1)
                        if g >= 2:
                            pe.wait_ge(S["o_done"], PAIRS * b + g - 1)
                        W1 = KL + 1
                        for i in range(2):
                            pe.matmul(PS[:, 6 + u, i * W1:i * W1 + W1], t0[:, u, i, 0:P], c1[:, 0, :], start=True, stop=True)
                        for i in range(2):
                            o = PS[:, 6 + u, (2 + i) * W1:(3 + i) * W1]
                            pe.matmul(o, t0[:, u, i, P:T], c1[:, 0, :], start=True, stop=False)
                            last = pe.matmul(o, t1[:, u, i, :], c1[:, 1, :], start=False, stop=True)
                        last.then_inc(S["o_ps"], 1)
                    pe.wait_ge(S["o_done"], PAIRS * b + PAIRS)
                    for j in range(PAIRS):
                        for k in range(TPB):
                            last = pe.transpose(PS[:, j // 2, j % 2 * T + k * P:j % 2 * T + k * P + P],
                                                oc[:, k, j * P:j * P + P], core.ident[:, :])
                        if j % 2:
                            last.then_inc(S["oct_ps"], 1)
                    pe.wait_ge(S["oct_ready"], 4 * b + 4)
                    for k in range(TPB):
                        for j in range(PAIRS):
                            last = pe.matmul(PS[:, 4 + k, 0:D], oT[:, j, k * P:k * P + P], out[:, j, :],
                                             start=(j == 0), stop=(j == PAIRS - 1))
                        last.then_inc(S["y_ps"], 1)

            @block.scalar
            def _(act):
                link = Chain(act, S["own2"], 2 * TPB)
                with act.Fori(0, B) as b:
                    act.wait_ge(S["xt_ps"], b + 1)
                    act.activation(xT[:, :, :], PS[:, 0, :].rearrange("p (h t) -> p h t", h=DH),
                                   ACT.Copy).then_inc(S["xt_ready"], 1)
                    link.start(b)
                    for k in range(TPB):
                        act.wait_ge(S["low_ps"], TPB * b + k + 1)
                        link(act.activation(low[:, k, :], PS[:, 1 + k, 0:LOW], ACT.Copy))
                        act.activation(junk[:, k, 0:QL], low[:, k, 0:QL], ACT.Square, scale=QL ** -0.5,
                                       accum_out=ms[:, k, 0:1])
                        link(act.activation(junk[:, k, QL:QL + KL], low[:, k, QL:QL + KL], ACT.Square, scale=KL ** -0.5,
                                            accum_out=ms[:, k, 1:2]))
                        act.sem_inc(S["ms_ready"], 1)
                    act.wait_ge(S["rs_ready"], b + 1)
                    for k in range(TPB):
                        act.activation(qn[:, k, :], low[:, k, 0:QL], ACT.Copy, scale=rs[:, k, 0:1]).then_inc(S["qn_ready"], 1)
                    act.wait_ge(S["qct_ps"], b + 1)
                    act.activation(qc1[:, :], PS[:, 3, 0:T], ACT.Copy)
                    act.activation(qc2[:, :], PS[0:R2, 3, T:2 * T], ACT.Copy).then_inc(S["qct_ready"], 1)
                    act.wait_ge(S["kt_ps"], b + 1)
                    act.activation(KT[:, :], PS[:, 4, 0:T], ACT.Copy).then_inc(S["kt_ready"], 1)
                    for k in range(TPB):
                        for j in range(4):
                            act.wait_ge(S["q_ps"], 8 * b + 4 * k + j + 1)
                            act.activation(qtok[:, k, 4 * j:4 * j + 4, :], PS[:, 4 * k + j, :].rearrange("p (h c) -> p h c", h=4),
                                           ACT.Copy).then_inc(S["q_ready"], 1)
                    for j in range(0, PAIRS, 2):
                        act.wait_ge(S["qt_ps"], PAIRS * b + j + 1)
                        act.activation(QT[:, 2 * j:2 * j + 2, :], PS[:, j, :].rearrange("p (i t) -> p i t", i=2),
                                       ACT.Copy).then_inc(S["qt_a"], 1)

                    def exps(g):
                        u = g % 2
                        act.wait_ge(S["negm_ready"], PAIRS * b + g + 1)
                        for i in range(2):
                            act.activation(p1[:, u, i, :], PS[:, 2 * u, i * T:i * T + T], ACT.Exp, bias=negm[:, u, i:i + 1])
                        for i in range(2):
                            last = act.activation(p0[:, u, i, :], PS[:, 2 * u + 1, i * P:i * P + P], ACT.Exp,
                                                  bias=negm[:, u, 2 + i:3 + i])
                        last.then_inc(S["exp_done"], 1)

                    exps(0)
                    for g in range(PAIRS):
                        if g + 1 < PAIRS:
                            exps(g + 1)
                        act.wait_ge(S["pt_ps"], PAIRS * b + g + 1)
                        act.activation(t0[:, g % 2, :, :], PS[:, 4, :].rearrange("p (i t) -> p i t", i=2),
                                       ACT.Copy).then_inc(S["pt_a"], 1)
                    for j in range(4):
                        act.wait_ge(S["oct_ps"], 4 * b + j + 1)
                        act.activation(oT[:, 2 * j:2 * j + 2, :], PS[:, j, :].rearrange("p (i t) -> p i t", i=2),
                                       ACT.Copy).then_inc(S["oct_ready"], 1)

            @block.gpsimd
            def _(pool):
                mz = S["consts"]
                pool.memset(c1[:, :, KL:KL + 1], 1.0)
                pool.memset(eps[:, :, :], RMS_EPS)
                pool.memset(mask[:, :], 0.0).then_inc(mz, 1)
                pool.wait_ge(mz, 1)
                pool.affine_select(out=mask[:, :], in_=mask[:, :], compare_op=ALU.is_ge, fill=-1e30, base=0,
                                   pattern=[[-1, P]], channel_multiplier=1).then_inc(S["mask_made"], 1)
                pool.wait_ge(S["loaded"], 4 * 16)
                rp = Chain(pool, S["pown"], 1 + 2 + 2 * TPB)

                def rotate(dst, src, k, n):
                    a, c = ra[:, 0:n, :], rb[:, 0:n, :]
                    cb = cos[:, k:k + 1, :].broadcast_to([P, n, ROPE])
                    sb_ = sin[:, k:k + 1, :].broadcast_to([P, n, ROPE])
                    pool.tensor_tensor(out=a, in0=src, in1=cb, op=ALU.mult)
                    pool.tensor_tensor(out=c[:, :, 0:H2], in0=src[:, :, H2:ROPE], in1=sb_[:, :, 0:H2], op=ALU.mult)
                    rp(pool.tensor_tensor(out=c[:, :, H2:ROPE], in0=src[:, :, 0:H2], in1=sb_[:, :, H2:ROPE], op=ALU.mult))
                    rp(pool.tensor_tensor(out=dst, in0=a, in1=c, op=ALU.add))

                with pool.Fori(0, B) as b:
                    pool.wait_ge(S["ms_ready"], TPB * b + TPB)
                    rp.start(b)
                    rp(pool.tensor_tensor(out=ms[:, :, :], in0=ms[:, :, :], in1=eps[:, :, :], op=ALU.add))
                    pool.tensor_tensor(out=rs[:, :, :], in0=ms[:, :, :],
                                       in1=core.half[:, 0:2 * TPB].rearrange("p (k c) -> p k c", k=TPB),
                                       op=ALU.pow).then_inc(S["rs_ready"], 1)
                    kr = low[:, :, QL + KL:LOW]
                    pool.tensor_tensor(out=ra[:, 0:TPB, :], in0=kr, in1=cos[:, :, :], op=ALU.mult)
                    pool.tensor_tensor(out=rb[:, 0:TPB, 0:H2], in0=kr[:, :, H2:ROPE], in1=sin[:, :, 0:H2], op=ALU.mult)
                    rp(pool.tensor_tensor(out=rb[:, 0:TPB, H2:ROPE], in0=kr[:, :, 0:H2], in1=sin[:, :, H2:ROPE], op=ALU.mult))
                    rp(pool.tensor_tensor(out=ktok[:, :, KL:QK], in0=ra[:, 0:TPB, :], in1=rb[:, 0:TPB, :], op=ALU.add))
                    pool.sem_inc(S["kr_ready"], 1)
                    for k in range(TPB):
                        pool.wait_ge(S["q_ready"], 8 * b + 4 * k + 4)
                        rotate(qtok[:, k, :, KL:QK], qtok[:, k, :, KL:QK], k, HEADS)
                        pool.sem_inc(S["roped"], 1)

            @block.vector
            def _(dve):
                link = Chain(dve, S["own"], 2 * PAIRS)
                dve.sem_inc(S["added"], 2)
                dve.wait_ge(S["loaded"], 4 * 16)
                with dve.Fori(0, B) as b:
                    for k in range(TPB):
                        t = TPB * b + k
                        last = dve.tensor_scalar(out=xn[:, k, :], in0=X[:, bass.ds(t, 1), :],
                                                 scalar1=core.mean[:, bass.ds(t, 1)], scalar2=core.rstd[:, bass.ds(t, 1)],
                                                 op0=ALU.subtract, op1=ALU.mult)
                    last.then_inc(S["xn_ready"], 1)
                    dve.wait_ge(S["rs_ready"], b + 1)
                    for k in range(TPB):
                        for d in (ktok[:, k, 0:KL], c1[:, k, 0:KL]):
                            last = dve.scalar_tensor_tensor(out=d, in0=low[:, k, QL:QL + KL], scalar=rs[:, k, 1:2],
                                                            in1=kvw[:, :], op0=ALU.mult, op1=ALU.mult)
                    last.then_inc(S["c_ready"], 1)
                    for j in range(1, PAIRS, 2):
                        dve.wait_ge(S["qt_ps"], PAIRS * b + j + 1)
                        dve.tensor_copy(QT[:, 2 * j:2 * j + 2, :],
                                        PS[:, j, :].rearrange("p (i t) -> p i t", i=2)).then_inc(S["qt_d"], 1)
                    link.start(b)

                    def maxima(g):
                        u = g % 2
                        dve.wait_ge(S["s_ps"], PAIRS * b + g + 1)
                        dve.tensor_reduce(out=negm[:, u, 0:2], in_=PS[:, 2 * u, :].rearrange("p (i t) -> p i t", i=2),
                                          axis=AX.X, op=ALU.max, negate=True)
                        link(dve.tensor_reduce(out=negm[:, u, 2:4], in_=PS[:, 2 * u + 1, 0:T].rearrange("p (i t) -> p i t", i=2),
                                               axis=AX.X, op=ALU.max, negate=True))
                        dve.sem_inc(S["negm_ready"], 1)

                    def finish(g):
                        u = g % 2
                        dve.wait_ge(S["o_ps"], PAIRS * b + g + 1)
                        o = PS[:, 6 + u, 0:4 * (KL + 1)].rearrange("p (q i c) -> p q i c", q=2, i=2)
                        link(dve.reciprocal(out=rz[:, u, :], in_=o[:, :, :, KL]))
                        r = rz[:, u, :].rearrange("p (q i c) -> p q i c", q=2, c=1).broadcast_to([P, 2, 2, KL])
                        dve.tensor_tensor(out=oc[:, :, 2 * g * KL:(2 * g + 2) * KL].rearrange("p q (i c) -> p q i c", i=2),
                                          in0=o[:, :, :, 0:KL], in1=r, op=ALU.mult).then_inc(S["o_done"], 1)

                    maxima(0)
                    for g in range(PAIRS):
                        if g + 1 < PAIRS:
                            maxima(g + 1)
                        dve.wait_ge(S["pt_ps"], PAIRS * b + g + 1)
                        dve.tensor_copy(t1[:, g % 2, :, :],
                                        PS[:, 5, 0:T].rearrange("p (i t) -> p i t", i=2)).then_inc(S["pt_d"], 1)
                        if g >= 1:
                            finish(g - 1)
                    finish(PAIRS - 1)
                    for k in range(TPB):
                        t = TPB * b + k
                        dve.wait_ge(S["y_ps"], t + 1)
                        dve.tensor_tensor(out=X[:, bass.ds(t, 1), :], in0=X[:, bass.ds(t, 1), :], in1=PS[:, 4 + k, 0:D],
                                          op=ALU.add).then_inc(S["added"], 1)


HD = 16
PAD = 32
SLOTS = NT + 32


def double_attention(core):
    nc, X, PS = core.nc, core.X, core.PS
    PAIRS = HEADS // 2
    statistics(core, "4", X, LN_EPS)
    with core.stage("da") as (sb, sem):
        WT = sb("WT", [P, DH, D])
        W = sb("W", [P, DH, D])
        g = sb("g", [P, 3, HEADS, HD])
        zero = sb("zero", [P, 2048])
        eps = sb("eps", [P, TPB * HEADS])
        xn = sb("xn", [P, TPB, D])
        xT = sb("xT", [P, DH, T])
        w = sb("w", [P, TPB * HEADS, HD])
        sq = sb("sq", [P, TPB * HEADS, HD])
        ms = sb("ms", [P, TPB * HEADS])
        rs = sb("rs", [P, TPB * HEADS])
        q = sb("q", [P, 2, TPB, HEADS, PAD])
        v = sb("v", [P, TPB, HEADS, HD])
        QT = sb("QT", [P, 2, 4, T])
        negm = sb("negm", [P, 2, 2, TPB])
        z = sb("z", [P, 2, 2, TPB])
        rz = sb("rz", [P, 2, 2, TPB])
        ex = sb("ex", [P, 2, 2, TPB, T])
        eT = sb("eT", [P, 2, 2, TPB, T])
        vz = sb("vz", [P, 2, TPB, 2, HD])
        o1 = sb("o1", [P, 2, TPB, 2, HD])
        y = sb("y", [P, TPB, D])
        yT = sb("yT", [P, DH, T])
        S = {n: sem(n) for n in (
            "loaded padded zeroed stored xn_ready xt_ps xt_ready w_ps w_ready sq_ready ms_ready rs_ready qk_ready v_ready "
            "qt_ps qt_ready s_ps negm_ready exp_done vz_ready et_ps et_a et_d o_ps o_done yt_ps yt_ready out_ps added "
            "own own_pre own_fin ownp ownr").split()}

        with nc.Block() as block:
            @block.sync
            def _(sp):
                sp.dma_start(WT[:, :, :], core.dram["W2T"].rearrange("(h p) e -> p h e", p=P)).then_inc(S["loaded"], 16)
                sp.dma_start(W[:, :, :], core.dram["W2"].rearrange("(h p) e -> p h e", p=P)).then_inc(S["loaded"], 16)
                sp.dma_start(g[:, :, :, :], core.dram["g2"].rearrange("p (a h d) -> p a h d", a=3, h=HEADS)).then_inc(S["loaded"], 16)
                sp.wait_ge(S["zeroed"], 1)
                slots = core.slots_x.rearrange("(n p r) d -> n p (r d)", p=P, r=8)
                for k in range(SLOTS // 8):
                    sp.dma_start(slots[k], zero[:, :]).then_inc(S["stored"], 16)
                sp.wait_ge(S["stored"], SLOTS // 8 * 16)

            @block.tensor
            def _(pe):
                pe.wait_ge(S["loaded"], 3 * 16)
                with pe.Fori(0, B) as b:
                    pe.wait_ge(S["xn_ready"], b + 1)
                    for h in range(DH):
                        for k in range(TPB):
                            last = pe.transpose(PS[:, 0, h * T + k * P:h * T + k * P + P], xn[:, k, h * P:h * P + P],
                                                core.ident[:, :])
                    last.then_inc(S["xt_ps"], 1)
                    pe.wait_ge(S["xt_ready"], b + 1)
                    pe.wait_ge(S["added"], b + 1)
                    for k in range(TPB):
                        for h in range(DH):
                            last = pe.matmul(PS[:, 1, k * D:k * D + D], xT[:, h, k * P:k * P + P], WT[:, h, :],
                                             start=(h == 0), stop=(h == DH - 1))
                    last.then_inc(S["w_ps"], 1)
                    pe.wait_ge(S["qk_ready"], b + 1)
                    for a in range(2):
                        for c in range(4):
                            for k in range(TPB):
                                last = pe.transpose(PS[:, 2 + 2 * a + c // 2, c % 2 * T + k * P:c % 2 * T + k * P + P],
                                                    q[:, a, k, 4 * c:4 * c + 4, :], core.ident[:, :])
                            if c % 2:
                                last.then_inc(S["qt_ps"], 1)
                    pe.wait_ge(S["qt_ready"], 4 * b + 4)
                    pe.wait_ge(S["v_ready"], b + 1)

                    def scores(c):
                        if c >= 2:
                            pe.wait_ge(S["exp_done"], PAIRS * b + c - 1)
                        for i in range(2):
                            h = 2 * c + i
                            r = slice(h % 4 * PAD, h % 4 * PAD + PAD)
                            for k in range(TPB):
                                last = pe.matmul(PS[:, 2 * (c % 2) + i, k * T:k * T + T], QT[r, 0, h // 4, k * P:k * P + P],
                                                 QT[r, 1, h // 4, :], start=True, stop=True)
                        last.then_inc(S["s_ps"], 1)

                    scores(0)
                    scores(1)
                    for c in range(PAIRS):
                        u = c % 2
                        pe.wait_ge(S["exp_done"], PAIRS * b + c + 1)
                        for i in range(2):
                            for j in range(TPB):
                                for k in range(TPB):
                                    last = pe.transpose(PS[:, 4 + i, j * T + k * P:j * T + k * P + P],
                                                        ex[:, u, i, k, j * P:j * P + P], core.ident[:, :])
                        last.then_inc(S["et_ps"], 1)
                        if c + 2 < PAIRS:
                            scores(c + 2)
                        pe.wait_ge(S["vz_ready"], PAIRS * b + c + 1)
                        pe.wait_ge(S["et_a"], PAIRS * b + c + 1)
                        pe.wait_ge(S["et_d"], PAIRS * b + c + 1)
                        if c >= 2:
                            pe.wait_ge(S["o_done"], PAIRS * b + c - 1)
                        for term in range(2):
                            for k in range(TPB):
                                for i in range(2):
                                    at = ((term * TPB + k) * 2 + i) * HD
                                    for j in range(TPB):
                                        a = eT if term == 0 else ex
                                        r = v[:, j, 2 * c + i, :] if term == 0 else vz[:, u, j, i, :]
                                        last = pe.matmul(PS[:, 6 + u, at:at + HD], a[:, u, i, j, k * P:k * P + P], r,
                                                         start=(j == 0), stop=(j == TPB - 1))
                        last.then_inc(S["o_ps"], 1)
                    pe.wait_ge(S["o_done"], PAIRS * b + PAIRS)
                    for h in range(DH):
                        for k in range(TPB):
                            last = pe.transpose(PS[:, 0, h * T + k * P:h * T + k * P + P], y[:, k, h * P:h * P + P],
                                                core.ident[:, :])
                    last.then_inc(S["yt_ps"], 1)
                    pe.wait_ge(S["yt_ready"], b + 1)
                    for k in range(TPB):
                        for h in range(DH):
                            last = pe.matmul(PS[:, 1, k * D:k * D + D], yT[:, h, k * P:k * P + P], W[:, h, :],
                                             start=(h == 0), stop=(h == DH - 1))
                    last.then_inc(S["out_ps"], 1)

            @block.scalar
            def _(act):
                with act.Fori(0, B) as b:
                    act.wait_ge(S["xt_ps"], b + 1)
                    act.activation(xT[:, :, :], PS[:, 0, :].rearrange("p (h t) -> p h t", h=DH),
                                   ACT.Copy).then_inc(S["xt_ready"], 1)
                    act.wait_ge(S["w_ps"], b + 1)
                    act.activation(w[:, :, :], PS[:, 1, :].rearrange("p (n d) -> p n d", d=HD), ACT.Copy).then_inc(S["w_ready"], 1)
                    for n in range(4):
                        act.wait_ge(S["qt_ps"], 4 * b + n + 1)
                        act.activation(QT[:, n // 2, 2 * (n % 2):2 * (n % 2) + 2, :],
                                       PS[:, 2 + n, :].rearrange("p (c t) -> p c t", c=2), ACT.Copy).then_inc(S["qt_ready"], 1)

                    def exps(c):
                        u = c % 2
                        act.wait_ge(S["negm_ready"], PAIRS * b + c + 1)
                        if c >= 2:
                            act.wait_ge(S["o_ps"], PAIRS * b + c - 1)
                        for i in range(2):
                            for k in range(TPB):
                                last = act.activation(ex[:, u, i, k, :], PS[:, 2 * u + i, k * T:k * T + T], ACT.Exp,
                                                      bias=negm[:, u, i, k:k + 1], accum_out=z[:, u, i, k:k + 1])
                        last.then_inc(S["exp_done"], 1)

                    exps(0)
                    for c in range(PAIRS):
                        act.wait_ge(S["et_ps"], PAIRS * b + c + 1)
                        act.activation(eT[:, c % 2, 0, :, :], PS[:, 4, :].rearrange("p (j t) -> p j t", j=TPB),
                                       ACT.Copy).then_inc(S["et_a"], 1)
                        if c + 1 < PAIRS:
                            exps(c + 1)
                    act.wait_ge(S["yt_ps"], b + 1)
                    act.activation(yT[:, :, :], PS[:, 0, :].rearrange("p (h t) -> p h t", h=DH),
                                   ACT.Copy).then_inc(S["yt_ready"], 1)

            @block.gpsimd
            def _(pool):
                pool.memset(zero[:, :], 0.0).then_inc(S["zeroed"], 1)
                pool.memset(eps[:, :], RMS_EPS)
                pool.memset(q[:, :, :, :, :], 0.0).then_inc(S["padded"], 1)
                pool.wait_ge(S["padded"], 1)
                pool.wait_ge(S["loaded"], 3 * 16)
                link = Chain(pool, S["ownp"], 1)
                with pool.Fori(0, B) as b:
                    pool.wait_ge(S["w_ready"], b + 1)
                    pool.tensor_tensor(out=sq[:, :, :], in0=w[:, :, :], in1=w[:, :, :], op=ALU.mult).then_inc(S["sq_ready"], 1)
                    pool.wait_ge(S["ms_ready"], b + 1)
                    link.start(b)
                    link(pool.tensor_tensor(out=rs[:, :], in0=ms[:, :], in1=core.half[:, 0:TPB * HEADS], op=ALU.pow))
                    pool.sem_inc(S["rs_ready"], 1)
                    pool.wait_ge(S["own_pre"], b + 1)
                    for k in range(TPB):
                        last = pool.tensor_tensor(out=v[:, k, :, :], in0=w[:, k * HEADS:k * HEADS + HEADS, :],
                                                  in1=g[:, 2, :, :], op=ALU.mult)
                    last.then_inc(S["v_ready"], 1)

            @block.vector
            def _(dve):
                link, fin = Chain(dve, S["own"], PAIRS), Chain(dve, S["own_fin"], 2 * PAIRS)
                dve.sem_inc(S["added"], 1)
                dve.wait_ge(S["loaded"], 3 * 16)
                dve.tensor_scalar(out=g[:, 1, :, :], in0=g[:, 1, :, :], scalar1=HD ** -0.5, scalar2=None,
                                  op0=ALU.mult)
                dve.wait_ge(S["padded"], 1)
                with dve.Fori(0, B) as b:
                    for k in range(TPB):
                        t = TPB * b + k
                        last = dve.tensor_scalar(out=xn[:, k, :], in0=X[:, bass.ds(t, 1), :],
                                                 scalar1=core.mean[:, bass.ds(t, 1)], scalar2=core.rstd[:, bass.ds(t, 1)],
                                                 op0=ALU.subtract, op1=ALU.mult)
                    last.then_inc(S["xn_ready"], 1)
                    dve.wait_ge(S["sq_ready"], b + 1)
                    red = Chain(dve, S["ownr"], 1)
                    red.start(b)
                    red(dve.tensor_reduce(out=ms[:, :], in_=sq[:, :, :], axis=AX.X, op=ALU.add))
                    dve.tensor_scalar(out=ms[:, :], in0=ms[:, :], scalar1=1.0 / HD, scalar2=RMS_EPS, op0=ALU.mult,
                                      op1=ALU.add).then_inc(S["ms_ready"], 1)
                    dve.wait_ge(S["rs_ready"], b + 1)
                    r = rs[:, :].rearrange("p (n d) -> p n d", d=1).broadcast_to([P, TPB * HEADS, HD])
                    dve.tensor_tensor(out=w[:, :, :], in0=w[:, :, :], in1=r, op=ALU.mult).then_inc(S["own_pre"], 1)
                    dve.wait_ge(S["own_pre"], b + 1)
                    for k in range(TPB):
                        for a in range(2):
                            last = dve.tensor_tensor(out=q[:, a, k, :, 0:HD], in0=w[:, k * HEADS:k * HEADS + HEADS, :],
                                                     in1=g[:, a, :, :], op=ALU.mult)
                    last.then_inc(S["qk_ready"], 1)
                    link.start(b)
                    fin.start(b)

                    def maxima(c):
                        u = c % 2
                        dve.wait_ge(S["s_ps"], PAIRS * b + c + 1)
                        dve.tensor_reduce(out=negm[:, u, 0, :], in_=PS[:, 2 * u, :].rearrange("p (k t) -> p k t", k=TPB),
                                          axis=AX.X, op=ALU.max, negate=True)
                        dve.tensor_reduce(out=negm[:, u, 1, :], in_=PS[:, 2 * u + 1, :].rearrange("p (k t) -> p k t", k=TPB),
                                          axis=AX.X, op=ALU.max, negate=True).then_inc(S["negm_ready"], 1)

                    def values(c):
                        u = c % 2
                        dve.wait_ge(S["exp_done"], PAIRS * b + c + 1)
                        link(dve.reciprocal(out=rz[:, u, :, :], in_=z[:, u, :, :]))
                        for i in range(2):
                            rr = rz[:, u, i, :].rearrange("p (k d) -> p k d", d=1).broadcast_to([P, TPB, HD])
                            last = dve.tensor_tensor(out=vz[:, u, :, i, :], in0=v[:, :, 2 * c + i, :], in1=rr, op=ALU.mult)
                        last.then_inc(S["vz_ready"], 1)

                    def finish(c):
                        u = c % 2
                        dve.wait_ge(S["o_ps"], PAIRS * b + c + 1)
                        o = PS[:, 6 + u, 0:8 * HD].rearrange("p (a k i d) -> p a k i d", a=2, k=TPB, i=2)
                        for i in range(2):
                            rr = rz[:, u, i, :].rearrange("p (k d) -> p k d", d=1).broadcast_to([P, TPB, HD])
                            fin(dve.tensor_tensor(out=o1[:, u, :, i, :], in0=o[:, 0, :, i, :], in1=rr, op=ALU.mult))
                        dve.tensor_tensor(out=y[:, :, 2 * c * HD:(2 * c + 2) * HD].rearrange("p k (i d) -> p k i d", i=2),
                                          in0=o[:, 1, :, :, :], in1=o1[:, u, :, :, :], op=ALU.add).then_inc(S["o_done"], 1)

                    dve.wait_ge(S["v_ready"], b + 1)
                    maxima(0)
                    for c in range(PAIRS):
                        if c + 1 < PAIRS:
                            maxima(c + 1)
                        values(c)
                        dve.wait_ge(S["et_ps"], PAIRS * b + c + 1)
                        dve.tensor_copy(eT[:, c % 2, 1, :, :],
                                        PS[:, 5, :].rearrange("p (j t) -> p j t", j=TPB)).then_inc(S["et_d"], 1)
                        if c >= 1:
                            finish(c - 1)
                    finish(PAIRS - 1)
                    dve.wait_ge(S["out_ps"], b + 1)
                    t = TPB * b
                    dve.tensor_tensor(out=X[:, bass.ds(t, TPB), :], in0=X[:, bass.ds(t, TPB), :],
                                      in1=PS[:, 1, :].rearrange("p (k d) -> p k d", k=TPB), op=ALU.add).then_inc(S["added"], 1)


EXPERTS = 32
TL = P // B


def crossed(rows, tl):
    return rows.rearrange("(s g l) d -> l s g d", s=B, l=TL)[tl]


def masked_experts(core):
    nc = core.nc
    statistics(core, "5", core.X, LN_EPS)
    with ExitStack() as keep:
        def sb(tag, shape, dt=F32):
            return keep.enter_context(nc.sbuf_tensor("me_" + tag, shape, dt))

        rows = sb("rows", [P, NT, D])
        logits = sb("logits", [P, NT, EXPERTS])
        slot = sb("slot", [P, NT], I32)
        slot_x = sb("slot_x", [P, NT], I32)
        weight_x = sb("weight_x", [P, NT])
        expert = sb("expert", [P, SLOTS], I32)
        Xc = sb("Xc", [P, NT, D])
        router_logits(core, rows, logits)
        route_top1(core, logits, slot, slot_x, weight_x, expert, Xc)
        expert_tiles(core, rows, slot, expert)
        collect_top1(core, rows, slot_x, weight_x, Xc)


def router_logits(core, rows, logits):
    nc, X, PS = core.nc, core.X, core.PS
    with core.stage("rl") as (sb, sem):
        R = sb("R", [P, DH, EXPERTS])
        xn = sb("xn", [P, 2, D])
        xT = sb("xT", [P, 2, DH, P])
        loaded, xn_ready, kept, xt_ps, xt_ready, lg_ps, lg_free = (
            sem(x) for x in ("loaded", "xn_ready", "kept", "xt_ps", "xt_ready", "lg_ps", "lg_free"))
        with nc.Block() as block:
            @block.sync
            def _(sp):
                sp.dma_start(R[:, :, :], core.dram["router"].rearrange("(h p) e -> p h e", p=P)).then_inc(loaded, 16)

            @block.vector
            def _(dve):
                dve.sem_inc(kept, 2)

                def step(t, u):
                    dve.wait_ge(kept, t + 1)
                    dve.tensor_scalar(out=xn[:, u, :], in0=X[:, bass.ds(t, 1), :], scalar1=core.mean[:, bass.ds(t, 1)],
                                      scalar2=core.rstd[:, bass.ds(t, 1)], op0=ALU.subtract,
                                      op1=ALU.mult).then_inc(xn_ready, 1)

                in_pairs(dve, NT, step)

            @block.gpsimd
            def _(pool):
                def step(t, u):
                    pool.wait_ge(xn_ready, t + 1)
                    pool.wait_ge(xt_ps, t + 1)
                    pool.tensor_copy(rows[:, bass.ds(t, 1), :], xn[:, u, :]).then_inc(kept, 1)

                in_pairs(pool, NT, step)

            @block.scalar
            def _(act):
                act.sem_inc(lg_free, 2)

                def front(t, u):
                    act.wait_ge(xt_ps, t + 1)
                    act.activation(xT[:, u, :, :], PS[:, u, 0:D].rearrange("p (h t) -> p h t", h=DH),
                                   ACT.Copy).then_inc(xt_ready, 1)

                def back(t, u):
                    act.wait_ge(lg_ps, t + 1)
                    act.activation(logits[:, bass.ds(t, 1), :], PS[:, 2 + u, 0:EXPERTS], ACT.Copy).then_inc(lg_free, 1)

                skewed(act, NT, front, back)

            @block.tensor
            def _(pe):
                pe.wait_ge(loaded, 16)

                def front(t, u):
                    pe.wait_ge(xn_ready, t + 1)
                    for h in range(DH):
                        last = pe.transpose(PS[:, u, h * P:h * P + P], xn[:, u, h * P:h * P + P], core.ident[:, :])
                    last.then_inc(xt_ps, 1)

                def back(t, u):
                    pe.wait_ge(xt_ready, t + 1)
                    pe.wait_ge(lg_free, t + 1)
                    for h in range(DH):
                        last = pe.matmul(PS[:, 2 + u, 0:EXPERTS], xT[:, u, h, :], R[:, h, :], start=(h == 0), stop=(h == DH - 1))
                    last.then_inc(lg_ps, 1)

                skewed(pe, NT, front, back)


def route_top1(core, logits, slot, slot_x, weight_x, expert, Xc):
    nc, X, PS = core.nc, core.X, core.PS
    E = EXPERTS
    HB = NT // 2
    with core.stage("rt") as (sb, sem):
        iota_e = sb("iota_e", [P, NT, E])
        iota_s = sb("iota_s", [P, SLOTS])
        reset = sb("reset", [P, E, NT])
        before = sb("before", [P, P], BF16)
        ones = sb("ones", [P, P], BF16)
        one_e = sb("one_e", [P, E])
        top = sb("top", [P, NT])
        shifted = sb("shifted", [P, NT, E])
        work = sb("work", [P, NT, E])
        first = sb("first", [P, NT])
        hot = sb("hot", [P, NT, E], BF16)
        count = sb("count", [P, E, NT])
        upto = sb("upto", [P, E, NT])
        tiles = sb("tiles", [P, 4, E])
        tiles_i = sb("tiles_i", [P, E], I32)
        slot_f = sb("slot_f", [P, NT])
        table = sb("table", [P, NT, 2])
        table_x = sb("table_x", [P, NT, 2])
        cmp = sb("cmp", [P, SLOTS, E])
        S = {n: sem(n) for n in "made x_stored x_loaded shifted exp_done hot_ready count_ps own table_ready table_stored table_loaded".split()}
        dram_x, dram_t = core.scratch_x, core.scratch_t
        with nc.Block() as block:
            @block.sync
            def _(sp):
                xr = dram_x.rearrange("(n p) d -> p n d", p=P)
                for k in range(4):
                    sp.dma_start(xr[:, 8 * k:8 * k + 8, :], X[:, 8 * k:8 * k + 8, :]).then_inc(S["x_stored"], 16)
                sp.wait_ge(S["x_stored"], 4 * 16)
                for tl in range(TL):
                    sp.dma_start(Xc[tl * B:tl * B + B, :, :], crossed(dram_x, tl)).then_inc(S["x_loaded"], 16)
                sp.wait_ge(S["table_ready"], 1)
                sp.dma_start(dram_t.rearrange("(n p) d -> p n d", p=P), table[:, :, :]).then_inc(S["table_stored"], 16)
                sp.wait_ge(S["table_stored"], 16)
                for tl in range(TL):
                    sp.dma_start(table_x[tl * B:tl * B + B, :, :], crossed(dram_t, tl)).then_inc(S["table_loaded"], 16)
                sp.wait_ge(S["x_loaded"], TL * 16)

            @block.gpsimd
            def _(pool):
                made = S["made"]
                pool.iota(iota_e[:, :, :], [[0, NT], [1, E]], base=-64, channel_multiplier=0,
                          allow_small_or_imprecise_dtypes=True).then_inc(made, 1)
                pool.iota(iota_s[:, :], [[1, SLOTS]], base=0, channel_multiplier=0,
                          allow_small_or_imprecise_dtypes=True).then_inc(made, 1)
                pool.memset(reset[:, :, :], 1.0).then_inc(made, 1)
                pool.memset(ones[:, :], 1.0).then_inc(made, 1)
                pool.memset(one_e[:, :], 1.0).then_inc(made, 1)
                pool.memset(before[:, :], 1.0).then_inc(made, 1)
                pool.wait_ge(made, 6)
                pool.memset(reset[:, :, 0:1], 0.0).then_inc(made, 1)
                pool.affine_select(out=before[:, :], in_=before[:, :], compare_op=ALU.is_gt, fill=0.0, base=0,
                                   pattern=[[1, P]], channel_multiplier=-1).then_inc(made, 1)

            @block.scalar
            def _(act):
                act.wait_ge(S["shifted"], 1)
                act.activation(shifted[:, :, :], shifted[:, :, :], ACT.Exp).then_inc(S["exp_done"], 1)

            @block.tensor
            def _(pe):
                pe.wait_ge(S["made"], 8)
                pe.wait_ge(S["hot_ready"], 1)
                for w, bank in ((before, 0), (ones, 2)):
                    for k in range(2):
                        last = pe.matmul(PS[:, bank + k, :], w[:, :], hot[:, k * HB:k * HB + HB, :], start=True, stop=True)
                last.then_inc(S["count_ps"], 1)

            @block.vector
            def _(dve):
                link = Chain(dve, S["own"], 40)

                def over_e(a, n=NT):
                    return a.rearrange("p (n e) -> p n e", e=1).broadcast_to([P, n, E])

                dve.wait_ge(S["made"], 8)
                link(dve.tensor_reduce(out=top[:, :], in_=logits[:, :, :], axis=AX.X, op=ALU.max))
                link(dve.tensor_tensor(out=shifted[:, :, :], in0=logits[:, :, :], in1=over_e(top[:, :]), op=ALU.subtract))
                link(dve.tensor_single_scalar(out=work[:, :, :], in_=shifted[:, :, :], scalar=0.0, op=ALU.is_equal))
                dve.sem_inc(S["shifted"], 1)
                link(dve.tensor_tensor(out=work[:, :, :], in0=work[:, :, :], in1=iota_e[:, :, :], op=ALU.mult))
                link(dve.tensor_reduce(out=first[:, :], in_=work[:, :, :], axis=AX.X, op=ALU.min))
                link(dve.tensor_tensor(out=hot[:, :, :], in0=iota_e[:, :, :], in1=over_e(first[:, :]), op=ALU.is_equal))
                dve.sem_inc(S["hot_ready"], 1)
                dve.wait_ge(S["exp_done"], 1)
                link(dve.tensor_reduce(out=top[:, :], in_=shifted[:, :, :], axis=AX.X, op=ALU.add))
                link(dve.reciprocal(out=table[:, :, 1], in_=top[:, :]))
                dve.wait_ge(S["count_ps"], 1)
                for k in range(2):
                    link(dve.tensor_copy(count[:, :, k * HB:k * HB + HB],
                                         PS[:, 2 + k, :].rearrange("p (n e) -> p e n", e=E)))
                link(dve.tensor_tensor_scan(out=upto[:, :, :].rearrange("p e n -> p (e n)"),
                                            data0=reset[:, :, :].rearrange("p e n -> p (e n)"),
                                            data1=count[:, :, :].rearrange("p e n -> p (e n)"), initial=0.0,
                                            op0=ALU.mult, op1=ALU.add))
                link(dve.tensor_tensor(out=count[:, :, :], in0=upto[:, :, :], in1=count[:, :, :], op=ALU.subtract))
                link(dve.tensor_scalar(out=tiles_i[:, :], in0=upto[:, :, NT - 1], scalar1=float(P - 1), scalar2=None, op0=ALU.add))
                link(dve.tensor_single_scalar(out=tiles_i[:, :], in_=tiles_i[:, :], scalar=7, op=ALU.arith_shift_right))
                link(dve.tensor_copy(tiles[:, 0, :], tiles_i[:, :]))
                link(dve.tensor_tensor_scan(out=tiles[:, 1, :], data0=one_e[:, :], data1=tiles[:, 0, :], initial=0.0,
                                            op0=ALU.mult, op1=ALU.add))
                link(dve.tensor_tensor(out=tiles[:, 2, :], in0=tiles[:, 1, :], in1=tiles[:, 0, :], op=ALU.subtract))
                link(dve.tensor_scalar(out=tiles[:, 2, :], in0=tiles[:, 2, :], scalar1=float(P), scalar2=None, op0=ALU.mult))
                first_slot = tiles[:, 2, :].rearrange("p (e n) -> p e n", n=1).broadcast_to([P, E, NT])
                link(dve.tensor_tensor(out=count[:, :, :], in0=count[:, :, :], in1=first_slot, op=ALU.add))
                for k in range(2):
                    link(dve.tensor_tensor(out=work[:, k * HB:k * HB + HB, :],
                                           in0=PS[:, k, :].rearrange("p (n e) -> p n e", e=E),
                                           in1=count[:, :, k * HB:k * HB + HB].rearrange("p e n -> p n e"), op=ALU.add))
                link(dve.tensor_tensor(out=work[:, :, :], in0=work[:, :, :], in1=hot[:, :, :], op=ALU.mult))
                link(dve.tensor_reduce(out=slot_f[:, :], in_=work[:, :, :], axis=AX.X, op=ALU.add))
                link(dve.tensor_copy(slot[:, :], slot_f[:, :]))
                link(dve.tensor_copy(table[:, :, 0], slot_f[:, :]))
                dve.sem_inc(S["table_ready"], 1)
                end = tiles[:, 1, :].rearrange("p (n e) -> p n e", n=1).broadcast_to([P, SLOTS, E])
                link(dve.tensor_tensor(out=cmp[:, :, :], in0=end, in1=over_e(iota_s[:, :], SLOTS), op=ALU.is_le))
                link(dve.tensor_reduce(out=iota_s[:, :], in_=cmp[:, :, :], axis=AX.X, op=ALU.add))
                link(dve.tensor_scalar(out=expert[:, :], in0=iota_s[:, :], scalar1=float(E - 1), scalar2=None, op0=ALU.min))
                dve.wait_ge(S["table_loaded"], TL * 16)
                dve.tensor_copy(slot_x[:, :], table_x[:, :, 0])
                dve.tensor_copy(weight_x[:, :], table_x[:, :, 1])


def expert_tiles(core, rows, slot, expert):
    nc, PS = core.nc, core.PS
    ROUND = 1.5 * 2.0 ** 23
    NB = 4
    with core.stage("et") as (sb, sem):
        wq = sb("wq", [P, DH, D])
        scale = sb("scale", [P, D])
        x = sb("x", [P, NB, D])
        mask = sb("mask", [P, NB, DH, D])
        Wm = sb("Wm", [P, 2, DH, D])
        xT = sb("xT", [P, 2, DH, P])
        y = sb("y", [P, NB, D])
        S = {n: sem(n) for n in "w_loaded own w_ready scattered free wm_ready xt_ps xt_ready y_ps y_read wm_free".split()}
        x_in = [sem(f"x_in{k}") for k in range(NB)]
        m_in = [sem(f"m_in{k}") for k in range(NB)]
        y_out = [sem(f"y_out{k}") for k in range(NB)]

        def in_fours(eng, step):
            with eng.Fori(0, SLOTS // NB) as i:
                for k in range(NB):
                    step(i, k)

        with nc.Block() as block:
            @block.sync
            def _(sp):
                sp.dma_start(wq[:, :, :], core.dram["W3T"].rearrange("(h p) e -> p h e", p=P)).then_inc(S["w_loaded"], 16)
                sp.dma_start(scale[:, :], core.dram["scale"]).then_inc(S["w_loaded"], 16)
                sp.wait_ge(S["scattered"], NT * 16)

                def step(i, k):
                    s = NB * i + k
                    sp.wait_ge(S["free"], s + 1)
                    e = sp.value_load(expert[0:1, bass.ds(s, 1)], min_val=0, max_val=EXPERTS - 1)
                    sp.dma_start(x[:, k, :], core.slots_x[bass.ds(s * P, P), :]).then_inc(x_in[k], 16)
                    sp.dma_start(mask[:, k, :, :], core.dram["masks"][bass.ds(e, 1), :, :].rearrange("n (h p) o -> p (n h) o", p=P)).then_inc(m_in[k], 16)

                in_fours(sp, step)

            @block.gpsimd
            def _(pool):
                for t in range(NT):
                    pool.indirect_dma_start(out=core.slots_x[:, :], out_offset=bass.IndirectOffsetOnAxis(ap=slot[:, t:t + 1], axis=0),
                                            in_=rows[:, t, :], in_offset=None).then_inc(S["scattered"], 16)
                pool.wait_ge(S["w_ready"], 1)

                def step(i, k):
                    pool.wait_ge(m_in[k], 16 * i + 16)
                    pool.wait_ge(S["wm_free"], NB * i + k + 1)
                    pool.tensor_tensor(out=Wm[:, k % 2, :, :], in0=mask[:, k, :, :], in1=wq[:, :, :],
                                       op=ALU.mult).then_inc(S["wm_ready"], 1)

                in_fours(pool, step)

            @block.vector
            def _(dve):
                link = Chain(dve, S["own"], 3)
                dve.wait_ge(S["w_loaded"], 2 * 16)
                link(dve.tensor_scalar(out=wq[:, :, :], in0=wq[:, :, :], scalar1=2.0, scalar2=ROUND, op0=ALU.mult, op1=ALU.add))
                link(dve.tensor_scalar(out=wq[:, :, :], in0=wq[:, :, :], scalar1=ROUND, scalar2=1.0, op0=ALU.subtract, op1=ALU.min))
                for h in range(DH):
                    last = dve.scalar_tensor_tensor(out=wq[:, h, :], in0=wq[:, h, :], scalar=-1.0, in1=scale[:, :],
                                                    op0=ALU.max, op1=ALU.mult)
                last.then_inc(S["w_ready"], 1)
                dve.sem_inc(S["free"], NB)
                dve.sem_inc(S["wm_free"], 2)

                def step(i, k):
                    s = NB * i + k
                    dve.wait_ge(S["xt_ps"], s + 1)
                    dve.tensor_copy(xT[:, k % 2, :, :], PS[:, k % 2, 0:D].rearrange("p (h t) -> p h t", h=DH)).then_inc(S["xt_ready"], 1)
                    dve.wait_ge(S["y_ps"], s + 1)
                    dve.sem_inc(S["wm_free"], 1)
                    dve.sem_inc(S["free"], 1)

                in_fours(dve, step)

            @block.tensor
            def _(pe):
                def front(i, k):
                    pe.wait_ge(x_in[k], 16 * i + 16)
                    for h in range(DH):
                        last = pe.transpose(PS[:, k % 2, h * P:h * P + P], x[:, k, h * P:h * P + P], core.ident[:, :])
                    last.then_inc(S["xt_ps"], 1)

                def back(i, k):
                    s = NB * i + k
                    pe.wait_ge(S["xt_ready"], s + 1)
                    pe.wait_ge(S["wm_ready"], s + 1)
                    pe.wait_ge(S["y_read"], s + 1)
                    for h in range(DH):
                        last = pe.matmul(PS[:, 2 + k % 2, 0:D], xT[:, k % 2, h, :], Wm[:, k % 2, h, :],
                                         start=(h == 0), stop=(h == DH - 1))
                    last.then_inc(S["y_ps"], 1)

                def step(i, k):
                    front(i, k)
                    back(i, k)

                in_fours(pe, step)

            @block.scalar
            def _(act):
                act.sem_inc(S["y_read"], 2)

                for k in range(NB):
                    act.sem_inc(y_out[k], 16)

                def step(i, k):
                    s = NB * i + k
                    act.wait_ge(S["y_ps"], s + 1)
                    act.wait_ge(y_out[k], 16 * i + 16)
                    act.activation(y[:, k, :], PS[:, 2 + k % 2, 0:D], ACT.Copy).then_inc(S["y_read"], 1)
                    act.wait_ge(S["y_read"], s + 3)
                    act.dma_start(core.slots_y[bass.ds(s * P, P), :], y[:, k, :]).then_inc(y_out[k], 16)

                in_fours(act, step)
                for k in range(NB):
                    act.wait_ge(y_out[k], 16 * (SLOTS // NB) + 16)


def collect_top1(core, rows, slot_x, weight_x, Xc):
    nc, X = core.nc, core.X
    with core.stage("ct") as (sb, sem):
        fetched = [sem(f"fetched{k}") for k in range(4)]
        with nc.Block() as block:
            @block.gpsimd
            def _(pool):
                for t in range(NT):
                    pool.indirect_dma_start(out=rows[:, t, :], out_offset=None, in_=core.slots_y[:, :],
                                            in_offset=bass.IndirectOffsetOnAxis(ap=slot_x[:, t:t + 1], axis=0)).then_inc(fetched[t // 8], 16)

            @block.vector
            def _(dve):
                for k in range(4):
                    dve.wait_ge(fetched[k], 8 * 16)
                    with dve.Fori(8 * k, 8 * k + 8) as t:
                        dve.scalar_tensor_tensor(out=X[:, bass.ds(t, 1), :], in0=rows[:, bass.ds(t, 1), :],
                                                 scalar=weight_x[:, bass.ds(t, 1)], in1=Xc[:, bass.ds(t, 1), :],
                                                 op0=ALU.mult, op1=ALU.add)


def crossed_attention(core):
    nc, X, PS = core.nc, core.X, core.PS
    G4 = 4
    NG4 = HEADS // G4
    V1 = HD + 1
    statistics(core, "6", X, LN_EPS)
    with core.stage("ca") as (sb, sem):
        W = sb("W", [P, DH, 3 * D])
        bias = sb("bias", [P, 3, HEADS, HD])
        Wo = sb("Wo", [P, DH, D])
        bias_o = sb("bias_o", [P, D])
        mask = sb("mask", [P, G4, TL, B], BF16)
        xn = sb("xn", [P, 2, D])
        xT = sb("xT", [P, 2, DH, P])
        q = sb("q", [P, 2, 2, HEADS, PAD])
        v = sb("v", [P, 2, HEADS, V1])
        QT = sb("QT", [P, 2, 2, NG4, P])
        negm = sb("negm", [P, 2, G4])
        ex = sb("ex", [P, 2, G4, P])
        eT = sb("eT", [P, 2, G4, P])
        rz = sb("rz", [P, 2, HEADS])
        y = sb("y", [P, 2, D])
        yT = sb("yT", [P, 2, DH, P])
        S = {n: sem(n) for n in (
            "loaded padded scaled masked xn_ready biased xt_ps xt_ready qkv_ps qkv_ready qt_ps qt_a qt_d s_ps negm_ready "
            "exp_done et_ps et_ready o_ps y_ready yt_ps yt_ready out_ps added own own2 ownm").split()}

        with nc.Block() as block:
            @block.sync
            def _(sp):
                sp.dma_start(W[:, :, :], core.dram["w_qkvT"].rearrange("(h p) e -> p h e", p=P)).then_inc(S["loaded"], 16)
                sp.dma_start(bias[:, :, :, :], core.dram["b_qkv"].rearrange("p (a h d) -> p a h d", a=3, h=HEADS)).then_inc(S["loaded"], 16)
                sp.dma_start(Wo[:, :, :], core.dram["w_denseT"].rearrange("(h p) e -> p h e", p=P)).then_inc(S["loaded"], 16)
                sp.dma_start(bias_o[:, :], core.dram["b_dense"]).then_inc(S["loaded"], 16)

            @block.gpsimd
            def _(pool):
                pool.memset(q[:, :, :, :, :], 0.0).then_inc(S["padded"], 1)
                pool.memset(v[:, :, :, HD:V1], 1.0).then_inc(S["padded"], 1)
                link = Chain(pool, S["ownm"], 4)
                m = mask[:, :, :, :]
                link(pool.memset(m, 0.0))
                link(pool.affine_select(out=m, in_=m, compare_op=ALU.is_ge, fill=-1e4 * HD ** 0.5, base=0,
                                        pattern=[[0, G4], [-B, TL], [-1, B]], channel_multiplier=1))
                link(pool.affine_select(out=m, in_=m, compare_op=ALU.is_ge, fill=-1e30, base=B - 1,
                                        pattern=[[0, G4], [B, TL], [0, B]], channel_multiplier=-1))
                link(pool.affine_select(out=m, in_=m, compare_op=ALU.is_ge, fill=-1e30, base=0,
                                        pattern=[[0, G4], [-B, TL], [0, B]], channel_multiplier=1))
                pool.sem_inc(S["masked"], 1)
                pool.wait_ge(S["loaded"], 4 * 16)

                def step(t, u):
                    pool.wait_ge(S["xn_ready"], t + 1)
                    pool.tensor_tensor(out=X[:, bass.ds(t, 1), :], in0=X[:, bass.ds(t, 1), :], in1=bias_o[:, :],
                                       op=ALU.add).then_inc(S["biased"], 1)

                in_pairs(pool, NT, step)

            @block.tensor
            def _(pe):
                pe.wait_ge(S["loaded"], 4 * 16)
                pe.wait_ge(S["masked"], 1)

                def tokens(t, u):
                    pe.wait_ge(S["xn_ready"], t + 1)
                    for h in range(DH):
                        last = pe.transpose(PS[:, 0, h * P:h * P + P], xn[:, u, h * P:h * P + P], core.ident[:, :])
                    last.then_inc(S["xt_ps"], 1)

                def project(t, u):
                    pe.wait_ge(S["xt_ready"], t + 1)
                    for bank, at, n in ((1, 0, 2 * D), (2, 2 * D, D)):
                        for h in range(DH):
                            last = pe.matmul(PS[:, bank, 0:n], xT[:, u, h, :], W[:, h, at:at + n], start=(h == 0), stop=(h == DH - 1))
                    last.then_inc(S["qkv_ps"], 1)

                def heads(t, u):
                    pe.wait_ge(S["qkv_ready"], t + 1)
                    for a in range(2):
                        for c in range(NG4):
                            last = pe.transpose(PS[:, 1 + a, c * P:c * P + P], q[:, u, a, G4 * c:G4 * c + G4, :], core.ident[:, :])
                        last.then_inc(S["qt_ps"], 1)

                def scores(t, u, c):
                    w = c % 2
                    pe.wait_ge(S["exp_done"], NG4 * t + c + 1)
                    pe.matmul(PS[:, 3 + w, :], core.identb[:, :], mask[:, :, :, :], start=True, stop=False, skip_group_check=True)
                    r = slice(c * PAD, c * PAD + PAD)
                    for i in range(G4):
                        last = pe.matmul(PS[:, 3 + w, i * P:i * P + P], QT[r, u, 0, i, :], QT[r, u, 1, i, :],
                                         start=False, stop=(i == G4 - 1), skip_group_check=True)
                    last.then_inc(S["s_ps"], 1)

                def turn(t, u, c):
                    w = c % 2
                    pe.wait_ge(S["exp_done"], NG4 * t + c + 3)
                    pe.wait_ge(S["et_ready"], NG4 * t + c + 1)
                    for i in range(G4):
                        last = pe.transpose(PS[:, 5 + w, i * P:i * P + P], ex[:, w, i, :], core.ident[:, :])
                    last.then_inc(S["et_ps"], 1)

                def mix(t, u, c):
                    w = c % 2
                    pe.wait_ge(S["et_ready"], NG4 * t + c + 3)
                    if c == 0:
                        pe.wait_ge(S["added"], t + 1)
                    for i in range(G4):
                        h = G4 * i + c
                        last = pe.matmul(PS[:, 7, h * V1:h * V1 + V1], eT[:, w, i, :], v[:, u, h, :], start=True, stop=True)
                    if c == NG4 - 1:
                        last.then_inc(S["o_ps"], 1)

                def output(t, u):
                    pe.wait_ge(S["y_ready"], t + 2)
                    for h in range(DH):
                        last = pe.transpose(PS[:, 7, h * P:h * P + P], y[:, u, h * P:h * P + P], core.ident[:, :])
                    last.then_inc(S["yt_ps"], 1)
                    pe.wait_ge(S["yt_ready"], t + 1)
                    for h in range(DH):
                        last = pe.matmul(PS[:, 7, 0:D], yT[:, u, h, :], Wo[:, h, :], start=(h == 0), stop=(h == DH - 1))
                    last.then_inc(S["out_ps"], 1)

                def front(t, u):
                    tokens(t, u)
                    project(t, u)
                    heads(t, u)

                def body(t, u, more):
                    pe.wait_ge(S["qt_a"], t + 1)
                    pe.wait_ge(S["qt_d"], t + 1)
                    if more:
                        tokens(t + 1, 1 - u)
                    scores(t, u, 0)
                    scores(t, u, 1)
                    if more:
                        project(t + 1, 1 - u)
                    turn(t, u, 0)
                    scores(t, u, 2)
                    mix(t, u, 0)
                    if more:
                        heads(t + 1, 1 - u)
                    turn(t, u, 1)
                    scores(t, u, 3)
                    mix(t, u, 1)
                    for c in (2, 3):
                        turn(t, u, c)
                        mix(t, u, c)
                    output(t, u)

                ahead(pe, NT, front, body)

            @block.scalar
            def _(act):
                act.sem_inc(S["exp_done"], 2)

                def tokens(t, u):
                    act.wait_ge(S["xt_ps"], t + 1)
                    act.activation(xT[:, u, :, :], PS[:, 0, 0:D].rearrange("p (h t) -> p h t", h=DH),
                                   ACT.Copy).then_inc(S["xt_ready"], 1)

                def heads(t, u):
                    act.wait_ge(S["qt_ps"], 2 * t + 1)
                    act.activation(QT[:, u, 0, :, :], PS[:, 1, :].rearrange("p (c t) -> p c t", c=NG4),
                                   ACT.Copy).then_inc(S["qt_a"], 1)

                def exps(t, c):
                    w = c % 2
                    act.wait_ge(S["negm_ready"], NG4 * t + c + 1)
                    for i in range(G4):
                        last = act.activation(ex[:, w, i, :], PS[:, 3 + w, i * P:i * P + P], ACT.Exp,
                                              bias=negm[:, w, i:i + 1], scale=HD ** -0.5)
                    last.then_inc(S["exp_done"], 1)

                def front(t, u):
                    tokens(t, u)
                    heads(t, u)

                def body(t, u, more):
                    if more:
                        tokens(t + 1, 1 - u)
                    exps(t, 0)
                    exps(t, 1)
                    exps(t, 2)
                    if more:
                        heads(t + 1, 1 - u)
                    exps(t, 3)
                    act.wait_ge(S["yt_ps"], t + 1)
                    act.activation(yT[:, u, :, :], PS[:, 7, 0:D].rearrange("p (h t) -> p h t", h=DH),
                                   ACT.Copy).then_inc(S["yt_ready"], 1)

                ahead(act, NT, front, body)

            @block.vector
            def _(dve):
                link, link2 = Chain(dve, S["own"], NG4), Chain(dve, S["own2"], 1)
                dve.sem_inc(S["added"], 1)
                dve.sem_inc(S["et_ready"], 2)
                dve.sem_inc(S["y_ready"], 1)
                dve.wait_ge(S["loaded"], 4 * 16)
                dve.wait_ge(S["padded"], 2)

                def tokens(t, u):
                    dve.tensor_scalar(out=xn[:, u, :], in0=X[:, bass.ds(t, 1), :], scalar1=core.mean[:, bass.ds(t, 1)],
                                      scalar2=core.rstd[:, bass.ds(t, 1)], op0=ALU.subtract,
                                      op1=ALU.mult).then_inc(S["xn_ready"], 1)

                def project(t, u):
                    dve.wait_ge(S["qkv_ps"], t + 1)
                    dve.tensor_tensor(out=q[:, u, :, :, 0:HD],
                                      in0=PS[:, 1, :].rearrange("p (a h d) -> p a h d", a=2, h=HEADS),
                                      in1=bias[:, 0:2, :, :], op=ALU.add)
                    dve.tensor_tensor(out=v[:, u, :, 0:HD], in0=PS[:, 2, 0:D].rearrange("p (h d) -> p h d", h=HEADS),
                                      in1=bias[:, 2, :, :], op=ALU.add).then_inc(S["qkv_ready"], 1)

                def heads(t, u):
                    dve.wait_ge(S["qt_ps"], 2 * t + 2)
                    dve.tensor_copy(QT[:, u, 1, :, :], PS[:, 2, :].rearrange("p (c t) -> p c t", c=NG4)).then_inc(S["qt_d"], 1)

                def front(t, u):
                    tokens(t, u)
                    project(t, u)
                    heads(t, u)

                def maxima(t, c):
                    w = c % 2
                    dve.wait_ge(S["s_ps"], NG4 * t + c + 1)
                    link(dve.tensor_reduce(out=negm[:, w, :], in_=PS[:, 3 + w, :].rearrange("p (i t) -> p i t", i=G4),
                                           axis=AX.X, op=ALU.max, negate=True))
                    dve.tensor_scalar(out=negm[:, w, :], in0=negm[:, w, :], scalar1=HD ** -0.5, scalar2=None,
                                      op0=ALU.mult).then_inc(S["negm_ready"], 1)

                def turned(t, c):
                    w = c % 2
                    dve.wait_ge(S["et_ps"], NG4 * t + c + 1)
                    dve.tensor_copy(eT[:, w, :, :], PS[:, 5 + w, :].rearrange("p (i t) -> p i t", i=G4)).then_inc(S["et_ready"], 1)

                def body(t, u, more):
                    if more:
                        tokens(t + 1, 1 - u)
                    link.start(t)
                    maxima(t, 0)
                    maxima(t, 1)
                    if more:
                        project(t + 1, 1 - u)
                    turned(t, 0)
                    maxima(t, 2)
                    if more:
                        heads(t + 1, 1 - u)
                    turned(t, 1)
                    maxima(t, 3)
                    turned(t, 2)
                    turned(t, 3)
                    o = PS[:, 7, 0:HEADS * V1].rearrange("p (h d) -> p h d", h=HEADS)
                    dve.wait_ge(S["o_ps"], t + 1)
                    link2.start(t)
                    link2(dve.reciprocal(out=rz[:, u, :], in_=o[:, :, HD]))
                    dve.tensor_tensor(out=y[:, u, :].rearrange("p (h d) -> p h d", h=HEADS), in0=o[:, :, 0:HD],
                                      in1=rz[:, u, :].rearrange("p (h d) -> p h d", d=1).broadcast_to([P, HEADS, HD]),
                                      op=ALU.mult).then_inc(S["y_ready"], 1)
                    dve.wait_ge(S["out_ps"], t + 1)
                    dve.wait_ge(S["biased"], t + 1)
                    dve.tensor_tensor(out=X[:, bass.ds(t, 1), :], in0=X[:, bass.ds(t, 1), :], in1=PS[:, 7, 0:D],
                                      op=ALU.add).then_inc(S["added"], 1)

                ahead(dve, NT, front, body)


E4 = 16
TOP = 4
INTER = 176
SHARED = 352
CAP = P


def routed_experts(core):
    nc = core.nc
    statistics(core, "7", core.X, LN_EPS)
    with ExitStack() as keep:
        def sb(tag, shape, dt=F32):
            return keep.enter_context(nc.sbuf_tensor("re_" + tag, shape, dt))

        R = sb("R", [P, DH, E4])
        logits = sb("logits", [P, NT, E4])
        place = sb("place", [P, E4], I32)
        weight = sb("weight", [P, E4])
        shared_expert(core, R, logits)
        route_top4(core, logits, place, weight)
        run_experts(core, place, weight)


def shared_expert(core, R, logits):
    size = blocks(SHARED)
    M = len(size)

    def prepare(sb, sem, Wg, Wu, Wd, w_ready):
        zero = sb("zero", [P, D])
        loaded, zeroed = sem("loaded"), sem("zeroed")

        def load(sp):
            full = (M - 1) * P
            for w, name in ((Wg, "sw_gate"), (Wu, "sw_up")):
                sp.dma_start(w[:, :, :], core.dram[name].rearrange("(h p) e -> p h e", p=P)).then_inc(loaded, 16)
            sp.dma_start(Wd[:, 0:M - 1, :], core.dram["sw_down"][0:full, :].rearrange("(m p) e -> p m e", p=P)).then_inc(loaded, 16)
            sp.dma_start(Wd[0:size[-1], M - 1, :], core.dram["sw_down"][full:SHARED, :]).then_inc(loaded, 16)
            sp.dma_start(R[:, :, :], core.dram["gateT"].rearrange("(h p) e -> p h e", p=P)).then_inc(loaded, 16)
            sp.wait_ge(zeroed, 1)
            sp.dma_start(core.rows_x[N:N + P, :], zero[:, :]).then_inc(loaded, 16)
            sp.dma_start(core.rows_y[N:N + P, :], zero[:, :]).then_inc(loaded, 16)

        def make(dve):
            dve.memset(zero[:, :], 0.0).then_inc(zeroed, 1)
            dve.wait_ge(loaded, 7 * 16)
            dve.sem_inc(w_ready, 1)

        return load, make

    gated_ffn(core, "se", SHARED, prepare, {"W": R, "E": E4, "logits": logits, "rows": core.rows_x[0:N, :]})


def route_top4(core, logits, place, weight):
    nc, X, PS = core.nc, core.X, core.PS
    C = 6
    with core.stage("r4") as (sb, sem):
        iota_e = sb("iota_e", [P, NT, E4])
        iota_p = sb("iota_p", [P, P], BF16)
        row_i = sb("row_i", [P, 3], I32)
        row_f = sb("row_f", [P, 3])
        col_l = sb("col_l", [P, TL, B])
        col_s = sb("col_s", [P, TL, B])
        same_s = sb("same_s", [P, P])
        later_l = sb("later_l", [P, P])
        later_s = sb("later_s", [P, P])
        here = sb("here", [P, P], BF16)
        behind = sb("behind", [P, P], BF16)
        beyond = sb("beyond", [P, P], BF16)
        prob = sb("prob", [P, NT, E4])
        work = sb("work", [P, NT, E4])
        top = sb("top", [P, NT])
        best = sb("best", [P, NT, 8])
        index = sb("index", [P, NT, 8], U32)
        index_f = sb("index_f", [P, NT, 8])
        chosen = sb("chosen", [P, E4, NT])
        chosen_b = sb("chosen_b", [P, 3, E4, NT], BF16)
        reset = sb("reset", [P, E4, NT])
        upto = sb("upto", [P, E4, NT])
        rank = sb("rank", [P, E4, NT])
        rank_b = sb("rank_b", [P, NT, E4], BF16)
        wts = sb("wts", [P, NT, E4])
        rest = sb("rest", [P, NT, E4])
        tell = sb("tell", [P, NT, E4, C], BF16)
        tile_no = sb("tile_no", [P, NT, E4])
        part_no = sb("part_no", [P, NT, E4])
        hit = sb("hit", [P, 2, E4, P], BF16)
        zero = sb("zero", [P, P], BF16)
        told = sb("told", [P, E4, C])
        spare = sb("spare", [P, 4, E4])
        S = {n: sem(n) for n in "made shifted exp_done masks_ready chosen_ready rank_ps own tell_ready hit_ready hit_used told_ps x_stored".split()}
        with nc.Block() as block:
            @block.sync
            def _(sp):
                rows = core.rows_y[0:N, :].rearrange("(n p) d -> p n d", p=P)
                for k in range(4):
                    sp.dma_start(rows[:, 8 * k:8 * k + 8, :], X[:, 8 * k:8 * k + 8, :]).then_inc(S["x_stored"], 16)
                sp.wait_ge(S["x_stored"], 4 * 16)

            @block.gpsimd
            def _(pool):
                made = S["made"]
                loose = dict(allow_small_or_imprecise_dtypes=True)
                pool.iota(iota_e[:, :, :], [[0, NT], [1, E4]], base=0, channel_multiplier=0, **loose).then_inc(made, 1)
                pool.iota(iota_p[:, :], [[1, P]], base=0, channel_multiplier=0, **loose).then_inc(made, 1)
                pool.iota(row_i[:, :], [[0, 3]], base=0, channel_multiplier=1).then_inc(made, 1)
                pool.iota(col_l[:, :, :], [[1, TL], [0, B]], base=0, channel_multiplier=0, **loose).then_inc(made, 1)
                pool.iota(col_s[:, :, :], [[0, TL], [1, B]], base=0, channel_multiplier=0, **loose).then_inc(made, 1)
                pool.iota(tile_no[:, :, :], [[1, NT], [0, E4]], base=0, channel_multiplier=0, **loose).then_inc(made, 1)
                pool.iota(part_no[:, :, :], [[0, NT], [0, E4]], base=0, channel_multiplier=1, **loose).then_inc(made, 1)
                pool.memset(zero[:, :], 0.0).then_inc(made, 1)
                pool.memset(reset[:, :, :], 1.0).then_inc(made, 1)
                pool.wait_ge(made, 9)
                pool.memset(reset[:, :, 0:1], 0.0).then_inc(made, 1)

            @block.scalar
            def _(act):
                act.wait_ge(S["shifted"], 1)
                act.activation(prob[:, :, :], prob[:, :, :], ACT.Exp).then_inc(S["exp_done"], 1)

            @block.tensor
            def _(pe):
                pe.wait_ge(S["masks_ready"], 1)
                pe.wait_ge(S["chosen_ready"], 1)
                for k, m in enumerate((here, behind, beyond)):
                    last = pe.matmul(PS[:, 0, :], m[:, :], chosen_b[:, k, :, :], start=(k == 0), stop=(k == 2))
                last.then_inc(S["rank_ps"], 1)
                pe.wait_ge(S["tell_ready"], 1)
                pe.matmul(PS[:, 1, 0:E4 * C], zero[:, :], zero[:, 0:E4 * C], start=True, stop=False, skip_group_check=True)

                def step(t, u):
                    pe.wait_ge(S["hit_ready"], t + 1)
                    for e in range(E4):
                        last = pe.matmul(PS[:, 1, e * C:e * C + C], hit[:, u, e, :], tell[:, bass.ds(t, 1), e, :],
                                         start=False, stop=False, skip_group_check=True)
                    last.then_inc(S["hit_used"], 1)

                in_pairs(pe, NT, step)
                pe.matmul(PS[:, 1, 0:E4 * C], zero[:, :], zero[:, 0:E4 * C], start=False, stop=True,
                          skip_group_check=True).then_inc(S["told_ps"], 1)

            @block.vector
            def _(dve):
                link = Chain(dve, S["own"], 90)

                def over_e(a):
                    return a.rearrange("p (n e) -> p n e", e=1).broadcast_to([P, NT, E4])

                dve.wait_ge(S["made"], 10)
                link(dve.tensor_single_scalar(out=row_i[:, 1:2], in_=row_i[:, 0:1], scalar=4, op=ALU.arith_shift_right))
                link(dve.tensor_single_scalar(out=row_i[:, 2:3], in_=row_i[:, 0:1], scalar=B - 1, op=ALU.bitwise_and))
                link(dve.tensor_copy(row_f[:, :], row_i[:, :]))
                cl, cs = (c[:, :, :].rearrange("p l s -> p (l s)") for c in (col_l, col_s))
                link(dve.tensor_scalar(out=later_s[:, :], in0=cs, scalar1=row_f[:, 2:3], scalar2=None, op0=ALU.is_gt))
                link(dve.tensor_scalar(out=same_s[:, :], in0=cs, scalar1=row_f[:, 2:3], scalar2=None, op0=ALU.is_equal))
                link(dve.tensor_scalar(out=later_l[:, :], in0=cl, scalar1=row_f[:, 1:2], scalar2=None, op0=ALU.is_gt))
                link(dve.tensor_copy(beyond[:, :], later_s[:, :]))
                link(dve.tensor_tensor(out=behind[:, :], in0=later_s[:, :], in1=same_s[:, :], op=ALU.add))
                link(dve.tensor_tensor(out=later_l[:, :], in0=later_l[:, :], in1=same_s[:, :], op=ALU.mult))
                link(dve.tensor_tensor(out=here[:, :], in0=later_s[:, :], in1=later_l[:, :], op=ALU.add))
                dve.sem_inc(S["masks_ready"], 1)
                link(dve.tensor_reduce(out=top[:, :], in_=logits[:, :, :], axis=AX.X, op=ALU.max))
                link(dve.tensor_tensor(out=prob[:, :, :], in0=logits[:, :, :], in1=over_e(top[:, :]), op=ALU.subtract))
                dve.sem_inc(S["shifted"], 1)
                dve.wait_ge(S["exp_done"], 1)
                link(dve.tensor_reduce(out=top[:, :], in_=prob[:, :, :], axis=AX.X, op=ALU.add))
                link(dve.reciprocal(out=top[:, :], in_=top[:, :]))
                link(dve.tensor_tensor(out=prob[:, :, :], in0=prob[:, :, :], in1=over_e(top[:, :]), op=ALU.mult))
                for t in range(NT):
                    last = dve.max(out=best[:, t, :], in_=prob[:, t, :])
                link(last)
                for t in range(NT):
                    last = dve.max_index(out=index[:, t, :], in_max=best[:, t, :], in_values=prob[:, t, :])
                link(last)
                link(dve.tensor_copy(index_f[:, :, :], index[:, :, :]))
                c_view = chosen[:, :, :].rearrange("p e n -> p n e")
                link(dve.tensor_tensor(out=c_view, in0=iota_e[:, :, :], in1=over_e(index_f[:, :, 0]), op=ALU.is_equal))
                for k in range(1, TOP):
                    link(dve.tensor_tensor(out=work[:, :, :], in0=iota_e[:, :, :], in1=over_e(index_f[:, :, k]), op=ALU.is_equal))
                    link(dve.tensor_tensor(out=c_view, in0=c_view, in1=work[:, :, :], op=ALU.add))
                link(dve.tensor_reduce(out=top[:, :], in_=best[:, :, 0:TOP], axis=AX.X, op=ALU.add))
                link(dve.tensor_scalar(out=top[:, :], in0=top[:, :], scalar1=1e-20, scalar2=None, op0=ALU.add))
                link(dve.reciprocal(out=top[:, :], in_=top[:, :]))
                link(dve.tensor_tensor(out=wts[:, :, :], in0=prob[:, :, :], in1=over_e(top[:, :]), op=ALU.mult))
                flat = lambda a: a[:, :, :].rearrange("p e n -> p (e n)")
                link(dve.tensor_copy(chosen_b[:, 0, :, :], chosen[:, :, :]))
                link(dve.tensor_tensor_scan(out=flat(upto), data0=flat(reset), data1=flat(chosen), initial=0.0,
                                            op0=ALU.mult, op1=ALU.add))
                link(dve.tensor_tensor(out=chosen_b[:, 1, :, :], in0=upto[:, :, :], in1=chosen[:, :, :], op=ALU.subtract))
                total = upto[:, :, NT - 1:NT].broadcast_to([P, E4, NT])
                link(dve.tensor_tensor(out=chosen_b[:, 2, :, :], in0=total, in1=upto[:, :, :], op=ALU.subtract))
                dve.sem_inc(S["chosen_ready"], 1)
                dve.wait_ge(S["rank_ps"], 1)
                link(dve.tensor_scalar(out=rank[:, :, :], in0=PS[:, 0, :].rearrange("p (e n) -> p e n", e=E4),
                                       scalar1=float(CAP), scalar2=1.0, op0=ALU.min, op1=ALU.add))
                link(dve.tensor_tensor(out=rank[:, :, :], in0=rank[:, :, :], in1=chosen[:, :, :], op=ALU.mult))
                link(dve.tensor_scalar(out=rank_b[:, :, :], in0=rank[:, :, :].rearrange("p e n -> p n e"), scalar1=1.0,
                                       scalar2=None, op0=ALU.subtract))
                link(dve.tensor_copy(tell[:, :, :, 0], tile_no[:, :, :]))
                link(dve.tensor_copy(tell[:, :, :, 1], part_no[:, :, :]))
                link(dve.memset(tell[:, :, :, 2], 1.0))
                link(dve.tensor_copy(tell[:, :, :, 3], wts[:, :, :]))
                link(dve.tensor_tensor(out=rest[:, :, :], in0=wts[:, :, :], in1=tell[:, :, :, 3], op=ALU.subtract))
                link(dve.tensor_copy(tell[:, :, :, 4], rest[:, :, :]))
                link(dve.tensor_tensor(out=tell[:, :, :, 5], in0=rest[:, :, :], in1=tell[:, :, :, 4], op=ALU.subtract))
                dve.sem_inc(S["tell_ready"], 1)
                dve.sem_inc(S["hit_used"], 2)

                def step(t, u):
                    dve.wait_ge(S["hit_used"], t + 1)
                    dve.tensor_tensor(out=hit[:, u, :, :], in0=iota_p[:, :].rearrange("p (e c) -> p e c", e=1).broadcast_to([P, E4, P]),
                                      in1=rank_b[:, bass.ds(t, 1), :].rearrange("p n e -> p (n e)").rearrange("p (e c) -> p e c", c=1).broadcast_to([P, E4, P]),
                                      op=ALU.is_equal).then_inc(S["hit_ready"], 1)

                in_pairs(dve, NT, step)
                dve.wait_ge(S["told_ps"], 1)
                link(dve.tensor_copy(told[:, :, :], PS[:, 1, 0:E4 * C].rearrange("p (e c) -> p e c", e=E4)))
                link(dve.tensor_scalar(out=spare[:, 0, :], in0=told[:, :, 0], scalar1=float(P), scalar2=None, op0=ALU.mult))
                link(dve.tensor_tensor(out=spare[:, 0, :], in0=spare[:, 0, :], in1=told[:, :, 1], op=ALU.add))
                link(dve.tensor_scalar(out=spare[:, 1, :], in0=told[:, :, 2], scalar1=-1.0, scalar2=-1.0, op0=ALU.add, op1=ALU.mult))
                link(dve.tensor_scalar(out=spare[:, 2, :], in0=part_no[:, 0, :], scalar1=float(N), scalar2=None, op0=ALU.add))
                link(dve.tensor_tensor(out=spare[:, 1, :], in0=spare[:, 1, :], in1=spare[:, 2, :], op=ALU.mult))
                link(dve.tensor_tensor(out=place[:, :], in0=spare[:, 0, :], in1=spare[:, 1, :], op=ALU.add))
                link(dve.tensor_tensor(out=spare[:, 3, :], in0=told[:, :, 4], in1=told[:, :, 5], op=ALU.add))
                link(dve.tensor_tensor(out=weight[:, :], in0=told[:, :, 3], in1=spare[:, 3, :], op=ALU.add))


def run_experts(core, place, weight):
    nc, PS = core.nc, core.PS
    size = blocks(INTER)
    with core.stage("rx") as (sb, sem):
        xg = sb("xg", [P, 2, D])
        xT = sb("xT", [P, 2, DH, P])
        Wgu = sb("Wgu", [P, 2, DH, 2 * INTER])
        Wd = sb("Wd", [P, 2, 2, D])
        sg = sb("sg", [P, 2, INTER])
        mid = sb("mid", [P, 2, INTER])
        mT = sb("mT", [P, 2, 2, P])
        y = sb("y", [P, 2, D])
        S = {n: sem(n) for n in "w_used g_used xt_ps xt_ready gu_ps silu mid_ready mt_ps mt_ready y_ps y_ready y_free own added copied".split()}
        w_in = [sem(f"w_in{k}") for k in range(2)]
        x_in = [sem(f"x_in{k}") for k in range(2)]
        with nc.Block() as block:
            @block.sync
            def _(sp):
                with sp.Fori(0, E4 // 2) as i:
                    for u in range(2):
                        e = 2 * i + u
                        sp.wait_ge(S["w_used"], e + 1)
                        for k, name in enumerate(("w_gate", "w_up")):
                            sp.dma_start(Wgu[:, u, :, k * INTER:(k + 1) * INTER],
                                         core.dram[name][bass.ds(e, 1), :, :].rearrange("n (h p) i -> p (n h) i", p=P)).then_inc(w_in[u], 16)
                        down = core.dram["w_down"]
                        sp.dma_start(Wd[:, u, 0, :], down[bass.ds(e, 1), 0:P, :].rearrange("n p d -> (n p) d")).then_inc(w_in[u], 16)
                        sp.dma_start(Wd[0:size[1], u, 1, :], down[bass.ds(e, 1), P:INTER, :].rearrange("n p d -> (n p) d")).then_inc(w_in[u], 16)
                sp.wait_ge(S["added"], 16 * E4)
                out = core.dram["out"].rearrange("(s g l) d -> l g s d", s=B, l=TL)
                rows = core.rows_y[0:N, :].rearrange("(g l s) d -> l g s d", l=TL, s=B)
                for tl in range(TL):
                    sp.dma_start(out[tl], rows[tl]).then_inc(S["copied"], 16)
                sp.wait_ge(S["copied"], 16 * TL)

            @block.gpsimd
            def _(pool):
                def gather(e):
                    pool.wait_ge(S["g_used"], e + 1)
                    pool.indirect_dma_start(out=xg[:, e % 2, :], out_offset=None, in_=core.rows_x[:, :],
                                            in_offset=bass.IndirectOffsetOnAxis(ap=place[:, e:e + 1], axis=0)).then_inc(x_in[e % 2], 16)

                gather(0)
                gather(1)
                for e in range(E4):
                    if e + 2 < E4:
                        gather(e + 2)
                    pool.wait_ge(S["y_ready"], e + 1)
                    if e:
                        pool.wait_ge(S["added"], 16 * e)
                        pool.sem_inc(S["y_free"], 1)
                    pool.indirect_dma_start(out=core.rows_y[:, :], out_offset=bass.IndirectOffsetOnAxis(ap=place[:, e:e + 1], axis=0),
                                            in_=y[:, e % 2, :], in_offset=None, compute_op=ALU.add).then_inc(S["added"], 16)

            @block.tensor
            def _(pe):
                def front(e, u, i):
                    pe.wait_ge(x_in[u], 16 * i + 16)
                    for h in range(DH):
                        last = pe.transpose(PS[:, 0, h * P:h * P + P], xg[:, u, h * P:h * P + P], core.ident[:, :])
                    last.then_inc(S["xt_ps"], 1)
                    pe.wait_ge(S["xt_ready"], e + 1)
                    pe.wait_ge(w_in[u], 64 * i + 64)
                    for h in range(DH):
                        last = pe.matmul(PS[:, 1 + u, 0:2 * INTER], xT[:, u, h, :], Wgu[:, u, h, :], start=(h == 0), stop=(h == DH - 1))
                    last.then_inc(S["gu_ps"], 1)
                    pe.wait_ge(S["mid_ready"], e + 1)
                    for k in range(2):
                        last = pe.transpose(PS[0:size[k], 3, k * P:k * P + P], mid[:, u, k * P:k * P + size[k]], core.ident[:, :])
                    last.then_inc(S["mt_ps"], 1)
                    pe.wait_ge(S["mt_ready"], e + 1)
                    for k in range(2):
                        last = pe.matmul(PS[:, 4 + u, 0:D], mT[0:size[k], u, k, :], Wd[0:size[k], u, k, :], start=(k == 0), stop=(k == 1))
                    last.then_inc(S["y_ps"], 1)

                with pe.Fori(0, E4 // 2) as i:
                    for u in range(2):
                        front(2 * i + u, u, i)

            @block.scalar
            def _(act):
                act.sem_inc(S["w_used"], 2)
                act.sem_inc(S["g_used"], 2)
                act.sem_inc(S["y_free"], 2)
                link = Chain(act, S["own"], 1)

                def step(e, u):
                    act.wait_ge(S["xt_ps"], e + 1)
                    act.sem_inc(S["g_used"], 1)
                    act.activation(xT[:, u, :, :], PS[:, 0, 0:D].rearrange("p (h t) -> p h t", h=DH),
                                   ACT.Copy).then_inc(S["xt_ready"], 1)
                    act.wait_ge(S["gu_ps"], e + 1)
                    act.activation(sg[:, u, :], PS[:, 1 + u, 0:INTER], ACT.Silu).then_inc(S["silu"], 1)
                    act.wait_ge(S["mt_ps"], e + 1)
                    act.activation(mT[:, u, 0, :], PS[:, 3, 0:P], ACT.Copy)
                    act.activation(mT[0:size[1], u, 1, :], PS[0:size[1], 3, P:2 * P], ACT.Copy).then_inc(S["mt_ready"], 1)
                    act.wait_ge(S["y_ps"], e + 1)
                    act.sem_inc(S["w_used"], 1)
                    act.wait_ge(S["y_free"], e + 1)
                    act.activation(y[:, u, :], PS[:, 4 + u, 0:D], ACT.Copy, scale=weight[:, bass.ds(e, 1)]).then_inc(S["y_ready"], 1)

                in_pairs(act, E4, step)

            @block.vector
            def _(dve):
                def step(e, u):
                    dve.wait_ge(S["silu"], e + 1)
                    dve.tensor_tensor(out=mid[:, u, :], in0=sg[:, u, :], in1=PS[:, 1 + u, INTER:2 * INTER],
                                      op=ALU.mult).then_inc(S["mid_ready"], 1)

                in_pairs(dve, E4, step)


STAGES = [rwkv, ternary, latent_attention, quantised_ffn, double_attention, masked_experts, crossed_attention, routed_experts]


def program(nc, dram):
    with ExitStack() as stack:
        core = Core(nc, dram, stack)
        load_x(core)
        constants(core)
        for stage in STAGES:
            stage(core)


def load_x(core):
    with core.stage("load") as (sb, sem):
        loaded = sem("loaded")
        with core.nc.Block() as block:
            @block.sync
            def _(sp):
                x = core.dram["x"].rearrange("(n p) d -> p n d", p=P)
                for k in range(8):
                    sp.dma_start(core.X[:, 4 * k:4 * k + 4, :], x[:, 4 * k:4 * k + 4, :]).then_inc(loaded, 16)
                sp.wait_ge(loaded, 8 * 16)


def halves(v):
    return np.ascontiguousarray(np.asarray(v).reshape(DH, P).T)


def rows(v):
    v = np.asarray(v).reshape(1, -1)
    return np.ascontiguousarray(np.broadcast_to(v, (P, v.shape[1])))


def layouts(a):
    t = lambda n: np.ascontiguousarray(np.asarray(a[n]).T)
    d = {
        "x": np.asarray(a["L0_attn_x"]).reshape(N, D),
        "WkT": t("L0_attn_Wk"), "WvT": t("L0_attn_Wv"), "WrT": t("L0_attn_Wr"), "WoT": t("L0_attn_Wo"),
        "tm": np.stack([halves(a[f"L0_attn_tm_{c}"]) for c in "kvr"], 1),
        "time_decay": halves(a["L0_attn_time_decay"]), "time_first": halves(a["L0_attn_time_first"]),
        "ln_g": rows(a["L0_attn_ln_g"]), "ln_b": rows(a["L0_attn_ln_b"]),
    }
    half = lambda w: np.concatenate([w[..., 0::2], w[..., 1::2]], -1)
    wqb = np.asarray(a["L1_attn_Wqb"]).reshape(QL, HEADS, NOPE + ROPE)
    wkvb = np.asarray(a["L1_attn_Wkvb"]).reshape(KL, HEADS, NOPE + VDIM)
    wkva = np.asarray(a["L1_attn_Wkva"])
    angle = (np.arange(T, dtype=np.float32)[:, None]
             * (1.0 / 10000.0 ** (np.arange(0, ROPE, 2, dtype=np.float32) / ROPE)).astype(np.float32)[None, :])
    cos, sin = np.cos(angle).astype(np.float32), np.sin(angle).astype(np.float32)
    d.update({
        "WtT": t("L0_ffn_weight"), "t_bias": rows(a["L0_ffn_bias"]),
        "Wqb_nopeT": wqb[:, :, :NOPE].transpose(2, 1, 0), "Wqb_rope": half(wqb[:, :, NOPE:]),
        "Wkvb_kT": wkvb[:, :, :NOPE].transpose(2, 1, 0), "Wkvb_vT": wkvb[:, :, NOPE:].transpose(2, 1, 0),
        "Wo_heads": np.asarray(a["L1_attn_Wo"]).reshape(HEADS, VDIM, D).transpose(1, 0, 2),
        "q_ln_w": np.asarray(a["L1_attn_q_ln_w"]).reshape(QL, 1), "kv_ln_w": rows(a["L1_attn_kv_ln_w"]),
        "Wa": np.concatenate([np.asarray(a["L1_attn_Wqa"]), wkva[:, :KL], half(wkva[:, KL:])], 1),
        "cos": np.concatenate([cos, cos], 1), "sin": np.concatenate([-sin, sin], 1),
        "wq_gateT": t("L1_ffn_wq_gate"), "wq_upT": t("L1_ffn_wq_up"), "wq_downT": t("L1_ffn_wq_down"),
        "s_gate": rows(a["L1_ffn_s_gate"]), "s_up": rows(a["L1_ffn_s_up"]), "s_down": rows(a["L1_ffn_s_down"]),
    })
    d.update({
        "W2T": t("L2_attn_W"), "W2": np.asarray(a["L2_attn_W"]),
        "g2": np.concatenate([rows(np.tile(np.asarray(a[f"L2_attn_g{n}"]), HEADS)) for n in (1, 2, 3)], 1),
    })
    d.update({
        "router": t("L2_ffn_router_w"), "W3T": t("L2_ffn_weight"), "scale": rows(a["L2_ffn_scale"]),
        "masks": np.asarray(a["L2_ffn_expert_masks"]).transpose(0, 2, 1),
    })
    w = np.asarray(a["L3_attn_w_qkv"]).reshape(HEADS, 3, HD, D).transpose(3, 1, 0, 2).reshape(D, 3 * D)
    b = np.asarray(a["L3_attn_b_qkv"]).reshape(HEADS, 3, HD).transpose(1, 0, 2).reshape(-1)
    d.update({
        "w_qkvT": w, "b_qkv": rows(b), "w_denseT": t("L3_attn_w_dense"), "b_dense": rows(a["L3_attn_b_dense"]),
        "gateT": t("L3_ffn_gate_w"),
        **{n: np.asarray(a["L3_ffn_" + n]) for n in ("w_gate", "w_up", "w_down", "sw_gate", "sw_up", "sw_down")},
    })
    return d


def kernel(**inputs):
    import concourse.bacc as bacc
    from concourse.bass_utils import run_bass_kernel_spmd

    nc = bacc.Bacc("TRN2", target_bir_lowering=False, num_devices=1)
    arrays, dram = {}, {}
    for name, a in layouts(inputs).items():
        a = np.ascontiguousarray(a)
        arrays[f"in_{name}_dram"] = a
        dram[name] = nc.dram_tensor(f"in_{name}_dram", a.shape, mybir.dt.from_np(a.dtype), kind="ExternalInput").ap()
    dram["out"] = nc.dram_tensor("out_0_dram", (N, D), F32, kind="ExternalOutput").ap()
    program(nc, dram)
    r = run_bass_kernel_spmd(nc, [arrays], core_ids=[0])
    return r.results[0]["out_0_dram"].reshape(B, T, D)
```

```python
import numpy as np
import concourse.bass as bass
from concourse import mybir
from contextlib import ExitStack, contextmanager

F32 = mybir.dt.float32
BF16 = mybir.dt.bfloat16
I32 = mybir.dt.int32
U32 = mybir.dt.uint32
ALU = mybir.AluOpType
ACT = mybir.ActivationFunctionType
AX = mybir.AxisListType

P = 128
D = 256
DH = D // P
B, T = 16, 256
N = B * T
NT = N // P
TPB = T // P
LN_EPS = 1e-5


class Chain:

    def __init__(self, eng, sem, per):
        self.eng, self.sem, self.per, self.base, self.n = eng, sem, per, 0, 0

    def start(self, t, at=0):
        self.base, self.n = t * self.per + at, 0

    def __call__(self, instruction):
        self.n += 1
        instruction.then_inc(self.sem, 1)
        self.eng.wait_ge(self.sem, self.base + self.n)


def in_pairs(eng, n, step):
    with eng.Fori(0, n // 2) as i:
        step(2 * i, 0)
        step(2 * i + 1, 1)


def skewed(eng, n, front, back):
    front(0, 0)
    with eng.Fori(0, n // 2 - 1) as i:
        front(2 * i + 1, 1)
        back(2 * i, 0)
        front(2 * i + 2, 0)
        back(2 * i + 1, 1)
    front(n - 1, 1)
    back(n - 2, 0)
    back(n - 1, 1)


class Core:

    def __init__(self, nc, dram, stack):
        self.nc, self.dram = nc, dram
        self.X = stack.enter_context(nc.sbuf_tensor("X", [P, NT, D], F32))
        self.ident = stack.enter_context(nc.sbuf_tensor("ident", [P, P], F32))
        self.identb = stack.enter_context(nc.sbuf_tensor("identb", [P, P], BF16))
        self.half = stack.enter_context(nc.sbuf_tensor("minus_half", [P, 64], F32))
        self.stats = stack.enter_context(nc.sbuf_tensor("bn_stats", [P, NT, 6], F32))
        self.mean = stack.enter_context(nc.sbuf_tensor("mean", [P, NT], F32))
        self.rstd = stack.enter_context(nc.sbuf_tensor("rstd", [P, NT], F32))
        self.tmp = stack.enter_context(nc.sbuf_tensor("stat_tmp", [P, 3, NT], F32))
        self.slots_x = nc.dram_tensor("slots_x", (SLOTS * P, D), F32, kind="Internal").ap()
        self.slots_y = nc.dram_tensor("slots_y", (SLOTS * P, D), F32, kind="Internal").ap()
        self.scratch_x = nc.dram_tensor("scratch_x", (N, D), F32, kind="Internal").ap()
        self.scratch_t = nc.dram_tensor("scratch_t", (N, 2), F32, kind="Internal").ap()
        self.rows_x = nc.dram_tensor("rows_x", (N + P, D), F32, kind="Internal").ap()
        self.rows_y = nc.dram_tensor("rows_y", (N + P, D), F32, kind="Internal").ap()
        self.PS = stack.enter_context(nc.psum_tensor("banks", [P, 8, 512], F32))

    @contextmanager
    def stage(self, name):
        nc, sems = self.nc, []
        with ExitStack() as stack:
            def sb(tag, shape, dt=F32):
                return stack.enter_context(nc.sbuf_tensor(f"{name}_{tag}", shape, dt))

            def sem(tag):
                sems.append(stack.enter_context(nc.semaphore(f"{name}_{tag}")))
                return sems[-1]

            yield sb, sem
            with nc.Block() as block:
                @block.gpsimd
                def _(pool):
                    for s in sems:
                        pool.sem_clear(s)


def constants(core):
    nc = core.nc
    with core.stage("const") as (sb, sem):
        zeroed = sem("zeroed")
        with nc.Block() as block:
            @block.gpsimd
            def _(pool):
                pool.memset(core.ident[:, :], 0.0).then_inc(zeroed, 1)
                pool.memset(core.identb[:, :], 0.0).then_inc(zeroed, 1)
                pool.memset(core.half[:, :], -0.5)
                pool.wait_ge(zeroed, 2)
                for m in (core.ident, core.identb):
                    pool.affine_select(out=m[:, :], in_=m[:, :], compare_op=ALU.not_equal, fill=1.0, base=0,
                                       pattern=[[-1, P]], channel_multiplier=1)


def statistics(core, tag, source, eps):
    nc = core.nc
    m, t0, t1, t2 = core.mean, core.tmp[:, 0, :], core.tmp[:, 1, :], core.tmp[:, 2, :]
    with core.stage("st" + tag) as (sb, sem):
        stats_done, own, var_ready, rstd_done = sem("stats"), sem("own"), sem("var"), sem("rstd")
        with nc.Block() as block:
            @block.vector
            def _(dve):
                link = Chain(dve, own, 8)
                with dve.Fori(0, NT // 4) as i:
                    for k in range(4):
                        dve.bn_stats(out=core.stats[:, bass.ds(4 * i + k, 1), :],
                                     in_=source[:, bass.ds(4 * i + k, 1), :]).then_inc(stats_done, 1)
                dve.wait_ge(stats_done, NT)
                me, ve, mo, vo = (core.stats[:, :, k] for k in (1, 2, 4, 5))
                link(dve.tensor_tensor(out=t0, in0=me, in1=mo, op=ALU.add))
                link(dve.tensor_scalar(out=m[:, :], in0=t0, scalar1=0.5, scalar2=None, op0=ALU.mult))
                link(dve.tensor_tensor(out=t0, in0=me, in1=mo, op=ALU.subtract))
                link(dve.tensor_tensor(out=t1, in0=t0, in1=t0, op=ALU.mult))
                link(dve.tensor_tensor(out=t2, in0=ve, in1=vo, op=ALU.add))
                link(dve.scalar_tensor_tensor(out=t1, in0=t1, scalar=D / 4.0, in1=t2, op0=ALU.mult, op1=ALU.add))
                dve.tensor_scalar(out=t0, in0=t1, scalar1=1.0 / D, scalar2=eps,
                                  op0=ALU.mult, op1=ALU.add).then_inc(var_ready, 1)

            @block.gpsimd
            def _(pool):
                pool.wait_ge(var_ready, 1)
                pool.tensor_tensor(out=core.rstd[:, :], in0=t0, in1=core.half[:, 0:NT],
                                   op=ALU.pow).then_inc(rstd_done, 1)


def rwkv(core):
    nc, X, PS = core.nc, core.X, core.PS
    with ExitStack() as keep:
        gate = keep.enter_context(nc.sbuf_tensor("rw_gate", [P, NT, D], F32))
        wkv = keep.enter_context(nc.sbuf_tensor("rw_wkv", [P, NT, D], F32))
        statistics(core, "0a", X, LN_EPS)
        rwkv_recurrence(core, gate, wkv)
        statistics(core, "0b", wkv, LN_EPS)
        rwkv_output(core, gate, wkv)


def rwkv_recurrence(core, gate, wkv):
    nc, X, PS = core.nc, core.X, core.PS
    START = -1e38
    with core.stage("rw") as (sb, sem):
        W = sb("W", [P, 3, DH, D])
        WA = sb("WA", [P, 3, DH, D])
        WB = sb("WB", [P, 3, DH, D])
        tm = sb("tm", [P, 3, DH])
        decay = sb("decay", [P, DH])
        first = sb("first", [P, DH])
        negdecay = sb("negdecay", [P, DH, T])
        xn = sb("xn", [P, 2, TPB, D])
        xnT = sb("xnT", [P, 2, DH, T + 1])
        pp = sb("pp", [P, 2, DH, T + 1])
        q = sb("q", [P, 2, DH, T])
        ex = sb("ex", [P, 2, 4, DH, T])
        f2v = sb("f2v", [P, DH, T])
        e2v = sb("e2v", [P, 2, DH, T])
        ab = sb("ab", [P, 2, 2, DH, T + 1])
        nd = sb("nd", [P, 2, 2, DH, T])
        rec = sb("rec", [P, DH, T])
        out = sb("out", [P, 2, DH, T])

        loaded, zeroed, edges, clamped = sem("loaded"), sem("zeroed"), sem("edges"), sem("clamped")
        exp_ready, weights_ready, xn_ready, xn_free = sem("expd"), sem("weights"), sem("xn_ready"), sem("xn_free")
        xt_ps, xt_ready, kvr_ready, r_free, kv_free = sem("xt_ps"), sem("xt_ready"), sem("kvr"), sem("r_free"), sem("kv_free")
        pp_ready, q_ready, args_dve, args_pool = sem("pp_ready"), sem("q_ready"), sem("args_d"), sem("args_p")
        exps_ready, scans_ready, e2v_ready, nd_ready = sem("exps"), sem("scans"), sem("e2v_ready"), sem("nd_ready")
        out_ready, out_free, w_ps, w_free = sem("out_ready"), sem("out_free"), sem("w_ps"), sem("w_free")
        own_prep, own_front, own_scans, own_finish, own_pool = (sem(f"own{k}") for k in range(5))

        with nc.Block() as block:
            @block.sync
            def _(sp):
                for n, name in enumerate(("WkT", "WvT", "WrT")):
                    sp.dma_start(W[:, n, :, :], core.dram[name].rearrange("(h p) e -> p h e", p=P)).then_inc(loaded, 16)
                sp.dma_start(tm[:, :, :], core.dram["tm"]).then_inc(loaded, 16)
                sp.dma_start(decay[:, :], core.dram["time_decay"]).then_inc(loaded, 16)
                sp.dma_start(first[:, :], core.dram["time_first"]).then_inc(loaded, 16)

            @block.tensor
            def _(pe):
                def front(b, u):
                    pe.wait_ge(xn_ready, b + 1)
                    for h in range(DH):
                        for k in range(TPB):
                            last = pe.transpose(PS[:, 0, h * T + k * P:h * T + k * P + P],
                                                xn[:, u, k, h * P:h * P + P], core.ident[:, :])
                    last.then_inc(xt_ps, 1)
                    pe.wait_ge(xt_ready, b + 1)
                    pe.wait_ge(kv_free, b + 1)
                    pe.wait_ge(r_free, b + 1)
                    for n in range(2):
                        for e in range(DH):
                            for j in range(4):
                                w, h = (WA, WB)[j % 2], j // 2
                                pe.matmul(PS[:, 2 + 2 * n + u, e * T:e * T + T], w[:, n, h, e * P:e * P + P],
                                          xnT[:, u, h, 1 - j % 2:1 - j % 2 + T], start=(j == 0), stop=(j == 3))
                    for k in range(TPB):
                        for j in range(4):
                            w, h = (WA, WB)[j % 2], j // 2
                            at = 1 - j % 2 + k * P
                            last = pe.matmul(PS[:, 6 + u, k * D:k * D + D], xnT[:, u, h, at:at + P], w[:, 2, h, :],
                                             start=(j == 0), stop=(j == 3))
                    last.then_inc(kvr_ready, 1)

                def back(b, u):
                    pe.wait_ge(out_ready, b + 1)
                    pe.wait_ge(w_free, b + 1)
                    for k in range(TPB):
                        for h in range(DH):
                            last = pe.transpose(PS[:, 1, k * D + h * P:k * D + h * P + P],
                                                out[:, u, h, k * P:k * P + P], core.ident[:, :])
                    last.then_inc(w_ps, 1)

                pe.wait_ge(weights_ready, 1)
                skewed(pe, B, front, back)

            @block.scalar
            def _(act):
                act.wait_ge(zeroed, 1)
                act.wait_ge(clamped, 1)
                act.activation(decay[:, :], decay[:, :], ACT.Exp).then_inc(exp_ready, 1)
                act.sem_inc(r_free, 2)
                act.sem_inc(w_free, 1)

                def front(b, u):
                    act.wait_ge(xt_ps, b + 1)
                    act.sem_inc(xn_free, 1)
                    act.activation(xnT[:, u, :, 1:T + 1], PS[:, 0, :].rearrange("p (h t) -> p h t", h=DH),
                                   ACT.Copy).then_inc(xt_ready, 1)
                    act.wait_ge(kvr_ready, b + 1)
                    act.activation(gate[:, bass.ds(TPB * b, TPB), :], PS[:, 6 + u, :].rearrange("p (k d) -> p k d", k=TPB),
                                   ACT.Tanh, scale=0.5).then_inc(r_free, 1)
                    act.wait_ge(args_dve, b + 1)
                    act.wait_ge(args_pool, b + 1)
                    act.activation(ex[:, u, :, :, :], ex[:, u, :, :, :], ACT.Exp).then_inc(exps_ready, 1)

                def back(b, u):
                    act.wait_ge(w_ps, b + 1)
                    act.sem_inc(out_free, 1)
                    act.activation(wkv[:, bass.ds(TPB * b, TPB), :], PS[:, 1, :].rearrange("p (k d) -> p k d", k=TPB),
                                   ACT.Copy).then_inc(w_free, 1)

                skewed(act, B, front, back)

            @block.gpsimd
            def _(pool):
                pool.memset(xnT[:, :, :, 0:1], 0.0).then_inc(zeroed, 1)
                pool.memset(pp[:, :, :, 0:1], START).then_inc(edges, 1)
                pool.memset(ab[:, :, :, :, 0:1], 0.0).then_inc(edges, 1)
                pool.wait_ge(edges, 2)
                link = Chain(pool, own_pool, 4)

                def step(b, u):
                    pool.wait_ge(pp_ready, b + 1)
                    pool.tensor_tensor(out=ex[:, u, 0, :, :], in0=pp[:, u, :, 0:T], in1=pp[:, u, :, 1:T + 1],
                                       op=ALU.subtract)
                    pool.wait_ge(q_ready, b + 1)
                    pool.tensor_tensor(out=ex[:, u, 2, :, :], in0=pp[:, u, :, 0:T], in1=q[:, u, :, :],
                                       op=ALU.subtract).then_inc(args_pool, 1)
                    pool.wait_ge(scans_ready, b + 1)
                    link.start(b)
                    for k in range(2):
                        link(pool.tensor_tensor(out=nd[:, u, k, :, :], in0=ab[:, u, k, :, 0:T], in1=ex[:, u, 2, :, :],
                                                op=ALU.mult))
                    pool.wait_ge(e2v_ready, b + 1)
                    link(pool.tensor_tensor(out=nd[:, u, 0, :, :], in0=nd[:, u, 0, :, :], in1=e2v[:, u, :, :],
                                            op=ALU.add))
                    link(pool.tensor_tensor(out=nd[:, u, 1, :, :], in0=nd[:, u, 1, :, :], in1=ex[:, u, 3, :, :],
                                            op=ALU.add))
                    pool.sem_inc(nd_ready, 1)

                in_pairs(pool, B, step)

            @block.vector
            def _(dve):
                dve.sem_inc(kv_free, 2)
                dve.sem_inc(xn_free, 2)
                dve.sem_inc(out_free, 2)
                dve.wait_ge(loaded, 6 * 16)
                link = Chain(dve, own_prep, 9)
                dve.tensor_scalar(out=decay[:, :], in0=decay[:, :], scalar1=87.0, scalar2=None,
                                  op0=ALU.min).then_inc(clamped, 1)
                link(dve.memset(negdecay[:, :, :], 0.0))
                for n in range(3):
                    for h in range(DH):
                        link(dve.tensor_scalar(out=WA[:, n, h, :], in0=W[:, n, h, :], scalar1=tm[:, n, h:h + 1],
                                               scalar2=None, op0=ALU.mult))
                dve.tensor_tensor(out=WB[:, :, :, :], in0=W[:, :, :, :], in1=WA[:, :, :, :],
                                  op=ALU.subtract).then_inc(weights_ready, 1)
                dve.wait_ge(exp_ready, 1)
                for h in range(DH):
                    link(dve.tensor_scalar(out=negdecay[:, h, :], in0=negdecay[:, h, :], scalar1=decay[:, h:h + 1],
                                           scalar2=None, op0=ALU.subtract))
                dve.wait_ge(edges, 2)
                link_front, link_scans, link_finish = (Chain(dve, own_front, 4), Chain(dve, own_scans, 2),
                                                       Chain(dve, own_finish, 2))

                def normalise(b, u):
                    dve.wait_ge(xn_free, b + 1)
                    for k in range(TPB):
                        t = TPB * b + k
                        last = dve.tensor_scalar(out=xn[:, u, k, :], in0=X[:, bass.ds(t, 1), :],
                                                 scalar1=core.mean[:, bass.ds(t, 1)], scalar2=core.rstd[:, bass.ds(t, 1)],
                                                 op0=ALU.subtract, op1=ALU.mult)
                    last.then_inc(xn_ready, 1)

                def front(b, u):
                    kp = PS[:, 2 + u, :].rearrange("p (h t) -> p h t", h=DH)
                    link = link_front
                    link.start(b)
                    dve.wait_ge(kvr_ready, b + 1)
                    for h in range(DH):
                        link(dve.tensor_tensor_scan(out=pp[:, u, h, 1:T + 1], data0=negdecay[:, h, :],
                                                    data1=kp[:, h, :], initial=START, op0=ALU.add, op1=ALU.max))
                    dve.sem_inc(pp_ready, 1)
                    dve.tensor_tensor(out=ex[:, u, 1, :, :], in0=kp, in1=pp[:, u, :, 1:T + 1], op=ALU.subtract)
                    for h in range(DH):
                        link(dve.scalar_tensor_tensor(out=q[:, u, h, :], in0=kp[:, h, :], scalar=first[:, h:h + 1],
                                                      in1=pp[:, u, h, 0:T], op0=ALU.add, op1=ALU.max))
                    dve.sem_inc(q_ready, 1)
                    for h in range(DH):
                        last = dve.scalar_tensor_tensor(out=ex[:, u, 3, h, :], in0=kp[:, h, :],
                                                        scalar=first[:, h:h + 1], in1=q[:, u, h, :],
                                                        op0=ALU.add, op1=ALU.subtract)
                    last.then_inc(args_dve, 1)

                def scans(b, u):
                    vp = PS[:, 4 + u, :].rearrange("p (h t) -> p h t", h=DH)
                    link = link_scans
                    link.start(b)
                    dve.wait_ge(exps_ready, b + 1)
                    link(dve.tensor_tensor(out=f2v[:, :, :], in0=ex[:, u, 1, :, :], in1=vp, op=ALU.mult))
                    for h in range(DH):
                        dve.tensor_tensor_scan(out=ab[:, u, 0, h, 1:T + 1], data0=ex[:, u, 0, h, :],
                                               data1=f2v[:, h, :], initial=0.0, op0=ALU.mult, op1=ALU.add)
                        last = dve.tensor_tensor_scan(out=ab[:, u, 1, h, 1:T + 1], data0=ex[:, u, 0, h, :],
                                                      data1=ex[:, u, 1, h, :], initial=0.0, op0=ALU.mult, op1=ALU.add)
                    last.then_inc(scans_ready, 1)
                    link(dve.tensor_tensor(out=e2v[:, u, :, :], in0=ex[:, u, 3, :, :], in1=vp, op=ALU.mult))
                    dve.sem_inc(kv_free, 1)
                    dve.sem_inc(e2v_ready, 1)

                def finish(b, u):
                    link = link_finish
                    link.start(b)
                    dve.wait_ge(nd_ready, b + 1)
                    link(dve.reciprocal(out=rec[:, :, :], in_=nd[:, u, 1, :, :]))
                    dve.wait_ge(out_free, b + 1)
                    link(dve.tensor_tensor(out=out[:, u, :, :], in0=nd[:, u, 0, :, :], in1=rec[:, :, :], op=ALU.mult))
                    dve.sem_inc(out_ready, 1)

                normalise(0, 0)
                normalise(1, 1)
                front(0, 0)
                scans(0, 0)
                with dve.Fori(0, B // 2 - 1) as i:
                    for k in (1, 2):
                        b, u = 2 * i + k, k % 2
                        normalise(b + 1, 1 - u)
                        front(b, u)
                        finish(b - 1, 1 - u)
                        scans(b, u)
                front(B - 1, 1)
                finish(B - 2, 0)
                scans(B - 1, 1)
                finish(B - 1, 1)


def rwkv_output(core, gate, wkv):
    nc, X, PS = core.nc, core.X, core.PS
    with core.stage("ro") as (sb, sem):
        WoT = sb("WoT", [P, DH, D])
        g = sb("g", [P, D])
        c = sb("c", [P, D])
        n = sb("n", [P, 2, D])
        ng = sb("ng", [P, 2, D])
        rn = sb("rn", [P, 2, D])
        rT = sb("rT", [P, 2, DH, P])
        loaded, w_ready, n_ready, ng_ready, rn_ready = (sem(x) for x in ("loaded", "w_ready", "n_ready", "ng_ready", "rn_ready"))
        rt_ps, rt_ready, y_ps, added, own = (sem(x) for x in ("rt_ps", "rt_ready", "y_ps", "added", "own"))
        with nc.Block() as block:
            @block.sync
            def _(sp):
                sp.dma_start(WoT[:, :, :], core.dram["WoT"].rearrange("(h p) e -> p h e", p=P)).then_inc(loaded, 16)
                sp.dma_start(g[:, :], core.dram["ln_g"]).then_inc(loaded, 16)
                sp.dma_start(c[:, :], core.dram["ln_b"]).then_inc(loaded, 16)

            @block.vector
            def _(dve):
                dve.sem_inc(added, 2)
                dve.wait_ge(loaded, 3 * 16)
                dve.tensor_scalar(out=WoT[:, :, :], in0=WoT[:, :, :], scalar1=0.5, scalar2=None,
                                  op0=ALU.mult).then_inc(w_ready, 1)

                def normalise(t, u):
                    dve.tensor_scalar(out=n[:, u, :], in0=wkv[:, bass.ds(t, 1), :], scalar1=core.mean[:, bass.ds(t, 1)],
                                      scalar2=core.rstd[:, bass.ds(t, 1)], op0=ALU.subtract,
                                      op1=ALU.mult).then_inc(n_ready, 1)

                def gated(t, u):
                    dve.wait_ge(ng_ready, t + 1)
                    dve.scalar_tensor_tensor(out=rn[:, u, :], in0=gate[:, bass.ds(t, 1), :], scalar=1.0, in1=ng[:, u, :],
                                             op0=ALU.add, op1=ALU.mult).then_inc(rn_ready, 1)

                def add(t, u):
                    dve.wait_ge(y_ps, t + 1)
                    dve.tensor_tensor(out=X[:, bass.ds(t, 1), :], in0=X[:, bass.ds(t, 1), :], in1=PS[:, 2 + u, 0:D],
                                      op=ALU.add).then_inc(added, 1)

                normalise(0, 0)
                normalise(1, 1)
                gated(0, 0)
                gated(1, 1)
                with dve.Fori(0, NT // 2 - 1) as i:
                    for k in range(2):
                        t = 2 * i + k
                        normalise(t + 2, k)
                        add(t, k)
                        gated(t + 2, k)
                add(NT - 2, 0)
                add(NT - 1, 1)

            @block.gpsimd
            def _(pool):
                pool.wait_ge(loaded, 3 * 16)
                link = Chain(pool, own, 1)

                def step(t, u):
                    pool.wait_ge(n_ready, t + 1)
                    link.start(t)
                    link(pool.tensor_tensor(out=ng[:, u, :], in0=n[:, u, :], in1=g[:, :], op=ALU.mult))
                    pool.tensor_tensor(out=ng[:, u, :], in0=ng[:, u, :], in1=c[:, :], op=ALU.add).then_inc(ng_ready, 1)

                in_pairs(pool, NT, step)

            @block.scalar
            def _(act):
                def step(t, u):
                    act.wait_ge(rt_ps, t + 1)
                    act.activation(rT[:, u, :, :], PS[:, u, 0:D].rearrange("p (h t) -> p h t", h=DH),
                                   ACT.Copy).then_inc(rt_ready, 1)

                in_pairs(act, NT, step)

            @block.tensor
            def _(pe):
                pe.wait_ge(w_ready, 1)

                def front(t, u):
                    pe.wait_ge(rn_ready, t + 1)
                    for h in range(DH):
                        last = pe.transpose(PS[:, u, h * P:h * P + P], rn[:, u, h * P:h * P + P], core.ident[:, :])
                    last.then_inc(rt_ps, 1)

                def back(t, u):
                    pe.wait_ge(rt_ready, t + 1)
                    pe.wait_ge(added, t + 1)
                    for h in range(DH):
                        last = pe.matmul(PS[:, 2 + u, 0:D], rT[:, u, h, :], WoT[:, h, :], start=(h == 0), stop=(h == DH - 1))
                    last.then_inc(y_ps, 1)

                skewed(pe, NT, front, back)


def ahead(eng, n, first, body):
    first(0, 0)
    with eng.Fori(0, n // 2 - 1) as i:
        body(2 * i, 0, True)
        body(2 * i + 1, 1, True)
    body(n - 2, 0, True)
    body(n - 1, 1, False)


def overlapped(eng, n, first, body, finish):
    first(0, 0)
    body(0, 0, False, True)
    with eng.Fori(0, n // 2 - 1) as i:
        body(2 * i + 1, 1, True, True)
        body(2 * i + 2, 0, True, True)
    body(n - 1, 1, True, False)
    finish(n - 1, 1)


def ternary(core):
    nc, X, PS = core.nc, core.X, core.PS
    ROUND = 1.5 * 2.0 ** 23
    statistics(core, "1", X, LN_EPS)
    with core.stage("te") as (sb, sem):
        W = sb("W", [P, DH, D])
        Wq = sb("Wq", [P, DH, D])
        ones = sb("ones", [P, P])
        part = sb("part", [P, 3])
        bias = sb("bias", [P, D])
        xn = sb("xn", [P, 2, D])
        xT = sb("xT", [P, 2, DH, P])
        loaded, ones_ready, part_ready, total_ps, w_ready = (sem(x) for x in ("loaded", "ones", "part", "total", "w_ready"))
        own, xn_ready, biased, xt_ps, xt_ready, y_ps, added = (
            sem(x) for x in ("own", "xn_ready", "biased", "xt_ps", "xt_ready", "y_ps", "added"))
        with nc.Block() as block:
            @block.sync
            def _(sp):
                sp.dma_start(W[:, :, :], core.dram["WtT"].rearrange("(h p) e -> p h e", p=P)).then_inc(loaded, 16)
                sp.dma_start(bias[:, :], core.dram["t_bias"]).then_inc(loaded, 16)

            @block.gpsimd
            def _(pool):
                pool.memset(ones[:, :], 1.0).then_inc(ones_ready, 1)
                pool.wait_ge(loaded, 2 * 16)

                def step(t, u):
                    pool.wait_ge(xn_ready, t + 1)
                    pool.tensor_tensor(out=X[:, bass.ds(t, 1), :], in0=X[:, bass.ds(t, 1), :], in1=bias[:, :],
                                       op=ALU.add).then_inc(biased, 1)

                in_pairs(pool, NT, step)

            @block.vector
            def _(dve):
                link = Chain(dve, own, 8)
                dve.sem_inc(added, 2)
                dve.wait_ge(loaded, 2 * 16)
                dve.tensor_reduce(out=part[:, 0:1], in_=W[:, :, :], axis=AX.XY, op=ALU.add,
                                  apply_absolute_value=True).then_inc(part_ready, 1)
                dve.wait_ge(total_ps, 1)
                link(dve.tensor_scalar(out=part[:, 1:2], in0=PS[:, 7, 0:1], scalar1=1.0 / (D * D), scalar2=None, op0=ALU.mult))
                link(dve.tensor_scalar(out=part[:, 0:1], in0=part[:, 1:2], scalar1=1e-10, scalar2=None, op0=ALU.add))
                link(dve.reciprocal(out=part[:, 2:3], in_=part[:, 0:1]))
                link(dve.tensor_scalar(out=Wq[:, :, :], in0=W[:, :, :], scalar1=part[:, 2:3], scalar2=ROUND,
                                       op0=ALU.mult, op1=ALU.add))
                link(dve.tensor_scalar(out=Wq[:, :, :], in0=Wq[:, :, :], scalar1=ROUND, scalar2=1.0,
                                       op0=ALU.subtract, op1=ALU.min))
                link(dve.tensor_scalar(out=Wq[:, :, :], in0=Wq[:, :, :], scalar1=-1.0, scalar2=part[:, 1:2],
                                       op0=ALU.max, op1=ALU.mult))
                link(dve.tensor_tensor(out=Wq[:, :, :], in0=Wq[:, :, :], in1=W[:, :, :], op=ALU.subtract))
                link(dve.tensor_tensor(out=Wq[:, :, :], in0=Wq[:, :, :], in1=W[:, :, :], op=ALU.add))
                dve.sem_inc(w_ready, 1)

                def normalise(t, u):
                    dve.tensor_scalar(out=xn[:, u, :], in0=X[:, bass.ds(t, 1), :], scalar1=core.mean[:, bass.ds(t, 1)],
                                      scalar2=core.rstd[:, bass.ds(t, 1)], op0=ALU.subtract,
                                      op1=ALU.mult).then_inc(xn_ready, 1)

                def add(t, u):
                    dve.wait_ge(y_ps, t + 1)
                    dve.wait_ge(biased, t + 1)
                    dve.tensor_tensor(out=X[:, bass.ds(t, 1), :], in0=X[:, bass.ds(t, 1), :], in1=PS[:, 2 + u, 0:D],
                                      op=ALU.add).then_inc(added, 1)

                normalise(0, 0)
                normalise(1, 1)
                with dve.Fori(0, NT // 2 - 1) as i:
                    for k in range(2):
                        add(2 * i + k, k)
                        normalise(2 * i + k + 2, k)
                add(NT - 2, 0)
                add(NT - 1, 1)

            @block.scalar
            def _(act):
                def step(t, u):
                    act.wait_ge(xt_ps, t + 1)
                    act.activation(xT[:, u, :, :], PS[:, u, 0:D].rearrange("p (h t) -> p h t", h=DH),
                                   ACT.Copy).then_inc(xt_ready, 1)

                in_pairs(act, NT, step)

            @block.tensor
            def _(pe):
                pe.wait_ge(ones_ready, 1)
                pe.wait_ge(part_ready, 1)
                pe.matmul(PS[:, 7, 0:1], ones[:, :], part[:, 0:1], start=True, stop=True).then_inc(total_ps, 1)
                pe.wait_ge(w_ready, 1)

                def front(t, u):
                    pe.wait_ge(xn_ready, t + 1)
                    for h in range(DH):
                        last = pe.transpose(PS[:, u, h * P:h * P + P], xn[:, u, h * P:h * P + P], core.ident[:, :])
                    last.then_inc(xt_ps, 1)

                def back(t, u):
                    pe.wait_ge(xt_ready, t + 1)
                    pe.wait_ge(added, t + 1)
                    for h in range(DH):
                        last = pe.matmul(PS[:, 2 + u, 0:D], xT[:, u, h, :], Wq[:, h, :], start=(h == 0), stop=(h == DH - 1))
                    last.then_inc(y_ps, 1)

                skewed(pe, NT, front, back)


HID = 704
ZERO_POINT = 128.0
GT = 4


def blocks(hid):
    return [min(P, hid - at) for at in range(0, hid, P)]


def gated_ffn(core, tag, hid, prepare, router=None):
    nc, X, PS = core.nc, core.X, core.PS
    NG = NT // GT
    size = blocks(hid)
    M = len(size)
    with core.stage(tag) as (sb, sem):
        Wg = sb("Wg", [P, DH, hid])
        Wu = sb("Wu", [P, DH, hid])
        Wd = sb("Wd", [P, M, D])
        xn = sb("xn", [P, 2, GT, D])
        xT = sb("xT", [P, 2, DH, GT * P])
        sg = sb("sg", [P, 2, GT * P])
        hT = sb("hT", [P, M, GT * P])
        w_ready = sem("w_ready")
        load, make = prepare(sb, sem, Wg, Wu, Wd, w_ready)
        xn_ready, xt_ps, xt_ready, gu_ps, silu_ready, h_ready, y_ps, added, lg_ps, lg_ready, n_stored, n_free = (
            sem(x) for x in ("xn_ready", "xt_ps", "xt_ready", "gu_ps", "silu", "h_ready", "y_ps", "added", "lg_ps",
                             "lg_ready", "n_stored", "n_free"))
        with nc.Block() as block:
            @block.sync
            def _(sp):
                load(sp)
                if router:
                    rows_of = router["rows"].rearrange("(n p) d -> p n d", p=P)

                    def store(g, u):
                        sp.wait_ge(xn_ready, g + 1)
                        sp.dma_start(rows_of[:, bass.ds(GT * g, GT), :], xn[:, u, :, :]).then_inc(n_stored, 16)
                        sp.wait_ge(n_stored, 16 * g + 16)
                        sp.sem_inc(n_free, 1)

                    in_pairs(sp, NG, store)

            @block.vector
            def _(dve):
                make(dve)
                dve.sem_inc(h_ready, 2)
                dve.sem_inc(added, 2)
                dve.sem_inc(n_free, 2)

                def normalise(g, u):
                    if router:
                        dve.wait_ge(n_free, g + 1)
                    for k in range(GT):
                        t = GT * g + k
                        last = dve.tensor_scalar(out=xn[:, u, k, :], in0=X[:, bass.ds(t, 1), :],
                                                 scalar1=core.mean[:, bass.ds(t, 1)], scalar2=core.rstd[:, bass.ds(t, 1)],
                                                 op0=ALU.subtract, op1=ALU.mult)
                    last.then_inc(xn_ready, 1)

                def body(g, u, more):
                    if more:
                        normalise(g + 1, 1 - u)
                    for m in range(M):
                        dve.wait_ge(silu_ready, M * g + m + 1)
                        r = slice(0, size[m])
                        dve.tensor_tensor(out=hT[r, m, :], in0=sg[r, (M * u + m) % 2, :],
                                          in1=PS[r, 4 + (M * u + m) % 2, :], op=ALU.mult).then_inc(h_ready, 1)
                    for k in range(2):
                        dve.wait_ge(y_ps, 2 * g + k + 1)
                        t = GT * g + 2 * k
                        dve.tensor_tensor(out=X[:, bass.ds(t, 2), :], in0=X[:, bass.ds(t, 2), :],
                                          in1=PS[:, 6 + k, :].rearrange("p (k d) -> p k d", k=2),
                                          op=ALU.add).then_inc(added, 1)

                ahead(dve, NG, normalise, body)

            @block.scalar
            def _(act):
                def copy(g, u):
                    for h in range(DH):
                        act.wait_ge(xt_ps, DH * g + h + 1)
                        act.activation(xT[:, u, h, :], PS[:, h, :], ACT.Copy).then_inc(xt_ready, 1)

                def body(g, u, more):
                    if router:
                        act.wait_ge(lg_ps, g + 1)
                        act.activation(router["logits"][:, bass.ds(GT * g, GT), :],
                                       PS[:, 0, 0:GT * router["E"]].rearrange("p (k e) -> p k e", k=GT),
                                       ACT.Copy).then_inc(lg_ready, 1)
                    for m in range(M):
                        act.wait_ge(gu_ps, M * g + m + 1)
                        r = slice(0, size[m])
                        act.activation(sg[r, (M * u + m) % 2, :], PS[r, 2 + (M * u + m) % 2, :],
                                       ACT.Silu).then_inc(silu_ready, 1)
                    if more:
                        copy(g + 1, 1 - u)

                ahead(act, NG, copy, body)

            @block.tensor
            def _(pe):
                def transposes(g, u):
                    pe.wait_ge(xn_ready, g + 1)
                    for h in range(DH):
                        for k in range(GT):
                            last = pe.transpose(PS[:, h, k * P:k * P + P], xn[:, u, k, h * P:h * P + P], core.ident[:, :])
                        last.then_inc(xt_ps, 1)

                def body(g, u, more):
                    pe.wait_ge(xt_ready, DH * g + DH)
                    if router:
                        E = router["E"]
                        for k in range(GT):
                            for h in range(DH):
                                last = pe.matmul(PS[:, 0, k * E:k * E + E], xT[:, u, h, k * P:k * P + P],
                                                 router["W"][:, h, :], start=(h == 0), stop=(h == DH - 1))
                        last.then_inc(lg_ps, 1)
                    for m in range(M):
                        pe.wait_ge(h_ready, M * g + m + 1)
                        for w, bank in ((Wg, 2), (Wu, 4)):
                            for h in range(DH):
                                last = pe.matmul(PS[0:size[m], bank + (M * u + m) % 2, :], w[:, h, m * P:m * P + size[m]],
                                                 xT[:, u, h, :], start=(h == 0), stop=(h == DH - 1))
                        last.then_inc(gu_ps, 1)
                    if more:
                        if router:
                            pe.wait_ge(lg_ready, g + 1)
                        transposes(g + 1, 1 - u)
                    pe.wait_ge(h_ready, M * g + M + 2)
                    for k in range(GT):
                        if k % 2 == 0:
                            pe.wait_ge(added, 2 * g + k // 2 + 1)
                        for m in range(M):
                            last = pe.matmul(PS[:, 6 + k // 2, k % 2 * D:k % 2 * D + D],
                                             hT[0:size[m], m, k * P:k * P + P], Wd[0:size[m], m, :],
                                             start=(m == 0), stop=(m == M - 1))
                        if k % 2:
                            last.then_inc(y_ps, 1)

                pe.wait_ge(w_ready, 1)
                ahead(pe, NG, transposes, body)


def quantised_ffn(core):
    statistics(core, "3", core.X, LN_EPS)
    size = blocks(HID)
    M = len(size)

    def prepare(sb, sem, Wg, Wu, Wd, w_ready):
        raw = sb("raw", [P, DH, HID], I32)
        raw_d = sb("raw_d", [P, M, D], I32)
        s_row = sb("s_row", [P, HID])
        s_down = sb("s_down", [P, D])
        load_g, load_u, load_d, own, gate_made = (sem(x) for x in ("load_g", "load_u", "load_d", "own", "gate_made"))

        def load(sp):
            full = (M - 1) * P
            sp.dma_start(raw[:, :, :], core.dram["wq_gateT"].rearrange("(h p) e -> p h e", p=P)).then_inc(load_g, 16)
            sp.dma_start(s_row[:, :], core.dram["s_gate"]).then_inc(load_g, 16)
            sp.dma_start(raw_d[:, 0:M - 1, :], core.dram["wq_downT"][0:full, :].rearrange("(m p) e -> p m e", p=P)).then_inc(load_d, 16)
            sp.dma_start(raw_d[0:size[-1], M - 1, :], core.dram["wq_downT"][full:HID, :]).then_inc(load_d, 16)
            sp.dma_start(s_down[:, :], core.dram["s_down"]).then_inc(load_d, 16)
            sp.wait_ge(gate_made, 1)
            sp.dma_start(raw[:, :, :], core.dram["wq_upT"].rearrange("(h p) e -> p h e", p=P)).then_inc(load_u, 16)
            sp.dma_start(s_row[:, :], core.dram["s_up"]).then_inc(load_u, 16)

        def make(dve):
            link = Chain(dve, own, 2)

            def dequantise(w, r, s):
                return dve.scalar_tensor_tensor(out=w, in0=r, scalar=ZERO_POINT, in1=s, op0=ALU.subtract, op1=ALU.mult)

            dve.wait_ge(load_g, 2 * 16)
            for h in range(DH):
                link(dequantise(Wg[:, h, :], raw[:, h, :], s_row[:, :]))
            dve.sem_inc(gate_made, 1)
            dve.wait_ge(load_d, 3 * 16)
            for m in range(M):
                dequantise(Wd[0:size[m], m, :], raw_d[0:size[m], m, :], s_down[0:size[m], :])
            dve.wait_ge(load_u, 2 * 16)
            for h in range(DH):
                last = dequantise(Wu[:, h, :], raw[:, h, :], s_row[:, :])
            last.then_inc(w_ready, 1)

        return load, make

    gated_ffn(core, "qf", HID, prepare)


HEADS = 16
NOPE, ROPE, VDIM = 128, 64, 128
QL, KL = 192, 64
QK = KL + ROPE
LOW = QL + KL + ROPE
RMS_EPS = float(np.finfo(np.float32).eps)


def latent_attention(core):
    with ExitStack() as keep:
        def sb(tag, shape, dt=F32):
            return keep.enter_context(core.nc.sbuf_tensor("la_" + tag, shape, dt))

        q1 = sb("q1", [P, HEADS, QK])
        q2 = sb("q2", [QL - P, HEADS, QK])
        out = sb("out", [P, HEADS // 2, D])
        latent_weights(core, q1, q2, out)
        statistics(core, "2", core.X, LN_EPS)
        latent_heads(core, q1, q2, out)


def latent_weights(core, q1, q2, out):
    nc, PS = core.nc, core.PS
    SCALE = 1.0 / float(np.sqrt(np.float32(NOPE + ROPE)))
    R2 = QL - P
    with core.stage("lw") as (sb, sem):
        wq = sb("wq", [P, HEADS, QL])
        wk = sb("wk", [P, HEADS, KL])
        wv = sb("wv", [P, HEADS, KL])
        wo = sb("wo", [P, HEADS, D])
        g1 = sb("g1", [P, 1])
        g2 = sb("g2", [R2, 1])
        loaded, loaded_o, own, prod_ps, prod_free, prod2_ps, rope_done = (
            sem(x) for x in ("loaded", "loaded_o", "own", "prod_ps", "prod_free", "prod2", "rope"))
        with nc.Block() as block:
            @block.sync
            def _(sp):
                for a, name in ((wq, "Wqb_nopeT"), (wk, "Wkvb_kT")):
                    sp.dma_start(a[:, :, :], core.dram[name]).then_inc(loaded, 16)
                sp.dma_start(q1[:, :, KL:QK], core.dram["Wqb_rope"][0:P, :, :]).then_inc(loaded, 16)
                sp.dma_start(q2[:, :, KL:QK], core.dram["Wqb_rope"][P:QL, :, :]).then_inc(loaded, 16)
                sp.dma_start(g1[:, :], core.dram["q_ln_w"][0:P, :]).then_inc(loaded, 16)
                sp.dma_start(g2[:, :], core.dram["q_ln_w"][P:QL, :]).then_inc(loaded, 16)
                for a, name in ((wv, "Wkvb_vT"), (wo, "Wo_heads")):
                    sp.dma_start(a[:, :, :], core.dram[name]).then_inc(loaded_o, 16)

            @block.tensor
            def _(pe):
                pe.wait_ge(loaded, 6 * 16)
                for h in range(HEADS):
                    at = h % 8 * KL
                    pe.matmul(PS[:, h // 8, at:at + KL], wq[:, h, 0:P], wk[:, h, :], start=True, stop=True)
                    last = pe.matmul(PS[0:R2, 2 + h // 8, at:at + KL], wq[:, h, P:QL], wk[:, h, :], start=True, stop=True)
                last.then_inc(prod_ps, 1)
                pe.wait_ge(loaded_o, 2 * 16)
                for j in range(HEADS // 2):
                    if j == 4:
                        pe.wait_ge(prod_free, 1)
                    for k in range(2):
                        last = pe.matmul(PS[k * KL:k * KL + KL, (4 + j) % 8, 0:D], wv[:, 2 * j + k, :],
                                         wo[:, 2 * j + k, :], start=True, stop=True)
                    last.then_inc(prod2_ps, 1)

            @block.vector
            def _(dve):
                link = Chain(dve, own, 4)
                dve.wait_ge(loaded, 6 * 16)
                link(dve.tensor_scalar(out=g1[:, :], in0=g1[:, :], scalar1=SCALE, scalar2=None, op0=ALU.mult))
                link(dve.tensor_scalar(out=g2[:, :], in0=g2[:, :], scalar1=SCALE, scalar2=None, op0=ALU.mult))
                for w, g in ((q1, g1), (q2, g2)):
                    dve.tensor_scalar(out=w[:, :, KL:QK], in0=w[:, :, KL:QK], scalar1=g[:, 0:1], scalar2=None, op0=ALU.mult)
                dve.wait_ge(prod_ps, 1)
                for k in range(2):
                    dve.tensor_scalar(out=q1[:, 8 * k:8 * k + 8, 0:KL], in0=PS[:, k, :].rearrange("p (h c) -> p h c", h=8),
                                      scalar1=g1[:, 0:1], scalar2=None, op0=ALU.mult)
                    link(dve.tensor_scalar(out=q2[:, 8 * k:8 * k + 8, 0:KL],
                                           in0=PS[0:R2, 2 + k, :].rearrange("p (h c) -> p h c", h=8),
                                           scalar1=g2[:, 0:1], scalar2=None, op0=ALU.mult))
                dve.sem_inc(prod_free, 1)

            @block.scalar
            def _(act):
                for j in range(HEADS // 2):
                    act.wait_ge(prod2_ps, j + 1)
                    act.activation(out[:, j, :], PS[:, (4 + j) % 8, 0:D], ACT.Copy)


def latent_heads(core, q1, q2, out):
    nc, X, PS = core.nc, core.X, core.PS
    R2 = QL - P
    PAIRS = HEADS // 2
    H2 = ROPE // 2
    W1 = KL + 1
    QUERIES = {2: ((0, 1), (2, 3)), 3: ((4,), (5,)), 4: ((6,), (7,))}
    TURNS = {5: ((0, 1), (2, 3)), 6: ((4, 5), (6, 7))}
    with core.stage("lh") as (sb, sem):
        Wa = sb("Wa", [P, DH, LOW])
        kvw = sb("kvw", [P, KL])
        cos = sb("cos", [P, TPB, ROPE])
        sin = sb("sin", [P, TPB, ROPE])
        mask = sb("mask", [P, P], BF16)
        xn = sb("xn", [P, TPB, D])
        xT = sb("xT", [P, DH, T])
        low = sb("low", [P, TPB, LOW])
        junk = sb("junk", [P, TPB, QL + KL])
        eps = sb("eps", [P, TPB, 2])
        ms = sb("ms", [P, TPB, 2])
        rs = sb("rs", [P, TPB, 2])
        qn = sb("qn", [P, TPB, QL])
        ktok = sb("ktok", [P, TPB, QK])
        c1 = sb("c1", [P, 2, TPB, W1])
        qc1 = sb("qc1", [P, T])
        qc2 = sb("qc2", [R2, T])
        KT = sb("KT", [P, 2, T])
        qtok = sb("qtok", [P, TPB, HEADS, QK])
        ra = sb("ra", [P, HEADS, ROPE])
        rb = sb("rb", [P, HEADS, ROPE])
        QT = sb("QT", [P, 2, HEADS, T])
        negm = sb("negm", [P, 4])
        p0 = sb("p0", [P, 2, 2, P])
        p1 = sb("p1", [P, 2, 2, T])
        t0 = sb("t0", [P, 2, 2, T])
        t1 = sb("t1", [P, 2, 2, P])
        rz = sb("rz", [P, 4])
        oc = sb("oc", [P, 2, TPB, 2 * KL])
        oT = sb("oT", [P, 2, T])
        names = ("loaded consts mask_made xn_ready xt_ps xt_ready low_ps low_read ms_ready rs_ready qn_ready c_ready kr_ready "
                 "qct_ps qct_ready kt_ps kt_ready q_ps q_ready roped qt_ps qt_a qt_d s_ps negm_ready exp_done pt_ps pt_a "
                 "pt_d o_ps o_done ot_ps ot_ready y_ps added own rz_ready own2 pown").split()
        S = {n: sem(n) for n in names}

        with nc.Block() as block:
            @block.sync
            def _(sp):
                sp.dma_start(Wa[:, :, :], core.dram["Wa"].rearrange("(h p) e -> p h e", p=P)).then_inc(S["loaded"], 16)
                sp.dma_start(kvw[:, :], core.dram["kv_ln_w"]).then_inc(S["loaded"], 16)
                sp.dma_start(cos[:, :, :], core.dram["cos"].rearrange("(k p) e -> p k e", p=P)).then_inc(S["loaded"], 16)
                sp.dma_start(sin[:, :, :], core.dram["sin"].rearrange("(k p) e -> p k e", p=P)).then_inc(S["loaded"], 16)

            @block.tensor
            def _(pe):
                pe.wait_ge(S["loaded"], 4 * 16)
                pe.wait_ge(S["mask_made"], 1)

                def tokens(b):
                    pe.wait_ge(S["xn_ready"], b + 1)
                    for h in range(DH):
                        for k in range(TPB):
                            last = pe.transpose(PS[:, 5, h * T + k * P:h * T + k * P + P], xn[:, k, h * P:h * P + P],
                                                core.ident[:, :])
                    last.then_inc(S["xt_ps"], 1)

                def lows(b):
                    pe.wait_ge(S["xt_ready"], b + 1)
                    for k in range(TPB):
                        for h in range(DH):
                            last = pe.matmul(PS[:, 6 - k, 0:LOW], xT[:, h, k * P:k * P + P], Wa[:, h, :],
                                             start=(h == 0), stop=(h == DH - 1))
                        last.then_inc(S["low_ps"], 1)

                def low_queries(b):
                    pe.wait_ge(S["qn_ready"], TPB * b + TPB)
                    pe.wait_ge(S["low_read"], TPB * b + TPB)
                    for k in range(TPB):
                        pe.transpose(PS[:, 6, k * P:k * P + P], qn[:, k, 0:P], core.ident[:, :])
                        last = pe.transpose(PS[0:R2, 6, T + k * P:T + k * P + P], qn[:, k, P:QL], core.ident[:, :])
                    last.then_inc(S["qct_ps"], 1)
                    pe.wait_ge(S["c_ready"], b + 1)
                    pe.wait_ge(S["kr_ready"], b + 1)
                    for k in range(TPB):
                        last = pe.transpose(PS[:, 5, k * P:k * P + P], ktok[:, k, :], core.ident[:, :])
                    last.then_inc(S["kt_ps"], 1)

                def queries(b, i):
                    k, j = i // 4, i % 4
                    if i == 0:
                        pe.wait_ge(S["qct_ready"], b + 1)
                        pe.wait_ge(S["kt_ready"], b + 1)
                    if i >= 2:
                        pe.wait_ge(S["q_ready"], 8 * b + i - 1)
                    pe.matmul(PS[:, 5 + i % 2, :], qc1[:, k * P:k * P + P], q1[:, 4 * j:4 * j + 4, :],
                              start=True, stop=False)
                    pe.matmul(PS[:, 5 + i % 2, :], qc2[:, k * P:k * P + P], q2[:, 4 * j:4 * j + 4, :],
                              start=False, stop=True).then_inc(S["q_ps"], 1)

                def turn(b, i):
                    k, j = i // 4, i % 4
                    if i < 2:
                        pe.wait_ge(S["q_ready"], 8 * b + 7 + i)
                    else:
                        pe.wait_ge((S["qt_a"], S["qt_d"])[i % 2], 4 * b + i // 2)
                    if j == 0:
                        pe.wait_ge(S["roped"], TPB * b + k + 1)
                    for h in range(4):
                        last = pe.transpose(PS[:, 5 + i % 2, h * P:h * P + P], qtok[:, k, 4 * j + h, :], core.ident[:, :])
                    last.then_inc(S["qt_ps"], 1)

                def scores(b, u, g):
                    if g == 0:
                        pe.wait_ge(S["qt_a"], 4 * b + 4)
                        pe.wait_ge(S["qt_d"], 4 * b + 4)
                    for i in range(2):
                        h = 2 * g + i
                        pe.matmul(PS[:, 0, i * T:i * T + T], QT[:, u, h, P:T], KT[:, u, :], start=True, stop=False)
                        pe.matmul(PS[:, 0, i * T + P:i * T + T], core.identb[:, :], mask[:, :], start=False, stop=True)
                    for i in range(2):
                        h = 2 * g + i
                        pe.matmul(PS[:, 1, i * P:i * P + P], QT[:, u, h, 0:P], KT[:, u, 0:P], start=True, stop=False)
                        last = pe.matmul(PS[:, 1, i * P:i * P + P], core.identb[:, :], mask[:, :], start=False, stop=True)
                    last.then_inc(S["s_ps"], 1)

                def turn_latents(b, g):
                    pe.wait_ge(S["o_done"], PAIRS * b + g + 1)
                    for k in range(TPB):
                        last = pe.transpose(PS[:, 3, T + k * P:T + k * P + P], oc[:, g % 2, k, :], core.ident[:, :])
                    last.then_inc(S["ot_ps"], 1)

                def output(b, g):
                    for k in range(TPB):
                        last = pe.matmul(PS[:, 7, k * D:k * D + D], oT[:, g % 2, k * P:k * P + P], out[:, g, :],
                                         start=(g == 0 and k == 0), stop=(g == PAIRS - 1 and k == TPB - 1),
                                         skip_group_check=True)
                    if g == PAIRS - 1:
                        last.then_inc(S["y_ps"], 1)

                def first(b, u):
                    tokens(b)
                    lows(b)
                    low_queries(b)
                    for i in range(8):
                        queries(b, i)
                    for i in range(8):
                        turn(b, i)
                    scores(b, u, 0)

                def body(b, u, prev, more):
                    for g in range(PAIRS):
                        n, w = PAIRS * b + g, g % 2
                        pe.wait_ge(S["exp_done"], n + 1)
                        if prev or g >= 2:
                            pe.wait_ge(S["ot_ready"], n - 1)
                        for i in range(2):
                            pe.transpose(PS[:, 2, i * T:i * T + P], p0[:, w, i, :], core.ident[:, :])
                            pe.transpose(PS[:, 2, i * T + P:i * T + T], p1[:, w, i, 0:P], core.ident[:, :])
                            last = pe.transpose(PS[:, 3, i * P:i * P + P], p1[:, w, i, P:T], core.ident[:, :])
                        last.then_inc(S["pt_ps"], 1)
                        if g + 1 < PAIRS:
                            scores(b, u, g + 1)
                        elif more:
                            scores(b + 1, 1 - u, 0)
                        if g >= 2:
                            if g == 2 and prev:
                                pe.wait_ge(S["added"], b)
                            output(b, g - 2)
                        elif prev:
                            output(b - 1, g - 2 + PAIRS)
                        if more:
                            if g == 0:
                                pe.wait_ge(S["qt_a"], 4 * b + 4)
                                tokens(b + 1)
                            for i in QUERIES.get(g, ((), ()))[0]:
                                queries(b + 1, i)
                            for i in TURNS.get(g, ((), ()))[0]:
                                turn(b + 1, i)
                        pe.wait_ge(S["pt_a"], n + 1)
                        pe.wait_ge(S["pt_d"], n + 1)
                        if prev or g >= 1:
                            pe.wait_ge(S["o_done"], n)
                        for i in range(2):
                            pe.matmul(PS[:, 4, i * W1:i * W1 + W1], t0[:, w, i, 0:P], c1[:, u, 0, :], start=True, stop=True)
                        for i in range(2):
                            o = PS[:, 4, (2 + i) * W1:(3 + i) * W1]
                            pe.matmul(o, t0[:, w, i, P:T], c1[:, u, 0, :], start=True, stop=False)
                            last = pe.matmul(o, t1[:, w, i, :], c1[:, u, 1, :], start=False, stop=True)
                        last.then_inc(S["o_ps"], 1)
                        if g >= 1:
                            turn_latents(b, g - 1)
                        elif prev:
                            turn_latents(b - 1, PAIRS - 1)
                        if more:
                            if g == 0:
                                lows(b + 1)
                            if g == 1:
                                low_queries(b + 1)
                            for i in QUERIES.get(g, ((), ()))[1]:
                                queries(b + 1, i)
                            for i in TURNS.get(g, ((), ()))[1]:
                                turn(b + 1, i)

                def finish(b, u):
                    pe.wait_ge(S["ot_ready"], PAIRS * b + PAIRS - 1)
                    turn_latents(b, PAIRS - 1)
                    output(b, PAIRS - 2)
                    pe.wait_ge(S["ot_ready"], PAIRS * b + PAIRS)
                    output(b, PAIRS - 1)

                overlapped(pe, B, first, body, finish)

            @block.scalar
            def _(act):
                link = Chain(act, S["own2"], 2 * TPB)

                def tokens(b):
                    act.wait_ge(S["xt_ps"], b + 1)
                    act.activation(xT[:, :, :], PS[:, 5, :].rearrange("p (h t) -> p h t", h=DH),
                                   ACT.Copy).then_inc(S["xt_ready"], 1)

                def lows(b):
                    link.start(b)
                    for k in range(TPB):
                        act.wait_ge(S["low_ps"], TPB * b + k + 1)
                        link(act.activation(low[:, k, :], PS[:, 6 - k, 0:LOW], ACT.Copy))
                        act.sem_inc(S["low_read"], 1)
                        act.activation(junk[:, k, 0:QL], low[:, k, 0:QL], ACT.Square, scale=QL ** -0.5,
                                       accum_out=ms[:, k, 0:1])
                        link(act.activation(junk[:, k, QL:QL + KL], low[:, k, QL:QL + KL], ACT.Square, scale=KL ** -0.5,
                                            accum_out=ms[:, k, 1:2]))
                        act.sem_inc(S["ms_ready"], 1)

                def low_queries(b):
                    act.wait_ge(S["rs_ready"], b + 1)
                    for k in range(TPB):
                        act.activation(qn[:, k, :], low[:, k, 0:QL], ACT.Copy, scale=rs[:, k, 0:1]).then_inc(S["qn_ready"], 1)

                def turned(b, u):
                    act.wait_ge(S["qct_ps"], b + 1)
                    act.activation(qc1[:, :], PS[:, 6, 0:T], ACT.Copy)
                    act.activation(qc2[:, :], PS[0:R2, 6, T:2 * T], ACT.Copy).then_inc(S["qct_ready"], 1)
                    act.wait_ge(S["kt_ps"], b + 1)
                    act.activation(KT[:, u, :], PS[:, 5, 0:T], ACT.Copy).then_inc(S["kt_ready"], 1)

                def queries(b, i):
                    k, j = i // 4, i % 4
                    act.wait_ge(S["q_ps"], 8 * b + i + 1)
                    act.activation(qtok[:, k, 4 * j:4 * j + 4, :], PS[:, 5 + i % 2, :].rearrange("p (h c) -> p h c", h=4),
                                   ACT.Copy).then_inc(S["q_ready"], 1)

                def turn(b, u, i):
                    if i % 2 == 0:
                        k, j = i // 4, i % 4
                        act.wait_ge(S["qt_ps"], 8 * b + i + 1)
                        act.activation(QT[:, u, 4 * j:4 * j + 4, k * P:k * P + P],
                                       PS[:, 5, :].rearrange("p (h t) -> p h t", h=4), ACT.Copy).then_inc(S["qt_a"], 1)

                def exps(b, g):
                    w = g % 2
                    act.wait_ge(S["negm_ready"], PAIRS * b + g + 1)
                    for i in range(2):
                        act.activation(p1[:, w, i, :], PS[:, 0, i * T:i * T + T], ACT.Exp, bias=negm[:, i:i + 1])
                    for i in range(2):
                        last = act.activation(p0[:, w, i, :], PS[:, 1, i * P:i * P + P], ACT.Exp, bias=negm[:, 2 + i:3 + i])
                    last.then_inc(S["exp_done"], 1)

                def first(b, u):
                    tokens(b)
                    lows(b)
                    low_queries(b)
                    turned(b, u)
                    for i in range(8):
                        queries(b, i)
                    for i in range(8):
                        turn(b, u, i)
                    exps(b, 0)

                def body(b, u, prev, more):
                    for g in range(PAIRS):
                        act.wait_ge(S["pt_ps"], PAIRS * b + g + 1)
                        act.activation(t0[:, g % 2, :, :], PS[:, 2, :].rearrange("p (i t) -> p i t", i=2),
                                       ACT.Copy).then_inc(S["pt_a"], 1)
                        if more:
                            if g == 0:
                                tokens(b + 1)
                            if g == 1:
                                low_queries(b + 1)
                        if g + 1 < PAIRS:
                            exps(b, g + 1)
                        elif more:
                            exps(b + 1, 0)
                        if more:
                            if g == 0:
                                lows(b + 1)
                            if g == 1:
                                turned(b + 1, 1 - u)
                            for i in sum(QUERIES.get(g, ()), ()):
                                queries(b + 1, i)
                            for i in sum(TURNS.get(g, ()), ()):
                                turn(b + 1, 1 - u, i)

                overlapped(act, B, first, body, lambda b, u: None)

            @block.gpsimd
            def _(pool):
                mz = S["consts"]
                pool.memset(c1[:, :, :, KL:KL + 1], 1.0)
                pool.memset(eps[:, :, :], RMS_EPS)
                pool.memset(mask[:, :], 0.0).then_inc(mz, 1)
                pool.wait_ge(mz, 1)
                pool.affine_select(out=mask[:, :], in_=mask[:, :], compare_op=ALU.is_ge, fill=-1e30, base=0,
                                   pattern=[[-1, P]], channel_multiplier=1).then_inc(S["mask_made"], 1)
                pool.wait_ge(S["loaded"], 4 * 16)
                rp = Chain(pool, S["pown"], 1 + 2 + 2 * TPB)

                def rotate(dst, src, k, n):
                    a, c = ra[:, 0:n, :], rb[:, 0:n, :]
                    cb = cos[:, k:k + 1, :].broadcast_to([P, n, ROPE])
                    sb_ = sin[:, k:k + 1, :].broadcast_to([P, n, ROPE])
                    pool.tensor_tensor(out=a, in0=src, in1=cb, op=ALU.mult)
                    pool.tensor_tensor(out=c[:, :, 0:H2], in0=src[:, :, H2:ROPE], in1=sb_[:, :, 0:H2], op=ALU.mult)
                    rp(pool.tensor_tensor(out=c[:, :, H2:ROPE], in0=src[:, :, 0:H2], in1=sb_[:, :, H2:ROPE], op=ALU.mult))
                    rp(pool.tensor_tensor(out=dst, in0=a, in1=c, op=ALU.add))

                with pool.Fori(0, B) as b:
                    pool.wait_ge(S["ms_ready"], TPB * b + TPB)
                    rp.start(b)
                    rp(pool.tensor_tensor(out=ms[:, :, :], in0=ms[:, :, :], in1=eps[:, :, :], op=ALU.add))
                    pool.tensor_tensor(out=rs[:, :, :], in0=ms[:, :, :],
                                       in1=core.half[:, 0:2 * TPB].rearrange("p (k c) -> p k c", k=TPB),
                                       op=ALU.pow).then_inc(S["rs_ready"], 1)
                    kr = low[:, :, QL + KL:LOW]
                    pool.tensor_tensor(out=ra[:, 0:TPB, :], in0=kr, in1=cos[:, :, :], op=ALU.mult)
                    pool.tensor_tensor(out=rb[:, 0:TPB, 0:H2], in0=kr[:, :, H2:ROPE], in1=sin[:, :, 0:H2], op=ALU.mult)
                    rp(pool.tensor_tensor(out=rb[:, 0:TPB, H2:ROPE], in0=kr[:, :, 0:H2], in1=sin[:, :, H2:ROPE], op=ALU.mult))
                    rp(pool.tensor_tensor(out=ktok[:, :, KL:QK], in0=ra[:, 0:TPB, :], in1=rb[:, 0:TPB, :], op=ALU.add))
                    pool.sem_inc(S["kr_ready"], 1)
                    for k in range(TPB):
                        pool.wait_ge(S["q_ready"], 8 * b + 4 * k + 4)
                        rotate(qtok[:, k, :, KL:QK], qtok[:, k, :, KL:QK], k, HEADS)
                        pool.sem_inc(S["roped"], 1)

            @block.vector
            def _(dve):
                link = Chain(dve, S["own"], PAIRS)
                dve.wait_ge(S["loaded"], 4 * 16)
                dve.wait_ge(S["mask_made"], 1)

                def normalise(b):
                    for k in range(TPB):
                        t = TPB * b + k
                        last = dve.tensor_scalar(out=xn[:, k, :], in0=X[:, bass.ds(t, 1), :],
                                                 scalar1=core.mean[:, bass.ds(t, 1)], scalar2=core.rstd[:, bass.ds(t, 1)],
                                                 op0=ALU.subtract, op1=ALU.mult)
                    last.then_inc(S["xn_ready"], 1)

                def latents(b, u):
                    dve.wait_ge(S["rs_ready"], b + 1)
                    for k in range(TPB):
                        for d in (ktok[:, k, 0:KL], c1[:, u, k, 0:KL]):
                            last = dve.scalar_tensor_tensor(out=d, in0=low[:, k, QL:QL + KL], scalar=rs[:, k, 1:2],
                                                            in1=kvw[:, :], op0=ALU.mult, op1=ALU.mult)
                    last.then_inc(S["c_ready"], 1)

                def turn(b, u, i):
                    if i % 2:
                        k, j = i // 4, i % 4
                        dve.wait_ge(S["qt_ps"], 8 * b + i + 1)
                        dve.tensor_copy(QT[:, u, 4 * j:4 * j + 4, k * P:k * P + P],
                                        PS[:, 6, :].rearrange("p (h t) -> p h t", h=4)).then_inc(S["qt_d"], 1)

                def maxima(b, g):
                    dve.wait_ge(S["s_ps"], PAIRS * b + g + 1)
                    dve.tensor_reduce(out=negm[:, 0:2], in_=PS[:, 0, :].rearrange("p (i t) -> p i t", i=2),
                                      axis=AX.X, op=ALU.max, negate=True)
                    link.start(b, g)
                    link(dve.tensor_reduce(out=negm[:, 2:4], in_=PS[:, 1, 0:T].rearrange("p (i t) -> p i t", i=2),
                                           axis=AX.X, op=ALU.max, negate=True))
                    dve.sem_inc(S["negm_ready"], 1)

                def finish_latents(b, g):
                    dve.wait_ge(S["o_ps"], PAIRS * b + g + 1)
                    o = PS[:, 4, 0:4 * W1].rearrange("p (q i c) -> p q i c", q=2, i=2)
                    dve.reciprocal(out=rz[:, :], in_=o[:, :, :, KL]).then_inc(S["rz_ready"], 1)
                    dve.wait_ge(S["rz_ready"], PAIRS * b + g + 1)
                    r = rz[:, :].rearrange("p (q i c) -> p q i c", q=2, c=1).broadcast_to([P, 2, 2, KL])
                    dve.tensor_tensor(out=oc[:, g % 2, :, :].rearrange("p q (i c) -> p q i c", i=2),
                                      in0=o[:, :, :, 0:KL], in1=r, op=ALU.mult).then_inc(S["o_done"], 1)

                def turned_latents(b, g):
                    dve.wait_ge(S["ot_ps"], PAIRS * b + g + 1)
                    dve.tensor_copy(oT[:, g % 2, :], PS[:, 3, T:2 * T]).then_inc(S["ot_ready"], 1)

                def add(b):
                    dve.wait_ge(S["y_ps"], b + 1)
                    t = TPB * b
                    dve.tensor_tensor(out=X[:, bass.ds(t, TPB), :], in0=X[:, bass.ds(t, TPB), :],
                                      in1=PS[:, 7, :].rearrange("p (k d) -> p k d", k=TPB), op=ALU.add).then_inc(S["added"], 1)

                def first(b, u):
                    normalise(b)
                    latents(b, u)
                    for i in range(8):
                        turn(b, u, i)
                    maxima(b, 0)

                def body(b, u, prev, more):
                    for g in range(PAIRS):
                        if g == 0 and more:
                            normalise(b + 1)
                        dve.wait_ge(S["pt_ps"], PAIRS * b + g + 1)
                        dve.tensor_copy(t1[:, g % 2, :, :],
                                        PS[:, 3, 0:T].rearrange("p (i t) -> p i t", i=2)).then_inc(S["pt_d"], 1)
                        if g + 1 < PAIRS:
                            maxima(b, g + 1)
                        elif more:
                            maxima(b + 1, 0)
                        if g == 1 and more:
                            latents(b + 1, 1 - u)
                        if more:
                            for i in TURNS.get(g, ((), ()))[0]:
                                turn(b + 1, 1 - u, i)
                        finish_latents(b, g)
                        if g >= 1:
                            turned_latents(b, g - 1)
                        elif prev:
                            turned_latents(b - 1, PAIRS - 1)
                        if g == 1 and prev:
                            add(b - 1)
                        if more:
                            for i in TURNS.get(g, ((), ()))[1]:
                                turn(b + 1, 1 - u, i)

                def finish(b, u):
                    turned_latents(b, PAIRS - 1)
                    add(b)

                overlapped(dve, B, first, body, finish)


HD = 16
PAD = 32
HPH = P // HD
SLOTS = NT + 32


def head_window(padded, h):
    at = h * P + P - HD - HD * (h % HPH)
    return padded[:, at:at + P]


def head_masks(pool, link, hmask):
    link(pool.memset(hmask[:, :], 1.0))
    link(pool.affine_select(out=hmask[:, :], in_=hmask[:, :], compare_op=ALU.is_ge, fill=0.0, base=0,
                            pattern=[[-HD, HPH]], channel_multiplier=1))
    link(pool.affine_select(out=hmask[:, :], in_=hmask[:, :], compare_op=ALU.is_ge, fill=0.0, base=HD - 1,
                            pattern=[[HD, HPH]], channel_multiplier=-1))


def mask_keys(pool, KTm, KT, hmask, half, n):
    return pool.tensor_tensor(out=KTm[:, half * HPH:half * HPH + HPH, :],
                              in0=KT[:, half:half + 1, :].broadcast_to([P, HPH, n]),
                              in1=hmask[:, :].rearrange("p (h t) -> p h t", t=1).broadcast_to([P, HPH, n]), op=ALU.mult)


def double_attention(core):
    nc, X, PS = core.nc, core.X, core.PS
    PAIRS = HEADS // 2
    statistics(core, "4", X, LN_EPS)
    with core.stage("da") as (sb, sem):
        WT = sb("WT", [P, DH, D])
        W = sb("W", [P, DH, D])
        g = sb("g", [P, 3, HEADS, HD])
        zero = sb("zero", [P, 2048])
        hmask = sb("hmask", [P, HPH])
        xn = sb("xn", [P, TPB, D])
        xT = sb("xT", [P, DH, T])
        w = sb("w", [P, TPB * HEADS, HD])
        sq = sb("sq", [P, TPB * HEADS, HD])
        ms = sb("ms", [P, TPB * HEADS])
        rs = sb("rs", [P, TPB * HEADS])
        q = sb("q", [P, 2, TPB, D])
        v = sb("v", [P, 2, TPB, HEADS * P + P - HD])
        QT = sb("QT", [P, 2, DH, T])
        KT = sb("KT", [P, DH, T])
        KTm = sb("KTm", [P, 2, HEADS, T])
        negm = sb("negm", [P, 2, 2, TPB])
        z = sb("z", [P, 2, 2, TPB])
        rz = sb("rz", [P, 2, 2, TPB])
        ex = sb("ex", [P, 2, 2, TPB, T])
        diag = sb("diag", [P, 2, 2, TPB, P])
        G = sb("G", [P, 2, 2, TPB, T])
        yT = sb("yT", [P, DH, T])
        S = {n: sem(n) for n in (
            "loaded padded zeroed stored hmade xn_ready xt_ps xt_ready w_ps w_ready sq_ready ms_ready rs_ready n_ready "
            "qk_ready v_ready qt_ps qt_ready kt_ps kt_ready km_ready s_ps negm_ready exp_done diag_ready pt_ps g_ready "
            "y_ps y_ready out_ps added own ownr").split()}

        with nc.Block() as block:
            @block.sync
            def _(sp):
                sp.dma_start(WT[:, :, :], core.dram["W2T"].rearrange("(h p) e -> p h e", p=P)).then_inc(S["loaded"], 16)
                sp.dma_start(W[:, :, :], core.dram["W2"].rearrange("(h p) e -> p h e", p=P)).then_inc(S["loaded"], 16)
                sp.dma_start(g[:, :, :, :], core.dram["g2"].rearrange("p (a h d) -> p a h d", a=3, h=HEADS)).then_inc(S["loaded"], 16)
                sp.wait_ge(S["zeroed"], 1)
                slots = core.slots_x.rearrange("(n p r) d -> n p (r d)", p=P, r=8)
                for k in range(SLOTS // 8):
                    sp.dma_start(slots[k], zero[:, :]).then_inc(S["stored"], 16)
                sp.wait_ge(S["stored"], SLOTS // 8 * 16)

            @block.tensor
            def _(pe):
                pe.wait_ge(S["loaded"], 3 * 16)

                def tokens(b):
                    pe.wait_ge(S["xn_ready"], b + 1)
                    for h in range(DH):
                        for k in range(TPB):
                            last = pe.transpose(PS[:, 7, h * T + k * P:h * T + k * P + P], xn[:, k, h * P:h * P + P],
                                                core.ident[:, :])
                    last.then_inc(S["xt_ps"], 1)

                def project(b):
                    pe.wait_ge(S["xt_ready"], b + 1)
                    for k in range(TPB):
                        for h in range(DH):
                            last = pe.matmul(PS[:, 7, k * D:k * D + D], xT[:, h, k * P:k * P + P], WT[:, h, :],
                                             start=(h == 0), stop=(h == DH - 1))
                    last.then_inc(S["w_ps"], 1)

                def turn(b, a, ready):
                    for h in range(DH):
                        for k in range(TPB):
                            last = pe.transpose(PS[:, 7, h * T + k * P:h * T + k * P + P], q[:, a, k, h * P:h * P + P],
                                                core.ident[:, :])
                    last.then_inc(ready, 1)

                def output(b):
                    pe.wait_ge(S["y_ready"], 2 * b + 3)
                    for k in range(TPB):
                        for h in range(DH):
                            last = pe.matmul(PS[:, 7, k * D:k * D + D], yT[:, h, k * P:k * P + P], W[:, h, :],
                                             start=(h == 0), stop=(h == DH - 1))
                    last.then_inc(S["out_ps"], 1)

                def scores(b, u, c):
                    if c % (PAIRS // 2) == 0:
                        pe.wait_ge(S["km_ready"], 2 * b + 1 + c // (PAIRS // 2))
                    for i in range(2):
                        h = 2 * c + i
                        for k in range(TPB):
                            last = pe.matmul(PS[:, 2 * (c % 2) + i, k * T:k * T + T], QT[:, u, h // HPH, k * P:k * P + P],
                                             KTm[:, u, h, :], start=True, stop=True)
                    last.then_inc(S["s_ps"], 1)

                def first(b, u):
                    tokens(b)
                    project(b)
                    pe.wait_ge(S["w_ready"], 1)
                    pe.wait_ge(S["qk_ready"], 1)
                    turn(b, 0, S["qt_ps"])
                    pe.wait_ge(S["qt_ready"], 1)
                    turn(b, 1, S["kt_ps"])
                    scores(b, u, 0)
                    scores(b, u, 1)

                def body(b, u, prev, more):
                    for c in range(PAIRS):
                        n, w_ = PAIRS * b + c, c % 2
                        if c == 1 and more:
                            project(b + 1)
                        if c == 4 and more:
                            pe.wait_ge(S["qk_ready"], b + 2)
                            if prev:
                                pe.wait_ge(S["added"], b)
                            else:
                                pe.wait_ge(S["w_ready"], b + 2)
                            turn(b + 1, 0, S["qt_ps"])
                        pe.wait_ge(S["diag_ready"], n + 1)
                        pe.wait_ge(S["g_ready"], n + 1)
                        for i in range(2):
                            for j in range(TPB):
                                for k in range(TPB):
                                    last = pe.matmul(PS[:, 4 + i, j * T + k * P:j * T + k * P + P],
                                                     ex[:, w_, i, k, j * P:j * P + P], diag[:, w_, i, k, :],
                                                     start=True, stop=True)
                        last.then_inc(S["pt_ps"], 1)
                        if c + 2 < PAIRS:
                            scores(b, u, c + 2)
                        elif more:
                            scores(b + 1, 1 - u, c + 2 - PAIRS)
                        if c == 0 and more:
                            pe.wait_ge(S["kt_ready"], b + 1)
                            tokens(b + 1)
                        if c == 1 and prev:
                            if more:
                                pe.wait_ge(S["w_ready"], b + 2)
                            output(b - 1)
                        if c == 4 and more:
                            pe.wait_ge(S["qt_ready"], b + 2)
                            turn(b + 1, 1, S["kt_ps"])
                        if c == 0:
                            pe.wait_ge(S["v_ready"], b + 1)
                        if c % (PAIRS // 2) == 0:
                            pe.wait_ge(S["y_ready"], 2 * b + c // (PAIRS // 2) + 1)
                        pe.wait_ge(S["g_ready"], n + 2)
                        for i in range(2):
                            h = 2 * c + i
                            for j in range(TPB):
                                last = pe.matmul(PS[:, 6, 0:T], head_window(v[:, u, j, :], h), G[:, w_, i, j, :],
                                                 start=(h % HPH == 0 and j == 0), stop=(h % HPH == HPH - 1 and j == TPB - 1))
                        if c % (PAIRS // 2) == PAIRS // 2 - 1:
                            last.then_inc(S["y_ps"], 1)

                def finish(b, u):
                    pe.wait_ge(S["added"], b)
                    output(b)

                overlapped(pe, B, first, body, finish)

            @block.scalar
            def _(act):
                act.sem_inc(S["y_ready"], 1)

                def bank7(out, sem_in, sem_out, b):
                    act.wait_ge(sem_in, b + 1)
                    act.activation(out, PS[:, 7, :].rearrange("p (h t) -> p h t", h=out.shape[1]), ACT.Copy).then_inc(sem_out, 1)

                def heads_of(half, b):
                    act.wait_ge(S["y_ps"], 2 * b + half + 1)
                    act.activation(yT[:, half, :], PS[:, 6, 0:T], ACT.Copy).then_inc(S["y_ready"], 1)

                def exps(b, c):
                    n, w_ = PAIRS * b + c, c % 2
                    act.wait_ge(S["negm_ready"], n + 1)
                    act.wait_ge(S["g_ready"], n)
                    for i in range(2):
                        for k in range(TPB):
                            last = act.activation(ex[:, w_, i, k, :], PS[:, 2 * w_ + i, k * T:k * T + T], ACT.Exp,
                                                  bias=negm[:, w_, i, k:k + 1], accum_out=z[:, w_, i, k:k + 1])
                    last.then_inc(S["exp_done"], 1)

                def first(b, u):
                    bank7(xT[:, :, :], S["xt_ps"], S["xt_ready"], b)
                    bank7(w[:, :, :], S["w_ps"], S["w_ready"], b)
                    bank7(QT[:, u, :, :], S["qt_ps"], S["qt_ready"], b)
                    bank7(KT[:, :, :], S["kt_ps"], S["kt_ready"], b)
                    act.wait_ge(S["negm_ready"], 1)
                    for i in range(2):
                        for k in range(TPB):
                            last = act.activation(ex[:, 0, i, k, :], PS[:, i, k * T:k * T + T], ACT.Exp,
                                                  bias=negm[:, 0, i, k:k + 1], accum_out=z[:, 0, i, k:k + 1])
                    last.then_inc(S["exp_done"], 1)

                def body(b, u, prev, more):
                    for c in range(PAIRS):
                        if c == 0 and prev:
                            heads_of(1, b - 1)
                        if c == 4:
                            if prev:
                                act.wait_ge(S["out_ps"], b)
                            heads_of(0, b)
                        if c + 1 < PAIRS:
                            exps(b, c + 1)
                        elif more:
                            exps(b + 1, 0)
                        if more and c == 0:
                            bank7(xT[:, :, :], S["xt_ps"], S["xt_ready"], b + 1)
                        if more and c == 1:
                            bank7(w[:, :, :], S["w_ps"], S["w_ready"], b + 1)
                        if more and c == 4:
                            bank7(QT[:, 1 - u, :, :], S["qt_ps"], S["qt_ready"], b + 1)
                            bank7(KT[:, :, :], S["kt_ps"], S["kt_ready"], b + 1)

                def finish(b, u):
                    heads_of(1, b)

                overlapped(act, B, first, body, finish)

            @block.gpsimd
            def _(pool):
                pool.memset(zero[:, :], 0.0).then_inc(S["zeroed"], 1)
                pool.memset(v[:, :, :, :], 0.0).then_inc(S["padded"], 1)
                head_masks(pool, Chain(pool, S["hmade"], 3), hmask)
                pool.wait_ge(S["padded"], 1)
                pool.wait_ge(S["loaded"], 3 * 16)

                def step(b, u):
                    pool.wait_ge(S["w_ready"], b + 1)
                    pool.tensor_tensor(out=sq[:, :, :], in0=w[:, :, :], in1=w[:, :, :], op=ALU.mult).then_inc(S["sq_ready"], 1)
                    pool.wait_ge(S["ms_ready"], b + 1)
                    pool.tensor_tensor(out=rs[:, :], in0=ms[:, :], in1=core.half[:, 0:TPB * HEADS],
                                       op=ALU.pow).then_inc(S["rs_ready"], 1)
                    pool.wait_ge(S["n_ready"], b + 1)
                    for k in range(TPB):
                        own = v[:, u, k, 0:HEADS * P].rearrange("p (h c) -> p h c", h=HEADS)[:, :, P - HD:P]
                        last = pool.tensor_tensor(out=own, in0=w[:, k * HEADS:k * HEADS + HEADS, :], in1=g[:, 2, :, :],
                                                  op=ALU.mult)
                    last.then_inc(S["v_ready"], 1)
                    pool.wait_ge(S["kt_ready"], b + 1)
                    for half in range(DH):
                        mask_keys(pool, KTm[:, u, :, :], KT, hmask, half, T).then_inc(S["km_ready"], 1)

                in_pairs(pool, B, step)

            @block.vector
            def _(dve):
                link = Chain(dve, S["own"], PAIRS)
                dve.sem_inc(S["g_ready"], 1)
                dve.wait_ge(S["loaded"], 3 * 16)
                dve.tensor_scalar(out=g[:, 1, :, :], in0=g[:, 1, :, :], scalar1=HD ** -0.5, scalar2=None,
                                  op0=ALU.mult)

                def normalise(b):
                    for k in range(TPB):
                        t = TPB * b + k
                        last = dve.tensor_scalar(out=xn[:, k, :], in0=X[:, bass.ds(t, 1), :],
                                                 scalar1=core.mean[:, bass.ds(t, 1)], scalar2=core.rstd[:, bass.ds(t, 1)],
                                                 op0=ALU.subtract, op1=ALU.mult)
                    last.then_inc(S["xn_ready"], 1)

                def squares(b):
                    dve.wait_ge(S["sq_ready"], b + 1)
                    red = Chain(dve, S["ownr"], 1)
                    red.start(b)
                    red(dve.tensor_reduce(out=ms[:, :], in_=sq[:, :, :], axis=AX.X, op=ALU.add))
                    dve.tensor_scalar(out=ms[:, :], in0=ms[:, :], scalar1=1.0 / HD, scalar2=RMS_EPS, op0=ALU.mult,
                                      op1=ALU.add).then_inc(S["ms_ready"], 1)

                def queries(b):
                    dve.wait_ge(S["rs_ready"], b + 1)
                    r = rs[:, :].rearrange("p (n d) -> p n d", d=1).broadcast_to([P, TPB * HEADS, HD])
                    dve.tensor_tensor(out=w[:, :, :], in0=w[:, :, :], in1=r, op=ALU.mult).then_inc(S["n_ready"], 1)
                    dve.wait_ge(S["n_ready"], b + 1)
                    for k in range(TPB):
                        for a in range(2):
                            last = dve.tensor_tensor(out=q[:, a, k, :].rearrange("p (h d) -> p h d", d=HD),
                                                     in0=w[:, k * HEADS:k * HEADS + HEADS, :], in1=g[:, a, :, :], op=ALU.mult)
                    last.then_inc(S["qk_ready"], 1)

                def maxima(b, c):
                    w_ = c % 2
                    dve.wait_ge(S["s_ps"], PAIRS * b + c + 1)
                    dve.tensor_reduce(out=negm[:, w_, :, :].rearrange("p i k -> p (i k)"),
                                      in_=PS[:, 2 * w_:2 * w_ + 2, :].rearrange("p i (k t) -> p (i k) t", k=TPB),
                                      axis=AX.X, op=ALU.max, negate=True).then_inc(S["negm_ready"], 1)

                def diagonals(b, c):
                    w_ = c % 2
                    dve.wait_ge(S["exp_done"], PAIRS * b + c + 1)
                    link.start(b, c)
                    link(dve.reciprocal(out=rz[:, w_, :, :], in_=z[:, w_, :, :]))
                    for i in range(2):
                        for k in range(TPB):
                            last = dve.tensor_scalar(out=diag[:, w_, i, k, :], in0=core.ident[:, :],
                                                     scalar1=rz[:, w_, i, k:k + 1], scalar2=None, op0=ALU.mult)
                    last.then_inc(S["diag_ready"], 1)

                def combine(b, c):
                    w_ = c % 2
                    dve.wait_ge(S["pt_ps"], PAIRS * b + c + 1)
                    for i in range(2):
                        for j in range(TPB):
                            last = dve.scalar_tensor_tensor(out=G[:, w_, i, j, :], in0=ex[:, w_, i, j, :],
                                                            scalar=rz[:, w_, i, j:j + 1], in1=PS[:, 4 + i, j * T:j * T + T],
                                                            op0=ALU.mult, op1=ALU.add)
                    last.then_inc(S["g_ready"], 1)

                def add(b):
                    dve.wait_ge(S["out_ps"], b + 1)
                    t = TPB * b
                    dve.tensor_tensor(out=X[:, bass.ds(t, TPB), :], in0=X[:, bass.ds(t, TPB), :],
                                      in1=PS[:, 7, :].rearrange("p (k d) -> p k d", k=TPB), op=ALU.add).then_inc(S["added"], 1)

                def first(b, u):
                    normalise(b)
                    squares(b)
                    queries(b)
                    maxima(b, 0)
                    maxima(b, 1)
                    diagonals(b, 0)

                def body(b, u, prev, more):
                    for c in range(PAIRS):
                        if c == 0 and more:
                            normalise(b + 1)
                        combine(b, c)
                        if c + 1 < PAIRS:
                            diagonals(b, c + 1)
                        elif more:
                            diagonals(b + 1, 0)
                        if c + 2 < PAIRS:
                            maxima(b, c + 2)
                        elif more:
                            maxima(b + 1, c + 2 - PAIRS)
                        if c == 1 and prev:
                            add(b - 1)
                        if c == 2 and more:
                            squares(b + 1)
                        if c == 3 and more:
                            queries(b + 1)

                def finish(b, u):
                    add(b)

                overlapped(dve, B, first, body, finish)


EXPERTS = 32
TL = P // B


def crossed(rows, tl):
    return rows.rearrange("(s g l) d -> l s g d", s=B, l=TL)[tl]


def masked_experts(core):
    nc = core.nc
    statistics(core, "5", core.X, LN_EPS)
    with ExitStack() as keep:
        def sb(tag, shape, dt=F32):
            return keep.enter_context(nc.sbuf_tensor("me_" + tag, shape, dt))

        rows = sb("rows", [P, NT, D])
        logits = sb("logits", [P, NT, EXPERTS])
        slot = sb("slot", [P, NT], I32)
        slot_x = sb("slot_x", [P, NT], I32)
        weight_x = sb("weight_x", [P, NT])
        expert = sb("expert", [P, SLOTS], I32)
        Xc = sb("Xc", [P, NT, D])
        router_logits(core, rows, logits)
        route_top1(core, logits, slot, slot_x, weight_x, expert, Xc)
        expert_tiles(core, rows, slot, expert)
        collect_top1(core, rows, slot_x, weight_x, Xc)


def router_logits(core, rows, logits):
    nc, X, PS = core.nc, core.X, core.PS
    with core.stage("rl") as (sb, sem):
        R = sb("R", [P, DH, EXPERTS])
        xn = sb("xn", [P, 2, D])
        xT = sb("xT", [P, 2, DH, P])
        loaded, xn_ready, kept, xt_ps, xt_ready, lg_ps, lg_free = (
            sem(x) for x in ("loaded", "xn_ready", "kept", "xt_ps", "xt_ready", "lg_ps", "lg_free"))
        with nc.Block() as block:
            @block.sync
            def _(sp):
                sp.dma_start(R[:, :, :], core.dram["router"].rearrange("(h p) e -> p h e", p=P)).then_inc(loaded, 16)

            @block.vector
            def _(dve):
                dve.sem_inc(kept, 2)

                def step(t, u):
                    dve.wait_ge(kept, t + 1)
                    dve.tensor_scalar(out=xn[:, u, :], in0=X[:, bass.ds(t, 1), :], scalar1=core.mean[:, bass.ds(t, 1)],
                                      scalar2=core.rstd[:, bass.ds(t, 1)], op0=ALU.subtract,
                                      op1=ALU.mult).then_inc(xn_ready, 1)

                in_pairs(dve, NT, step)

            @block.gpsimd
            def _(pool):
                def step(t, u):
                    pool.wait_ge(xn_ready, t + 1)
                    pool.wait_ge(xt_ps, t + 1)
                    pool.tensor_copy(rows[:, bass.ds(t, 1), :], xn[:, u, :]).then_inc(kept, 1)

                in_pairs(pool, NT, step)

            @block.scalar
            def _(act):
                act.sem_inc(lg_free, 2)

                def front(t, u):
                    act.wait_ge(xt_ps, t + 1)
                    act.activation(xT[:, u, :, :], PS[:, u, 0:D].rearrange("p (h t) -> p h t", h=DH),
                                   ACT.Copy).then_inc(xt_ready, 1)

                def back(t, u):
                    act.wait_ge(lg_ps, t + 1)
                    act.activation(logits[:, bass.ds(t, 1), :], PS[:, 2 + u, 0:EXPERTS], ACT.Copy).then_inc(lg_free, 1)

                skewed(act, NT, front, back)

            @block.tensor
            def _(pe):
                pe.wait_ge(loaded, 16)

                def front(t, u):
                    pe.wait_ge(xn_ready, t + 1)
                    for h in range(DH):
                        last = pe.transpose(PS[:, u, h * P:h * P + P], xn[:, u, h * P:h * P + P], core.ident[:, :])
                    last.then_inc(xt_ps, 1)

                def back(t, u):
                    pe.wait_ge(xt_ready, t + 1)
                    pe.wait_ge(lg_free, t + 1)
                    for h in range(DH):
                        last = pe.matmul(PS[:, 2 + u, 0:EXPERTS], xT[:, u, h, :], R[:, h, :], start=(h == 0), stop=(h == DH - 1))
                    last.then_inc(lg_ps, 1)

                skewed(pe, NT, front, back)


def route_top1(core, logits, slot, slot_x, weight_x, expert, Xc):
    nc, X, PS = core.nc, core.X, core.PS
    E = EXPERTS
    HB = NT // 2
    with core.stage("rt") as (sb, sem):
        iota_e = sb("iota_e", [P, NT, E])
        iota_s = sb("iota_s", [P, SLOTS])
        reset = sb("reset", [P, E, NT])
        before = sb("before", [P, P], BF16)
        ones = sb("ones", [P, P], BF16)
        one_e = sb("one_e", [P, E])
        top = sb("top", [P, NT])
        shifted = sb("shifted", [P, NT, E])
        work = sb("work", [P, NT, E])
        first = sb("first", [P, NT])
        hot = sb("hot", [P, NT, E], BF16)
        count = sb("count", [P, E, NT])
        upto = sb("upto", [P, E, NT])
        tiles = sb("tiles", [P, 4, E])
        tiles_i = sb("tiles_i", [P, E], I32)
        slot_f = sb("slot_f", [P, NT])
        table = sb("table", [P, NT, 2])
        table_x = sb("table_x", [P, NT, 2])
        cmp = sb("cmp", [P, SLOTS, E])
        S = {n: sem(n) for n in "made x_stored x_loaded shifted exp_done hot_ready count_ps own table_ready table_stored table_loaded".split()}
        dram_x, dram_t = core.scratch_x, core.scratch_t
        with nc.Block() as block:
            @block.sync
            def _(sp):
                xr = dram_x.rearrange("(n p) d -> p n d", p=P)
                for k in range(4):
                    sp.dma_start(xr[:, 8 * k:8 * k + 8, :], X[:, 8 * k:8 * k + 8, :]).then_inc(S["x_stored"], 16)
                sp.wait_ge(S["x_stored"], 4 * 16)
                for tl in range(TL):
                    sp.dma_start(Xc[tl * B:tl * B + B, :, :], crossed(dram_x, tl)).then_inc(S["x_loaded"], 16)
                sp.wait_ge(S["table_ready"], 1)
                sp.dma_start(dram_t.rearrange("(n p) d -> p n d", p=P), table[:, :, :]).then_inc(S["table_stored"], 16)
                sp.wait_ge(S["table_stored"], 16)
                for tl in range(TL):
                    sp.dma_start(table_x[tl * B:tl * B + B, :, :], crossed(dram_t, tl)).then_inc(S["table_loaded"], 16)
                sp.wait_ge(S["x_loaded"], TL * 16)

            @block.gpsimd
            def _(pool):
                made = S["made"]
                pool.iota(iota_e[:, :, :], [[0, NT], [1, E]], base=-64, channel_multiplier=0,
                          allow_small_or_imprecise_dtypes=True).then_inc(made, 1)
                pool.iota(iota_s[:, :], [[1, SLOTS]], base=0, channel_multiplier=0,
                          allow_small_or_imprecise_dtypes=True).then_inc(made, 1)
                pool.memset(reset[:, :, :], 1.0).then_inc(made, 1)
                pool.memset(ones[:, :], 1.0).then_inc(made, 1)
                pool.memset(one_e[:, :], 1.0).then_inc(made, 1)
                pool.memset(before[:, :], 1.0).then_inc(made, 1)
                pool.wait_ge(made, 6)
                pool.memset(reset[:, :, 0:1], 0.0).then_inc(made, 1)
                pool.affine_select(out=before[:, :], in_=before[:, :], compare_op=ALU.is_gt, fill=0.0, base=0,
                                   pattern=[[1, P]], channel_multiplier=-1).then_inc(made, 1)

            @block.scalar
            def _(act):
                act.wait_ge(S["shifted"], 1)
                act.activation(shifted[:, :, :], shifted[:, :, :], ACT.Exp).then_inc(S["exp_done"], 1)

            @block.tensor
            def _(pe):
                pe.wait_ge(S["made"], 8)
                pe.wait_ge(S["hot_ready"], 1)
                for w, bank in ((before, 0), (ones, 2)):
                    for k in range(2):
                        last = pe.matmul(PS[:, bank + k, :], w[:, :], hot[:, k * HB:k * HB + HB, :], start=True, stop=True)
                last.then_inc(S["count_ps"], 1)

            @block.vector
            def _(dve):
                link = Chain(dve, S["own"], 40)

                def over_e(a, n=NT):
                    return a.rearrange("p (n e) -> p n e", e=1).broadcast_to([P, n, E])

                dve.wait_ge(S["made"], 8)
                link(dve.tensor_reduce(out=top[:, :], in_=logits[:, :, :], axis=AX.X, op=ALU.max))
                link(dve.tensor_tensor(out=shifted[:, :, :], in0=logits[:, :, :], in1=over_e(top[:, :]), op=ALU.subtract))
                link(dve.tensor_single_scalar(out=work[:, :, :], in_=shifted[:, :, :], scalar=0.0, op=ALU.is_equal))
                dve.sem_inc(S["shifted"], 1)
                link(dve.tensor_tensor(out=work[:, :, :], in0=work[:, :, :], in1=iota_e[:, :, :], op=ALU.mult))
                link(dve.tensor_reduce(out=first[:, :], in_=work[:, :, :], axis=AX.X, op=ALU.min))
                link(dve.tensor_tensor(out=hot[:, :, :], in0=iota_e[:, :, :], in1=over_e(first[:, :]), op=ALU.is_equal))
                dve.sem_inc(S["hot_ready"], 1)
                dve.wait_ge(S["exp_done"], 1)
                link(dve.tensor_reduce(out=top[:, :], in_=shifted[:, :, :], axis=AX.X, op=ALU.add))
                link(dve.reciprocal(out=table[:, :, 1], in_=top[:, :]))
                dve.wait_ge(S["count_ps"], 1)
                for k in range(2):
                    link(dve.tensor_copy(count[:, :, k * HB:k * HB + HB],
                                         PS[:, 2 + k, :].rearrange("p (n e) -> p e n", e=E)))
                link(dve.tensor_tensor_scan(out=upto[:, :, :].rearrange("p e n -> p (e n)"),
                                            data0=reset[:, :, :].rearrange("p e n -> p (e n)"),
                                            data1=count[:, :, :].rearrange("p e n -> p (e n)"), initial=0.0,
                                            op0=ALU.mult, op1=ALU.add))
                link(dve.tensor_tensor(out=count[:, :, :], in0=upto[:, :, :], in1=count[:, :, :], op=ALU.subtract))
                link(dve.tensor_scalar(out=tiles_i[:, :], in0=upto[:, :, NT - 1], scalar1=float(P - 1), scalar2=None, op0=ALU.add))
                link(dve.tensor_single_scalar(out=tiles_i[:, :], in_=tiles_i[:, :], scalar=7, op=ALU.arith_shift_right))
                link(dve.tensor_copy(tiles[:, 0, :], tiles_i[:, :]))
                link(dve.tensor_tensor_scan(out=tiles[:, 1, :], data0=one_e[:, :], data1=tiles[:, 0, :], initial=0.0,
                                            op0=ALU.mult, op1=ALU.add))
                link(dve.tensor_tensor(out=tiles[:, 2, :], in0=tiles[:, 1, :], in1=tiles[:, 0, :], op=ALU.subtract))
                link(dve.tensor_scalar(out=tiles[:, 2, :], in0=tiles[:, 2, :], scalar1=float(P), scalar2=None, op0=ALU.mult))
                first_slot = tiles[:, 2, :].rearrange("p (e n) -> p e n", n=1).broadcast_to([P, E, NT])
                link(dve.tensor_tensor(out=count[:, :, :], in0=count[:, :, :], in1=first_slot, op=ALU.add))
                for k in range(2):
                    link(dve.tensor_tensor(out=work[:, k * HB:k * HB + HB, :],
                                           in0=PS[:, k, :].rearrange("p (n e) -> p n e", e=E),
                                           in1=count[:, :, k * HB:k * HB + HB].rearrange("p e n -> p n e"), op=ALU.add))
                link(dve.tensor_tensor(out=work[:, :, :], in0=work[:, :, :], in1=hot[:, :, :], op=ALU.mult))
                link(dve.tensor_reduce(out=slot_f[:, :], in_=work[:, :, :], axis=AX.X, op=ALU.add))
                link(dve.tensor_copy(slot[:, :], slot_f[:, :]))
                link(dve.tensor_copy(table[:, :, 0], slot_f[:, :]))
                dve.sem_inc(S["table_ready"], 1)
                end = tiles[:, 1, :].rearrange("p (n e) -> p n e", n=1).broadcast_to([P, SLOTS, E])
                link(dve.tensor_tensor(out=cmp[:, :, :], in0=end, in1=over_e(iota_s[:, :], SLOTS), op=ALU.is_le))
                link(dve.tensor_reduce(out=iota_s[:, :], in_=cmp[:, :, :], axis=AX.X, op=ALU.add))
                link(dve.tensor_scalar(out=expert[:, :], in0=iota_s[:, :], scalar1=float(E - 1), scalar2=None, op0=ALU.min))
                dve.wait_ge(S["table_loaded"], TL * 16)
                dve.tensor_copy(slot_x[:, :], table_x[:, :, 0])
                dve.tensor_copy(weight_x[:, :], table_x[:, :, 1])


def expert_tiles(core, rows, slot, expert):
    nc, PS = core.nc, core.PS
    ROUND = 1.5 * 2.0 ** 23
    NB = 4
    with core.stage("et") as (sb, sem):
        wq = sb("wq", [P, DH, D])
        scale = sb("scale", [P, D])
        x = sb("x", [P, NB, D])
        mask = sb("mask", [P, NB, DH, D])
        Wm = sb("Wm", [P, 2, DH, D])
        xT = sb("xT", [P, 2, DH, P])
        y = sb("y", [P, NB, D])
        S = {n: sem(n) for n in "w_loaded own w_ready scattered free wm_ready xt_ps xt_ready y_ps y_read wm_free".split()}
        x_in = [sem(f"x_in{k}") for k in range(NB)]
        m_in = [sem(f"m_in{k}") for k in range(NB)]
        y_out = [sem(f"y_out{k}") for k in range(NB)]

        def in_fours(eng, step):
            with eng.Fori(0, SLOTS // NB) as i:
                for k in range(NB):
                    step(i, k)

        with nc.Block() as block:
            @block.sync
            def _(sp):
                sp.dma_start(wq[:, :, :], core.dram["W3T"].rearrange("(h p) e -> p h e", p=P)).then_inc(S["w_loaded"], 16)
                sp.dma_start(scale[:, :], core.dram["scale"]).then_inc(S["w_loaded"], 16)
                sp.wait_ge(S["scattered"], NT * 16)

                def step(i, k):
                    s = NB * i + k
                    sp.wait_ge(S["free"], s + 1)
                    e = sp.value_load(expert[0:1, bass.ds(s, 1)], min_val=0, max_val=EXPERTS - 1)
                    sp.dma_start(x[:, k, :], core.slots_x[bass.ds(s * P, P), :]).then_inc(x_in[k], 16)
                    sp.dma_start(mask[:, k, :, :], core.dram["masks"][bass.ds(e, 1), :, :].rearrange("n (h p) o -> p (n h) o", p=P)).then_inc(m_in[k], 16)

                in_fours(sp, step)

            @block.gpsimd
            def _(pool):
                for t in range(NT):
                    pool.indirect_dma_start(out=core.slots_x[:, :], out_offset=bass.IndirectOffsetOnAxis(ap=slot[:, t:t + 1], axis=0),
                                            in_=rows[:, t, :], in_offset=None).then_inc(S["scattered"], 16)
                pool.wait_ge(S["w_ready"], 1)

                def step(i, k):
                    pool.wait_ge(m_in[k], 16 * i + 16)
                    pool.wait_ge(S["wm_free"], NB * i + k + 1)
                    pool.tensor_tensor(out=Wm[:, k % 2, :, :], in0=mask[:, k, :, :], in1=wq[:, :, :],
                                       op=ALU.mult).then_inc(S["wm_ready"], 1)

                in_fours(pool, step)

            @block.vector
            def _(dve):
                link = Chain(dve, S["own"], 3)
                dve.wait_ge(S["w_loaded"], 2 * 16)
                link(dve.tensor_scalar(out=wq[:, :, :], in0=wq[:, :, :], scalar1=2.0, scalar2=ROUND, op0=ALU.mult, op1=ALU.add))
                link(dve.tensor_scalar(out=wq[:, :, :], in0=wq[:, :, :], scalar1=ROUND, scalar2=1.0, op0=ALU.subtract, op1=ALU.min))
                for h in range(DH):
                    last = dve.scalar_tensor_tensor(out=wq[:, h, :], in0=wq[:, h, :], scalar=-1.0, in1=scale[:, :],
                                                    op0=ALU.max, op1=ALU.mult)
                last.then_inc(S["w_ready"], 1)
                dve.sem_inc(S["free"], NB)
                dve.sem_inc(S["wm_free"], 2)

                def step(i, k):
                    s = NB * i + k
                    dve.wait_ge(S["xt_ps"], s + 1)
                    dve.tensor_copy(xT[:, k % 2, :, :], PS[:, k % 2, 0:D].rearrange("p (h t) -> p h t", h=DH)).then_inc(S["xt_ready"], 1)
                    dve.wait_ge(S["y_ps"], s + 1)
                    dve.sem_inc(S["wm_free"], 1)
                    dve.sem_inc(S["free"], 1)

                in_fours(dve, step)

            @block.tensor
            def _(pe):
                def front(i, k):
                    pe.wait_ge(x_in[k], 16 * i + 16)
                    for h in range(DH):
                        last = pe.transpose(PS[:, k % 2, h * P:h * P + P], x[:, k, h * P:h * P + P], core.ident[:, :])
                    last.then_inc(S["xt_ps"], 1)

                def back(i, k):
                    s = NB * i + k
                    pe.wait_ge(S["xt_ready"], s + 1)
                    pe.wait_ge(S["wm_ready"], s + 1)
                    pe.wait_ge(S["y_read"], s + 1)
                    for h in range(DH):
                        last = pe.matmul(PS[:, 2 + k % 2, 0:D], xT[:, k % 2, h, :], Wm[:, k % 2, h, :],
                                         start=(h == 0), stop=(h == DH - 1))
                    last.then_inc(S["y_ps"], 1)

                def step(i, k):
                    front(i, k)
                    back(i, k)

                in_fours(pe, step)

            @block.scalar
            def _(act):
                act.sem_inc(S["y_read"], 2)

                for k in range(NB):
                    act.sem_inc(y_out[k], 16)

                def step(i, k):
                    s = NB * i + k
                    act.wait_ge(S["y_ps"], s + 1)
                    act.wait_ge(y_out[k], 16 * i + 16)
                    act.activation(y[:, k, :], PS[:, 2 + k % 2, 0:D], ACT.Copy).then_inc(S["y_read"], 1)
                    act.wait_ge(S["y_read"], s + 3)
                    act.dma_start(core.slots_y[bass.ds(s * P, P), :], y[:, k, :]).then_inc(y_out[k], 16)

                in_fours(act, step)
                for k in range(NB):
                    act.wait_ge(y_out[k], 16 * (SLOTS // NB) + 16)


def collect_top1(core, rows, slot_x, weight_x, Xc):
    nc, X = core.nc, core.X
    with core.stage("ct") as (sb, sem):
        fetched = [sem(f"fetched{k}") for k in range(4)]
        with nc.Block() as block:
            @block.gpsimd
            def _(pool):
                for t in range(NT):
                    pool.indirect_dma_start(out=rows[:, t, :], out_offset=None, in_=core.slots_y[:, :],
                                            in_offset=bass.IndirectOffsetOnAxis(ap=slot_x[:, t:t + 1], axis=0)).then_inc(fetched[t // 8], 16)

            @block.vector
            def _(dve):
                for k in range(4):
                    dve.wait_ge(fetched[k], 8 * 16)
                    with dve.Fori(8 * k, 8 * k + 8) as t:
                        dve.scalar_tensor_tensor(out=X[:, bass.ds(t, 1), :], in0=rows[:, bass.ds(t, 1), :],
                                                 scalar=weight_x[:, bass.ds(t, 1)], in1=Xc[:, bass.ds(t, 1), :],
                                                 op0=ALU.mult, op1=ALU.add)


def crossed_attention(core):
    nc, X, PS = core.nc, core.X, core.PS
    G4 = 4
    NG4 = HEADS // G4
    V1 = HD + 1
    statistics(core, "6", X, LN_EPS)
    with core.stage("ca") as (sb, sem):
        W = sb("W", [P, DH, 3 * D])
        bias = sb("bias", [P, 3, HEADS, HD])
        Wo = sb("Wo", [P, DH, D])
        bias_o = sb("bias_o", [P, D])
        mask = sb("mask", [P, G4, TL, B], BF16)
        xn = sb("xn", [P, 2, D])
        xT = sb("xT", [P, 2, DH, P])
        q = sb("q", [P, 2, 2, HEADS, PAD])
        v = sb("v", [P, 2, HEADS, V1])
        QT = sb("QT", [P, 2, 2, NG4, P])
        negm = sb("negm", [P, 2, G4])
        ex = sb("ex", [P, 2, G4, P])
        eT = sb("eT", [P, 2, G4, P])
        rz = sb("rz", [P, 2, HEADS])
        y = sb("y", [P, 2, D])
        yT = sb("yT", [P, 2, DH, P])
        S = {n: sem(n) for n in (
            "loaded padded scaled masked xn_ready biased xt_ps xt_ready qkv_ps qkv_ready qt_ps qt_a qt_d s_ps negm_ready "
            "exp_done et_ps et_ready o_ps y_ready yt_ps yt_ready out_ps added own own2 ownm").split()}

        with nc.Block() as block:
            @block.sync
            def _(sp):
                sp.dma_start(W[:, :, :], core.dram["w_qkvT"].rearrange("(h p) e -> p h e", p=P)).then_inc(S["loaded"], 16)
                sp.dma_start(bias[:, :, :, :], core.dram["b_qkv"].rearrange("p (a h d) -> p a h d", a=3, h=HEADS)).then_inc(S["loaded"], 16)
                sp.dma_start(Wo[:, :, :], core.dram["w_denseT"].rearrange("(h p) e -> p h e", p=P)).then_inc(S["loaded"], 16)
                sp.dma_start(bias_o[:, :], core.dram["b_dense"]).then_inc(S["loaded"], 16)

            @block.gpsimd
            def _(pool):
                pool.memset(q[:, :, :, :, :], 0.0).then_inc(S["padded"], 1)
                pool.memset(v[:, :, :, HD:V1], 1.0).then_inc(S["padded"], 1)
                link = Chain(pool, S["ownm"], 4)
                m = mask[:, :, :, :]
                link(pool.memset(m, 0.0))
                link(pool.affine_select(out=m, in_=m, compare_op=ALU.is_ge, fill=-1e4 * HD ** 0.5, base=0,
                                        pattern=[[0, G4], [-B, TL], [-1, B]], channel_multiplier=1))
                link(pool.affine_select(out=m, in_=m, compare_op=ALU.is_ge, fill=-1e30, base=B - 1,
                                        pattern=[[0, G4], [B, TL], [0, B]], channel_multiplier=-1))
                link(pool.affine_select(out=m, in_=m, compare_op=ALU.is_ge, fill=-1e30, base=0,
                                        pattern=[[0, G4], [-B, TL], [0, B]], channel_multiplier=1))
                pool.sem_inc(S["masked"], 1)
                pool.wait_ge(S["loaded"], 4 * 16)

                def step(t, u):
                    pool.wait_ge(S["xn_ready"], t + 1)
                    pool.tensor_tensor(out=X[:, bass.ds(t, 1), :], in0=X[:, bass.ds(t, 1), :], in1=bias_o[:, :],
                                       op=ALU.add).then_inc(S["biased"], 1)

                in_pairs(pool, NT, step)

            @block.tensor
            def _(pe):
                pe.wait_ge(S["loaded"], 4 * 16)
                pe.wait_ge(S["masked"], 1)

                def tokens(t, u):
                    pe.wait_ge(S["xn_ready"], t + 1)
                    for h in range(DH):
                        last = pe.transpose(PS[:, 0, h * P:h * P + P], xn[:, u, h * P:h * P + P], core.ident[:, :])
                    last.then_inc(S["xt_ps"], 1)

                def project(t, u):
                    pe.wait_ge(S["xt_ready"], t + 1)
                    for bank, at, n in ((1, 0, 2 * D), (2, 2 * D, D)):
                        for h in range(DH):
                            last = pe.matmul(PS[:, bank, 0:n], xT[:, u, h, :], W[:, h, at:at + n], start=(h == 0), stop=(h == DH - 1))
                    last.then_inc(S["qkv_ps"], 1)

                def heads(t, u):
                    pe.wait_ge(S["qkv_ready"], t + 1)
                    for a in range(2):
                        for c in range(NG4):
                            last = pe.transpose(PS[:, 1 + a, c * P:c * P + P], q[:, u, a, G4 * c:G4 * c + G4, :], core.ident[:, :])
                        last.then_inc(S["qt_ps"], 1)

                def scores(t, u, c):
                    w = c % 2
                    pe.wait_ge(S["exp_done"], NG4 * t + c + 1)
                    pe.matmul(PS[:, 3 + w, :], core.identb[:, :], mask[:, :, :, :], start=True, stop=False, skip_group_check=True)
                    r = slice(c * PAD, c * PAD + PAD)
                    for i in range(G4):
                        last = pe.matmul(PS[:, 3 + w, i * P:i * P + P], QT[r, u, 0, i, :], QT[r, u, 1, i, :],
                                         start=False, stop=(i == G4 - 1), skip_group_check=True)
                    last.then_inc(S["s_ps"], 1)

                def turn(t, u, c):
                    w = c % 2
                    pe.wait_ge(S["exp_done"], NG4 * t + c + 3)
                    pe.wait_ge(S["et_ready"], NG4 * t + c + 1)
                    for i in range(G4):
                        last = pe.transpose(PS[:, 5 + w, i * P:i * P + P], ex[:, w, i, :], core.ident[:, :])
                    last.then_inc(S["et_ps"], 1)

                def mix(t, u, c):
                    w = c % 2
                    pe.wait_ge(S["et_ready"], NG4 * t + c + 3)
                    if c == 0:
                        pe.wait_ge(S["added"], t + 1)
                    for i in range(G4):
                        h = G4 * i + c
                        last = pe.matmul(PS[:, 7, h * V1:h * V1 + V1], eT[:, w, i, :], v[:, u, h, :], start=True, stop=True)
                    if c == NG4 - 1:
                        last.then_inc(S["o_ps"], 1)

                def output(t, u):
                    pe.wait_ge(S["y_ready"], t + 2)
                    for h in range(DH):
                        last = pe.transpose(PS[:, 7, h * P:h * P + P], y[:, u, h * P:h * P + P], core.ident[:, :])
                    last.then_inc(S["yt_ps"], 1)
                    pe.wait_ge(S["yt_ready"], t + 1)
                    for h in range(DH):
                        last = pe.matmul(PS[:, 7, 0:D], yT[:, u, h, :], Wo[:, h, :], start=(h == 0), stop=(h == DH - 1))
                    last.then_inc(S["out_ps"], 1)

                def front(t, u):
                    tokens(t, u)
                    project(t, u)
                    heads(t, u)

                def body(t, u, more):
                    pe.wait_ge(S["qt_a"], t + 1)
                    pe.wait_ge(S["qt_d"], t + 1)
                    if more:
                        tokens(t + 1, 1 - u)
                    scores(t, u, 0)
                    scores(t, u, 1)
                    if more:
                        project(t + 1, 1 - u)
                    turn(t, u, 0)
                    scores(t, u, 2)
                    mix(t, u, 0)
                    if more:
                        heads(t + 1, 1 - u)
                    turn(t, u, 1)
                    scores(t, u, 3)
                    mix(t, u, 1)
                    for c in (2, 3):
                        turn(t, u, c)
                        mix(t, u, c)
                    output(t, u)

                ahead(pe, NT, front, body)

            @block.scalar
            def _(act):
                act.sem_inc(S["exp_done"], 2)

                def tokens(t, u):
                    act.wait_ge(S["xt_ps"], t + 1)
                    act.activation(xT[:, u, :, :], PS[:, 0, 0:D].rearrange("p (h t) -> p h t", h=DH),
                                   ACT.Copy).then_inc(S["xt_ready"], 1)

                def heads(t, u):
                    act.wait_ge(S["qt_ps"], 2 * t + 1)
                    act.activation(QT[:, u, 0, :, :], PS[:, 1, :].rearrange("p (c t) -> p c t", c=NG4),
                                   ACT.Copy).then_inc(S["qt_a"], 1)

                def exps(t, c):
                    w = c % 2
                    act.wait_ge(S["negm_ready"], NG4 * t + c + 1)
                    for i in range(G4):
                        last = act.activation(ex[:, w, i, :], PS[:, 3 + w, i * P:i * P + P], ACT.Exp,
                                              bias=negm[:, w, i:i + 1], scale=HD ** -0.5)
                    last.then_inc(S["exp_done"], 1)

                def front(t, u):
                    tokens(t, u)
                    heads(t, u)

                def body(t, u, more):
                    if more:
                        tokens(t + 1, 1 - u)
                    exps(t, 0)
                    exps(t, 1)
                    exps(t, 2)
                    if more:
                        heads(t + 1, 1 - u)
                    exps(t, 3)
                    act.wait_ge(S["yt_ps"], t + 1)
                    act.activation(yT[:, u, :, :], PS[:, 7, 0:D].rearrange("p (h t) -> p h t", h=DH),
                                   ACT.Copy).then_inc(S["yt_ready"], 1)

                ahead(act, NT, front, body)

            @block.vector
            def _(dve):
                link, link2 = Chain(dve, S["own"], NG4), Chain(dve, S["own2"], 1)
                dve.sem_inc(S["added"], 1)
                dve.sem_inc(S["et_ready"], 2)
                dve.sem_inc(S["y_ready"], 1)
                dve.wait_ge(S["loaded"], 4 * 16)
                dve.wait_ge(S["padded"], 2)

                def tokens(t, u):
                    dve.tensor_scalar(out=xn[:, u, :], in0=X[:, bass.ds(t, 1), :], scalar1=core.mean[:, bass.ds(t, 1)],
                                      scalar2=core.rstd[:, bass.ds(t, 1)], op0=ALU.subtract,
                                      op1=ALU.mult).then_inc(S["xn_ready"], 1)

                def project(t, u):
                    dve.wait_ge(S["qkv_ps"], t + 1)
                    dve.tensor_tensor(out=q[:, u, :, :, 0:HD],
                                      in0=PS[:, 1, :].rearrange("p (a h d) -> p a h d", a=2, h=HEADS),
                                      in1=bias[:, 0:2, :, :], op=ALU.add)
                    dve.tensor_tensor(out=v[:, u, :, 0:HD], in0=PS[:, 2, 0:D].rearrange("p (h d) -> p h d", h=HEADS),
                                      in1=bias[:, 2, :, :], op=ALU.add).then_inc(S["qkv_ready"], 1)

                def heads(t, u):
                    dve.wait_ge(S["qt_ps"], 2 * t + 2)
                    dve.tensor_copy(QT[:, u, 1, :, :], PS[:, 2, :].rearrange("p (c t) -> p c t", c=NG4)).then_inc(S["qt_d"], 1)

                def front(t, u):
                    tokens(t, u)
                    project(t, u)
                    heads(t, u)

                def maxima(t, c):
                    w = c % 2
                    dve.wait_ge(S["s_ps"], NG4 * t + c + 1)
                    link(dve.tensor_reduce(out=negm[:, w, :], in_=PS[:, 3 + w, :].rearrange("p (i t) -> p i t", i=G4),
                                           axis=AX.X, op=ALU.max, negate=True))
                    dve.tensor_scalar(out=negm[:, w, :], in0=negm[:, w, :], scalar1=HD ** -0.5, scalar2=None,
                                      op0=ALU.mult).then_inc(S["negm_ready"], 1)

                def turned(t, c):
                    w = c % 2
                    dve.wait_ge(S["et_ps"], NG4 * t + c + 1)
                    dve.tensor_copy(eT[:, w, :, :], PS[:, 5 + w, :].rearrange("p (i t) -> p i t", i=G4)).then_inc(S["et_ready"], 1)

                def body(t, u, more):
                    if more:
                        tokens(t + 1, 1 - u)
                    link.start(t)
                    maxima(t, 0)
                    maxima(t, 1)
                    if more:
                        project(t + 1, 1 - u)
                    turned(t, 0)
                    maxima(t, 2)
                    if more:
                        heads(t + 1, 1 - u)
                    turned(t, 1)
                    maxima(t, 3)
                    turned(t, 2)
                    turned(t, 3)
                    o = PS[:, 7, 0:HEADS * V1].rearrange("p (h d) -> p h d", h=HEADS)
                    dve.wait_ge(S["o_ps"], t + 1)
                    link2.start(t)
                    link2(dve.reciprocal(out=rz[:, u, :], in_=o[:, :, HD]))
                    dve.tensor_tensor(out=y[:, u, :].rearrange("p (h d) -> p h d", h=HEADS), in0=o[:, :, 0:HD],
                                      in1=rz[:, u, :].rearrange("p (h d) -> p h d", d=1).broadcast_to([P, HEADS, HD]),
                                      op=ALU.mult).then_inc(S["y_ready"], 1)
                    dve.wait_ge(S["out_ps"], t + 1)
                    dve.wait_ge(S["biased"], t + 1)
                    dve.tensor_tensor(out=X[:, bass.ds(t, 1), :], in0=X[:, bass.ds(t, 1), :], in1=PS[:, 7, 0:D],
                                      op=ALU.add).then_inc(S["added"], 1)

                ahead(dve, NT, front, body)


E4 = 16
TOP = 4
INTER = 176
SHARED = 352
CAP = P


def routed_experts(core):
    nc = core.nc
    statistics(core, "7", core.X, LN_EPS)
    with ExitStack() as keep:
        def sb(tag, shape, dt=F32):
            return keep.enter_context(nc.sbuf_tensor("re_" + tag, shape, dt))

        R = sb("R", [P, DH, E4])
        logits = sb("logits", [P, NT, E4])
        place = sb("place", [P, E4], I32)
        weight = sb("weight", [P, E4])
        shared_expert(core, R, logits)
        route_top4(core, logits, place, weight)
        run_experts(core, place, weight)


def shared_expert(core, R, logits):
    size = blocks(SHARED)
    M = len(size)

    def prepare(sb, sem, Wg, Wu, Wd, w_ready):
        zero = sb("zero", [P, D])
        loaded, zeroed = sem("loaded"), sem("zeroed")

        def load(sp):
            full = (M - 1) * P
            for w, name in ((Wg, "sw_gate"), (Wu, "sw_up")):
                sp.dma_start(w[:, :, :], core.dram[name].rearrange("(h p) e -> p h e", p=P)).then_inc(loaded, 16)
            sp.dma_start(Wd[:, 0:M - 1, :], core.dram["sw_down"][0:full, :].rearrange("(m p) e -> p m e", p=P)).then_inc(loaded, 16)
            sp.dma_start(Wd[0:size[-1], M - 1, :], core.dram["sw_down"][full:SHARED, :]).then_inc(loaded, 16)
            sp.dma_start(R[:, :, :], core.dram["gateT"].rearrange("(h p) e -> p h e", p=P)).then_inc(loaded, 16)
            sp.wait_ge(zeroed, 1)
            sp.dma_start(core.rows_x[N:N + P, :], zero[:, :]).then_inc(loaded, 16)
            sp.dma_start(core.rows_y[N:N + P, :], zero[:, :]).then_inc(loaded, 16)

        def make(dve):
            dve.memset(zero[:, :], 0.0).then_inc(zeroed, 1)
            dve.wait_ge(loaded, 7 * 16)
            dve.sem_inc(w_ready, 1)

        return load, make

    gated_ffn(core, "se", SHARED, prepare, {"W": R, "E": E4, "logits": logits, "rows": core.rows_x[0:N, :]})


def route_top4(core, logits, place, weight):
    nc, X, PS = core.nc, core.X, core.PS
    C = 6
    with core.stage("r4") as (sb, sem):
        iota_e = sb("iota_e", [P, NT, E4])
        iota_p = sb("iota_p", [P, P], BF16)
        row_i = sb("row_i", [P, 3], I32)
        row_f = sb("row_f", [P, 3])
        col_l = sb("col_l", [P, TL, B])
        col_s = sb("col_s", [P, TL, B])
        same_s = sb("same_s", [P, P])
        later_l = sb("later_l", [P, P])
        later_s = sb("later_s", [P, P])
        here = sb("here", [P, P], BF16)
        behind = sb("behind", [P, P], BF16)
        beyond = sb("beyond", [P, P], BF16)
        prob = sb("prob", [P, NT, E4])
        work = sb("work", [P, NT, E4])
        top = sb("top", [P, NT])
        best = sb("best", [P, NT, 8])
        index = sb("index", [P, NT, 8], U32)
        index_f = sb("index_f", [P, NT, 8])
        chosen = sb("chosen", [P, E4, NT])
        chosen_b = sb("chosen_b", [P, 3, E4, NT], BF16)
        reset = sb("reset", [P, E4, NT])
        upto = sb("upto", [P, E4, NT])
        rank = sb("rank", [P, E4, NT])
        rank_b = sb("rank_b", [P, NT, E4], BF16)
        wts = sb("wts", [P, NT, E4])
        rest = sb("rest", [P, NT, E4])
        tell = sb("tell", [P, NT, E4, C], BF16)
        tile_no = sb("tile_no", [P, NT, E4])
        part_no = sb("part_no", [P, NT, E4])
        hit = sb("hit", [P, 2, E4, P], BF16)
        zero = sb("zero", [P, P], BF16)
        told = sb("told", [P, E4, C])
        spare = sb("spare", [P, 4, E4])
        S = {n: sem(n) for n in "made shifted exp_done masks_ready chosen_ready rank_ps own tell_ready hit_ready hit_used told_ps x_stored".split()}
        with nc.Block() as block:
            @block.sync
            def _(sp):
                rows = core.rows_y[0:N, :].rearrange("(n p) d -> p n d", p=P)
                for k in range(4):
                    sp.dma_start(rows[:, 8 * k:8 * k + 8, :], X[:, 8 * k:8 * k + 8, :]).then_inc(S["x_stored"], 16)
                sp.wait_ge(S["x_stored"], 4 * 16)

            @block.gpsimd
            def _(pool):
                made = S["made"]
                loose = dict(allow_small_or_imprecise_dtypes=True)
                pool.iota(iota_e[:, :, :], [[0, NT], [1, E4]], base=0, channel_multiplier=0, **loose).then_inc(made, 1)
                pool.iota(iota_p[:, :], [[1, P]], base=0, channel_multiplier=0, **loose).then_inc(made, 1)
                pool.iota(row_i[:, :], [[0, 3]], base=0, channel_multiplier=1).then_inc(made, 1)
                pool.iota(col_l[:, :, :], [[1, TL], [0, B]], base=0, channel_multiplier=0, **loose).then_inc(made, 1)
                pool.iota(col_s[:, :, :], [[0, TL], [1, B]], base=0, channel_multiplier=0, **loose).then_inc(made, 1)
                pool.iota(tile_no[:, :, :], [[1, NT], [0, E4]], base=0, channel_multiplier=0, **loose).then_inc(made, 1)
                pool.iota(part_no[:, :, :], [[0, NT], [0, E4]], base=0, channel_multiplier=1, **loose).then_inc(made, 1)
                pool.memset(zero[:, :], 0.0).then_inc(made, 1)
                pool.memset(reset[:, :, :], 1.0).then_inc(made, 1)
                pool.wait_ge(made, 9)
                pool.memset(reset[:, :, 0:1], 0.0).then_inc(made, 1)

            @block.scalar
            def _(act):
                act.wait_ge(S["shifted"], 1)
                act.activation(prob[:, :, :], prob[:, :, :], ACT.Exp).then_inc(S["exp_done"], 1)

            @block.tensor
            def _(pe):
                pe.wait_ge(S["masks_ready"], 1)
                pe.wait_ge(S["chosen_ready"], 1)
                for k, m in enumerate((here, behind, beyond)):
                    last = pe.matmul(PS[:, 0, :], m[:, :], chosen_b[:, k, :, :], start=(k == 0), stop=(k == 2))
                last.then_inc(S["rank_ps"], 1)
                pe.wait_ge(S["tell_ready"], 1)
                pe.matmul(PS[:, 1, 0:E4 * C], zero[:, :], zero[:, 0:E4 * C], start=True, stop=False, skip_group_check=True)

                def step(t, u):
                    pe.wait_ge(S["hit_ready"], t + 1)
                    for e in range(E4):
                        last = pe.matmul(PS[:, 1, e * C:e * C + C], hit[:, u, e, :], tell[:, bass.ds(t, 1), e, :],
                                         start=False, stop=False, skip_group_check=True)
                    last.then_inc(S["hit_used"], 1)

                in_pairs(pe, NT, step)
                pe.matmul(PS[:, 1, 0:E4 * C], zero[:, :], zero[:, 0:E4 * C], start=False, stop=True,
                          skip_group_check=True).then_inc(S["told_ps"], 1)

            @block.vector
            def _(dve):
                link = Chain(dve, S["own"], 90)

                def over_e(a):
                    return a.rearrange("p (n e) -> p n e", e=1).broadcast_to([P, NT, E4])

                dve.wait_ge(S["made"], 10)
                link(dve.tensor_single_scalar(out=row_i[:, 1:2], in_=row_i[:, 0:1], scalar=4, op=ALU.arith_shift_right))
                link(dve.tensor_single_scalar(out=row_i[:, 2:3], in_=row_i[:, 0:1], scalar=B - 1, op=ALU.bitwise_and))
                link(dve.tensor_copy(row_f[:, :], row_i[:, :]))
                cl, cs = (c[:, :, :].rearrange("p l s -> p (l s)") for c in (col_l, col_s))
                link(dve.tensor_scalar(out=later_s[:, :], in0=cs, scalar1=row_f[:, 2:3], scalar2=None, op0=ALU.is_gt))
                link(dve.tensor_scalar(out=same_s[:, :], in0=cs, scalar1=row_f[:, 2:3], scalar2=None, op0=ALU.is_equal))
                link(dve.tensor_scalar(out=later_l[:, :], in0=cl, scalar1=row_f[:, 1:2], scalar2=None, op0=ALU.is_gt))
                link(dve.tensor_copy(beyond[:, :], later_s[:, :]))
                link(dve.tensor_tensor(out=behind[:, :], in0=later_s[:, :], in1=same_s[:, :], op=ALU.add))
                link(dve.tensor_tensor(out=later_l[:, :], in0=later_l[:, :], in1=same_s[:, :], op=ALU.mult))
                link(dve.tensor_tensor(out=here[:, :], in0=later_s[:, :], in1=later_l[:, :], op=ALU.add))
                dve.sem_inc(S["masks_ready"], 1)
                link(dve.tensor_reduce(out=top[:, :], in_=logits[:, :, :], axis=AX.X, op=ALU.max))
                link(dve.tensor_tensor(out=prob[:, :, :], in0=logits[:, :, :], in1=over_e(top[:, :]), op=ALU.subtract))
                dve.sem_inc(S["shifted"], 1)
                dve.wait_ge(S["exp_done"], 1)
                link(dve.tensor_reduce(out=top[:, :], in_=prob[:, :, :], axis=AX.X, op=ALU.add))
                link(dve.reciprocal(out=top[:, :], in_=top[:, :]))
                link(dve.tensor_tensor(out=prob[:, :, :], in0=prob[:, :, :], in1=over_e(top[:, :]), op=ALU.mult))
                for t in range(NT):
                    last = dve.max(out=best[:, t, :], in_=prob[:, t, :])
                link(last)
                for t in range(NT):
                    last = dve.max_index(out=index[:, t, :], in_max=best[:, t, :], in_values=prob[:, t, :])
                link(last)
                link(dve.tensor_copy(index_f[:, :, :], index[:, :, :]))
                c_view = chosen[:, :, :].rearrange("p e n -> p n e")
                link(dve.tensor_tensor(out=c_view, in0=iota_e[:, :, :], in1=over_e(index_f[:, :, 0]), op=ALU.is_equal))
                for k in range(1, TOP):
                    link(dve.tensor_tensor(out=work[:, :, :], in0=iota_e[:, :, :], in1=over_e(index_f[:, :, k]), op=ALU.is_equal))
                    link(dve.tensor_tensor(out=c_view, in0=c_view, in1=work[:, :, :], op=ALU.add))
                link(dve.tensor_reduce(out=top[:, :], in_=best[:, :, 0:TOP], axis=AX.X, op=ALU.add))
                link(dve.tensor_scalar(out=top[:, :], in0=top[:, :], scalar1=1e-20, scalar2=None, op0=ALU.add))
                link(dve.reciprocal(out=top[:, :], in_=top[:, :]))
                link(dve.tensor_tensor(out=wts[:, :, :], in0=prob[:, :, :], in1=over_e(top[:, :]), op=ALU.mult))
                flat = lambda a: a[:, :, :].rearrange("p e n -> p (e n)")
                link(dve.tensor_copy(chosen_b[:, 0, :, :], chosen[:, :, :]))
                link(dve.tensor_tensor_scan(out=flat(upto), data0=flat(reset), data1=flat(chosen), initial=0.0,
                                            op0=ALU.mult, op1=ALU.add))
                link(dve.tensor_tensor(out=chosen_b[:, 1, :, :], in0=upto[:, :, :], in1=chosen[:, :, :], op=ALU.subtract))
                total = upto[:, :, NT - 1:NT].broadcast_to([P, E4, NT])
                link(dve.tensor_tensor(out=chosen_b[:, 2, :, :], in0=total, in1=upto[:, :, :], op=ALU.subtract))
                dve.sem_inc(S["chosen_ready"], 1)
                dve.wait_ge(S["rank_ps"], 1)
                link(dve.tensor_scalar(out=rank[:, :, :], in0=PS[:, 0, :].rearrange("p (e n) -> p e n", e=E4),
                                       scalar1=float(CAP), scalar2=1.0, op0=ALU.min, op1=ALU.add))
                link(dve.tensor_tensor(out=rank[:, :, :], in0=rank[:, :, :], in1=chosen[:, :, :], op=ALU.mult))
                link(dve.tensor_scalar(out=rank_b[:, :, :], in0=rank[:, :, :].rearrange("p e n -> p n e"), scalar1=1.0,
                                       scalar2=None, op0=ALU.subtract))
                link(dve.tensor_copy(tell[:, :, :, 0], tile_no[:, :, :]))
                link(dve.tensor_copy(tell[:, :, :, 1], part_no[:, :, :]))
                link(dve.memset(tell[:, :, :, 2], 1.0))
                link(dve.tensor_copy(tell[:, :, :, 3], wts[:, :, :]))
                link(dve.tensor_tensor(out=rest[:, :, :], in0=wts[:, :, :], in1=tell[:, :, :, 3], op=ALU.subtract))
                link(dve.tensor_copy(tell[:, :, :, 4], rest[:, :, :]))
                link(dve.tensor_tensor(out=tell[:, :, :, 5], in0=rest[:, :, :], in1=tell[:, :, :, 4], op=ALU.subtract))
                dve.sem_inc(S["tell_ready"], 1)
                dve.sem_inc(S["hit_used"], 2)

                def step(t, u):
                    dve.wait_ge(S["hit_used"], t + 1)
                    dve.tensor_tensor(out=hit[:, u, :, :], in0=iota_p[:, :].rearrange("p (e c) -> p e c", e=1).broadcast_to([P, E4, P]),
                                      in1=rank_b[:, bass.ds(t, 1), :].rearrange("p n e -> p (n e)").rearrange("p (e c) -> p e c", c=1).broadcast_to([P, E4, P]),
                                      op=ALU.is_equal).then_inc(S["hit_ready"], 1)

                in_pairs(dve, NT, step)
                dve.wait_ge(S["told_ps"], 1)
                link(dve.tensor_copy(told[:, :, :], PS[:, 1, 0:E4 * C].rearrange("p (e c) -> p e c", e=E4)))
                link(dve.tensor_scalar(out=spare[:, 0, :], in0=told[:, :, 0], scalar1=float(P), scalar2=None, op0=ALU.mult))
                link(dve.tensor_tensor(out=spare[:, 0, :], in0=spare[:, 0, :], in1=told[:, :, 1], op=ALU.add))
                link(dve.tensor_scalar(out=spare[:, 1, :], in0=told[:, :, 2], scalar1=-1.0, scalar2=-1.0, op0=ALU.add, op1=ALU.mult))
                link(dve.tensor_scalar(out=spare[:, 2, :], in0=part_no[:, 0, :], scalar1=float(N), scalar2=None, op0=ALU.add))
                link(dve.tensor_tensor(out=spare[:, 1, :], in0=spare[:, 1, :], in1=spare[:, 2, :], op=ALU.mult))
                link(dve.tensor_tensor(out=place[:, :], in0=spare[:, 0, :], in1=spare[:, 1, :], op=ALU.add))
                link(dve.tensor_tensor(out=spare[:, 3, :], in0=told[:, :, 4], in1=told[:, :, 5], op=ALU.add))
                link(dve.tensor_tensor(out=weight[:, :], in0=told[:, :, 3], in1=spare[:, 3, :], op=ALU.add))


def run_experts(core, place, weight):
    nc, PS = core.nc, core.PS
    size = blocks(INTER)
    with core.stage("rx") as (sb, sem):
        xg = sb("xg", [P, 2, D])
        xT = sb("xT", [P, 2, DH, P])
        Wgu = sb("Wgu", [P, 2, DH, 2 * INTER])
        Wd = sb("Wd", [P, 2, 2, D])
        sg = sb("sg", [P, 2, INTER])
        mid = sb("mid", [P, 2, INTER])
        mT = sb("mT", [P, 2, 2, P])
        y = sb("y", [P, 2, D])
        S = {n: sem(n) for n in "w_used g_used xt_ps xt_ready gu_ps silu mid_ready mt_ps mt_ready y_ps y_ready y_free own added copied".split()}
        w_in = [sem(f"w_in{k}") for k in range(2)]
        x_in = [sem(f"x_in{k}") for k in range(2)]
        with nc.Block() as block:
            @block.sync
            def _(sp):
                with sp.Fori(0, E4 // 2) as i:
                    for u in range(2):
                        e = 2 * i + u
                        sp.wait_ge(S["w_used"], e + 1)
                        for k, name in enumerate(("w_gate", "w_up")):
                            sp.dma_start(Wgu[:, u, :, k * INTER:(k + 1) * INTER],
                                         core.dram[name][bass.ds(e, 1), :, :].rearrange("n (h p) i -> p (n h) i", p=P)).then_inc(w_in[u], 16)
                        down = core.dram["w_down"]
                        sp.dma_start(Wd[:, u, 0, :], down[bass.ds(e, 1), 0:P, :].rearrange("n p d -> (n p) d")).then_inc(w_in[u], 16)
                        sp.dma_start(Wd[0:size[1], u, 1, :], down[bass.ds(e, 1), P:INTER, :].rearrange("n p d -> (n p) d")).then_inc(w_in[u], 16)
                sp.wait_ge(S["added"], 16 * E4)
                out = core.dram["out"].rearrange("(s g l) d -> l g s d", s=B, l=TL)
                rows = core.rows_y[0:N, :].rearrange("(g l s) d -> l g s d", l=TL, s=B)
                for tl in range(TL):
                    sp.dma_start(out[tl], rows[tl]).then_inc(S["copied"], 16)
                sp.wait_ge(S["copied"], 16 * TL)

            @block.gpsimd
            def _(pool):
                def gather(e):
                    pool.wait_ge(S["g_used"], e + 1)
                    pool.indirect_dma_start(out=xg[:, e % 2, :], out_offset=None, in_=core.rows_x[:, :],
                                            in_offset=bass.IndirectOffsetOnAxis(ap=place[:, e:e + 1], axis=0)).then_inc(x_in[e % 2], 16)

                gather(0)
                gather(1)
                for e in range(E4):
                    if e + 2 < E4:
                        gather(e + 2)
                    pool.wait_ge(S["y_ready"], e + 1)
                    if e:
                        pool.wait_ge(S["added"], 16 * e)
                        pool.sem_inc(S["y_free"], 1)
                    pool.indirect_dma_start(out=core.rows_y[:, :], out_offset=bass.IndirectOffsetOnAxis(ap=place[:, e:e + 1], axis=0),
                                            in_=y[:, e % 2, :], in_offset=None, compute_op=ALU.add).then_inc(S["added"], 16)

            @block.tensor
            def _(pe):
                def front(e, u, i):
                    pe.wait_ge(x_in[u], 16 * i + 16)
                    for h in range(DH):
                        last = pe.transpose(PS[:, 0, h * P:h * P + P], xg[:, u, h * P:h * P + P], core.ident[:, :])
                    last.then_inc(S["xt_ps"], 1)
                    pe.wait_ge(S["xt_ready"], e + 1)
                    pe.wait_ge(w_in[u], 64 * i + 64)
                    for h in range(DH):
                        last = pe.matmul(PS[:, 1 + u, 0:2 * INTER], xT[:, u, h, :], Wgu[:, u, h, :], start=(h == 0), stop=(h == DH - 1))
                    last.then_inc(S["gu_ps"], 1)
                    pe.wait_ge(S["mid_ready"], e + 1)
                    for k in range(2):
                        last = pe.transpose(PS[0:size[k], 3, k * P:k * P + P], mid[:, u, k * P:k * P + size[k]], core.ident[:, :])
                    last.then_inc(S["mt_ps"], 1)
                    pe.wait_ge(S["mt_ready"], e + 1)
                    for k in range(2):
                        last = pe.matmul(PS[:, 4 + u, 0:D], mT[0:size[k], u, k, :], Wd[0:size[k], u, k, :], start=(k == 0), stop=(k == 1))
                    last.then_inc(S["y_ps"], 1)

                with pe.Fori(0, E4 // 2) as i:
                    for u in range(2):
                        front(2 * i + u, u, i)

            @block.scalar
            def _(act):
                act.sem_inc(S["w_used"], 2)
                act.sem_inc(S["g_used"], 2)
                act.sem_inc(S["y_free"], 2)
                link = Chain(act, S["own"], 1)

                def step(e, u):
                    act.wait_ge(S["xt_ps"], e + 1)
                    act.sem_inc(S["g_used"], 1)
                    act.activation(xT[:, u, :, :], PS[:, 0, 0:D].rearrange("p (h t) -> p h t", h=DH),
                                   ACT.Copy).then_inc(S["xt_ready"], 1)
                    act.wait_ge(S["gu_ps"], e + 1)
                    act.activation(sg[:, u, :], PS[:, 1 + u, 0:INTER], ACT.Silu).then_inc(S["silu"], 1)
                    act.wait_ge(S["mt_ps"], e + 1)
                    act.activation(mT[:, u, 0, :], PS[:, 3, 0:P], ACT.Copy)
                    act.activation(mT[0:size[1], u, 1, :], PS[0:size[1], 3, P:2 * P], ACT.Copy).then_inc(S["mt_ready"], 1)
                    act.wait_ge(S["y_ps"], e + 1)
                    act.sem_inc(S["w_used"], 1)
                    act.wait_ge(S["y_free"], e + 1)
                    act.activation(y[:, u, :], PS[:, 4 + u, 0:D], ACT.Copy, scale=weight[:, bass.ds(e, 1)]).then_inc(S["y_ready"], 1)

                in_pairs(act, E4, step)

            @block.vector
            def _(dve):
                def step(e, u):
                    dve.wait_ge(S["silu"], e + 1)
                    dve.tensor_tensor(out=mid[:, u, :], in0=sg[:, u, :], in1=PS[:, 1 + u, INTER:2 * INTER],
                                      op=ALU.mult).then_inc(S["mid_ready"], 1)

                in_pairs(dve, E4, step)


STAGES = [rwkv, ternary, latent_attention, quantised_ffn, double_attention, masked_experts, crossed_attention, routed_experts]


def program(nc, dram):
    with ExitStack() as stack:
        core = Core(nc, dram, stack)
        load_x(core)
        constants(core)
        for stage in STAGES:
            stage(core)


def load_x(core):
    with core.stage("load") as (sb, sem):
        loaded = sem("loaded")
        with core.nc.Block() as block:
            @block.sync
            def _(sp):
                x = core.dram["x"].rearrange("(n p) d -> p n d", p=P)
                for k in range(8):
                    sp.dma_start(core.X[:, 4 * k:4 * k + 4, :], x[:, 4 * k:4 * k + 4, :]).then_inc(loaded, 16)
                sp.wait_ge(loaded, 8 * 16)


def halves(v):
    return np.ascontiguousarray(np.asarray(v).reshape(DH, P).T)


def rows(v):
    v = np.asarray(v).reshape(1, -1)
    return np.ascontiguousarray(np.broadcast_to(v, (P, v.shape[1])))


def layouts(a):
    t = lambda n: np.ascontiguousarray(np.asarray(a[n]).T)
    d = {
        "x": np.asarray(a["L0_attn_x"]).reshape(N, D),
        "WkT": t("L0_attn_Wk"), "WvT": t("L0_attn_Wv"), "WrT": t("L0_attn_Wr"), "WoT": t("L0_attn_Wo"),
        "tm": np.stack([halves(a[f"L0_attn_tm_{c}"]) for c in "kvr"], 1),
        "time_decay": halves(a["L0_attn_time_decay"]), "time_first": halves(a["L0_attn_time_first"]),
        "ln_g": rows(a["L0_attn_ln_g"]), "ln_b": rows(a["L0_attn_ln_b"]),
    }
    half = lambda w: np.concatenate([w[..., 0::2], w[..., 1::2]], -1)
    wqb = np.asarray(a["L1_attn_Wqb"]).reshape(QL, HEADS, NOPE + ROPE)
    wkvb = np.asarray(a["L1_attn_Wkvb"]).reshape(KL, HEADS, NOPE + VDIM)
    wkva = np.asarray(a["L1_attn_Wkva"])
    angle = (np.arange(T, dtype=np.float32)[:, None]
             * (1.0 / 10000.0 ** (np.arange(0, ROPE, 2, dtype=np.float32) / ROPE)).astype(np.float32)[None, :])
    cos, sin = np.cos(angle).astype(np.float32), np.sin(angle).astype(np.float32)
    d.update({
        "WtT": t("L0_ffn_weight"), "t_bias": rows(a["L0_ffn_bias"]),
        "Wqb_nopeT": wqb[:, :, :NOPE].transpose(2, 1, 0), "Wqb_rope": half(wqb[:, :, NOPE:]),
        "Wkvb_kT": wkvb[:, :, :NOPE].transpose(2, 1, 0), "Wkvb_vT": wkvb[:, :, NOPE:].transpose(2, 1, 0),
        "Wo_heads": np.asarray(a["L1_attn_Wo"]).reshape(HEADS, VDIM, D).transpose(1, 0, 2),
        "q_ln_w": np.asarray(a["L1_attn_q_ln_w"]).reshape(QL, 1), "kv_ln_w": rows(a["L1_attn_kv_ln_w"]),
        "Wa": np.concatenate([np.asarray(a["L1_attn_Wqa"]), wkva[:, :KL], half(wkva[:, KL:])], 1),
        "cos": np.concatenate([cos, cos], 1), "sin": np.concatenate([-sin, sin], 1),
        "wq_gateT": t("L1_ffn_wq_gate"), "wq_upT": t("L1_ffn_wq_up"), "wq_downT": t("L1_ffn_wq_down"),
        "s_gate": rows(a["L1_ffn_s_gate"]), "s_up": rows(a["L1_ffn_s_up"]), "s_down": rows(a["L1_ffn_s_down"]),
    })
    d.update({
        "W2T": t("L2_attn_W"), "W2": np.asarray(a["L2_attn_W"]),
        "g2": np.concatenate([rows(np.tile(np.asarray(a[f"L2_attn_g{n}"]), HEADS)) for n in (1, 2, 3)], 1),
    })
    d.update({
        "router": t("L2_ffn_router_w"), "W3T": t("L2_ffn_weight"), "scale": rows(a["L2_ffn_scale"]),
        "masks": np.asarray(a["L2_ffn_expert_masks"]).transpose(0, 2, 1),
    })
    w = np.asarray(a["L3_attn_w_qkv"]).reshape(HEADS, 3, HD, D).transpose(3, 1, 0, 2).reshape(D, 3 * D)
    b = np.asarray(a["L3_attn_b_qkv"]).reshape(HEADS, 3, HD).transpose(1, 0, 2).reshape(-1)
    d.update({
        "w_qkvT": w, "b_qkv": rows(b), "w_denseT": t("L3_attn_w_dense"), "b_dense": rows(a["L3_attn_b_dense"]),
        "gateT": t("L3_ffn_gate_w"),
        **{n: np.asarray(a["L3_ffn_" + n]) for n in ("w_gate", "w_up", "w_down", "sw_gate", "sw_up", "sw_down")},
    })
    return d


def kernel(**inputs):
    import concourse.bacc as bacc
    from concourse.bass_utils import run_bass_kernel_spmd

    nc = bacc.Bacc("TRN2", target_bir_lowering=False, num_devices=1)
    arrays, dram = {}, {}
    for name, a in layouts(inputs).items():
        a = np.ascontiguousarray(a)
        arrays[f"in_{name}_dram"] = a
        dram[name] = nc.dram_tensor(f"in_{name}_dram", a.shape, mybir.dt.from_np(a.dtype), kind="ExternalInput").ap()
    dram["out"] = nc.dram_tensor("out_0_dram", (N, D), F32, kind="ExternalOutput").ap()
    program(nc, dram)
    r = run_bass_kernel_spmd(nc, [arrays], core_ids=[0])
    return r.results[0]["out_0_dram"].reshape(B, T, D)
```

```python
import numpy as np
import concourse.bass as bass
from concourse import mybir
from contextlib import ExitStack, contextmanager

F32 = mybir.dt.float32
BF16 = mybir.dt.bfloat16
I32 = mybir.dt.int32
U32 = mybir.dt.uint32
ALU = mybir.AluOpType
ACT = mybir.ActivationFunctionType
AX = mybir.AxisListType

P = 128
D = 256
DH = D // P
B, T = 16, 256
N = B * T
NT = N // P
TPB = T // P
LN_EPS = 1e-5


class Chain:

    def __init__(self, eng, sem, per):
        self.eng, self.sem, self.per, self.base, self.n = eng, sem, per, 0, 0

    def start(self, t, at=0):
        self.base, self.n = t * self.per + at, 0

    def __call__(self, instruction):
        self.n += 1
        instruction.then_inc(self.sem, 1)
        self.eng.wait_ge(self.sem, self.base + self.n)


def in_pairs(eng, n, step):
    with eng.Fori(0, n // 2) as i:
        step(2 * i, 0)
        step(2 * i + 1, 1)


def skewed(eng, n, front, back):
    front(0, 0)
    with eng.Fori(0, n // 2 - 1) as i:
        front(2 * i + 1, 1)
        back(2 * i, 0)
        front(2 * i + 2, 0)
        back(2 * i + 1, 1)
    front(n - 1, 1)
    back(n - 2, 0)
    back(n - 1, 1)


class Core:

    def __init__(self, nc, dram, stack):
        self.nc, self.dram = nc, dram
        self.X = stack.enter_context(nc.sbuf_tensor("X", [P, NT, D], F32))
        self.ident = stack.enter_context(nc.sbuf_tensor("ident", [P, P], F32))
        self.identb = stack.enter_context(nc.sbuf_tensor("identb", [P, P], BF16))
        self.half = stack.enter_context(nc.sbuf_tensor("minus_half", [P, 64], F32))
        self.stats = stack.enter_context(nc.sbuf_tensor("bn_stats", [P, NT, 6], F32))
        self.mean = stack.enter_context(nc.sbuf_tensor("mean", [P, NT], F32))
        self.rstd = stack.enter_context(nc.sbuf_tensor("rstd", [P, NT], F32))
        self.tmp = stack.enter_context(nc.sbuf_tensor("stat_tmp", [P, 3, NT], F32))
        self.slots_x = nc.dram_tensor("slots_x", (SLOTS * P, D), F32, kind="Internal").ap()
        self.slots_y = nc.dram_tensor("slots_y", (SLOTS * P, D), F32, kind="Internal").ap()
        self.scratch_x = nc.dram_tensor("scratch_x", (N, D), F32, kind="Internal").ap()
        self.scratch_t = nc.dram_tensor("scratch_t", (N, 2), F32, kind="Internal").ap()
        self.rows_x = nc.dram_tensor("rows_x", (N + P, D), F32, kind="Internal").ap()
        self.rows_y = nc.dram_tensor("rows_y", (N + P, D), F32, kind="Internal").ap()
        self.PS = stack.enter_context(nc.psum_tensor("banks", [P, 8, 512], F32))

    @contextmanager
    def stage(self, name):
        nc, sems = self.nc, []
        with ExitStack() as stack:
            def sb(tag, shape, dt=F32):
                return stack.enter_context(nc.sbuf_tensor(f"{name}_{tag}", shape, dt))

            def sem(tag):
                sems.append(stack.enter_context(nc.semaphore(f"{name}_{tag}")))
                return sems[-1]

            yield sb, sem
            with nc.Block() as block:
                @block.gpsimd
                def _(pool):
                    for s in sems:
                        pool.sem_clear(s)


def constants(core):
    nc = core.nc
    with core.stage("const") as (sb, sem):
        zeroed = sem("zeroed")
        with nc.Block() as block:
            @block.gpsimd
            def _(pool):
                pool.memset(core.ident[:, :], 0.0).then_inc(zeroed, 1)
                pool.memset(core.identb[:, :], 0.0).then_inc(zeroed, 1)
                pool.memset(core.half[:, :], -0.5)
                pool.wait_ge(zeroed, 2)
                for m in (core.ident, core.identb):
                    pool.affine_select(out=m[:, :], in_=m[:, :], compare_op=ALU.not_equal, fill=1.0, base=0,
                                       pattern=[[-1, P]], channel_multiplier=1)


def tile_statistics(core, dve, source, t, n=1):
    for k in range(n):
        last = dve.bn_stats(out=core.stats[:, bass.ds(t + k, 1), :], in_=source[:, bass.ds(t + k, 1), :])
    return last


class Moments:

    def __init__(self, core, sem):
        self.core = core
        self.own, self.var_ready, self.rstd_done = sem("m_own"), sem("m_var"), sem("m_rstd")

    def dve(self, dve):
        core = self.core
        t0, t1, t2 = core.tmp[:, 0, :], core.tmp[:, 1, :], core.tmp[:, 2, :]
        link = Chain(dve, self.own, 6)
        me, ve, mo, vo = (core.stats[:, :, k] for k in (1, 2, 4, 5))
        dve.tensor_tensor(out=t2, in0=ve, in1=vo, op=ALU.add)
        link(dve.tensor_tensor(out=t0, in0=me, in1=mo, op=ALU.subtract))
        link(dve.tensor_tensor(out=t1, in0=t0, in1=t0, op=ALU.mult))
        link(dve.scalar_tensor_tensor(out=t1, in0=t1, scalar=D / 4.0, in1=t2, op0=ALU.mult, op1=ALU.add))
        dve.tensor_scalar(out=t1, in0=t1, scalar1=1.0 / D, scalar2=LN_EPS, op0=ALU.mult, op1=ALU.add).then_inc(self.var_ready, 1)
        link(dve.tensor_tensor(out=t0, in0=me, in1=mo, op=ALU.add))
        link(dve.tensor_scalar(out=core.mean[:, :], in0=t0, scalar1=0.5, scalar2=None, op0=ALU.mult))
        dve.wait_ge(self.rstd_done, 1)

    def pool(self, pool):
        pool.wait_ge(self.var_ready, 1)
        pool.tensor_tensor(out=self.core.rstd[:, :], in0=self.core.tmp[:, 1, :], in1=self.core.half[:, 0:NT],
                           op=ALU.pow).then_inc(self.rstd_done, 1)


def rwkv(core):
    nc, X, PS = core.nc, core.X, core.PS
    with ExitStack() as keep:
        gate = keep.enter_context(nc.sbuf_tensor("rw_gate", [P, NT, D], F32))
        wkv = keep.enter_context(nc.sbuf_tensor("rw_wkv", [P, NT, D], F32))
        rwkv_recurrence(core, gate, wkv)
        rwkv_output(core, gate, wkv)


def rwkv_recurrence(core, gate, wkv):
    nc, X, PS = core.nc, core.X, core.PS
    START = -1e38
    with core.stage("rw") as (sb, sem):
        W = sb("W", [P, 3, DH, D])
        WA = sb("WA", [P, 3, DH, D])
        WB = sb("WB", [P, 3, DH, D])
        tm = sb("tm", [P, 3, DH])
        decay = sb("decay", [P, DH])
        first = sb("first", [P, DH])
        negdecay = sb("negdecay", [P, DH, T])
        xn = sb("xn", [P, 2, TPB, D])
        xnT = sb("xnT", [P, 2, DH, T + 1])
        pp = sb("pp", [P, 2, DH, T + 1])
        q = sb("q", [P, 2, DH, T])
        ex = sb("ex", [P, 2, 4, DH, T])
        f2v = sb("f2v", [P, DH, T])
        e2v = sb("e2v", [P, 2, DH, T])
        ab = sb("ab", [P, 2, 2, DH, T + 1])
        nd = sb("nd", [P, 2, 2, DH, T])
        rec = sb("rec", [P, DH, T])
        out = sb("out", [P, 2, DH, T])

        loaded, zeroed, edges, clamped = sem("loaded"), sem("zeroed"), sem("edges"), sem("clamped")
        exp_ready, weights_ready, xn_ready, xn_free = sem("expd"), sem("weights"), sem("xn_ready"), sem("xn_free")
        xt_ps, xt_ready, kvr_ready, r_free, kv_free = sem("xt_ps"), sem("xt_ready"), sem("kvr"), sem("r_free"), sem("kv_free")
        pp_ready, q_ready, args_dve, args_pool = sem("pp_ready"), sem("q_ready"), sem("args_d"), sem("args_p")
        exps_ready, scans_ready, e2v_ready, nd_ready = sem("exps"), sem("scans"), sem("e2v_ready"), sem("nd_ready")
        out_ready, out_free, w_ps, w_free = sem("out_ready"), sem("out_free"), sem("w_ps"), sem("w_free")
        own_prep, own_front, own_scans, own_finish, own_pool = (sem(f"own{k}") for k in range(5))

        moments = Moments(core, sem)
        with nc.Block() as block:
            @block.sync
            def _(sp):
                for n, name in enumerate(("WkT", "WvT", "WrT")):
                    sp.dma_start(W[:, n, :, :], core.dram[name].rearrange("(h p) e -> p h e", p=P)).then_inc(loaded, 16)
                sp.dma_start(tm[:, :, :], core.dram["tm"]).then_inc(loaded, 16)
                sp.dma_start(decay[:, :], core.dram["time_decay"]).then_inc(loaded, 16)
                sp.dma_start(first[:, :], core.dram["time_first"]).then_inc(loaded, 16)

            @block.tensor
            def _(pe):
                def front(b, u):
                    pe.wait_ge(xn_ready, b + 1)
                    for h in range(DH):
                        for k in range(TPB):
                            last = pe.transpose(PS[:, 0, h * T + k * P:h * T + k * P + P],
                                                xn[:, u, k, h * P:h * P + P], core.ident[:, :])
                    last.then_inc(xt_ps, 1)
                    pe.wait_ge(xt_ready, b + 1)
                    pe.wait_ge(kv_free, b + 1)
                    pe.wait_ge(r_free, b + 1)
                    for n in range(2):
                        for e in range(DH):
                            for j in range(4):
                                w, h = (WA, WB)[j % 2], j // 2
                                pe.matmul(PS[:, 2 + 2 * n + u, e * T:e * T + T], w[:, n, h, e * P:e * P + P],
                                          xnT[:, u, h, 1 - j % 2:1 - j % 2 + T], start=(j == 0), stop=(j == 3))
                    for k in range(TPB):
                        for j in range(4):
                            w, h = (WA, WB)[j % 2], j // 2
                            at = 1 - j % 2 + k * P
                            last = pe.matmul(PS[:, 6 + u, k * D:k * D + D], xnT[:, u, h, at:at + P], w[:, 2, h, :],
                                             start=(j == 0), stop=(j == 3))
                    last.then_inc(kvr_ready, 1)

                def back(b, u):
                    pe.wait_ge(out_ready, b + 1)
                    pe.wait_ge(w_free, b + 1)
                    for k in range(TPB):
                        for h in range(DH):
                            last = pe.transpose(PS[:, 1, k * D + h * P:k * D + h * P + P],
                                                out[:, u, h, k * P:k * P + P], core.ident[:, :])
                    last.then_inc(w_ps, 1)

                pe.wait_ge(weights_ready, 1)
                front(0, 0)
                front(1, 1)
                with pe.Fori(1, B // 2) as i:
                    for u in range(2):
                        front(2 * i + u, u)
                        back(2 * i + u - 2, u)
                back(B - 2, 0)
                back(B - 1, 1)

            @block.scalar
            def _(act):
                act.wait_ge(zeroed, 1)
                act.wait_ge(clamped, 1)
                act.activation(decay[:, :], decay[:, :], ACT.Exp).then_inc(exp_ready, 1)
                act.sem_inc(r_free, 2)
                act.sem_inc(w_free, 1)

                def tokens(b, u):
                    act.wait_ge(xt_ps, b + 1)
                    act.sem_inc(xn_free, 1)
                    act.activation(xnT[:, u, :, 1:T + 1], PS[:, 0, :].rearrange("p (h t) -> p h t", h=DH),
                                   ACT.Copy).then_inc(xt_ready, 1)

                def gates(b, u):
                    act.wait_ge(kvr_ready, b + 1)
                    act.activation(gate[:, bass.ds(TPB * b, TPB), :], PS[:, 6 + u, :].rearrange("p (k d) -> p k d", k=TPB),
                                   ACT.Tanh, scale=0.5).then_inc(r_free, 1)

                def exps(b, u):
                    act.wait_ge(args_dve, b + 1)
                    act.wait_ge(args_pool, b + 1)
                    act.activation(ex[:, u, :, :, :], ex[:, u, :, :, :], ACT.Exp).then_inc(exps_ready, 1)

                def back(b, u):
                    act.wait_ge(w_ps, b + 1)
                    act.sem_inc(out_free, 1)
                    act.activation(wkv[:, bass.ds(TPB * b, TPB), :], PS[:, 1, :].rearrange("p (k d) -> p k d", k=TPB),
                                   ACT.Copy).then_inc(w_free, 1)

                def step(b, u, behind, more):
                    gates(b, u)
                    if behind:
                        back(b - 2, u)
                    if more:
                        tokens(b + 1, 1 - u)
                    exps(b, u)

                tokens(0, 0)
                step(0, 0, False, True)
                step(1, 1, False, True)
                with act.Fori(1, B // 2 - 1) as i:
                    for u in range(2):
                        step(2 * i + u, u, True, True)
                step(B - 2, 0, True, True)
                step(B - 1, 1, True, False)
                back(B - 2, 0)
                back(B - 1, 1)

            @block.gpsimd
            def _(pool):
                moments.pool(pool)
                pool.memset(xnT[:, :, :, 0:1], 0.0).then_inc(zeroed, 1)
                pool.memset(pp[:, :, :, 0:1], START).then_inc(edges, 1)
                pool.memset(ab[:, :, :, :, 0:1], 0.0).then_inc(edges, 1)
                pool.wait_ge(edges, 2)
                link = Chain(pool, own_pool, 4)

                def step(b, u):
                    pool.wait_ge(pp_ready, b + 1)
                    pool.tensor_tensor(out=ex[:, u, 0, :, :], in0=pp[:, u, :, 0:T], in1=pp[:, u, :, 1:T + 1],
                                       op=ALU.subtract)
                    pool.wait_ge(q_ready, b + 1)
                    pool.tensor_tensor(out=ex[:, u, 2, :, :], in0=pp[:, u, :, 0:T], in1=q[:, u, :, :],
                                       op=ALU.subtract).then_inc(args_pool, 1)
                    pool.wait_ge(scans_ready, b + 1)
                    link.start(b)
                    for k in range(2):
                        link(pool.tensor_tensor(out=nd[:, u, k, :, :], in0=ab[:, u, k, :, 0:T], in1=ex[:, u, 2, :, :],
                                                op=ALU.mult))
                    pool.wait_ge(e2v_ready, b + 1)
                    link(pool.tensor_tensor(out=nd[:, u, 0, :, :], in0=nd[:, u, 0, :, :], in1=e2v[:, u, :, :],
                                            op=ALU.add))
                    link(pool.tensor_tensor(out=nd[:, u, 1, :, :], in0=nd[:, u, 1, :, :], in1=ex[:, u, 3, :, :],
                                            op=ALU.add))
                    pool.sem_inc(nd_ready, 1)

                in_pairs(pool, B, step)

            @block.vector
            def _(dve):
                moments.dve(dve)
                dve.sem_inc(kv_free, 2)
                dve.sem_inc(xn_free, 2)
                dve.sem_inc(out_free, 2)
                dve.wait_ge(loaded, 6 * 16)
                link = Chain(dve, own_prep, 9)
                dve.tensor_scalar(out=decay[:, :], in0=decay[:, :], scalar1=87.0, scalar2=None,
                                  op0=ALU.min).then_inc(clamped, 1)
                link(dve.memset(negdecay[:, :, :], 0.0))
                for n in range(3):
                    for h in range(DH):
                        link(dve.tensor_scalar(out=WA[:, n, h, :], in0=W[:, n, h, :], scalar1=tm[:, n, h:h + 1],
                                               scalar2=None, op0=ALU.mult))
                dve.tensor_tensor(out=WB[:, :, :, :], in0=W[:, :, :, :], in1=WA[:, :, :, :],
                                  op=ALU.subtract).then_inc(weights_ready, 1)
                dve.wait_ge(exp_ready, 1)
                for h in range(DH):
                    link(dve.tensor_scalar(out=negdecay[:, h, :], in0=negdecay[:, h, :], scalar1=decay[:, h:h + 1],
                                           scalar2=None, op0=ALU.subtract))
                dve.wait_ge(edges, 2)
                link_front, link_scans, link_finish = (Chain(dve, own_front, 4), Chain(dve, own_scans, 2),
                                                       Chain(dve, own_finish, 2))

                def normalise(b, u):
                    dve.wait_ge(xn_free, b + 1)
                    for k in range(TPB):
                        t = TPB * b + k
                        last = dve.tensor_scalar(out=xn[:, u, k, :], in0=X[:, bass.ds(t, 1), :],
                                                 scalar1=core.mean[:, bass.ds(t, 1)], scalar2=core.rstd[:, bass.ds(t, 1)],
                                                 op0=ALU.subtract, op1=ALU.mult)
                    last.then_inc(xn_ready, 1)

                def front(b, u):
                    kp = PS[:, 2 + u, :].rearrange("p (h t) -> p h t", h=DH)
                    link = link_front
                    link.start(b)
                    dve.wait_ge(kvr_ready, b + 1)
                    for h in range(DH):
                        link(dve.tensor_tensor_scan(out=pp[:, u, h, 1:T + 1], data0=negdecay[:, h, :],
                                                    data1=kp[:, h, :], initial=START, op0=ALU.add, op1=ALU.max))
                    dve.sem_inc(pp_ready, 1)
                    dve.tensor_tensor(out=ex[:, u, 1, :, :], in0=kp, in1=pp[:, u, :, 1:T + 1], op=ALU.subtract)
                    for h in range(DH):
                        link(dve.scalar_tensor_tensor(out=q[:, u, h, :], in0=kp[:, h, :], scalar=first[:, h:h + 1],
                                                      in1=pp[:, u, h, 0:T], op0=ALU.add, op1=ALU.max))
                    dve.sem_inc(q_ready, 1)
                    for h in range(DH):
                        last = dve.scalar_tensor_tensor(out=ex[:, u, 3, h, :], in0=kp[:, h, :],
                                                        scalar=first[:, h:h + 1], in1=q[:, u, h, :],
                                                        op0=ALU.add, op1=ALU.subtract)
                    last.then_inc(args_dve, 1)

                def scans(b, u):
                    vp = PS[:, 4 + u, :].rearrange("p (h t) -> p h t", h=DH)
                    link = link_scans
                    link.start(b)
                    dve.wait_ge(exps_ready, b + 1)
                    link(dve.tensor_tensor(out=f2v[:, :, :], in0=ex[:, u, 1, :, :], in1=vp, op=ALU.mult))
                    for h in range(DH):
                        dve.tensor_tensor_scan(out=ab[:, u, 0, h, 1:T + 1], data0=ex[:, u, 0, h, :],
                                               data1=f2v[:, h, :], initial=0.0, op0=ALU.mult, op1=ALU.add)
                        last = dve.tensor_tensor_scan(out=ab[:, u, 1, h, 1:T + 1], data0=ex[:, u, 0, h, :],
                                                      data1=ex[:, u, 1, h, :], initial=0.0, op0=ALU.mult, op1=ALU.add)
                    last.then_inc(scans_ready, 1)
                    link(dve.tensor_tensor(out=e2v[:, u, :, :], in0=ex[:, u, 3, :, :], in1=vp, op=ALU.mult))
                    dve.sem_inc(kv_free, 1)
                    dve.sem_inc(e2v_ready, 1)

                def finish(b, u):
                    link = link_finish
                    link.start(b)
                    dve.wait_ge(nd_ready, b + 1)
                    link(dve.reciprocal(out=rec[:, :, :], in_=nd[:, u, 1, :, :]))
                    dve.wait_ge(out_free, b + 1)
                    link(dve.tensor_tensor(out=out[:, u, :, :], in0=nd[:, u, 0, :, :], in1=rec[:, :, :], op=ALU.mult))
                    dve.sem_inc(out_ready, 1)

                normalise(0, 0)
                normalise(1, 1)
                front(0, 0)
                scans(0, 0)
                with dve.Fori(0, B // 2 - 1) as i:
                    for k in (1, 2):
                        b, u = 2 * i + k, k % 2
                        normalise(b + 1, 1 - u)
                        front(b, u)
                        finish(b - 1, 1 - u)
                        scans(b, u)
                front(B - 1, 1)
                finish(B - 2, 0)
                scans(B - 1, 1)
                finish(B - 1, 1)


def rwkv_output(core, gate, wkv):
    nc, X, PS = core.nc, core.X, core.PS
    with core.stage("ro") as (sb, sem):
        WoT = sb("WoT", [P, DH, D])
        g = sb("g", [P, D])
        c = sb("c", [P, D])
        n = sb("n", [P, 2, D])
        ng = sb("ng", [P, 2, D])
        rn = sb("rn", [P, 2, D])
        rT = sb("rT", [P, 2, DH, P])
        loaded, w_ready, n_ready, ng_ready, rn_ready = (sem(x) for x in ("loaded", "w_ready", "n_ready", "ng_ready", "rn_ready"))
        rt_ps, rt_ready, y_ps, added, own, stats_done = (
            sem(x) for x in ("rt_ps", "rt_ready", "y_ps", "added", "own", "stats_done"))
        moments = Moments(core, sem)
        with nc.Block() as block:
            @block.sync
            def _(sp):
                sp.dma_start(WoT[:, :, :], core.dram["WoT"].rearrange("(h p) e -> p h e", p=P)).then_inc(loaded, 16)
                sp.dma_start(g[:, :], core.dram["ln_g"]).then_inc(loaded, 16)
                sp.dma_start(c[:, :], core.dram["ln_b"]).then_inc(loaded, 16)

            @block.vector
            def _(dve):
                with dve.Fori(0, NT // 4) as i:
                    tile_statistics(core, dve, wkv, 4 * i, 4).then_inc(stats_done, 1)
                dve.wait_ge(stats_done, NT // 4)
                moments.dve(dve)
                dve.sem_inc(added, 2)
                dve.wait_ge(loaded, 3 * 16)
                dve.tensor_scalar(out=WoT[:, :, :], in0=WoT[:, :, :], scalar1=0.5, scalar2=None,
                                  op0=ALU.mult).then_inc(w_ready, 1)

                def normalise(t, u):
                    dve.tensor_scalar(out=n[:, u, :], in0=wkv[:, bass.ds(t, 1), :], scalar1=core.mean[:, bass.ds(t, 1)],
                                      scalar2=core.rstd[:, bass.ds(t, 1)], op0=ALU.subtract,
                                      op1=ALU.mult).then_inc(n_ready, 1)

                def gated(t, u):
                    dve.wait_ge(ng_ready, t + 1)
                    dve.scalar_tensor_tensor(out=rn[:, u, :], in0=gate[:, bass.ds(t, 1), :], scalar=1.0, in1=ng[:, u, :],
                                             op0=ALU.add, op1=ALU.mult).then_inc(rn_ready, 1)

                def add(t, u):
                    dve.wait_ge(y_ps, t + 1)
                    dve.tensor_tensor(out=X[:, bass.ds(t, 1), :], in0=X[:, bass.ds(t, 1), :], in1=PS[:, 2 + u, 0:D],
                                      op=ALU.add).then_inc(added, 1)
                    dve.wait_ge(added, t + 3)
                    tile_statistics(core, dve, X, t)

                def step(t, u):
                    normalise(t + 3, 1 - u)
                    dve.wait_ge(rt_ps, t + 1)
                    gated(t + 2, u)
                    add(t, u)

                normalise(0, 0)
                normalise(1, 1)
                gated(0, 0)
                normalise(2, 0)
                gated(1, 1)
                with dve.Fori(0, NT // 2 - 2) as i:
                    for k in range(2):
                        step(2 * i + k, k)
                step(NT - 4, 0)
                dve.wait_ge(rt_ps, NT - 2)
                gated(NT - 1, 1)
                add(NT - 3, 1)
                add(NT - 2, 0)
                add(NT - 1, 1)

            @block.gpsimd
            def _(pool):
                moments.pool(pool)
                pool.wait_ge(loaded, 3 * 16)
                link = Chain(pool, own, 1)

                def step(t, u):
                    pool.wait_ge(n_ready, t + 1)
                    link.start(t)
                    link(pool.tensor_tensor(out=ng[:, u, :], in0=n[:, u, :], in1=g[:, :], op=ALU.mult))
                    pool.tensor_tensor(out=ng[:, u, :], in0=ng[:, u, :], in1=c[:, :], op=ALU.add).then_inc(ng_ready, 1)

                in_pairs(pool, NT, step)

            @block.scalar
            def _(act):
                def step(t, u):
                    act.wait_ge(rt_ps, t + 1)
                    act.activation(rT[:, u, :, :], PS[:, u, 0:D].rearrange("p (h t) -> p h t", h=DH),
                                   ACT.Copy).then_inc(rt_ready, 1)

                in_pairs(act, NT, step)

            @block.tensor
            def _(pe):
                pe.wait_ge(w_ready, 1)

                def front(t, u):
                    pe.wait_ge(rn_ready, t + 1)
                    for h in range(DH):
                        last = pe.transpose(PS[:, u, h * P:h * P + P], rn[:, u, h * P:h * P + P], core.ident[:, :])
                    last.then_inc(rt_ps, 1)

                def back(t, u):
                    pe.wait_ge(rt_ready, t + 1)
                    pe.wait_ge(added, t + 1)
                    for h in range(DH):
                        last = pe.matmul(PS[:, 2 + u, 0:D], rT[:, u, h, :], WoT[:, h, :], start=(h == 0), stop=(h == DH - 1))
                    last.then_inc(y_ps, 1)

                skewed(pe, NT, front, back)


def ahead(eng, n, first, body):
    first(0, 0)
    with eng.Fori(0, n // 2 - 1) as i:
        body(2 * i, 0, True)
        body(2 * i + 1, 1, True)
    body(n - 2, 0, True)
    body(n - 1, 1, False)


def overlapped(eng, n, first, body, finish):
    first(0, 0)
    body(0, 0, False, True)
    with eng.Fori(0, n // 2 - 1) as i:
        body(2 * i + 1, 1, True, True)
        body(2 * i + 2, 0, True, True)
    body(n - 1, 1, True, False)
    finish(n - 1, 1)


def ternary_and_latent(core):
    with ExitStack() as keep:
        def sb(tag, shape, dt=F32):
            return keep.enter_context(core.nc.sbuf_tensor("la_" + tag, shape, dt))

        q1 = sb("q1", [QH, HEADS, QK])
        q2 = sb("q2", [QH, HEADS, QK])
        out = sb("out", [P, HEADS // 2, D])
        ternary(core, lambda sb, sem: latent_weights(core, sb, sem, q1, q2, out))
        latent_heads(core, q1, q2, out)


def ternary(core, beside):
    nc, X, PS = core.nc, core.X, core.PS
    ROUND = 1.5 * 2.0 ** 23
    with core.stage("te") as (sb, sem):
        W = sb("W", [P, DH, D])
        Wq = sb("Wq", [P, DH, D])
        ones = sb("ones", [P, P])
        part = sb("part", [P, 3])
        bias = sb("bias", [P, D])
        xn = sb("xn", [P, 2, D])
        xT = sb("xT", [P, 2, DH, P])
        loaded, ones_ready, part_ready, total_ps, w_ready = (sem(x) for x in ("loaded", "ones", "part", "total", "w_ready"))
        own, xn_ready, biased, xt_ps, xt_ready, y_ps, added = (
            sem(x) for x in ("own", "xn_ready", "biased", "xt_ps", "xt_ready", "y_ps", "added"))
        moments = Moments(core, sem)
        beside_sp, beside_pe, beside_dve, beside_act = beside(sb, sem)
        with nc.Block() as block:
            @block.sync
            def _(sp):
                sp.dma_start(W[:, :, :], core.dram["WtT"].rearrange("(h p) e -> p h e", p=P)).then_inc(loaded, 16)
                sp.dma_start(bias[:, :], core.dram["t_bias"]).then_inc(loaded, 16)
                beside_sp(sp)

            @block.gpsimd
            def _(pool):
                moments.pool(pool)
                pool.memset(ones[:, :], 1.0).then_inc(ones_ready, 1)
                pool.wait_ge(loaded, 2 * 16)

                def step(t, u):
                    pool.wait_ge(xn_ready, t + 1)
                    pool.tensor_tensor(out=X[:, bass.ds(t, 1), :], in0=X[:, bass.ds(t, 1), :], in1=bias[:, :],
                                       op=ALU.add).then_inc(biased, 1)

                in_pairs(pool, NT, step)

            @block.vector
            def _(dve):
                moments.dve(dve)
                link = Chain(dve, own, 8)
                dve.sem_inc(added, 2)
                dve.wait_ge(loaded, 2 * 16)
                dve.tensor_reduce(out=part[:, 0:1], in_=W[:, :, :], axis=AX.XY, op=ALU.add,
                                  apply_absolute_value=True).then_inc(part_ready, 1)
                dve.wait_ge(total_ps, 1)
                link(dve.tensor_scalar(out=part[:, 1:2], in0=PS[:, 7, 0:1], scalar1=1.0 / (D * D), scalar2=None, op0=ALU.mult))
                link(dve.tensor_scalar(out=part[:, 0:1], in0=part[:, 1:2], scalar1=1e-10, scalar2=None, op0=ALU.add))
                link(dve.reciprocal(out=part[:, 2:3], in_=part[:, 0:1]))
                link(dve.tensor_scalar(out=Wq[:, :, :], in0=W[:, :, :], scalar1=part[:, 2:3], scalar2=ROUND,
                                       op0=ALU.mult, op1=ALU.add))
                link(dve.tensor_scalar(out=Wq[:, :, :], in0=Wq[:, :, :], scalar1=ROUND, scalar2=1.0,
                                       op0=ALU.subtract, op1=ALU.min))
                link(dve.tensor_scalar(out=Wq[:, :, :], in0=Wq[:, :, :], scalar1=-1.0, scalar2=part[:, 1:2],
                                       op0=ALU.max, op1=ALU.mult))
                link(dve.tensor_tensor(out=Wq[:, :, :], in0=Wq[:, :, :], in1=W[:, :, :], op=ALU.subtract))
                link(dve.tensor_tensor(out=Wq[:, :, :], in0=Wq[:, :, :], in1=W[:, :, :], op=ALU.add))
                dve.sem_inc(w_ready, 1)

                def normalise(t, u):
                    dve.tensor_scalar(out=xn[:, u, :], in0=X[:, bass.ds(t, 1), :], scalar1=core.mean[:, bass.ds(t, 1)],
                                      scalar2=core.rstd[:, bass.ds(t, 1)], op0=ALU.subtract,
                                      op1=ALU.mult).then_inc(xn_ready, 1)

                def add(t, u):
                    dve.wait_ge(y_ps, t + 1)
                    dve.wait_ge(biased, t + 1)
                    dve.tensor_tensor(out=X[:, bass.ds(t, 1), :], in0=X[:, bass.ds(t, 1), :], in1=PS[:, 2 + u, 0:D],
                                      op=ALU.add).then_inc(added, 1)
                    dve.wait_ge(added, t + 3)
                    tile_statistics(core, dve, X, t)

                normalise(0, 0)
                normalise(1, 1)
                with dve.Fori(0, NT // 2 - 1) as i:
                    for k in range(2):
                        dve.wait_ge(xt_ps, 2 * i + k + 1)
                        normalise(2 * i + k + 2, k)
                        add(2 * i + k, k)
                add(NT - 2, 0)
                add(NT - 1, 1)
                beside_dve(dve)

            @block.scalar
            def _(act):
                def step(t, u):
                    act.wait_ge(xt_ps, t + 1)
                    act.activation(xT[:, u, :, :], PS[:, u, 0:D].rearrange("p (h t) -> p h t", h=DH),
                                   ACT.Copy).then_inc(xt_ready, 1)

                in_pairs(act, NT, step)
                beside_act(act)

            @block.tensor
            def _(pe):
                pe.wait_ge(ones_ready, 1)
                pe.wait_ge(part_ready, 1)
                pe.matmul(PS[:, 7, 0:1], ones[:, :], part[:, 0:1], start=True, stop=True).then_inc(total_ps, 1)
                pe.wait_ge(w_ready, 1)

                def front(t, u):
                    pe.wait_ge(xn_ready, t + 1)
                    for h in range(DH):
                        last = pe.transpose(PS[:, u, h * P:h * P + P], xn[:, u, h * P:h * P + P], core.ident[:, :])
                    last.then_inc(xt_ps, 1)

                def back(t, u):
                    pe.wait_ge(xt_ready, t + 1)
                    pe.wait_ge(added, t + 1)
                    for h in range(DH):
                        last = pe.matmul(PS[:, 2 + u, 0:D], xT[:, u, h, :], Wq[:, h, :], start=(h == 0), stop=(h == DH - 1))
                    last.then_inc(y_ps, 1)

                skewed(pe, NT, front, back)
                pe.wait_ge(added, NT + 2)
                beside_pe(pe)


HID = 704
ZERO_POINT = 128.0
GT = 4


def blocks(hid):
    full = hid // P if hid % P > P // 2 else hid // P - 1
    rest = hid - full * P
    return [P] * full + ([rest] if rest <= P else [rest // 2] * 2)


def gated_ffn(core, tag, hid, prepare, router=None):
    nc, X, PS = core.nc, core.X, core.PS
    NG = NT // GT
    size = blocks(hid)
    M = len(size)
    m_at = [sum(size[:m]) for m in range(M)]
    with core.stage(tag) as (sb, sem):
        Wg = sb("Wg", [P, DH, hid])
        Wu = sb("Wu", [P, DH, hid])
        Wd = sb("Wd", [P, M, D])
        xn = sb("xn", [P, 2, GT, D])
        xT = sb("xT", [P, 2, DH, GT * P])
        sg = sb("sg", [P, 2, GT * P])
        hT = sb("hT", [P, M, GT * P])
        w_ready = sem("w_ready")
        load, make = prepare(sb, sem, Wg, Wu, Wd, w_ready)
        xn_ready, xt_ps, xt_ready, gu_ps, silu_ready, h_ready, y_ps, added, lg_ps, lg_ready, n_stored, n_free = (
            sem(x) for x in ("xn_ready", "xt_ps", "xt_ready", "gu_ps", "silu", "h_ready", "y_ps", "added", "lg_ps",
                             "lg_ready", "n_stored", "n_free"))
        moments = Moments(core, sem)
        with nc.Block() as block:
            @block.sync
            def _(sp):
                load(sp)
                if router:
                    rows_of = router["rows"].rearrange("(n p) d -> p n d", p=P)

                    def store(g, u):
                        sp.wait_ge(xn_ready, g + 1)
                        sp.dma_start(rows_of[:, bass.ds(GT * g, GT), :], xn[:, u, :, :]).then_inc(n_stored, 16)
                        sp.wait_ge(n_stored, 16 * g + 16)
                        sp.sem_inc(n_free, 1)

                    in_pairs(sp, NG, store)

            @block.vector
            def _(dve):
                moments.dve(dve)
                make(dve)
                dve.sem_inc(h_ready, 2)
                dve.sem_inc(added, 2)
                dve.sem_inc(n_free, 2)

                def normalise(g, u):
                    if router:
                        dve.wait_ge(n_free, g + 1)
                    for k in range(GT):
                        t = GT * g + k
                        last = dve.tensor_scalar(out=xn[:, u, k, :], in0=X[:, bass.ds(t, 1), :],
                                                 scalar1=core.mean[:, bass.ds(t, 1)], scalar2=core.rstd[:, bass.ds(t, 1)],
                                                 op0=ALU.subtract, op1=ALU.mult)
                    last.then_inc(xn_ready, 1)

                def body(g, u, more):
                    if more:
                        normalise(g + 1, 1 - u)
                    for m in range(M):
                        dve.wait_ge(silu_ready, M * g + m + 1)
                        r = slice(0, size[m])
                        dve.tensor_tensor(out=hT[r, m, :], in0=sg[r, (M * u + m) % 2, :],
                                          in1=PS[r, 4 + (M * u + m) % 2, :], op=ALU.mult).then_inc(h_ready, 1)
                    for k in range(2):
                        dve.wait_ge(y_ps, 2 * g + k + 1)
                        t = GT * g + 2 * k
                        dve.tensor_tensor(out=X[:, bass.ds(t, 2), :], in0=X[:, bass.ds(t, 2), :],
                                          in1=PS[:, 6 + k, :].rearrange("p (k d) -> p k d", k=2),
                                          op=ALU.add).then_inc(added, 1)
                        if not router:
                            dve.wait_ge(added, 2 * g + k + 3)
                            tile_statistics(core, dve, X, t, 2)

                ahead(dve, NG, normalise, body)

            @block.gpsimd
            def _(pool):
                moments.pool(pool)

            @block.scalar
            def _(act):
                def copy(g, u):
                    for h in range(DH):
                        act.wait_ge(xt_ps, DH * g + h + 1)
                        act.activation(xT[:, u, h, :], PS[:, h, :], ACT.Copy).then_inc(xt_ready, 1)

                def body(g, u, more):
                    if router:
                        act.wait_ge(lg_ps, g + 1)
                        act.activation(router["logits"][:, bass.ds(GT * g, GT), :],
                                       PS[:, 0, 0:GT * router["E"]].rearrange("p (k e) -> p k e", k=GT),
                                       ACT.Copy).then_inc(lg_ready, 1)
                    for m in range(M):
                        act.wait_ge(gu_ps, M * g + m + 1)
                        r = slice(0, size[m])
                        act.activation(sg[r, (M * u + m) % 2, :], PS[r, 2 + (M * u + m) % 2, :],
                                       ACT.Silu).then_inc(silu_ready, 1)
                    if more:
                        copy(g + 1, 1 - u)

                ahead(act, NG, copy, body)

            @block.tensor
            def _(pe):
                def transposes(g, u):
                    pe.wait_ge(xn_ready, g + 1)
                    for h in range(DH):
                        for k in range(GT):
                            last = pe.transpose(PS[:, h, k * P:k * P + P], xn[:, u, k, h * P:h * P + P], core.ident[:, :])
                        last.then_inc(xt_ps, 1)

                def body(g, u, more):
                    pe.wait_ge(xt_ready, DH * g + DH)
                    if router:
                        E = router["E"]
                        for k in range(GT):
                            for h in range(DH):
                                last = pe.matmul(PS[:, 0, k * E:k * E + E], xT[:, u, h, k * P:k * P + P],
                                                 router["W"][:, h, :], start=(h == 0), stop=(h == DH - 1))
                        last.then_inc(lg_ps, 1)
                    for m in range(M):
                        pe.wait_ge(h_ready, M * g + m + 1)
                        for w, bank in ((Wg, 2), (Wu, 4)):
                            for h in range(DH):
                                last = pe.matmul(PS[0:size[m], bank + (M * u + m) % 2, :], w[:, h, m_at[m]:m_at[m] + size[m]],
                                                 xT[:, u, h, :], start=(h == 0), stop=(h == DH - 1))
                        last.then_inc(gu_ps, 1)
                    if more:
                        if router:
                            pe.wait_ge(lg_ready, g + 1)
                        transposes(g + 1, 1 - u)
                    pe.wait_ge(h_ready, M * g + M + 2)
                    for k in range(GT):
                        if k % 2 == 0:
                            pe.wait_ge(added, 2 * g + k // 2 + 1)
                        for m in range(M):
                            last = pe.matmul(PS[:, 6 + k // 2, k % 2 * D:k % 2 * D + D],
                                             hT[0:size[m], m, k * P:k * P + P], Wd[0:size[m], m, :],
                                             start=(m == 0), stop=(m == M - 1))
                        if k % 2:
                            last.then_inc(y_ps, 1)

                pe.wait_ge(w_ready, 1)
                ahead(pe, NG, transposes, body)


def quantised_ffn(core):
    size = blocks(HID)
    M = len(size)

    def prepare(sb, sem, Wg, Wu, Wd, w_ready):
        raw = sb("raw", [P, DH, HID], I32)
        raw_d = sb("raw_d", [P, M, D], I32)
        s_row = sb("s_row", [P, HID])
        s_down = sb("s_down", [P, D])
        load_g, load_u, load_d, own, gate_made = (sem(x) for x in ("load_g", "load_u", "load_d", "own", "gate_made"))

        def load(sp):
            sp.dma_start(raw[:, :, :], core.dram["wq_gateT"].rearrange("(h p) e -> p h e", p=P)).then_inc(load_g, 16)
            sp.dma_start(s_row[:, :], core.dram["s_gate"]).then_inc(load_g, 16)
            for m in range(M):
                at = sum(size[:m])
                sp.dma_start(raw_d[0:size[m], m, :], core.dram["wq_downT"][at:at + size[m], :]).then_inc(load_d, 16)
            sp.dma_start(s_down[:, :], core.dram["s_down"]).then_inc(load_d, 16)
            sp.wait_ge(gate_made, 1)
            sp.dma_start(raw[:, :, :], core.dram["wq_upT"].rearrange("(h p) e -> p h e", p=P)).then_inc(load_u, 16)
            sp.dma_start(s_row[:, :], core.dram["s_up"]).then_inc(load_u, 16)

        def make(dve):
            link = Chain(dve, own, 2)

            def dequantise(w, r, s):
                return dve.scalar_tensor_tensor(out=w, in0=r, scalar=ZERO_POINT, in1=s, op0=ALU.subtract, op1=ALU.mult)

            dve.wait_ge(load_g, 2 * 16)
            for h in range(DH):
                link(dequantise(Wg[:, h, :], raw[:, h, :], s_row[:, :]))
            dve.sem_inc(gate_made, 1)
            dve.wait_ge(load_d, (M + 1) * 16)
            for m in range(M):
                dequantise(Wd[0:size[m], m, :], raw_d[0:size[m], m, :], s_down[0:size[m], :])
            dve.wait_ge(load_u, 2 * 16)
            for h in range(DH):
                last = dequantise(Wu[:, h, :], raw[:, h, :], s_row[:, :])
            last.then_inc(w_ready, 1)

        return load, make

    gated_ffn(core, "qf", HID, prepare)


HEADS = 16
NOPE, ROPE, VDIM = 128, 64, 128
QL, KL = 192, 64
QH = QL // 2
QK = KL + ROPE
LOW = QL + KL + ROPE
RMS_EPS = float(np.finfo(np.float32).eps)


def latent_weights(core, sb, sem, q1, q2, out):
    nc, PS = core.nc, core.PS
    SCALE = 1.0 / float(np.sqrt(np.float32(NOPE + ROPE)))
    wq = sb("wq", [P, HEADS, QL])
    wk = sb("wk", [P, HEADS, KL])
    wv = sb("wv", [P, HEADS, KL])
    wo = sb("wo", [P, HEADS, D])
    g1 = sb("g1", [QH, 1])
    g2 = sb("g2", [QH, 1])
    loaded, loaded_o, own, prod_ps, prod_free, prod2_ps = (
        sem(x) for x in ("w_loaded", "loaded_o", "w_own", "prod_ps", "prod_free", "prod2"))

    def load(sp):
        for a, name in ((wq, "Wqb_nopeT"), (wk, "Wkvb_kT")):
            sp.dma_start(a[:, :, :], core.dram[name]).then_inc(loaded, 16)
        sp.dma_start(q1[:, :, KL:QK], core.dram["Wqb_rope"][0:QH, :, :]).then_inc(loaded, 16)
        sp.dma_start(q2[:, :, KL:QK], core.dram["Wqb_rope"][QH:QL, :, :]).then_inc(loaded, 16)
        sp.dma_start(g1[:, :], core.dram["q_ln_w"][0:QH, :]).then_inc(loaded, 16)
        sp.dma_start(g2[:, :], core.dram["q_ln_w"][QH:QL, :]).then_inc(loaded, 16)
        for a, name in ((wv, "Wkvb_vT"), (wo, "Wo_heads")):
            sp.dma_start(a[:, :, :], core.dram[name]).then_inc(loaded_o, 16)

    def multiply(pe):
        pe.wait_ge(loaded, 6 * 16)
        for h in range(HEADS):
            at = h % 8 * KL
            pe.matmul(PS[0:QH, h // 8, at:at + KL], wq[:, h, 0:QH], wk[:, h, :], start=True, stop=True)
            last = pe.matmul(PS[0:QH, 2 + h // 8, at:at + KL], wq[:, h, QH:QL], wk[:, h, :], start=True, stop=True)
        last.then_inc(prod_ps, 1)
        pe.wait_ge(loaded_o, 2 * 16)
        for j in range(HEADS // 2):
            if j == 4:
                pe.wait_ge(prod_free, 1)
            for k in range(2):
                last = pe.matmul(PS[k * KL:k * KL + KL, (4 + j) % 8, 0:D], wv[:, 2 * j + k, :],
                                 wo[:, 2 * j + k, :], start=True, stop=True)
            last.then_inc(prod2_ps, 1)

    def scale(dve):
        link = Chain(dve, own, 4)
        dve.wait_ge(loaded, 6 * 16)
        link(dve.tensor_scalar(out=g1[:, :], in0=g1[:, :], scalar1=SCALE, scalar2=None, op0=ALU.mult))
        link(dve.tensor_scalar(out=g2[:, :], in0=g2[:, :], scalar1=SCALE, scalar2=None, op0=ALU.mult))
        for w, g in ((q1, g1), (q2, g2)):
            dve.tensor_scalar(out=w[:, :, KL:QK], in0=w[:, :, KL:QK], scalar1=g[:, 0:1], scalar2=None, op0=ALU.mult)
        dve.wait_ge(prod_ps, 1)
        for k in range(2):
            dve.tensor_scalar(out=q1[:, 8 * k:8 * k + 8, 0:KL], in0=PS[0:QH, k, :].rearrange("p (h c) -> p h c", h=8),
                              scalar1=g1[:, 0:1], scalar2=None, op0=ALU.mult)
            link(dve.tensor_scalar(out=q2[:, 8 * k:8 * k + 8, 0:KL],
                                   in0=PS[0:QH, 2 + k, :].rearrange("p (h c) -> p h c", h=8),
                                   scalar1=g2[:, 0:1], scalar2=None, op0=ALU.mult))
        dve.sem_inc(prod_free, 1)

    def keep_out(act):
        for j in range(HEADS // 2):
            act.wait_ge(prod2_ps, j + 1)
            act.activation(out[:, j, :], PS[:, (4 + j) % 8, 0:D], ACT.Copy)

    return load, multiply, scale, keep_out


def latent_heads(core, q1, q2, out):
    nc, X, PS = core.nc, core.X, core.PS
    PAIRS = HEADS // 2
    H2 = ROPE // 2
    W1 = KL + 1
    QUERIES = {2: ((0, 1), (2, 3)), 3: ((4,), (5,)), 4: ((6,), (7,))}
    TURNS = {5: ((0, 1), (2, 3)), 6: ((4, 5), (6, 7))}
    with core.stage("lh") as (sb, sem):
        Wa = sb("Wa", [P, DH, LOW])
        kvw = sb("kvw", [P, KL])
        cos = sb("cos", [P, TPB, ROPE])
        sin = sb("sin", [P, TPB, ROPE])
        mask = sb("mask", [P, P], BF16)
        xn = sb("xn", [P, TPB, D])
        xT = sb("xT", [P, DH, T])
        low = sb("low", [P, TPB, LOW])
        junk = sb("junk", [P, TPB, QL + KL])
        eps = sb("eps", [P, TPB, 2])
        ms = sb("ms", [P, TPB, 2])
        rs = sb("rs", [P, TPB, 2])
        qn = sb("qn", [P, TPB, QL])
        ktok = sb("ktok", [P, TPB, QK])
        c1 = sb("c1", [P, 2, TPB, W1])
        qc = sb("qc", [QH, 2, T])
        KT = sb("KT", [P, 2, T])
        qtok = sb("qtok", [P, TPB, HEADS, QK])
        ra = sb("ra", [P, HEADS, ROPE])
        rb = sb("rb", [P, HEADS, ROPE])
        QT = sb("QT", [P, 2, HEADS, T])
        negm = sb("negm", [P, 4])
        p0 = sb("p0", [P, 2, 2, P])
        p1 = sb("p1", [P, 2, 2, T])
        t0 = sb("t0", [P, 2, 2, T])
        t1 = sb("t1", [P, 2, 2, P])
        rz = sb("rz", [P, 4])
        oc = sb("oc", [P, 2, TPB, 2 * KL])
        oT = sb("oT", [P, 2, T])
        names = ("loaded consts mask_made xn_ready xt_ps xt_ready low_ps low_read ms_ready rs_ready qn_ready c_ready kr_ready "
                 "qct_ps qct_ready kt_ps kt_ready q_ps q_ready roped qt_ps qt_a qt_d s_ps negm_ready exp_done pt_ps pt_a "
                 "pt_d o_ps o_done ot_ps ot_ready y_ps added own rz_ready own2 pown").split()
        S = {n: sem(n) for n in names}

        moments = Moments(core, sem)
        with nc.Block() as block:
            @block.sync
            def _(sp):
                sp.dma_start(Wa[:, :, :], core.dram["Wa"].rearrange("(h p) e -> p h e", p=P)).then_inc(S["loaded"], 16)
                sp.dma_start(kvw[:, :], core.dram["kv_ln_w"]).then_inc(S["loaded"], 16)
                sp.dma_start(cos[:, :, :], core.dram["cos"].rearrange("(k p) e -> p k e", p=P)).then_inc(S["loaded"], 16)
                sp.dma_start(sin[:, :, :], core.dram["sin"].rearrange("(k p) e -> p k e", p=P)).then_inc(S["loaded"], 16)

            @block.tensor
            def _(pe):
                pe.wait_ge(S["loaded"], 4 * 16)
                pe.wait_ge(S["mask_made"], 1)

                def tokens(b):
                    pe.wait_ge(S["xn_ready"], b + 1)
                    for h in range(DH):
                        for k in range(TPB):
                            last = pe.transpose(PS[:, 5, h * T + k * P:h * T + k * P + P], xn[:, k, h * P:h * P + P],
                                                core.ident[:, :])
                    last.then_inc(S["xt_ps"], 1)

                def lows(b):
                    pe.wait_ge(S["xt_ready"], b + 1)
                    for k in range(TPB):
                        for h in range(DH):
                            last = pe.matmul(PS[:, 6 - k, 0:LOW], xT[:, h, k * P:k * P + P], Wa[:, h, :],
                                             start=(h == 0), stop=(h == DH - 1))
                        last.then_inc(S["low_ps"], 1)

                def low_queries(b):
                    pe.wait_ge(S["qn_ready"], TPB * b + TPB)
                    pe.wait_ge(S["low_read"], TPB * b + TPB)
                    for k in range(TPB):
                        pe.transpose(PS[0:QH, 6, k * P:k * P + P], qn[:, k, 0:QH], core.ident[:, :])
                        last = pe.transpose(PS[0:QH, 6, T + k * P:T + k * P + P], qn[:, k, QH:QL], core.ident[:, :])
                    last.then_inc(S["qct_ps"], 1)
                    pe.wait_ge(S["c_ready"], b + 1)
                    pe.wait_ge(S["kr_ready"], b + 1)
                    for k in range(TPB):
                        last = pe.transpose(PS[:, 5, k * P:k * P + P], ktok[:, k, :], core.ident[:, :])
                    last.then_inc(S["kt_ps"], 1)

                def queries(b, i):
                    k, j = i // 4, i % 4
                    if i == 0:
                        pe.wait_ge(S["qct_ready"], b + 1)
                        pe.wait_ge(S["kt_ready"], b + 1)
                    if i >= 2:
                        pe.wait_ge(S["q_ready"], 8 * b + i - 1)
                    pe.matmul(PS[:, 5 + i % 2, :], qc[:, 0, k * P:k * P + P], q1[:, 4 * j:4 * j + 4, :],
                              start=True, stop=False)
                    pe.matmul(PS[:, 5 + i % 2, :], qc[:, 1, k * P:k * P + P], q2[:, 4 * j:4 * j + 4, :],
                              start=False, stop=True).then_inc(S["q_ps"], 1)

                def turn(b, i):
                    k, j = i // 4, i % 4
                    if i < 2:
                        pe.wait_ge(S["q_ready"], 8 * b + 7 + i)
                    else:
                        pe.wait_ge((S["qt_a"], S["qt_d"])[i % 2], 4 * b + i // 2)
                    if j == 0:
                        pe.wait_ge(S["roped"], TPB * b + k + 1)
                    for h in range(4):
                        last = pe.transpose(PS[:, 5 + i % 2, h * P:h * P + P], qtok[:, k, 4 * j + h, :], core.ident[:, :])
                    last.then_inc(S["qt_ps"], 1)

                def scores(b, u, g):
                    if g == 0:
                        pe.wait_ge(S["qt_a"], 4 * b + 4)
                        pe.wait_ge(S["qt_d"], 4 * b + 4)
                    for i in range(2):
                        h = 2 * g + i
                        pe.matmul(PS[:, 0, i * T:i * T + T], QT[:, u, h, P:T], KT[:, u, :], start=True, stop=False)
                        pe.matmul(PS[:, 0, i * T + P:i * T + T], core.identb[:, :], mask[:, :], start=False, stop=True)
                    for i in range(2):
                        h = 2 * g + i
                        pe.matmul(PS[:, 1, i * P:i * P + P], QT[:, u, h, 0:P], KT[:, u, 0:P], start=True, stop=False)
                        last = pe.matmul(PS[:, 1, i * P:i * P + P], core.identb[:, :], mask[:, :], start=False, stop=True)
                    last.then_inc(S["s_ps"], 1)

                def turn_latents(b, g):
                    pe.wait_ge(S["o_done"], PAIRS * b + g + 1)
                    for k in range(TPB):
                        last = pe.transpose(PS[:, 3, T + k * P:T + k * P + P], oc[:, g % 2, k, :], core.ident[:, :])
                    last.then_inc(S["ot_ps"], 1)

                def output(b, g):
                    for k in range(TPB):
                        last = pe.matmul(PS[:, 7, k * D:k * D + D], oT[:, g % 2, k * P:k * P + P], out[:, g, :],
                                         start=(g == 0 and k == 0), stop=(g == PAIRS - 1 and k == TPB - 1),
                                         skip_group_check=True)
                    if g == PAIRS - 1:
                        last.then_inc(S["y_ps"], 1)

                def first(b, u):
                    tokens(b)
                    lows(b)
                    low_queries(b)
                    for i in range(8):
                        queries(b, i)
                    for i in range(8):
                        turn(b, i)
                    scores(b, u, 0)

                def body(b, u, prev, more):
                    for g in range(PAIRS):
                        n, w = PAIRS * b + g, g % 2
                        pe.wait_ge(S["exp_done"], n + 1)
                        if prev or g >= 2:
                            pe.wait_ge(S["ot_ready"], n - 1)
                        for i in range(2):
                            pe.transpose(PS[:, 2, i * T:i * T + P], p0[:, w, i, :], core.ident[:, :])
                            pe.transpose(PS[:, 2, i * T + P:i * T + T], p1[:, w, i, 0:P], core.ident[:, :])
                            last = pe.transpose(PS[:, 3, i * P:i * P + P], p1[:, w, i, P:T], core.ident[:, :])
                        last.then_inc(S["pt_ps"], 1)
                        if g + 1 < PAIRS:
                            scores(b, u, g + 1)
                        elif more:
                            scores(b + 1, 1 - u, 0)
                        if g >= 2:
                            if g == 2 and prev:
                                pe.wait_ge(S["added"], b)
                            output(b, g - 2)
                        elif prev:
                            output(b - 1, g - 2 + PAIRS)
                        if more:
                            if g == 0:
                                pe.wait_ge(S["qt_a"], 4 * b + 4)
                                tokens(b + 1)
                            for i in QUERIES.get(g, ((), ()))[0]:
                                queries(b + 1, i)
                            for i in TURNS.get(g, ((), ()))[0]:
                                turn(b + 1, i)
                        pe.wait_ge(S["pt_a"], n + 1)
                        pe.wait_ge(S["pt_d"], n + 1)
                        if prev or g >= 1:
                            pe.wait_ge(S["o_done"], n)
                        for i in range(2):
                            pe.matmul(PS[:, 4, i * W1:i * W1 + W1], t0[:, w, i, 0:P], c1[:, u, 0, :], start=True, stop=True)
                        for i in range(2):
                            o = PS[:, 4, (2 + i) * W1:(3 + i) * W1]
                            pe.matmul(o, t0[:, w, i, P:T], c1[:, u, 0, :], start=True, stop=False)
                            last = pe.matmul(o, t1[:, w, i, :], c1[:, u, 1, :], start=False, stop=True)
                        last.then_inc(S["o_ps"], 1)
                        if g >= 1:
                            turn_latents(b, g - 1)
                        elif prev:
                            turn_latents(b - 1, PAIRS - 1)
                        if more:
                            if g == 0:
                                lows(b + 1)
                            if g == 1:
                                low_queries(b + 1)
                            for i in QUERIES.get(g, ((), ()))[1]:
                                queries(b + 1, i)
                            for i in TURNS.get(g, ((), ()))[1]:
                                turn(b + 1, i)

                def finish(b, u):
                    pe.wait_ge(S["ot_ready"], PAIRS * b + PAIRS - 1)
                    turn_latents(b, PAIRS - 1)
                    output(b, PAIRS - 2)
                    pe.wait_ge(S["ot_ready"], PAIRS * b + PAIRS)
                    output(b, PAIRS - 1)

                overlapped(pe, B, first, body, finish)

            @block.scalar
            def _(act):
                link = Chain(act, S["own2"], 2 * TPB)

                def tokens(b):
                    act.wait_ge(S["xt_ps"], b + 1)
                    act.activation(xT[:, :, :], PS[:, 5, :].rearrange("p (h t) -> p h t", h=DH),
                                   ACT.Copy).then_inc(S["xt_ready"], 1)

                def lows(b):
                    link.start(b)
                    for k in range(TPB):
                        act.wait_ge(S["low_ps"], TPB * b + k + 1)
                        link(act.activation(low[:, k, :], PS[:, 6 - k, 0:LOW], ACT.Copy))
                        act.sem_inc(S["low_read"], 1)
                        act.activation(junk[:, k, 0:QL], low[:, k, 0:QL], ACT.Square, scale=QL ** -0.5,
                                       accum_out=ms[:, k, 0:1])
                        link(act.activation(junk[:, k, QL:QL + KL], low[:, k, QL:QL + KL], ACT.Square, scale=KL ** -0.5,
                                            accum_out=ms[:, k, 1:2]))
                        act.sem_inc(S["ms_ready"], 1)

                def low_queries(b):
                    act.wait_ge(S["rs_ready"], b + 1)
                    for k in range(TPB):
                        act.activation(qn[:, k, :], low[:, k, 0:QL], ACT.Copy, scale=rs[:, k, 0:1]).then_inc(S["qn_ready"], 1)

                def turned(b, u):
                    act.wait_ge(S["qct_ps"], b + 1)
                    act.activation(qc[:, :, :], PS[0:QH, 6, :].rearrange("p (a t) -> p a t", a=2),
                                   ACT.Copy).then_inc(S["qct_ready"], 1)
                    act.wait_ge(S["kt_ps"], b + 1)
                    act.activation(KT[:, u, :], PS[:, 5, 0:T], ACT.Copy).then_inc(S["kt_ready"], 1)

                def queries(b, i):
                    k, j = i // 4, i % 4
                    act.wait_ge(S["q_ps"], 8 * b + i + 1)
                    act.activation(qtok[:, k, 4 * j:4 * j + 4, :], PS[:, 5 + i % 2, :].rearrange("p (h c) -> p h c", h=4),
                                   ACT.Copy).then_inc(S["q_ready"], 1)

                def turn(b, u, i):
                    if i % 2 == 0:
                        k, j = i // 4, i % 4
                        act.wait_ge(S["qt_ps"], 8 * b + i + 1)
                        act.activation(QT[:, u, 4 * j:4 * j + 4, k * P:k * P + P],
                                       PS[:, 5, :].rearrange("p (h t) -> p h t", h=4), ACT.Copy).then_inc(S["qt_a"], 1)

                def exps(b, g):
                    w = g % 2
                    act.wait_ge(S["negm_ready"], PAIRS * b + g + 1)
                    for i in range(2):
                        act.activation(p1[:, w, i, :], PS[:, 0, i * T:i * T + T], ACT.Exp, bias=negm[:, i:i + 1])
                    for i in range(2):
                        last = act.activation(p0[:, w, i, :], PS[:, 1, i * P:i * P + P], ACT.Exp, bias=negm[:, 2 + i:3 + i])
                    last.then_inc(S["exp_done"], 1)

                def first(b, u):
                    tokens(b)
                    lows(b)
                    low_queries(b)
                    turned(b, u)
                    for i in range(8):
                        queries(b, i)
                    for i in range(8):
                        turn(b, u, i)
                    exps(b, 0)

                def body(b, u, prev, more):
                    for g in range(PAIRS):
                        act.wait_ge(S["pt_ps"], PAIRS * b + g + 1)
                        act.activation(t0[:, g % 2, :, :], PS[:, 2, :].rearrange("p (i t) -> p i t", i=2),
                                       ACT.Copy).then_inc(S["pt_a"], 1)
                        if more:
                            if g == 0:
                                tokens(b + 1)
                            if g == 1:
                                low_queries(b + 1)
                        if g + 1 < PAIRS:
                            exps(b, g + 1)
                        elif more:
                            exps(b + 1, 0)
                        if more:
                            if g == 0:
                                lows(b + 1)
                            if g == 1:
                                turned(b + 1, 1 - u)
                            for i in sum(QUERIES.get(g, ()), ()):
                                queries(b + 1, i)
                            for i in sum(TURNS.get(g, ()), ()):
                                turn(b + 1, 1 - u, i)

                overlapped(act, B, first, body, lambda b, u: None)

            @block.gpsimd
            def _(pool):
                moments.pool(pool)
                mz = S["consts"]
                pool.memset(c1[:, :, :, KL:KL + 1], 1.0)
                pool.memset(eps[:, :, :], RMS_EPS)
                pool.memset(mask[:, :], 0.0).then_inc(mz, 1)
                pool.wait_ge(mz, 1)
                pool.affine_select(out=mask[:, :], in_=mask[:, :], compare_op=ALU.is_ge, fill=-1e30, base=0,
                                   pattern=[[-1, P]], channel_multiplier=1).then_inc(S["mask_made"], 1)
                pool.wait_ge(S["loaded"], 4 * 16)
                rp = Chain(pool, S["pown"], 1 + 2 + 2 * TPB)

                def rotate(dst, src, k, n):
                    a, c = ra[:, 0:n, :], rb[:, 0:n, :]
                    cb = cos[:, k:k + 1, :].broadcast_to([P, n, ROPE])
                    sb_ = sin[:, k:k + 1, :].broadcast_to([P, n, ROPE])
                    pool.tensor_tensor(out=a, in0=src, in1=cb, op=ALU.mult)
                    pool.tensor_tensor(out=c[:, :, 0:H2], in0=src[:, :, H2:ROPE], in1=sb_[:, :, 0:H2], op=ALU.mult)
                    rp(pool.tensor_tensor(out=c[:, :, H2:ROPE], in0=src[:, :, 0:H2], in1=sb_[:, :, H2:ROPE], op=ALU.mult))
                    rp(pool.tensor_tensor(out=dst, in0=a, in1=c, op=ALU.add))

                with pool.Fori(0, B) as b:
                    pool.wait_ge(S["ms_ready"], TPB * b + TPB)
                    rp.start(b)
                    rp(pool.tensor_tensor(out=ms[:, :, :], in0=ms[:, :, :], in1=eps[:, :, :], op=ALU.add))
                    pool.tensor_tensor(out=rs[:, :, :], in0=ms[:, :, :],
                                       in1=core.half[:, 0:2 * TPB].rearrange("p (k c) -> p k c", k=TPB),
                                       op=ALU.pow).then_inc(S["rs_ready"], 1)
                    kr = low[:, :, QL + KL:LOW]
                    pool.tensor_tensor(out=ra[:, 0:TPB, :], in0=kr, in1=cos[:, :, :], op=ALU.mult)
                    pool.tensor_tensor(out=rb[:, 0:TPB, 0:H2], in0=kr[:, :, H2:ROPE], in1=sin[:, :, 0:H2], op=ALU.mult)
                    rp(pool.tensor_tensor(out=rb[:, 0:TPB, H2:ROPE], in0=kr[:, :, 0:H2], in1=sin[:, :, H2:ROPE], op=ALU.mult))
                    rp(pool.tensor_tensor(out=ktok[:, :, KL:QK], in0=ra[:, 0:TPB, :], in1=rb[:, 0:TPB, :], op=ALU.add))
                    pool.sem_inc(S["kr_ready"], 1)
                    for k in range(TPB):
                        pool.wait_ge(S["q_ready"], 8 * b + 4 * k + 4)
                        rotate(qtok[:, k, :, KL:QK], qtok[:, k, :, KL:QK], k, HEADS)
                        pool.sem_inc(S["roped"], 1)

            @block.vector
            def _(dve):
                moments.dve(dve)
                link = Chain(dve, S["own"], PAIRS)
                dve.wait_ge(S["loaded"], 4 * 16)
                dve.wait_ge(S["mask_made"], 1)

                def normalise(b):
                    for k in range(TPB):
                        t = TPB * b + k
                        last = dve.tensor_scalar(out=xn[:, k, :], in0=X[:, bass.ds(t, 1), :],
                                                 scalar1=core.mean[:, bass.ds(t, 1)], scalar2=core.rstd[:, bass.ds(t, 1)],
                                                 op0=ALU.subtract, op1=ALU.mult)
                    last.then_inc(S["xn_ready"], 1)

                def latents(b, u):
                    dve.wait_ge(S["rs_ready"], b + 1)
                    for k in range(TPB):
                        for d in (ktok[:, k, 0:KL], c1[:, u, k, 0:KL]):
                            last = dve.scalar_tensor_tensor(out=d, in0=low[:, k, QL:QL + KL], scalar=rs[:, k, 1:2],
                                                            in1=kvw[:, :], op0=ALU.mult, op1=ALU.mult)
                    last.then_inc(S["c_ready"], 1)

                def turn(b, u, i):
                    if i % 2:
                        k, j = i // 4, i % 4
                        dve.wait_ge(S["qt_ps"], 8 * b + i + 1)
                        dve.tensor_copy(QT[:, u, 4 * j:4 * j + 4, k * P:k * P + P],
                                        PS[:, 6, :].rearrange("p (h t) -> p h t", h=4)).then_inc(S["qt_d"], 1)

                def maxima(b, g):
                    dve.wait_ge(S["s_ps"], PAIRS * b + g + 1)
                    dve.tensor_reduce(out=negm[:, 0:2], in_=PS[:, 0, :].rearrange("p (i t) -> p i t", i=2),
                                      axis=AX.X, op=ALU.max, negate=True)
                    link.start(b, g)
                    link(dve.tensor_reduce(out=negm[:, 2:4], in_=PS[:, 1, 0:T].rearrange("p (i t) -> p i t", i=2),
                                           axis=AX.X, op=ALU.max, negate=True))
                    dve.sem_inc(S["negm_ready"], 1)

                def finish_latents(b, g):
                    dve.wait_ge(S["o_ps"], PAIRS * b + g + 1)
                    o = PS[:, 4, 0:4 * W1].rearrange("p (q i c) -> p q i c", q=2, i=2)
                    dve.reciprocal(out=rz[:, :], in_=o[:, :, :, KL]).then_inc(S["rz_ready"], 1)
                    dve.wait_ge(S["rz_ready"], PAIRS * b + g + 1)
                    r = rz[:, :].rearrange("p (q i c) -> p q i c", q=2, c=1).broadcast_to([P, 2, 2, KL])
                    dve.tensor_tensor(out=oc[:, g % 2, :, :].rearrange("p q (i c) -> p q i c", i=2),
                                      in0=o[:, :, :, 0:KL], in1=r, op=ALU.mult).then_inc(S["o_done"], 1)

                def turned_latents(b, g):
                    dve.wait_ge(S["ot_ps"], PAIRS * b + g + 1)
                    dve.tensor_copy(oT[:, g % 2, :], PS[:, 3, T:2 * T]).then_inc(S["ot_ready"], 1)

                def add(b):
                    dve.wait_ge(S["y_ps"], b + 1)
                    t = TPB * b
                    dve.tensor_tensor(out=X[:, bass.ds(t, TPB), :], in0=X[:, bass.ds(t, TPB), :],
                                      in1=PS[:, 7, :].rearrange("p (k d) -> p k d", k=TPB), op=ALU.add).then_inc(S["added"], 1)
                    dve.wait_ge(S["added"], b + 1)
                    tile_statistics(core, dve, X, t, TPB)

                def first(b, u):
                    normalise(b)
                    latents(b, u)
                    for i in range(8):
                        turn(b, u, i)
                    maxima(b, 0)

                def body(b, u, prev, more):
                    for g in range(PAIRS):
                        if g == 0 and more:
                            normalise(b + 1)
                        dve.wait_ge(S["pt_ps"], PAIRS * b + g + 1)
                        dve.tensor_copy(t1[:, g % 2, :, :],
                                        PS[:, 3, 0:T].rearrange("p (i t) -> p i t", i=2)).then_inc(S["pt_d"], 1)
                        if g + 1 < PAIRS:
                            maxima(b, g + 1)
                        elif more:
                            maxima(b + 1, 0)
                        if g == 1 and more:
                            latents(b + 1, 1 - u)
                        if more:
                            for i in TURNS.get(g, ((), ()))[0]:
                                turn(b + 1, 1 - u, i)
                        finish_latents(b, g)
                        if g >= 1:
                            turned_latents(b, g - 1)
                        elif prev:
                            turned_latents(b - 1, PAIRS - 1)
                        if g == 1 and prev:
                            add(b - 1)
                        if more:
                            for i in TURNS.get(g, ((), ()))[1]:
                                turn(b + 1, 1 - u, i)

                def finish(b, u):
                    turned_latents(b, PAIRS - 1)
                    add(b)

                overlapped(dve, B, first, body, finish)


HD = 16
HPH = P // HD
SLOTS = NT + 32


def head_window(padded, h):
    at = h * P + P - HD - HD * (h % HPH)
    return padded[:, at:at + P]


def head_masks(pool, link, hmask):
    link(pool.memset(hmask[:, :], 1.0))
    link(pool.affine_select(out=hmask[:, :], in_=hmask[:, :], compare_op=ALU.is_ge, fill=0.0, base=0,
                            pattern=[[-HD, HPH]], channel_multiplier=1))
    link(pool.affine_select(out=hmask[:, :], in_=hmask[:, :], compare_op=ALU.is_ge, fill=0.0, base=HD - 1,
                            pattern=[[HD, HPH]], channel_multiplier=-1))


def mask_keys(pool, KTm, KT, hmask, half, n):
    return pool.tensor_tensor(out=KTm[:, half * HPH:half * HPH + HPH, :],
                              in0=KT[:, half:half + 1, :].broadcast_to([P, HPH, n]),
                              in1=hmask[:, :].rearrange("p (h t) -> p h t", t=1).broadcast_to([P, HPH, n]), op=ALU.mult)


def double_attention(core):
    nc, X, PS = core.nc, core.X, core.PS
    PAIRS = HEADS // 2
    with core.stage("da") as (sb, sem):
        WT = sb("WT", [P, DH, D])
        W = sb("W", [P, DH, D])
        g = sb("g", [P, 3, HEADS, HD])
        zero = sb("zero", [P, 2048])
        hmask = sb("hmask", [P, HPH])
        xn = sb("xn", [P, TPB, D])
        xT = sb("xT", [P, DH, T])
        w = sb("w", [P, TPB * HEADS, HD])
        sq = sb("sq", [P, TPB * HEADS, HD])
        ms = sb("ms", [P, TPB * HEADS])
        rs = sb("rs", [P, TPB * HEADS])
        q = sb("q", [P, 2, TPB, D])
        v = sb("v", [P, 2, TPB, HEADS * P + P - HD])
        QT = sb("QT", [P, 2, DH, T])
        KT = sb("KT", [P, DH, T])
        KTm = sb("KTm", [P, 2, HEADS, T])
        negm = sb("negm", [P, 2, 2, TPB])
        z = sb("z", [P, 2, 2, TPB])
        rz = sb("rz", [P, 2, 2, TPB])
        ex = sb("ex", [P, 2, 2, TPB, T])
        diag = sb("diag", [P, 2, 2, TPB, P])
        G = sb("G", [P, 2, 2, TPB, T])
        yT = sb("yT", [P, DH, T])
        S = {n: sem(n) for n in (
            "loaded padded zeroed stored hmade xn_ready xt_ps xt_ready w_ps w_ready sq_ready ms_ready rs_ready n_ready "
            "qk_ready v_ready qt_ps qt_ready kt_ps kt_ready km_ready s_ps negm_ready exp_done diag_ready pt_ps g_ready "
            "y_ps y_ready out_ps added own ownr").split()}

        moments = Moments(core, sem)
        with nc.Block() as block:
            @block.sync
            def _(sp):
                sp.dma_start(WT[:, :, :], core.dram["W2T"].rearrange("(h p) e -> p h e", p=P)).then_inc(S["loaded"], 16)
                sp.dma_start(W[:, :, :], core.dram["W2"].rearrange("(h p) e -> p h e", p=P)).then_inc(S["loaded"], 16)
                sp.dma_start(g[:, :, :, :], core.dram["g2"].rearrange("p (a h d) -> p a h d", a=3, h=HEADS)).then_inc(S["loaded"], 16)
                sp.wait_ge(S["zeroed"], 1)
                slots = core.slots_x.rearrange("(n p r) d -> n p (r d)", p=P, r=8)
                for k in range(SLOTS // 8):
                    sp.dma_start(slots[k], zero[:, :]).then_inc(S["stored"], 16)
                sp.wait_ge(S["stored"], SLOTS // 8 * 16)

            @block.tensor
            def _(pe):
                pe.wait_ge(S["loaded"], 3 * 16)

                def tokens(b):
                    pe.wait_ge(S["xn_ready"], b + 1)
                    for h in range(DH):
                        for k in range(TPB):
                            last = pe.transpose(PS[:, 7, h * T + k * P:h * T + k * P + P], xn[:, k, h * P:h * P + P],
                                                core.ident[:, :])
                    last.then_inc(S["xt_ps"], 1)

                def project(b):
                    pe.wait_ge(S["xt_ready"], b + 1)
                    for k in range(TPB):
                        for h in range(DH):
                            last = pe.matmul(PS[:, 7, k * D:k * D + D], xT[:, h, k * P:k * P + P], WT[:, h, :],
                                             start=(h == 0), stop=(h == DH - 1))
                    last.then_inc(S["w_ps"], 1)

                def turn(b, a, ready):
                    for h in range(DH):
                        for k in range(TPB):
                            last = pe.transpose(PS[:, 7, h * T + k * P:h * T + k * P + P], q[:, a, k, h * P:h * P + P],
                                                core.ident[:, :])
                    last.then_inc(ready, 1)

                def output(b):
                    pe.wait_ge(S["y_ready"], 2 * b + 3)
                    for k in range(TPB):
                        for h in range(DH):
                            last = pe.matmul(PS[:, 7, k * D:k * D + D], yT[:, h, k * P:k * P + P], W[:, h, :],
                                             start=(h == 0), stop=(h == DH - 1))
                    last.then_inc(S["out_ps"], 1)

                def scores(b, u, c):
                    if c == 0:
                        pe.wait_ge(S["qt_ready"], b + 1)
                    if c % (PAIRS // 2) == 0:
                        pe.wait_ge(S["km_ready"], 2 * b + 1 + c // (PAIRS // 2))
                    for i in range(2):
                        h = 2 * c + i
                        for k in range(TPB):
                            last = pe.matmul(PS[:, 2 * (c % 2) + i, k * T:k * T + T], QT[:, u, h // HPH, k * P:k * P + P],
                                             KTm[:, u, h, :], start=True, stop=True)
                    last.then_inc(S["s_ps"], 1)

                def first(b, u):
                    tokens(b)
                    project(b)
                    pe.wait_ge(S["w_ready"], 1)
                    pe.wait_ge(S["qk_ready"], 1)
                    turn(b, 1, S["kt_ps"])
                    pe.wait_ge(S["kt_ready"], 1)
                    turn(b, 0, S["qt_ps"])
                    scores(b, u, 0)
                    scores(b, u, 1)

                def body(b, u, prev, more):
                    for c in range(PAIRS):
                        n, w_ = PAIRS * b + c, c % 2
                        if c == 1 and more:
                            project(b + 1)
                        if c == 5 and more:
                            pe.wait_ge(S["kt_ready"], b + 2)
                            turn(b + 1, 0, S["qt_ps"])
                        pe.wait_ge(S["diag_ready"], n + 1)
                        pe.wait_ge(S["g_ready"], n + 1)
                        for i in range(2):
                            for j in range(TPB):
                                for k in range(TPB):
                                    last = pe.matmul(PS[:, 4 + i, j * T + k * P:j * T + k * P + P],
                                                     ex[:, w_, i, k, j * P:j * P + P], diag[:, w_, i, k, :],
                                                     start=True, stop=True)
                        last.then_inc(S["pt_ps"], 1)
                        if c + 2 < PAIRS:
                            scores(b, u, c + 2)
                        elif more:
                            scores(b + 1, 1 - u, c + 2 - PAIRS)
                        if c == 0 and more:
                            pe.wait_ge(S["qt_ready"], b + 1)
                            tokens(b + 1)
                        if c == 1 and prev:
                            if more:
                                pe.wait_ge(S["w_ready"], b + 2)
                            output(b - 1)
                        if c == 4 and more:
                            pe.wait_ge(S["qk_ready"], b + 2)
                            if prev:
                                pe.wait_ge(S["added"], b)
                            else:
                                pe.wait_ge(S["w_ready"], b + 2)
                            turn(b + 1, 1, S["kt_ps"])
                        if c == 0:
                            pe.wait_ge(S["v_ready"], b + 1)
                        if c % (PAIRS // 2) == 0:
                            pe.wait_ge(S["y_ready"], 2 * b + c // (PAIRS // 2) + 1)
                        pe.wait_ge(S["g_ready"], n + 2)
                        for i in range(2):
                            h = 2 * c + i
                            for j in range(TPB):
                                last = pe.matmul(PS[:, 6, 0:T], head_window(v[:, u, j, :], h), G[:, w_, i, j, :],
                                                 start=(h % HPH == 0 and j == 0), stop=(h % HPH == HPH - 1 and j == TPB - 1))
                        if c % (PAIRS // 2) == PAIRS // 2 - 1:
                            last.then_inc(S["y_ps"], 1)

                def finish(b, u):
                    pe.wait_ge(S["added"], b)
                    output(b)

                overlapped(pe, B, first, body, finish)

            @block.scalar
            def _(act):
                act.sem_inc(S["y_ready"], 1)

                def bank7(out, sem_in, sem_out, b):
                    act.wait_ge(sem_in, b + 1)
                    act.activation(out, PS[:, 7, :].rearrange("p (h t) -> p h t", h=out.shape[1]), ACT.Copy).then_inc(sem_out, 1)

                def heads_of(half, b):
                    act.wait_ge(S["y_ps"], 2 * b + half + 1)
                    act.activation(yT[:, half, :], PS[:, 6, 0:T], ACT.Copy).then_inc(S["y_ready"], 1)

                def exps(b, c):
                    n, w_ = PAIRS * b + c, c % 2
                    act.wait_ge(S["negm_ready"], n + 1)
                    act.wait_ge(S["g_ready"], n)
                    for i in range(2):
                        for k in range(TPB):
                            last = act.activation(ex[:, w_, i, k, :], PS[:, 2 * w_ + i, k * T:k * T + T], ACT.Exp,
                                                  bias=negm[:, w_, i, k:k + 1], accum_out=z[:, w_, i, k:k + 1])
                    last.then_inc(S["exp_done"], 1)

                def first(b, u):
                    bank7(xT[:, :, :], S["xt_ps"], S["xt_ready"], b)
                    bank7(w[:, :, :], S["w_ps"], S["w_ready"], b)
                    bank7(KT[:, :, :], S["kt_ps"], S["kt_ready"], b)
                    bank7(QT[:, u, :, :], S["qt_ps"], S["qt_ready"], b)
                    act.wait_ge(S["negm_ready"], 1)
                    for i in range(2):
                        for k in range(TPB):
                            last = act.activation(ex[:, 0, i, k, :], PS[:, i, k * T:k * T + T], ACT.Exp,
                                                  bias=negm[:, 0, i, k:k + 1], accum_out=z[:, 0, i, k:k + 1])
                    last.then_inc(S["exp_done"], 1)

                def body(b, u, prev, more):
                    for c in range(PAIRS):
                        if c == 0 and prev:
                            heads_of(1, b - 1)
                        if c == 4:
                            if prev:
                                act.wait_ge(S["out_ps"], b)
                            heads_of(0, b)
                        if c + 1 < PAIRS:
                            exps(b, c + 1)
                        elif more:
                            exps(b + 1, 0)
                        if more and c == 0:
                            bank7(xT[:, :, :], S["xt_ps"], S["xt_ready"], b + 1)
                        if more and c == 1:
                            bank7(w[:, :, :], S["w_ps"], S["w_ready"], b + 1)
                        if more and c == 4:
                            bank7(KT[:, :, :], S["kt_ps"], S["kt_ready"], b + 1)
                        if more and c == 5:
                            bank7(QT[:, 1 - u, :, :], S["qt_ps"], S["qt_ready"], b + 1)

                def finish(b, u):
                    heads_of(1, b)

                overlapped(act, B, first, body, finish)

            @block.gpsimd
            def _(pool):
                moments.pool(pool)
                pool.memset(zero[:, :], 0.0).then_inc(S["zeroed"], 1)
                pool.memset(v[:, :, :, :], 0.0).then_inc(S["padded"], 1)
                head_masks(pool, Chain(pool, S["hmade"], 3), hmask)
                pool.wait_ge(S["padded"], 1)
                pool.wait_ge(S["loaded"], 3 * 16)

                def step(b, u):
                    pool.wait_ge(S["w_ready"], b + 1)
                    pool.tensor_tensor(out=sq[:, :, :], in0=w[:, :, :], in1=w[:, :, :], op=ALU.mult).then_inc(S["sq_ready"], 1)
                    pool.wait_ge(S["ms_ready"], b + 1)
                    pool.tensor_tensor(out=rs[:, :], in0=ms[:, :], in1=core.half[:, 0:TPB * HEADS],
                                       op=ALU.pow).then_inc(S["rs_ready"], 1)
                    pool.wait_ge(S["n_ready"], b + 1)
                    for k in range(TPB):
                        own = v[:, u, k, 0:HEADS * P].rearrange("p (h c) -> p h c", h=HEADS)[:, :, P - HD:P]
                        last = pool.tensor_tensor(out=own, in0=w[:, k * HEADS:k * HEADS + HEADS, :], in1=g[:, 2, :, :],
                                                  op=ALU.mult)
                    last.then_inc(S["v_ready"], 1)
                    pool.wait_ge(S["kt_ready"], b + 1)
                    for half in range(DH):
                        mask_keys(pool, KTm[:, u, :, :], KT, hmask, half, T).then_inc(S["km_ready"], 1)

                in_pairs(pool, B, step)

            @block.vector
            def _(dve):
                moments.dve(dve)
                link = Chain(dve, S["own"], PAIRS)
                dve.sem_inc(S["g_ready"], 1)
                dve.wait_ge(S["loaded"], 3 * 16)
                dve.tensor_scalar(out=g[:, 1, :, :], in0=g[:, 1, :, :], scalar1=HD ** -0.5, scalar2=None,
                                  op0=ALU.mult)

                def normalise(b):
                    for k in range(TPB):
                        t = TPB * b + k
                        last = dve.tensor_scalar(out=xn[:, k, :], in0=X[:, bass.ds(t, 1), :],
                                                 scalar1=core.mean[:, bass.ds(t, 1)], scalar2=core.rstd[:, bass.ds(t, 1)],
                                                 op0=ALU.subtract, op1=ALU.mult)
                    last.then_inc(S["xn_ready"], 1)

                def squares(b):
                    dve.wait_ge(S["sq_ready"], b + 1)
                    red = Chain(dve, S["ownr"], 1)
                    red.start(b)
                    red(dve.tensor_reduce(out=ms[:, :], in_=sq[:, :, :], axis=AX.X, op=ALU.add))
                    dve.tensor_scalar(out=ms[:, :], in0=ms[:, :], scalar1=1.0 / HD, scalar2=RMS_EPS, op0=ALU.mult,
                                      op1=ALU.add).then_inc(S["ms_ready"], 1)

                def queries(b):
                    dve.wait_ge(S["rs_ready"], b + 1)
                    r = rs[:, :].rearrange("p (n d) -> p n d", d=1).broadcast_to([P, TPB * HEADS, HD])
                    dve.tensor_tensor(out=w[:, :, :], in0=w[:, :, :], in1=r, op=ALU.mult).then_inc(S["n_ready"], 1)
                    dve.wait_ge(S["n_ready"], b + 1)
                    for k in range(TPB):
                        for a in range(2):
                            last = dve.tensor_tensor(out=q[:, a, k, :].rearrange("p (h d) -> p h d", d=HD),
                                                     in0=w[:, k * HEADS:k * HEADS + HEADS, :], in1=g[:, a, :, :], op=ALU.mult)
                    last.then_inc(S["qk_ready"], 1)

                def maxima(b, c):
                    w_ = c % 2
                    dve.wait_ge(S["s_ps"], PAIRS * b + c + 1)
                    dve.tensor_reduce(out=negm[:, w_, :, :].rearrange("p i k -> p (i k)"),
                                      in_=PS[:, 2 * w_:2 * w_ + 2, :].rearrange("p i (k t) -> p (i k) t", k=TPB),
                                      axis=AX.X, op=ALU.max, negate=True).then_inc(S["negm_ready"], 1)

                def diagonals(b, c):
                    w_ = c % 2
                    dve.wait_ge(S["exp_done"], PAIRS * b + c + 1)
                    link.start(b, c)
                    link(dve.reciprocal(out=rz[:, w_, :, :], in_=z[:, w_, :, :]))
                    for i in range(2):
                        for k in range(TPB):
                            last = dve.tensor_scalar(out=diag[:, w_, i, k, :], in0=core.ident[:, :],
                                                     scalar1=rz[:, w_, i, k:k + 1], scalar2=None, op0=ALU.mult)
                    last.then_inc(S["diag_ready"], 1)

                def combine(b, c):
                    w_ = c % 2
                    dve.wait_ge(S["pt_ps"], PAIRS * b + c + 1)
                    for i in range(2):
                        for j in range(TPB):
                            last = dve.scalar_tensor_tensor(out=G[:, w_, i, j, :], in0=ex[:, w_, i, j, :],
                                                            scalar=rz[:, w_, i, j:j + 1], in1=PS[:, 4 + i, j * T:j * T + T],
                                                            op0=ALU.mult, op1=ALU.add)
                    last.then_inc(S["g_ready"], 1)

                def add(b):
                    dve.wait_ge(S["out_ps"], b + 1)
                    t = TPB * b
                    dve.tensor_tensor(out=X[:, bass.ds(t, TPB), :], in0=X[:, bass.ds(t, TPB), :],
                                      in1=PS[:, 7, :].rearrange("p (k d) -> p k d", k=TPB), op=ALU.add).then_inc(S["added"], 1)
                    dve.wait_ge(S["added"], b + 1)
                    tile_statistics(core, dve, X, t, TPB)

                def first(b, u):
                    normalise(b)
                    squares(b)
                    queries(b)
                    maxima(b, 0)
                    maxima(b, 1)
                    diagonals(b, 0)

                def body(b, u, prev, more):
                    for c in range(PAIRS):
                        if c == 0 and more:
                            normalise(b + 1)
                        combine(b, c)
                        if c + 1 < PAIRS:
                            diagonals(b, c + 1)
                        elif more:
                            diagonals(b + 1, 0)
                        if c + 2 < PAIRS:
                            maxima(b, c + 2)
                        elif more:
                            maxima(b + 1, c + 2 - PAIRS)
                        if c == 1 and prev:
                            add(b - 1)
                        if c == 2 and more:
                            squares(b + 1)
                        if c == 3 and more:
                            queries(b + 1)

                def finish(b, u):
                    add(b)

                overlapped(dve, B, first, body, finish)


EXPERTS = 32
TL = P // B


def crossed(rows, tl):
    return rows.rearrange("(s g l) d -> l s g d", s=B, l=TL)[tl]


def masked_experts(core):
    nc = core.nc
    with ExitStack() as keep:
        def sb(tag, shape, dt=F32):
            return keep.enter_context(nc.sbuf_tensor("me_" + tag, shape, dt))

        rows = sb("rows", [P, NT, D])
        logits = sb("logits", [P, NT, EXPERTS])
        slot = sb("slot", [P, NT], I32)
        slot_x = sb("slot_x", [P, NT], I32)
        weight_x = sb("weight_x", [P, NT])
        expert = sb("expert", [P, SLOTS], I32)
        Xc = sb("Xc", [P, NT, D])
        router_logits(core, rows, logits)
        route_top1(core, rows, logits, slot, slot_x, weight_x, expert, Xc)
        expert_tiles(core, expert)
        collect_top1(core, rows, slot_x, weight_x, Xc)


def router_logits(core, rows, logits):
    nc, X, PS = core.nc, core.X, core.PS
    with core.stage("rl") as (sb, sem):
        R = sb("R", [P, DH, EXPERTS])
        xn = sb("xn", [P, 2, D])
        xT = sb("xT", [P, 2, DH, P])
        loaded, xn_ready, xt_ps, xt_ready, lg_ps, lg_free = (
            sem(x) for x in ("loaded", "xn_ready", "xt_ps", "xt_ready", "lg_ps", "lg_free"))
        moments = Moments(core, sem)
        with nc.Block() as block:
            @block.sync
            def _(sp):
                sp.dma_start(R[:, :, :], core.dram["router"].rearrange("(h p) e -> p h e", p=P)).then_inc(loaded, 16)

            @block.vector
            def _(dve):
                moments.dve(dve)
                dve.sem_inc(xt_ps, 2)

                def normalise(out, t):
                    return dve.tensor_scalar(out=out, in0=X[:, bass.ds(t, 1), :], scalar1=core.mean[:, bass.ds(t, 1)],
                                             scalar2=core.rstd[:, bass.ds(t, 1)], op0=ALU.subtract, op1=ALU.mult)

                def step(t, u):
                    dve.wait_ge(xt_ps, t + 1)
                    normalise(xn[:, u, :], t).then_inc(xn_ready, 1)
                    normalise(rows[:, bass.ds(t, 1), :], t)

                in_pairs(dve, NT, step)

            @block.gpsimd
            def _(pool):
                moments.pool(pool)

            @block.scalar
            def _(act):
                act.sem_inc(lg_free, 2)

                def front(t, u):
                    act.wait_ge(xt_ps, t + 3)
                    act.activation(xT[:, u, :, :], PS[:, u, 0:D].rearrange("p (h t) -> p h t", h=DH),
                                   ACT.Copy).then_inc(xt_ready, 1)

                def back(t, u):
                    act.wait_ge(lg_ps, t + 1)
                    act.activation(logits[:, bass.ds(t, 1), :], PS[:, 2 + u, 0:EXPERTS], ACT.Copy).then_inc(lg_free, 1)

                skewed(act, NT, front, back)

            @block.tensor
            def _(pe):
                pe.wait_ge(loaded, 16)

                def front(t, u):
                    pe.wait_ge(xn_ready, t + 1)
                    for h in range(DH):
                        last = pe.transpose(PS[:, u, h * P:h * P + P], xn[:, u, h * P:h * P + P], core.ident[:, :])
                    last.then_inc(xt_ps, 1)

                def back(t, u):
                    pe.wait_ge(xt_ready, t + 1)
                    pe.wait_ge(lg_free, t + 1)
                    for h in range(DH):
                        last = pe.matmul(PS[:, 2 + u, 0:EXPERTS], xT[:, u, h, :], R[:, h, :], start=(h == 0), stop=(h == DH - 1))
                    last.then_inc(lg_ps, 1)

                skewed(pe, NT, front, back)


def route_top1(core, rows, logits, slot, slot_x, weight_x, expert, Xc):
    nc, X, PS = core.nc, core.X, core.PS
    E = EXPERTS
    HB = NT // 2
    with core.stage("rt") as (sb, sem):
        iota_e = sb("iota_e", [P, NT, E])
        iota_s = sb("iota_s", [P, SLOTS])
        reset = sb("reset", [P, E, NT])
        before = sb("before", [P, P], BF16)
        ones = sb("ones", [P, P], BF16)
        one_e = sb("one_e", [P, E])
        top = sb("top", [P, NT])
        shifted = sb("shifted", [P, NT, E])
        work = sb("work", [P, NT, E])
        first = sb("first", [P, NT])
        hot = sb("hot", [P, NT, E], BF16)
        count = sb("count", [P, E, NT])
        upto = sb("upto", [P, E, NT])
        tiles = sb("tiles", [P, 4, E])
        tiles_i = sb("tiles_i", [P, E], I32)
        slot_f = sb("slot_f", [P, NT])
        table = sb("table", [P, NT, 2])
        table_x = sb("table_x", [P, NT, 2])
        cmp = sb("cmp", [P, SLOTS, E])
        S = {n: sem(n) for n in "made slot_ready scattered x_stored x_loaded shifted exp_done hot_ready count_ps own table_ready table_stored table_loaded".split()}
        dram_x, dram_t = core.scratch_x, core.scratch_t
        with nc.Block() as block:
            @block.sync
            def _(sp):
                xr = dram_x.rearrange("(n p) d -> p n d", p=P)
                for k in range(4):
                    sp.dma_start(xr[:, 8 * k:8 * k + 8, :], X[:, 8 * k:8 * k + 8, :]).then_inc(S["x_stored"], 16)
                sp.wait_ge(S["x_stored"], 4 * 16)
                for tl in range(TL):
                    sp.dma_start(Xc[tl * B:tl * B + B, :, :], crossed(dram_x, tl)).then_inc(S["x_loaded"], 16)
                sp.wait_ge(S["table_ready"], 1)
                sp.dma_start(dram_t.rearrange("(n p) d -> p n d", p=P), table[:, :, :]).then_inc(S["table_stored"], 16)
                sp.wait_ge(S["table_stored"], 16)
                for tl in range(TL):
                    sp.dma_start(table_x[tl * B:tl * B + B, :, :], crossed(dram_t, tl)).then_inc(S["table_loaded"], 16)
                sp.wait_ge(S["x_loaded"], TL * 16)

            @block.gpsimd
            def _(pool):
                made = S["made"]
                pool.iota(iota_e[:, :, :], [[0, NT], [1, E]], base=-64, channel_multiplier=0,
                          allow_small_or_imprecise_dtypes=True).then_inc(made, 1)
                pool.iota(iota_s[:, :], [[1, SLOTS]], base=0, channel_multiplier=0,
                          allow_small_or_imprecise_dtypes=True).then_inc(made, 1)
                pool.memset(reset[:, :, :], 1.0).then_inc(made, 1)
                pool.memset(ones[:, :], 1.0).then_inc(made, 1)
                pool.memset(one_e[:, :], 1.0).then_inc(made, 1)
                pool.memset(before[:, :], 1.0).then_inc(made, 1)
                pool.wait_ge(made, 6)
                pool.memset(reset[:, :, 0:1], 0.0).then_inc(made, 1)
                pool.affine_select(out=before[:, :], in_=before[:, :], compare_op=ALU.is_gt, fill=0.0, base=0,
                                   pattern=[[1, P]], channel_multiplier=-1).then_inc(made, 1)
                pool.wait_ge(S["slot_ready"], 1)
                for t in range(NT):
                    pool.indirect_dma_start(out=core.slots_x[:, :], out_offset=bass.IndirectOffsetOnAxis(ap=slot[:, t:t + 1], axis=0),
                                            in_=rows[:, t, :], in_offset=None).then_inc(S["scattered"], 16)
                pool.wait_ge(S["scattered"], NT * 16)

            @block.scalar
            def _(act):
                act.wait_ge(S["shifted"], 1)
                act.activation(shifted[:, :, :], shifted[:, :, :], ACT.Exp).then_inc(S["exp_done"], 1)

            @block.tensor
            def _(pe):
                pe.wait_ge(S["made"], 8)
                pe.wait_ge(S["hot_ready"], 1)
                for w, bank in ((before, 0), (ones, 2)):
                    for k in range(2):
                        last = pe.matmul(PS[:, bank + k, :], w[:, :], hot[:, k * HB:k * HB + HB, :], start=True, stop=True)
                last.then_inc(S["count_ps"], 1)

            @block.vector
            def _(dve):
                link = Chain(dve, S["own"], 40)

                def over_e(a, n=NT):
                    return a.rearrange("p (n e) -> p n e", e=1).broadcast_to([P, n, E])

                dve.wait_ge(S["made"], 8)
                link(dve.tensor_reduce(out=top[:, :], in_=logits[:, :, :], axis=AX.X, op=ALU.max))
                link(dve.tensor_tensor(out=shifted[:, :, :], in0=logits[:, :, :], in1=over_e(top[:, :]), op=ALU.subtract))
                link(dve.tensor_single_scalar(out=work[:, :, :], in_=shifted[:, :, :], scalar=0.0, op=ALU.is_equal))
                dve.sem_inc(S["shifted"], 1)
                link(dve.tensor_tensor(out=work[:, :, :], in0=work[:, :, :], in1=iota_e[:, :, :], op=ALU.mult))
                link(dve.tensor_reduce(out=first[:, :], in_=work[:, :, :], axis=AX.X, op=ALU.min))
                link(dve.tensor_tensor(out=hot[:, :, :], in0=iota_e[:, :, :], in1=over_e(first[:, :]), op=ALU.is_equal))
                dve.sem_inc(S["hot_ready"], 1)
                dve.wait_ge(S["exp_done"], 1)
                link(dve.tensor_reduce(out=top[:, :], in_=shifted[:, :, :], axis=AX.X, op=ALU.add))
                link(dve.reciprocal(out=table[:, :, 1], in_=top[:, :]))
                dve.wait_ge(S["count_ps"], 1)
                for k in range(2):
                    link(dve.tensor_copy(count[:, :, k * HB:k * HB + HB],
                                         PS[:, 2 + k, :].rearrange("p (n e) -> p e n", e=E)))
                link(dve.tensor_tensor_scan(out=upto[:, :, :].rearrange("p e n -> p (e n)"),
                                            data0=reset[:, :, :].rearrange("p e n -> p (e n)"),
                                            data1=count[:, :, :].rearrange("p e n -> p (e n)"), initial=0.0,
                                            op0=ALU.mult, op1=ALU.add))
                link(dve.tensor_tensor(out=count[:, :, :], in0=upto[:, :, :], in1=count[:, :, :], op=ALU.subtract))
                link(dve.tensor_scalar(out=tiles_i[:, :], in0=upto[:, :, NT - 1], scalar1=float(P - 1), scalar2=None, op0=ALU.add))
                link(dve.tensor_single_scalar(out=tiles_i[:, :], in_=tiles_i[:, :], scalar=7, op=ALU.arith_shift_right))
                link(dve.tensor_copy(tiles[:, 0, :], tiles_i[:, :]))
                link(dve.tensor_tensor_scan(out=tiles[:, 1, :], data0=one_e[:, :], data1=tiles[:, 0, :], initial=0.0,
                                            op0=ALU.mult, op1=ALU.add))
                link(dve.tensor_tensor(out=tiles[:, 2, :], in0=tiles[:, 1, :], in1=tiles[:, 0, :], op=ALU.subtract))
                link(dve.tensor_scalar(out=tiles[:, 2, :], in0=tiles[:, 2, :], scalar1=float(P), scalar2=None, op0=ALU.mult))
                first_slot = tiles[:, 2, :].rearrange("p (e n) -> p e n", n=1).broadcast_to([P, E, NT])
                link(dve.tensor_tensor(out=count[:, :, :], in0=count[:, :, :], in1=first_slot, op=ALU.add))
                for k in range(2):
                    link(dve.tensor_tensor(out=work[:, k * HB:k * HB + HB, :],
                                           in0=PS[:, k, :].rearrange("p (n e) -> p n e", e=E),
                                           in1=count[:, :, k * HB:k * HB + HB].rearrange("p e n -> p n e"), op=ALU.add))
                link(dve.tensor_tensor(out=work[:, :, :], in0=work[:, :, :], in1=hot[:, :, :], op=ALU.mult))
                link(dve.tensor_reduce(out=slot_f[:, :], in_=work[:, :, :], axis=AX.X, op=ALU.add))
                link(dve.tensor_copy(slot[:, :], slot_f[:, :]))
                dve.sem_inc(S["slot_ready"], 1)
                link(dve.tensor_copy(table[:, :, 0], slot_f[:, :]))
                dve.sem_inc(S["table_ready"], 1)
                end = tiles[:, 1, :].rearrange("p (n e) -> p n e", n=1).broadcast_to([P, SLOTS, E])
                link(dve.tensor_tensor(out=cmp[:, :, :], in0=end, in1=over_e(iota_s[:, :], SLOTS), op=ALU.is_le))
                link(dve.tensor_reduce(out=iota_s[:, :], in_=cmp[:, :, :], axis=AX.X, op=ALU.add))
                link(dve.tensor_scalar(out=expert[:, :], in0=iota_s[:, :], scalar1=float(E - 1), scalar2=None, op0=ALU.min))
                dve.wait_ge(S["table_loaded"], TL * 16)
                dve.tensor_copy(slot_x[:, :], table_x[:, :, 0])
                dve.tensor_copy(weight_x[:, :], table_x[:, :, 1])


def expert_tiles(core, expert):
    nc, PS = core.nc, core.PS
    ROUND = 1.5 * 2.0 ** 23
    NB = 4
    with core.stage("et") as (sb, sem):
        wq = sb("wq", [P, DH, D])
        scale = sb("scale", [P, D])
        x = sb("x", [P, NB, D])
        mask = sb("mask", [P, NB, DH, D])
        Wm = sb("Wm", [P, 2, DH, D])
        xT = sb("xT", [P, 2, DH, P])
        y = sb("y", [P, NB, D])
        S = {n: sem(n) for n in "w_loaded own w_ready free wm_ready xt_ps xt_ready y_ps y_read wm_free".split()}
        x_in = [sem(f"x_in{k}") for k in range(NB)]
        m_in = [sem(f"m_in{k}") for k in range(NB)]
        y_out = [sem(f"y_out{k}") for k in range(NB)]

        def in_fours(eng, step):
            with eng.Fori(0, SLOTS // NB) as i:
                for k in range(NB):
                    step(i, k)

        with nc.Block() as block:
            @block.sync
            def _(sp):
                sp.dma_start(wq[:, :, :], core.dram["W3T"].rearrange("(h p) e -> p h e", p=P)).then_inc(S["w_loaded"], 16)
                sp.dma_start(scale[:, :], core.dram["scale"]).then_inc(S["w_loaded"], 16)
                def step(i, k):
                    s = NB * i + k
                    sp.wait_ge(S["free"], s + 1)
                    e = sp.value_load(expert[0:1, bass.ds(s, 1)], min_val=0, max_val=EXPERTS - 1)
                    sp.dma_start(x[:, k, :], core.slots_x[bass.ds(s * P, P), :]).then_inc(x_in[k], 16)
                    sp.dma_start(mask[:, k, :, :], core.dram["masks"][bass.ds(e, 1), :, :].rearrange("n (h p) o -> p (n h) o", p=P)).then_inc(m_in[k], 16)

                in_fours(sp, step)

            @block.gpsimd
            def _(pool):
                pool.wait_ge(S["w_ready"], 1)

                def step(i, k):
                    pool.wait_ge(m_in[k], 16 * i + 16)
                    pool.wait_ge(S["wm_free"], NB * i + k + 1)
                    pool.tensor_tensor(out=Wm[:, k % 2, :, :], in0=mask[:, k, :, :], in1=wq[:, :, :],
                                       op=ALU.mult).then_inc(S["wm_ready"], 1)

                in_fours(pool, step)

            @block.vector
            def _(dve):
                link = Chain(dve, S["own"], 3)
                dve.wait_ge(S["w_loaded"], 2 * 16)
                link(dve.tensor_scalar(out=wq[:, :, :], in0=wq[:, :, :], scalar1=2.0, scalar2=ROUND, op0=ALU.mult, op1=ALU.add))
                link(dve.tensor_scalar(out=wq[:, :, :], in0=wq[:, :, :], scalar1=ROUND, scalar2=1.0, op0=ALU.subtract, op1=ALU.min))
                for h in range(DH):
                    last = dve.scalar_tensor_tensor(out=wq[:, h, :], in0=wq[:, h, :], scalar=-1.0, in1=scale[:, :],
                                                    op0=ALU.max, op1=ALU.mult)
                last.then_inc(S["w_ready"], 1)
                dve.sem_inc(S["free"], NB)
                dve.sem_inc(S["wm_free"], 2)

                def step(i, k):
                    s = NB * i + k
                    dve.wait_ge(S["xt_ps"], s + 1)
                    dve.tensor_copy(xT[:, k % 2, :, :], PS[:, k % 2, 0:D].rearrange("p (h t) -> p h t", h=DH)).then_inc(S["xt_ready"], 1)
                    dve.wait_ge(S["y_ps"], s + 1)
                    dve.sem_inc(S["wm_free"], 1)
                    dve.sem_inc(S["free"], 1)

                in_fours(dve, step)

            @block.tensor
            def _(pe):
                def front(i, k):
                    pe.wait_ge(x_in[k], 16 * i + 16)
                    for h in range(DH):
                        last = pe.transpose(PS[:, k % 2, h * P:h * P + P], x[:, k, h * P:h * P + P], core.ident[:, :])
                    last.then_inc(S["xt_ps"], 1)

                def back(i, k):
                    s = NB * i + k
                    pe.wait_ge(S["xt_ready"], s + 1)
                    pe.wait_ge(S["wm_ready"], s + 1)
                    pe.wait_ge(S["y_read"], s + 1)
                    for h in range(DH):
                        last = pe.matmul(PS[:, 2 + k % 2, 0:D], xT[:, k % 2, h, :], Wm[:, k % 2, h, :],
                                         start=(h == 0), stop=(h == DH - 1))
                    last.then_inc(S["y_ps"], 1)

                front(0, 0)
                with pe.Fori(0, SLOTS // NB - 1) as i:
                    for k in range(NB):
                        front(i + (k + 1) // NB, (k + 1) % NB)
                        back(i, k)
                last = SLOTS // NB - 1
                for k in range(NB):
                    if k + 1 < NB:
                        front(last, k + 1)
                    back(last, k)

            @block.scalar
            def _(act):
                act.sem_inc(S["y_read"], 2)

                for k in range(NB):
                    act.sem_inc(y_out[k], 16)

                def step(i, k):
                    s = NB * i + k
                    act.wait_ge(S["y_ps"], s + 1)
                    act.wait_ge(y_out[k], 16 * i + 16)
                    act.activation(y[:, k, :], PS[:, 2 + k % 2, 0:D], ACT.Copy).then_inc(S["y_read"], 1)
                    act.wait_ge(S["y_read"], s + 3)
                    act.dma_start(core.slots_y[bass.ds(s * P, P), :], y[:, k, :]).then_inc(y_out[k], 16)

                in_fours(act, step)
                for k in range(NB):
                    act.wait_ge(y_out[k], 16 * (SLOTS // NB) + 16)


def collect_top1(core, rows, slot_x, weight_x, Xc):
    nc, X = core.nc, core.X
    with core.stage("ct") as (sb, sem):
        fetched = [sem(f"fetched{k}") for k in range(4)]
        added = sem("added")
        with nc.Block() as block:
            @block.gpsimd
            def _(pool):
                for t in range(NT):
                    pool.indirect_dma_start(out=rows[:, t, :], out_offset=None, in_=core.slots_y[:, :],
                                            in_offset=bass.IndirectOffsetOnAxis(ap=slot_x[:, t:t + 1], axis=0)).then_inc(fetched[t // 8], 16)

            @block.vector
            def _(dve):
                def add(t):
                    dve.scalar_tensor_tensor(out=X[:, bass.ds(t, 1), :], in0=rows[:, bass.ds(t, 1), :],
                                             scalar=weight_x[:, bass.ds(t, 1)], in1=Xc[:, bass.ds(t, 1), :],
                                             op0=ALU.mult, op1=ALU.add).then_inc(added, 1)

                for k in range(4):
                    dve.wait_ge(fetched[k], 8 * 16)
                    add(8 * k)
                    with dve.Fori(8 * k + 1, 8 * k + 8) as t:
                        add(t)
                        dve.wait_ge(added, t)
                        tile_statistics(core, dve, X, t - 1)
                    dve.wait_ge(added, 8 * k + 8)
                    tile_statistics(core, dve, X, 8 * k + 7)


def crossed_attention(core):
    nc, X, PS = core.nc, core.X, core.PS
    G4 = 4
    NG4 = HEADS // G4
    with core.stage("ca") as (sb, sem):
        W = sb("W", [P, DH, 3 * D])
        bias = sb("bias", [P, 3, D])
        Wo = sb("Wo", [P, DH, D])
        bias_o = sb("bias_o", [P, D])
        mask = sb("mask", [P, G4, TL, B], BF16)
        hmask = sb("hmask", [P, HPH])
        xn = sb("xn", [P, D])
        xT = sb("xT", [P, DH, P])
        qk = sb("qk", [P, 2, D])
        v = sb("v", [P, 2, HEADS * P + P - HD])
        QT = sb("QT", [P, 2, DH, P])
        KT = sb("KT", [P, 2, DH, P])
        KTm = sb("KTm", [P, 2, HEADS, P])
        negm = sb("negm", [P, 2, G4])
        z = sb("z", [P, 2, G4])
        rz = sb("rz", [P, 2, G4])
        ex = sb("ex", [P, 2, G4, P])
        diag = sb("diag", [P, 2, G4, P])
        PT = sb("PT", [P, 2, G4, P])
        yT = sb("yT", [P, 2, DH, P])
        S = {n: sem(n) for n in (
            "loaded padded masked hmade ownm xn_ready biased xt_ps xt_ready qkv_ps qkv_ready qt_ps kt_ps qt_ready kt_ready "
            "km_ready s_ps negm_ready exp_done diag_ready pt_ps pt_ready y_ps y_ready out_ps added own").split()}

        moments = Moments(core, sem)
        with nc.Block() as block:
            @block.sync
            def _(sp):
                sp.dma_start(W[:, :, :], core.dram["w_qkvT"].rearrange("(h p) e -> p h e", p=P)).then_inc(S["loaded"], 16)
                sp.dma_start(bias[:, :, :], core.dram["b_qkv"].rearrange("p (a d) -> p a d", a=3)).then_inc(S["loaded"], 16)
                sp.dma_start(Wo[:, :, :], core.dram["w_denseT"].rearrange("(h p) e -> p h e", p=P)).then_inc(S["loaded"], 16)
                sp.dma_start(bias_o[:, :], core.dram["b_dense"]).then_inc(S["loaded"], 16)

            @block.gpsimd
            def _(pool):
                moments.pool(pool)
                pool.memset(v[:, :, :], 0.0).then_inc(S["padded"], 1)
                head_masks(pool, Chain(pool, S["hmade"], 3), hmask)
                link = Chain(pool, S["ownm"], 4)
                m = mask[:, :, :, :]
                link(pool.memset(m, 0.0))
                link(pool.affine_select(out=m, in_=m, compare_op=ALU.is_ge, fill=-1e4, base=0,
                                        pattern=[[0, G4], [-B, TL], [-1, B]], channel_multiplier=1))
                link(pool.affine_select(out=m, in_=m, compare_op=ALU.is_ge, fill=-1e30, base=B - 1,
                                        pattern=[[0, G4], [B, TL], [0, B]], channel_multiplier=-1))
                link(pool.affine_select(out=m, in_=m, compare_op=ALU.is_ge, fill=-1e30, base=0,
                                        pattern=[[0, G4], [-B, TL], [0, B]], channel_multiplier=1))
                pool.sem_inc(S["masked"], 1)
                pool.wait_ge(S["loaded"], 4 * 16)

                def step(t, u):
                    pool.wait_ge(S["kt_ready"], t + 1)
                    for c in range(NG4):
                        r = slice(G4 * c % HPH, G4 * c % HPH + G4)
                        pool.tensor_tensor(out=KTm[:, u, G4 * c:G4 * c + G4, :],
                                           in0=KT[:, u, c // 2:c // 2 + 1, :].broadcast_to([P, G4, P]),
                                           in1=hmask[:, r].rearrange("p (h t) -> p h t", t=1).broadcast_to([P, G4, P]),
                                           op=ALU.mult).then_inc(S["km_ready"], 1)
                    pool.wait_ge(S["xn_ready"], t + 1)
                    pool.tensor_tensor(out=X[:, bass.ds(t, 1), :], in0=X[:, bass.ds(t, 1), :], in1=bias_o[:, :],
                                       op=ALU.add).then_inc(S["biased"], 1)

                in_pairs(pool, NT, step)

            @block.tensor
            def _(pe):
                pe.wait_ge(S["loaded"], 4 * 16)
                pe.wait_ge(S["masked"], 1)

                def tokens(t):
                    pe.wait_ge(S["xn_ready"], t + 1)
                    for h in range(DH):
                        last = pe.transpose(PS[:, 5, h * P:h * P + P], xn[:, h * P:h * P + P], core.ident[:, :])
                    last.then_inc(S["xt_ps"], 1)

                def project(t):
                    pe.wait_ge(S["xt_ready"], t + 1)
                    for bank, at, n in ((6, 0, 2 * D), (7, 2 * D, D)):
                        for h in range(DH):
                            last = pe.matmul(PS[:, bank, 0:n], xT[:, h, :], W[:, h, at:at + n], start=(h == 0), stop=(h == DH - 1))
                    last.then_inc(S["qkv_ps"], 1)

                def heads(t):
                    pe.wait_ge(S["qkv_ready"], t + 1)
                    for a, ready in ((1, S["kt_ps"]), (0, S["qt_ps"])):
                        for h in range(DH):
                            last = pe.transpose(PS[:, 5, (a * DH + h) * P:(a * DH + h) * P + P], qk[:, a, h * P:h * P + P],
                                                core.ident[:, :])
                        last.then_inc(ready, 1)

                def scores(t, u, c):
                    if c == 0:
                        pe.wait_ge(S["qt_ready"], t + 1)
                    pe.wait_ge(S["km_ready"], NG4 * t + c + 1)
                    pe.matmul(PS[:, c % 2, :], core.identb[:, :], mask[:, :, :, :], start=True, stop=False)
                    pe.matmul(PS[:, c % 2, :], QT[:, u, c // 2, :], KTm[:, u, G4 * c:G4 * c + G4, :],
                              start=False, stop=True).then_inc(S["s_ps"], 1)

                def output(t, u):
                    pe.wait_ge(S["y_ready"], 2 * t + 3)
                    for h in range(DH):
                        last = pe.matmul(PS[:, 7, 0:D], yT[:, u, h, :], Wo[:, h, :], start=(h == 0), stop=(h == DH - 1))
                    last.then_inc(S["out_ps"], 1)

                def first(t, u):
                    tokens(t)
                    project(t)
                    heads(t)
                    scores(t, u, 0)
                    scores(t, u, 1)

                def body(t, u, prev, more):
                    for c in range(NG4):
                        n, w = NG4 * t + c, c % 2
                        pe.wait_ge(S["diag_ready"], n + 1)
                        for i in range(G4):
                            last = pe.matmul(PS[:, 2 + w, i * P:i * P + P], ex[:, w, i, :], diag[:, w, i, :],
                                             start=True, stop=True)
                        last.then_inc(S["pt_ps"], 1)
                        if c == 0 and more:
                            tokens(t + 1)
                        if c + 2 < NG4:
                            scores(t, u, c + 2)
                        elif more:
                            scores(t + 1, 1 - u, c + 2 - NG4)
                        if c == 2 and prev:
                            output(t - 1, 1 - u)
                        if c == 0 and more:
                            if prev:
                                pe.wait_ge(S["added"], t - 1 + 1)
                            project(t + 1)
                        if c % 2 == 0:
                            pe.wait_ge(S["y_ready"], 2 * t + c // 2 + 1)
                        pe.wait_ge(S["pt_ready"], n + 1)
                        for i in range(G4):
                            h = G4 * c + i
                            last = pe.matmul(PS[:, 4, 0:P], head_window(v[:, u, :], h), PT[:, w, i, :],
                                             start=(h % HPH == 0), stop=(h % HPH == HPH - 1))
                        if c % 2:
                            last.then_inc(S["y_ps"], 1)
                        if c == 0 and more:
                            heads(t + 1)

                def finish(t, u):
                    pe.wait_ge(S["added"], t + 1)
                    output(t, u)

                overlapped(pe, NT, first, body, finish)

            @block.scalar
            def _(act):
                act.sem_inc(S["y_ready"], 1)

                def tokens(t):
                    act.wait_ge(S["xt_ps"], t + 1)
                    act.activation(xT[:, :, :], PS[:, 5, 0:D].rearrange("p (h t) -> p h t", h=DH),
                                   ACT.Copy).then_inc(S["xt_ready"], 1)

                def heads(t, u):
                    act.wait_ge(S["kt_ps"], t + 1)
                    act.wait_ge(S["qt_ps"], t + 1)
                    act.activation(KT[:, u, :, :], PS[:, 5, D:2 * D].rearrange("p (h t) -> p h t", h=DH),
                                   ACT.Copy).then_inc(S["kt_ready"], 1)
                    act.activation(QT[:, u, :, :], PS[:, 5, 0:D].rearrange("p (h t) -> p h t", h=DH),
                                   ACT.Copy, scale=HD ** -0.5).then_inc(S["qt_ready"], 1)

                def exps(t, c, start=False):
                    w = c % 2
                    act.wait_ge(S["negm_ready"], NG4 * t + c + 1)
                    if not start:
                        act.wait_ge(S["pt_ps"], NG4 * t + c - 1)
                    for i in range(G4):
                        last = act.activation(ex[:, w, i, :], PS[:, w, i * P:i * P + P], ACT.Exp,
                                              bias=negm[:, w, i:i + 1], accum_out=z[:, w, i:i + 1])
                    last.then_inc(S["exp_done"], 1)

                def heads_of(half, t, u):
                    act.wait_ge(S["y_ps"], 2 * t + half + 1)
                    act.activation(yT[:, u, half, :], PS[:, 4, 0:P], ACT.Copy).then_inc(S["y_ready"], 1)

                def first(t, u):
                    tokens(t)
                    heads(t, u)
                    exps(t, 0, True)

                def body(t, u, prev, more):
                    for c in range(NG4):
                        if c == 0 and prev:
                            heads_of(1, t - 1, 1 - u)
                        if c == 1 and more:
                            heads(t + 1, 1 - u)
                        if c == 2:
                            heads_of(0, t, u)
                        if c + 1 < NG4:
                            exps(t, c + 1, not prev and c == 0)
                        elif more:
                            exps(t + 1, 0)
                        if c == 0 and more:
                            tokens(t + 1)

                def finish(t, u):
                    heads_of(1, t, u)

                overlapped(act, NT, first, body, finish)

            @block.vector
            def _(dve):
                moments.dve(dve)
                link = Chain(dve, S["own"], NG4)
                dve.sem_inc(S["added"], 1)
                dve.wait_ge(S["loaded"], 4 * 16)
                dve.wait_ge(S["padded"], 1)

                def tokens(t):
                    dve.tensor_scalar(out=xn[:, :], in0=X[:, bass.ds(t, 1), :], scalar1=core.mean[:, bass.ds(t, 1)],
                                      scalar2=core.rstd[:, bass.ds(t, 1)], op0=ALU.subtract,
                                      op1=ALU.mult).then_inc(S["xn_ready"], 1)

                def project(t, u):
                    dve.wait_ge(S["qkv_ps"], t + 1)
                    dve.tensor_tensor(out=qk[:, :, :], in0=PS[:, 6, :].rearrange("p (a d) -> p a d", a=2),
                                      in1=bias[:, 0:2, :], op=ALU.add)
                    own = v[:, u, 0:HEADS * P].rearrange("p (h c) -> p h c", h=HEADS)[:, :, P - HD:P]
                    dve.tensor_tensor(out=own, in0=PS[:, 7, 0:D].rearrange("p (h d) -> p h d", h=HEADS),
                                      in1=bias[:, 2, :].rearrange("p (h d) -> p h d", h=HEADS),
                                      op=ALU.add).then_inc(S["qkv_ready"], 1)

                def maxima(t, c):
                    dve.wait_ge(S["s_ps"], NG4 * t + c + 1)
                    dve.tensor_reduce(out=negm[:, c % 2, :], in_=PS[:, c % 2, :].rearrange("p (i t) -> p i t", i=G4),
                                      axis=AX.X, op=ALU.max, negate=True).then_inc(S["negm_ready"], 1)

                def diagonals(t, c):
                    w = c % 2
                    dve.wait_ge(S["exp_done"], NG4 * t + c + 1)
                    link.start(t, c)
                    link(dve.reciprocal(out=rz[:, w, :], in_=z[:, w, :]))
                    for i in range(G4):
                        last = dve.tensor_scalar(out=diag[:, w, i, :], in0=core.ident[:, :], scalar1=rz[:, w, i:i + 1],
                                                 scalar2=None, op0=ALU.mult)
                    last.then_inc(S["diag_ready"], 1)

                def add(t):
                    dve.wait_ge(S["out_ps"], t + 1)
                    dve.wait_ge(S["biased"], t + 1)
                    dve.tensor_tensor(out=X[:, bass.ds(t, 1), :], in0=X[:, bass.ds(t, 1), :], in1=PS[:, 7, 0:D],
                                      op=ALU.add).then_inc(S["added"], 1)
                    dve.wait_ge(S["added"], t + 2)
                    tile_statistics(core, dve, X, t)

                def first(t, u):
                    tokens(t)
                    project(t, u)
                    maxima(t, 0)
                    maxima(t, 1)
                    diagonals(t, 0)

                def body(t, u, prev, more):
                    for c in range(NG4):
                        if c == 0 and more:
                            tokens(t + 1)
                        dve.wait_ge(S["pt_ps"], NG4 * t + c + 1)
                        dve.tensor_copy(PT[:, c % 2, :, :],
                                        PS[:, 2 + c % 2, :].rearrange("p (i t) -> p i t", i=G4)).then_inc(S["pt_ready"], 1)
                        if c + 1 < NG4:
                            diagonals(t, c + 1)
                        elif more:
                            diagonals(t + 1, 0)
                        if c + 2 < NG4:
                            maxima(t, c + 2)
                        elif more:
                            maxima(t + 1, c + 2 - NG4)
                        if c == 0 and more:
                            project(t + 1, 1 - u)
                        if c == 2 and prev:
                            add(t - 1)

                def finish(t, u):
                    add(t)

                overlapped(dve, NT, first, body, finish)


E4 = 16
TOP = 4
INTER = 176
SHARED = 352
CAP = P


def routed_experts(core):
    nc = core.nc
    with ExitStack() as keep:
        def sb(tag, shape, dt=F32):
            return keep.enter_context(nc.sbuf_tensor("re_" + tag, shape, dt))

        R = sb("R", [P, DH, E4])
        logits = sb("logits", [P, NT, E4])
        place = sb("place", [P, E4], I32)
        weight = sb("weight", [P, E4])
        Wgu = sb("Wgu", [P, E4, DH, 2 * INTER])
        Wd = sb("Wd", [INTER // 2, E4, 2, D])
        shared_expert(core, R, logits)
        route_top4(core, logits, place, weight, Wgu, Wd)
        run_experts(core, place, weight, Wgu, Wd)


def shared_expert(core, R, logits):
    size = blocks(SHARED)
    M = len(size)

    def prepare(sb, sem, Wg, Wu, Wd, w_ready):
        zero = sb("zero", [P, D])
        loaded, zeroed = sem("loaded"), sem("zeroed")

        def load(sp):
            full = (M - 1) * P
            for w, name in ((Wg, "sw_gate"), (Wu, "sw_up")):
                sp.dma_start(w[:, :, :], core.dram[name].rearrange("(h p) e -> p h e", p=P)).then_inc(loaded, 16)
            sp.dma_start(Wd[:, 0:M - 1, :], core.dram["sw_down"][0:full, :].rearrange("(m p) e -> p m e", p=P)).then_inc(loaded, 16)
            sp.dma_start(Wd[0:size[-1], M - 1, :], core.dram["sw_down"][full:SHARED, :]).then_inc(loaded, 16)
            sp.dma_start(R[:, :, :], core.dram["gateT"].rearrange("(h p) e -> p h e", p=P)).then_inc(loaded, 16)
            sp.wait_ge(zeroed, 1)
            sp.dma_start(core.rows_x[N:N + P, :], zero[:, :]).then_inc(loaded, 16)
            sp.dma_start(core.rows_y[N:N + P, :], zero[:, :]).then_inc(loaded, 16)

        def make(dve):
            dve.memset(zero[:, :], 0.0).then_inc(zeroed, 1)
            dve.wait_ge(loaded, 7 * 16)
            dve.sem_inc(w_ready, 1)

        return load, make

    gated_ffn(core, "se", SHARED, prepare, {"W": R, "E": E4, "logits": logits, "rows": core.rows_x[0:N, :]})


def route_top4(core, logits, place, weight, Wgu, Wd):
    nc, X, PS = core.nc, core.X, core.PS
    C = 6
    with core.stage("r4") as (sb, sem):
        iota_e = sb("iota_e", [P, NT, E4])
        iota_p = sb("iota_p", [P, P, E4], BF16)
        row_i = sb("row_i", [P, 3], I32)
        row_f = sb("row_f", [P, 3])
        col_l = sb("col_l", [P, TL, B])
        col_s = sb("col_s", [P, TL, B])
        same_s = sb("same_s", [P, P])
        later_l = sb("later_l", [P, P])
        later_s = sb("later_s", [P, P])
        here = sb("here", [P, P], BF16)
        behind = sb("behind", [P, P], BF16)
        beyond = sb("beyond", [P, P], BF16)
        prob = sb("prob", [P, NT, E4])
        work = sb("work", [P, NT, E4])
        top = sb("top", [P, NT])
        best = sb("best", [P, NT, 8])
        index = sb("index", [P, NT, 8], U32)
        index_f = sb("index_f", [P, NT, 8])
        chosen = sb("chosen", [P, E4, NT])
        chosen_b = sb("chosen_b", [P, 3, E4, NT], BF16)
        reset = sb("reset", [P, E4, NT])
        upto = sb("upto", [P, E4, NT])
        rank = sb("rank", [P, E4, NT])
        rank_b = sb("rank_b", [P, NT, E4], BF16)
        wts = sb("wts", [P, NT, E4])
        rest = sb("rest", [P, NT, E4])
        tell = sb("tell", [P, NT, E4, C], BF16)
        tile_no = sb("tile_no", [P, NT, E4])
        part_no = sb("part_no", [P, NT, E4])
        hit = sb("hit", [P, 4, P, E4], BF16)
        zero = sb("zero", [P, P], BF16)
        tell_now = sb("tell_now", [P, 4, E4, C], BF16)
        told_rows = sb("told_rows", [C, E4 * P])
        told = sb("told", [P, E4, C])
        spare = sb("spare", [P, 4, E4])
        S = {n: sem(n) for n in "made shifted exp_done masks_ready chosen_ready rank_ps own tell_ready hit_ready hit_used w_loaded tell_copied gathered rows_ready told_ps x_stored".split()}
        with nc.Block() as block:
            @block.sync
            def _(sp):
                rows = core.rows_y[0:N, :].rearrange("(n p) d -> p n d", p=P)
                for k in range(4):
                    sp.dma_start(rows[:, 8 * k:8 * k + 8, :], X[:, 8 * k:8 * k + 8, :]).then_inc(S["x_stored"], 16)
                Q = E4 // 4
                down = core.dram["w_down"].rearrange("e (k p) d -> p (e k) d", k=2)
                for c in range(0, E4, Q):
                    for k, name in enumerate(("w_gate", "w_up")):
                        sp.dma_start(Wgu[:, c:c + Q, :, k * INTER:(k + 1) * INTER].rearrange("p e h i -> p (e h) i"),
                                     core.dram[name][c:c + Q].rearrange("e (h p) i -> p (e h) i", p=P)).then_inc(S["w_loaded"], 16)
                    sp.dma_start(Wd[:, c:c + Q, :, :].rearrange("p e k d -> p (e k) d"),
                                 down[:, 2 * c:2 * c + 2 * Q, :]).then_inc(S["w_loaded"], 16)
                sp.wait_ge(S["x_stored"], 4 * 16)
                sp.wait_ge(S["w_loaded"], 3 * 4 * 16)

            @block.gpsimd
            def _(pool):
                made = S["made"]
                loose = dict(allow_small_or_imprecise_dtypes=True)
                pool.iota(iota_e[:, :, :], [[0, NT], [1, E4]], base=0, channel_multiplier=0, **loose).then_inc(made, 1)
                pool.iota(iota_p[:, :, :], [[1, P], [0, E4]], base=0, channel_multiplier=0, **loose).then_inc(made, 1)
                pool.iota(row_i[:, :], [[0, 3]], base=0, channel_multiplier=1).then_inc(made, 1)
                pool.iota(col_l[:, :, :], [[1, TL], [0, B]], base=0, channel_multiplier=0, **loose).then_inc(made, 1)
                pool.iota(col_s[:, :, :], [[0, TL], [1, B]], base=0, channel_multiplier=0, **loose).then_inc(made, 1)
                pool.iota(tile_no[:, :, :], [[1, NT], [0, E4]], base=0, channel_multiplier=0, **loose).then_inc(made, 1)
                pool.iota(part_no[:, :, :], [[0, NT], [0, E4]], base=0, channel_multiplier=1, **loose).then_inc(made, 1)
                pool.memset(zero[:, :], 0.0).then_inc(made, 1)
                pool.memset(reset[:, :, :], 1.0).then_inc(made, 1)
                pool.wait_ge(made, 9)
                pool.memset(reset[:, :, 0:1], 0.0).then_inc(made, 1)

            @block.scalar
            def _(act):
                act.wait_ge(S["shifted"], 1)
                act.activation(prob[:, :, :], prob[:, :, :], ACT.Exp).then_inc(S["exp_done"], 1)
                act.wait_ge(S["tell_ready"], 1)
                with act.Fori(0, NT // 4) as i:
                    for k in range(4):
                        act.wait_ge(S["hit_used"], 4 * i + k + 1)
                        act.activation(tell_now[:, k, :, :], tell[:, bass.ds(4 * i + k, 1), :, :].rearrange("p n e c -> p (n e) c"),
                                       ACT.Copy).then_inc(S["tell_copied"], 1)
                act.wait_ge(S["gathered"], 1)
                act.activation(told_rows[:, :].rearrange("c (n t) -> c n t", n=4), PS[0:C, 1:5, :],
                               ACT.Copy).then_inc(S["rows_ready"], 1)

            @block.tensor
            def _(pe):
                pe.wait_ge(S["masks_ready"], 1)
                pe.wait_ge(S["chosen_ready"], 1)
                for k, m in enumerate((here, behind, beyond)):
                    last = pe.matmul(PS[:, 0, :], m[:, :], chosen_b[:, k, :, :], start=(k == 0), stop=(k == 2))
                last.then_inc(S["rank_ps"], 1)
                pe.wait_ge(S["tell_ready"], 1)
                for bank in range(1, 5):
                    pe.matmul(PS[0:C, bank, 0:P], zero[:, 0:C], zero[:, :], start=True, stop=False, skip_group_check=True)

                with pe.Fori(0, NT // 4) as i:
                    for k in range(4):
                        pe.wait_ge(S["hit_ready"], 4 * i + k + 1)
                        pe.wait_ge(S["tell_copied"], 4 * i + k + 1)
                        for e in range(E4):
                            last = pe.matmul(PS[0:C, 1 + e // 4, e % 4 * P:e % 4 * P + P], tell_now[:, k, e, :],
                                             hit[:, k, :, e], start=False, stop=False, skip_group_check=True)
                        last.then_inc(S["hit_used"], 1)

                for bank in range(1, 5):
                    last = pe.matmul(PS[0:C, bank, 0:P], zero[:, 0:C], zero[:, :], start=False, stop=True,
                                     skip_group_check=True)
                last.then_inc(S["gathered"], 1)
                pe.wait_ge(S["rows_ready"], 1)
                for e in range(E4):
                    last = pe.transpose(PS[:, 5, e * C:e * C + C], told_rows[:, e * P:e * P + P], core.ident[0:C, 0:C])
                last.then_inc(S["told_ps"], 1)

            @block.vector
            def _(dve):
                link = Chain(dve, S["own"], 90)

                def over_e(a):
                    return a.rearrange("p (n e) -> p n e", e=1).broadcast_to([P, NT, E4])

                dve.wait_ge(S["made"], 10)
                link(dve.tensor_single_scalar(out=row_i[:, 1:2], in_=row_i[:, 0:1], scalar=4, op=ALU.arith_shift_right))
                link(dve.tensor_single_scalar(out=row_i[:, 2:3], in_=row_i[:, 0:1], scalar=B - 1, op=ALU.bitwise_and))
                link(dve.tensor_copy(row_f[:, :], row_i[:, :]))
                cl, cs = (c[:, :, :].rearrange("p l s -> p (l s)") for c in (col_l, col_s))
                link(dve.tensor_scalar(out=later_s[:, :], in0=cs, scalar1=row_f[:, 2:3], scalar2=None, op0=ALU.is_gt))
                link(dve.tensor_scalar(out=same_s[:, :], in0=cs, scalar1=row_f[:, 2:3], scalar2=None, op0=ALU.is_equal))
                link(dve.tensor_scalar(out=later_l[:, :], in0=cl, scalar1=row_f[:, 1:2], scalar2=None, op0=ALU.is_gt))
                link(dve.tensor_copy(beyond[:, :], later_s[:, :]))
                link(dve.tensor_tensor(out=behind[:, :], in0=later_s[:, :], in1=same_s[:, :], op=ALU.add))
                link(dve.tensor_tensor(out=later_l[:, :], in0=later_l[:, :], in1=same_s[:, :], op=ALU.mult))
                link(dve.tensor_tensor(out=here[:, :], in0=later_s[:, :], in1=later_l[:, :], op=ALU.add))
                dve.sem_inc(S["masks_ready"], 1)
                link(dve.tensor_reduce(out=top[:, :], in_=logits[:, :, :], axis=AX.X, op=ALU.max))
                link(dve.tensor_tensor(out=prob[:, :, :], in0=logits[:, :, :], in1=over_e(top[:, :]), op=ALU.subtract))
                dve.sem_inc(S["shifted"], 1)
                dve.wait_ge(S["exp_done"], 1)
                link(dve.tensor_reduce(out=top[:, :], in_=prob[:, :, :], axis=AX.X, op=ALU.add))
                link(dve.reciprocal(out=top[:, :], in_=top[:, :]))
                link(dve.tensor_tensor(out=prob[:, :, :], in0=prob[:, :, :], in1=over_e(top[:, :]), op=ALU.mult))
                for t in range(NT):
                    last = dve.max(out=best[:, t, :], in_=prob[:, t, :])
                link(last)
                for t in range(NT):
                    last = dve.max_index(out=index[:, t, :], in_max=best[:, t, :], in_values=prob[:, t, :])
                link(last)
                link(dve.tensor_copy(index_f[:, :, :], index[:, :, :]))
                c_view = chosen[:, :, :].rearrange("p e n -> p n e")
                link(dve.tensor_tensor(out=c_view, in0=iota_e[:, :, :], in1=over_e(index_f[:, :, 0]), op=ALU.is_equal))
                for k in range(1, TOP):
                    link(dve.tensor_tensor(out=work[:, :, :], in0=iota_e[:, :, :], in1=over_e(index_f[:, :, k]), op=ALU.is_equal))
                    link(dve.tensor_tensor(out=c_view, in0=c_view, in1=work[:, :, :], op=ALU.add))
                link(dve.tensor_reduce(out=top[:, :], in_=best[:, :, 0:TOP], axis=AX.X, op=ALU.add))
                link(dve.tensor_scalar(out=top[:, :], in0=top[:, :], scalar1=1e-20, scalar2=None, op0=ALU.add))
                link(dve.reciprocal(out=top[:, :], in_=top[:, :]))
                link(dve.tensor_tensor(out=wts[:, :, :], in0=prob[:, :, :], in1=over_e(top[:, :]), op=ALU.mult))
                flat = lambda a: a[:, :, :].rearrange("p e n -> p (e n)")
                link(dve.tensor_copy(chosen_b[:, 0, :, :], chosen[:, :, :]))
                link(dve.tensor_tensor_scan(out=flat(upto), data0=flat(reset), data1=flat(chosen), initial=0.0,
                                            op0=ALU.mult, op1=ALU.add))
                link(dve.tensor_tensor(out=chosen_b[:, 1, :, :], in0=upto[:, :, :], in1=chosen[:, :, :], op=ALU.subtract))
                total = upto[:, :, NT - 1:NT].broadcast_to([P, E4, NT])
                link(dve.tensor_tensor(out=chosen_b[:, 2, :, :], in0=total, in1=upto[:, :, :], op=ALU.subtract))
                dve.sem_inc(S["chosen_ready"], 1)
                dve.wait_ge(S["rank_ps"], 1)
                link(dve.tensor_scalar(out=rank[:, :, :], in0=PS[:, 0, :].rearrange("p (e n) -> p e n", e=E4),
                                       scalar1=float(CAP), scalar2=1.0, op0=ALU.min, op1=ALU.add))
                link(dve.tensor_tensor(out=rank[:, :, :], in0=rank[:, :, :], in1=chosen[:, :, :], op=ALU.mult))
                link(dve.tensor_scalar(out=rank_b[:, :, :], in0=rank[:, :, :].rearrange("p e n -> p n e"), scalar1=1.0,
                                       scalar2=None, op0=ALU.subtract))
                link(dve.tensor_copy(tell[:, :, :, 0], tile_no[:, :, :]))
                link(dve.tensor_copy(tell[:, :, :, 1], part_no[:, :, :]))
                link(dve.memset(tell[:, :, :, 2], 1.0))
                link(dve.tensor_copy(tell[:, :, :, 3], wts[:, :, :]))
                link(dve.tensor_tensor(out=rest[:, :, :], in0=wts[:, :, :], in1=tell[:, :, :, 3], op=ALU.subtract))
                link(dve.tensor_copy(tell[:, :, :, 4], rest[:, :, :]))
                link(dve.tensor_tensor(out=tell[:, :, :, 5], in0=rest[:, :, :], in1=tell[:, :, :, 4], op=ALU.subtract))
                dve.sem_inc(S["tell_ready"], 1)
                dve.sem_inc(S["hit_used"], 4)
                with dve.Fori(0, NT // 4) as i:
                    for k in range(4):
                        dve.wait_ge(S["hit_used"], 4 * i + k + 1)
                        dve.tensor_tensor(out=hit[:, k, :, :], in0=iota_p[:, :, :],
                                          in1=rank_b[:, bass.ds(4 * i + k, 1), :].broadcast_to([P, P, E4]),
                                          op=ALU.is_equal).then_inc(S["hit_ready"], 1)

                dve.wait_ge(S["told_ps"], 1)
                link(dve.tensor_copy(told[:, :, :], PS[:, 5, 0:E4 * C].rearrange("p (e c) -> p e c", e=E4)))
                link(dve.tensor_scalar(out=spare[:, 0, :], in0=told[:, :, 0], scalar1=float(P), scalar2=None, op0=ALU.mult))
                link(dve.tensor_tensor(out=spare[:, 0, :], in0=spare[:, 0, :], in1=told[:, :, 1], op=ALU.add))
                link(dve.tensor_scalar(out=spare[:, 1, :], in0=told[:, :, 2], scalar1=-1.0, scalar2=-1.0, op0=ALU.add, op1=ALU.mult))
                link(dve.tensor_scalar(out=spare[:, 2, :], in0=part_no[:, 0, :], scalar1=float(N), scalar2=None, op0=ALU.add))
                link(dve.tensor_tensor(out=spare[:, 1, :], in0=spare[:, 1, :], in1=spare[:, 2, :], op=ALU.mult))
                link(dve.tensor_tensor(out=place[:, :], in0=spare[:, 0, :], in1=spare[:, 1, :], op=ALU.add))
                link(dve.tensor_tensor(out=spare[:, 3, :], in0=told[:, :, 4], in1=told[:, :, 5], op=ALU.add))
                link(dve.tensor_tensor(out=weight[:, :], in0=told[:, :, 3], in1=spare[:, 3, :], op=ALU.add))


def run_experts(core, place, weight, Wgu, Wd):
    nc, PS = core.nc, core.PS
    IH = INTER // 2
    with core.stage("rx") as (sb, sem):
        xg = sb("xg", [P, 2, D])
        xT = sb("xT", [P, 2, DH, P])
        sg = sb("sg", [P, 2, INTER])
        mid = sb("mid", [P, 2, INTER])
        mT = sb("mT", [IH, 2, 2, P])
        y = sb("y", [P, 2, D])
        S = {n: sem(n) for n in "g_used xt_ps xt_ready gu_ps silu mid_ready mt_ps mt_ready y_ps y_ready y_free own added copied".split()}
        x_in = [sem(f"x_in{k}") for k in range(2)]
        with nc.Block() as block:
            @block.sync
            def _(sp):
                sp.wait_ge(S["added"], 16 * E4)
                out = core.dram["out"].rearrange("(s g l) d -> l g s d", s=B, l=TL)
                rows = core.rows_y[0:N, :].rearrange("(g l s) d -> l g s d", l=TL, s=B)
                for tl in range(TL):
                    sp.dma_start(out[tl], rows[tl]).then_inc(S["copied"], 16)
                sp.wait_ge(S["copied"], 16 * TL)

            @block.gpsimd
            def _(pool):
                def gather(e):
                    pool.wait_ge(S["g_used"], e + 1)
                    pool.indirect_dma_start(out=xg[:, e % 2, :], out_offset=None, in_=core.rows_x[:, :],
                                            in_offset=bass.IndirectOffsetOnAxis(ap=place[:, e:e + 1], axis=0)).then_inc(x_in[e % 2], 16)

                gather(0)
                gather(1)
                for e in range(E4):
                    if e + 2 < E4:
                        gather(e + 2)
                    pool.wait_ge(S["y_ready"], e + 3)
                    if e:
                        pool.wait_ge(S["added"], 16 * e)
                        pool.sem_inc(S["y_free"], 1)
                    pool.indirect_dma_start(out=core.rows_y[:, :], out_offset=bass.IndirectOffsetOnAxis(ap=place[:, e:e + 1], axis=0),
                                            in_=y[:, e % 2, :], in_offset=None, compute_op=ALU.add).then_inc(S["added"], 16)

            @block.tensor
            def _(pe):
                def turn_in(e, u, i):
                    pe.wait_ge(x_in[u], 16 * i + 16)
                    for h in range(DH):
                        last = pe.transpose(PS[:, 0, h * P:h * P + P], xg[:, u, h * P:h * P + P], core.ident[:, :])
                    last.then_inc(S["xt_ps"], 1)

                def expand(e, u):
                    pe.wait_ge(S["xt_ready"], e + 1)
                    for h in range(DH):
                        last = pe.matmul(PS[:, 1 + u, 0:2 * INTER], xT[:, u, h, :], Wgu[:, bass.ds(e, 1), h, :], start=(h == 0), stop=(h == DH - 1))
                    last.then_inc(S["gu_ps"], 1)

                def turn_mid(e, u):
                    pe.wait_ge(S["mid_ready"], e + 1)
                    for k in range(2):
                        last = pe.transpose(PS[0:IH, 3, k * P:k * P + P], mid[:, u, k * IH:k * IH + IH], core.ident[:, :])
                    last.then_inc(S["mt_ps"], 1)

                def contract(e, u):
                    pe.wait_ge(S["mt_ready"], e + 1)
                    pe.wait_ge(S["y_ready"], e + 1)
                    for k in range(2):
                        last = pe.matmul(PS[:, 4 + u, 0:D], mT[:, u, k, :], Wd[:, bass.ds(e, 1), k, :], start=(k == 0), stop=(k == 1))
                    last.then_inc(S["y_ps"], 1)

                def step(e, u, i, more):
                    if more:
                        turn_in(e + 1, 1 - u, i + u)
                    turn_mid(e, u)
                    if more:
                        expand(e + 1, 1 - u)
                    contract(e, u)

                turn_in(0, 0, 0)
                expand(0, 0)
                with pe.Fori(0, E4 // 2 - 1) as i:
                    step(2 * i, 0, i, True)
                    step(2 * i + 1, 1, i, True)
                step(E4 - 2, 0, E4 // 2 - 1, True)
                step(E4 - 1, 1, E4 // 2 - 1, False)

            @block.scalar
            def _(act):
                act.sem_inc(S["g_used"], 2)
                act.sem_inc(S["y_free"], 2)
                act.sem_inc(S["y_ready"], 2)

                def turn_in(e, u):
                    act.wait_ge(S["xt_ps"], e + 1)
                    act.sem_inc(S["g_used"], 1)
                    act.activation(xT[:, u, :, :], PS[:, 0, 0:D].rearrange("p (h t) -> p h t", h=DH),
                                   ACT.Copy).then_inc(S["xt_ready"], 1)

                def expand(e, u):
                    act.wait_ge(S["gu_ps"], e + 1)
                    act.activation(sg[:, u, :], PS[:, 1 + u, 0:INTER], ACT.Silu).then_inc(S["silu"], 1)

                def first(e, u):
                    turn_in(e, u)
                    expand(e, u)

                def body(e, u, more):
                    if more:
                        turn_in(e + 1, 1 - u)
                    act.wait_ge(S["mt_ps"], e + 1)
                    act.activation(mT[:, u, :, :], PS[0:IH, 3, 0:2 * P].rearrange("p (k t) -> p k t", k=2),
                                   ACT.Copy).then_inc(S["mt_ready"], 1)
                    if more:
                        expand(e + 1, 1 - u)
                    act.wait_ge(S["y_ps"], e + 1)
                    act.wait_ge(S["y_free"], e + 1)
                    act.activation(y[:, u, :], PS[:, 4 + u, 0:D], ACT.Copy, scale=weight[:, bass.ds(e, 1)]).then_inc(S["y_ready"], 1)

                ahead(act, E4, first, body)

            @block.vector
            def _(dve):
                def step(e, u):
                    dve.wait_ge(S["silu"], e + 1)
                    dve.tensor_tensor(out=mid[:, u, :], in0=sg[:, u, :], in1=PS[:, 1 + u, INTER:2 * INTER],
                                      op=ALU.mult).then_inc(S["mid_ready"], 1)

                in_pairs(dve, E4, step)


STAGES = [rwkv, ternary_and_latent, quantised_ffn, double_attention, masked_experts, crossed_attention, routed_experts]


def program(nc, dram):
    with ExitStack() as stack:
        core = Core(nc, dram, stack)
        load_x(core)
        constants(core)
        for stage in STAGES:
            stage(core)


def load_x(core):
    CH = 4
    with core.stage("load") as (sb, sem):
        loaded = [sem(f"loaded{k}") for k in range(NT // CH)]
        with core.nc.Block() as block:
            @block.sync
            def _(sp):
                x = core.dram["x"].rearrange("(n p) d -> p n d", p=P)
                for k in range(NT // CH):
                    sp.dma_start(core.X[:, CH * k:CH * k + CH, :], x[:, CH * k:CH * k + CH, :]).then_inc(loaded[k], 16)

            @block.vector
            def _(dve):
                for k in range(NT // CH):
                    dve.wait_ge(loaded[k], 16)
                    tile_statistics(core, dve, core.X, CH * k, CH)


def halves(v):
    return np.ascontiguousarray(np.asarray(v).reshape(DH, P).T)


def rows(v):
    v = np.asarray(v).reshape(1, -1)
    return np.ascontiguousarray(np.broadcast_to(v, (P, v.shape[1])))


def layouts(a):
    t = lambda n: np.ascontiguousarray(np.asarray(a[n]).T)
    d = {
        "x": np.asarray(a["L0_attn_x"]).reshape(N, D),
        "WkT": t("L0_attn_Wk"), "WvT": t("L0_attn_Wv"), "WrT": t("L0_attn_Wr"), "WoT": t("L0_attn_Wo"),
        "tm": np.stack([halves(a[f"L0_attn_tm_{c}"]) for c in "kvr"], 1),
        "time_decay": halves(a["L0_attn_time_decay"]), "time_first": halves(a["L0_attn_time_first"]),
        "ln_g": rows(a["L0_attn_ln_g"]), "ln_b": rows(a["L0_attn_ln_b"]),
    }
    half = lambda w: np.concatenate([w[..., 0::2], w[..., 1::2]], -1)
    wqb = np.asarray(a["L1_attn_Wqb"]).reshape(QL, HEADS, NOPE + ROPE)
    wkvb = np.asarray(a["L1_attn_Wkvb"]).reshape(KL, HEADS, NOPE + VDIM)
    wkva = np.asarray(a["L1_attn_Wkva"])
    angle = (np.arange(T, dtype=np.float32)[:, None]
             * (1.0 / 10000.0 ** (np.arange(0, ROPE, 2, dtype=np.float32) / ROPE)).astype(np.float32)[None, :])
    cos, sin = np.cos(angle).astype(np.float32), np.sin(angle).astype(np.float32)
    d.update({
        "WtT": t("L0_ffn_weight"), "t_bias": rows(a["L0_ffn_bias"]),
        "Wqb_nopeT": wqb[:, :, :NOPE].transpose(2, 1, 0), "Wqb_rope": half(wqb[:, :, NOPE:]),
        "Wkvb_kT": wkvb[:, :, :NOPE].transpose(2, 1, 0), "Wkvb_vT": wkvb[:, :, NOPE:].transpose(2, 1, 0),
        "Wo_heads": np.asarray(a["L1_attn_Wo"]).reshape(HEADS, VDIM, D).transpose(1, 0, 2),
        "q_ln_w": np.asarray(a["L1_attn_q_ln_w"]).reshape(QL, 1), "kv_ln_w": rows(a["L1_attn_kv_ln_w"]),
        "Wa": np.concatenate([np.asarray(a["L1_attn_Wqa"]), wkva[:, :KL], half(wkva[:, KL:])], 1),
        "cos": np.concatenate([cos, cos], 1), "sin": np.concatenate([-sin, sin], 1),
        "wq_gateT": t("L1_ffn_wq_gate"), "wq_upT": t("L1_ffn_wq_up"), "wq_downT": t("L1_ffn_wq_down"),
        "s_gate": rows(a["L1_ffn_s_gate"]), "s_up": rows(a["L1_ffn_s_up"]), "s_down": rows(a["L1_ffn_s_down"]),
    })
    d.update({
        "W2T": t("L2_attn_W"), "W2": np.asarray(a["L2_attn_W"]),
        "g2": np.concatenate([rows(np.tile(np.asarray(a[f"L2_attn_g{n}"]), HEADS)) for n in (1, 2, 3)], 1),
    })
    d.update({
        "router": t("L2_ffn_router_w"), "W3T": t("L2_ffn_weight"), "scale": rows(a["L2_ffn_scale"]),
        "masks": np.asarray(a["L2_ffn_expert_masks"]).transpose(0, 2, 1),
    })
    w = np.asarray(a["L3_attn_w_qkv"]).reshape(HEADS, 3, HD, D).transpose(3, 1, 0, 2).reshape(D, 3 * D)
    b = np.asarray(a["L3_attn_b_qkv"]).reshape(HEADS, 3, HD).transpose(1, 0, 2).reshape(-1)
    d.update({
        "w_qkvT": w, "b_qkv": rows(b), "w_denseT": t("L3_attn_w_dense"), "b_dense": rows(a["L3_attn_b_dense"]),
        "gateT": t("L3_ffn_gate_w"),
        **{n: np.asarray(a["L3_ffn_" + n]) for n in ("w_gate", "w_up", "w_down", "sw_gate", "sw_up", "sw_down")},
    })
    return d


def kernel(**inputs):
    import concourse.bacc as bacc
    from concourse.bass_utils import run_bass_kernel_spmd

    nc = bacc.Bacc("TRN2", target_bir_lowering=False, num_devices=1)
    arrays, dram = {}, {}
    for name, a in layouts(inputs).items():
        a = np.ascontiguousarray(a)
        arrays[f"in_{name}_dram"] = a
        dram[name] = nc.dram_tensor(f"in_{name}_dram", a.shape, mybir.dt.from_np(a.dtype), kind="ExternalInput").ap()
    dram["out"] = nc.dram_tensor("out_0_dram", (N, D), F32, kind="ExternalOutput").ap()
    program(nc, dram)
    r = run_bass_kernel_spmd(nc, [arrays], core_ids=[0])
    return r.results[0]["out_0_dram"].reshape(B, T, D)
```
